# Optimizing a Trainium2 kernel written in Bass

```python
import numpy as np
import jax
import jax.numpy as jnp

def _softmax(x, axis=-1):
    return jax.nn.softmax(x, axis=axis)

def _gelu(x):
    return jax.nn.gelu(x, approximate=True)

def _silu(x):
    return jax.nn.silu(x)

def _sigmoid(x):
    return jax.nn.sigmoid(x)

def _layernorm(x, axis=-1, eps=1e-05):
    m = jnp.mean(x, axis=axis, keepdims=True)
    v = jnp.var(x, axis=axis, keepdims=True)
    return (x - m) / jnp.sqrt(v + eps)

def _scatter_add(tgt, idx, src, axis=0):
    return tgt.at[idx].add(src)

def _segment_sum(src, seg, n):
    return jax.ops.segment_sum(src, seg, n)
kernel_name = 'mk_perceiver_d4_seqx_r8_ad24fa'

def setup_inputs(seed: int=0):
    np.random.seed(seed)
    _w = jnp.asarray

    def _rec_inputs():
        import jax
        import jax.numpy as jnp
        _rk = jax.random.key(seed)
        x = 7.22e-05 + 1 * jax.random.normal(jax.random.fold_in(_rk, 1), (128, 32, 128), jnp.float32)
        _lenS = 32 - jax.random.randint(jax.random.fold_in(_rk, 7), (128,), 0, max(1, 32 // 4) + 1, jnp.int32)
        _lenS2 = 257 - jax.random.randint(jax.random.fold_in(_rk, 8), (128,), 0, max(1, 257 // 4) + 1, jnp.int32)
        _ctx_1024P = jax.random.normal(jax.random.fold_in(_rk, 11), (128, 16, 128), jnp.float32)
        _ctx_1024c = jax.random.dirichlet(jax.random.fold_in(_rk, 511), 0.3 * jnp.ones((16,), jnp.float32), (128, 257))
        _ctx_1024t = jnp.einsum('bsk,bkd->bsd', _ctx_1024c, _ctx_1024P)
        _ctx_1024t = _ctx_1024t * jax.lax.rsqrt(jnp.mean(jnp.square(_ctx_1024t)) + 1e-12) * 0.953939
        ctx_1024 = 4.13588e-05 + 0.999923 * (_ctx_1024t + 0.3 * jax.random.normal(jax.random.fold_in(_rk, 611), (128, 257, 128), jnp.float32))
        _validS = jnp.arange(32)[None, :] < _lenS[:, None]
        _validS2 = jnp.arange(257)[None, :] < _lenS2[:, None]
        _causal = jnp.tril(jnp.ones((32, 32), dtype=bool))
        mask_Bx1xSxS2_bf0 = jnp.logical_not(jnp.ones((128, 1, 32, 257), dtype=bool))
        mask_Bx1xSxS2_if1 = jnp.where(jnp.ones((128, 1, 32, 257), dtype=bool), 1, 0).astype(jnp.int32)
        return (x, ctx_1024, mask_Bx1xSxS2_bf0, mask_Bx1xSxS2_if1)
    x, ctx_1024, mask_Bx1xSxS2_bf0, mask_Bx1xSxS2_if1 = _rec_inputs()

    def _L0_xattn_setup():
        import jax, jax.numpy as jnp
        import numpy as np
        N_HEAD = 16
        key = jax.random.key(seed)
        ks = jax.random.split(key, 5)
        b, l, d = (4, 256, 128)
        dh = d // N_HEAD
        return {'q': jax.random.normal(ks[0], (b, l, d), dtype=jnp.float32), 'kv': jax.random.normal(ks[1], (b, l, d), dtype=jnp.float32), 'Wq': jax.random.normal(ks[2], (d, d), dtype=jnp.float32) * 0.02, 'Wkv': jax.random.normal(ks[3], (2 * dh, d), dtype=jnp.float32) * 0.02, 'Wc': jax.random.normal(ks[4], (d, d), dtype=jnp.float32) * 0.02}
    _L0_xattn_all = _L0_xattn_setup()
    _L0_xattn_in = {k: v for k, v in _L0_xattn_all.items() if k in ('Wq', 'Wkv', 'Wc')}
    del _L0_xattn_all

    def _L0_attn_setup():
        import jax, jax.numpy as jnp
        import numpy as np
        D_MODEL = 128
        N_HEADS = 16
        HEAD_DIM = D_MODEL // N_HEADS
        WINDOW = 128

        def _window_starts(seq_len, window):
            starts = []
            for i in range(0, seq_len, window // 2):
                end = min(i + window, seq_len)
                starts.append(max(0, end - window))
                if end == seq_len:
                    break
            return np.asarray(starts, dtype=np.int32)
        key = jax.random.key(seed)
        ks = jax.random.split(key, 9)
        B, S = (4, 512)
        sc = 1.0 / np.sqrt(D_MODEL)
        return {'x': jax.random.normal(ks[0], (B, S, D_MODEL), jnp.float32), 'Wq': jax.random.normal(ks[1], (D_MODEL, D_MODEL), jnp.float32) * sc, 'bq': jax.random.normal(ks[2], (D_MODEL,), jnp.float32) * 0.02, 'Wk': jax.random.normal(ks[3], (D_MODEL, D_MODEL), jnp.float32) * sc, 'bk': jax.random.normal(ks[4], (D_MODEL,), jnp.float32) * 0.02, 'Wv': jax.random.normal(ks[5], (D_MODEL, D_MODEL), jnp.float32) * sc, 'bv': jax.random.normal(ks[6], (D_MODEL,), jnp.float32) * 0.02, 'Wo': jax.random.normal(ks[7], (D_MODEL, D_MODEL), jnp.float32) * sc, 'bo': jax.random.normal(ks[8], (D_MODEL,), jnp.float32) * 0.02}
    _L0_attn_all = _L0_attn_setup()
    _L0_attn_in = {k: v for k, v in _L0_attn_all.items() if k in ('Wq', 'bq', 'Wk', 'bk', 'Wv', 'bv', 'Wo', 'bo')}
    del _L0_attn_all

    def _L0_ffn_setup():
        import jax, jax.numpy as jnp
        import numpy as np
        CAPACITY_FACTOR = 1.0

        def _route(token_inputs, Wg, capacity):
            dt = token_inputs.dtype
            logits = jnp.einsum('bnd,de->bne', token_inputs, Wg)
            gates = jax.nn.softmax(logits, axis=-1)
            expert_idx = jnp.argmax(gates, axis=-1)
            mask = jax.nn.one_hot(expert_idx, Wg.shape[1], dtype=dt)
            gate = jnp.sum(gates * mask, axis=-1)
            pos = jnp.cumsum(mask, axis=1) * mask - mask
            keep = mask * (pos < capacity).astype(dt)
            pos_oh = jax.nn.one_hot(pos.astype(jnp.int32), capacity, dtype=dt)
            dispatch = keep[..., None] * pos_oh
            combine = dispatch * gate[:, :, None, None]
            return (dispatch, combine)
        key = jax.random.key(seed)
        k1, k2, k3, k4 = jax.random.split(key, 4)
        B, N, D, E, H = (8, 256, 128, 8, 512)
        return {'token_inputs': jax.random.normal(k1, (B, N, D), dtype=jnp.float32), 'Wg': jax.random.normal(k2, (D, E), dtype=jnp.float32) * 0.02, 'W1': jax.random.normal(k3, (E, D, H), dtype=jnp.float32) * 0.02, 'W2': jax.random.normal(k4, (E, H, D), dtype=jnp.float32) * 0.02}
    _L0_ffn_all = _L0_ffn_setup()
    _L0_ffn_in = {k: v for k, v in _L0_ffn_all.items() if k in ('Wg', 'W1', 'W2')}
    del _L0_ffn_all

    def _L1_xattn_setup():
        import jax, jax.numpy as jnp
        import numpy as np
        B, S, D, H = (2, 256, 128, 16)
        HD = D // H
        LN_EPS = 1e-05

        def _linear(x, w, b):
            return jnp.einsum('bsd,od->bso', x, w) + b

        def _split_heads(x):
            b, s, _ = x.shape
            return x.reshape(b, s, H, HD).transpose(0, 2, 1, 3)
        key = jax.random.key(seed)
        ks = jax.random.split(key, 14)
        w = 0.02
        return {'q': jax.random.normal(ks[0], (B, S, D), jnp.float32), 'k': jax.random.normal(ks[1], (B, S, D), jnp.float32), 'v': jax.random.normal(ks[2], (B, S, D), jnp.float32), 'mask': jnp.zeros((B, 1, S, S), dtype=bool), 'training': 0, 'wq_w': jax.random.normal(ks[3], (D, D), jnp.float32) * w, 'wq_b': jnp.zeros((D,), jnp.float32), 'wk_w': jax.random.normal(ks[4], (D, D), jnp.float32) * w, 'wk_b': jnp.zeros((D,), jnp.float32), 'wv_w': jax.random.normal(ks[5], (D, D), jnp.float32) * w, 'wv_b': jnp.zeros((D,), jnp.float32), 'wo_w': jax.random.normal(ks[6], (D, D), jnp.float32) * w, 'wo_b': jnp.zeros((D,), jnp.float32), 'ln_g': jnp.ones((D,), jnp.float32), 'ln_b': jnp.zeros((D,), jnp.float32)}
    _L1_xattn_all = _L1_xattn_setup()
    _L1_xattn_in = {k: v for k, v in _L1_xattn_all.items() if k in ('wq_w', 'wq_b', 'wk_w', 'wk_b', 'wv_w', 'wv_b', 'wo_w', 'wo_b', 'ln_g', 'ln_b')}
    del _L1_xattn_all

    def _L1_attn_setup():
        import jax, jax.numpy as jnp
        import numpy as np
        FOCUS = 3
        EPS = 1e-06

        def _norm_last(t):
            return t / jnp.sum(t, axis=-1, keepdims=True)
        key = jax.random.key(seed)
        ks = jax.random.split(key, 6)
        B, N, C = (4, 512, 128)
        s = 0.02
        return {'x': jax.random.normal(ks[0], (B, N, C), jnp.float32), 'w_qkv': jax.random.normal(ks[1], (3 * C, C), jnp.float32) * s, 'w_proj': jax.random.normal(ks[2], (C, C), jnp.float32) * s, 'b_proj': jax.random.normal(ks[3], (C,), jnp.float32) * s, 'w_dwc': jax.random.normal(ks[4], (C, 3), jnp.float32) * s, 'b_dwc': jax.random.normal(ks[5], (C,), jnp.float32) * s}
    _L1_attn_all = _L1_attn_setup()
    _L1_attn_in = {k: v for k, v in _L1_attn_all.items() if k in ('w_qkv', 'w_proj', 'b_proj', 'w_dwc', 'b_dwc')}
    del _L1_attn_all

    def _L1_ffn_setup():
        import jax, jax.numpy as jnp
        import numpy as np
        CAP_FACTOR = 1.5
        key = jax.random.key(seed)
        ks = jax.random.split(key, 6)
        E, S, D, M = (48, 4, 128, 128)
        K = D // S
        x = jax.random.normal(ks[0], (4, 512, D), dtype=jnp.float32)
        Wr = jax.random.normal(ks[1], (E, D), dtype=jnp.float32) * 0.02
        W1 = jax.random.normal(ks[2], (E, S, D, M), dtype=jnp.float32) * (1.0 / np.sqrt(D))
        b1 = jnp.zeros((E, S, M), dtype=jnp.float32)
        W2 = jax.random.normal(ks[3], (E, S, M, K), dtype=jnp.float32) * (1.0 / np.sqrt(M))
        b2 = jnp.zeros((E, S, K), dtype=jnp.float32)
        return {'x': x, 'Wr': Wr, 'W1': W1, 'b1': b1, 'W2': W2, 'b2': b2}
    _L1_ffn_all = _L1_ffn_setup()
    _L1_ffn_in = {k: v for k, v in _L1_ffn_all.items() if k in ('Wr', 'W1', 'b1', 'W2', 'b2')}
    del _L1_ffn_all

    def _L2_xattn_setup():
        import jax, jax.numpy as jnp
        import numpy as np
        B, C_LEN, Q_LEN, D = (8, 256, 64, 128)
        key = jax.random.key(seed)
        ks = jax.random.split(key, 10)
        scale = 1.0 / np.sqrt(D)
        return {'c': jax.random.normal(ks[0], (B, C_LEN, D), dtype=jnp.float32), 'q': jax.random.normal(ks[1], (B, Q_LEN, D), dtype=jnp.float32), 'w_cq': jax.random.normal(ks[2], (D,), dtype=jnp.float32) * scale, 'b_cq': jax.random.normal(ks[3], (), dtype=jnp.float32) * scale, 'w_c': jax.random.normal(ks[4], (D,), dtype=jnp.float32) * scale, 'b_c': jax.random.normal(ks[5], (), dtype=jnp.float32) * scale, 'w_q': jax.random.normal(ks[6], (D,), dtype=jnp.float32) * scale, 'b_q': jax.random.normal(ks[7], (), dtype=jnp.float32) * scale, 'W_l': jax.random.normal(ks[8], (D, 4 * D), dtype=jnp.float32) * (1.0 / np.sqrt(4 * D)), 'b_l': jax.random.normal(ks[9], (D,), dtype=jnp.float32) * (1.0 / np.sqrt(4 * D))}
    _L2_xattn_all = _L2_xattn_setup()
    _L2_xattn_in = {k: v for k, v in _L2_xattn_all.items() if k in ('w_cq', 'b_cq', 'w_c', 'b_c', 'w_q', 'b_q', 'W_l', 'b_l')}
    del _L2_xattn_all

    def _L2_attn_setup():
        import jax, jax.numpy as jnp
        import numpy as np
        B, T, EMB, HEADS = (4, 256, 128, 16)
        CHUNK = EMB // HEADS
        key = jax.random.key(seed)
        kx, kq, kk, kv, ku = jax.random.split(key, 5)
        s = CHUNK ** (-0.5)
        return {'x': jax.random.normal(kx, (B, T, EMB), jnp.float32), 'Wq': jax.random.normal(kq, (CHUNK, CHUNK), jnp.float32) * s, 'Wk': jax.random.normal(kk, (CHUNK, CHUNK), jnp.float32) * s, 'Wv': jax.random.normal(kv, (CHUNK, CHUNK), jnp.float32) * s, 'Wu': jax.random.normal(ku, (EMB, EMB), jnp.float32) * EMB ** (-0.5), 'bu': jnp.zeros((EMB,), jnp.float32)}
    _L2_attn_all = _L2_attn_setup()
    _L2_attn_in = {k: v for k, v in _L2_attn_all.items() if k in ('Wq', 'Wk', 'Wv', 'Wu', 'bu')}
    del _L2_attn_all

    def _L2_ffn_setup():
        import jax, jax.numpy as jnp
        import numpy as np
        BLOCK = 32
        W_BITS = 4
        ACT_BITS = 16

        def act_qdq(x):
            qmax = 2.0 ** (ACT_BITS - 1) - 1.0
            scale = jnp.maximum(jnp.max(jnp.abs(x)) / qmax, 1e-12)
            return jnp.clip(jnp.round(x / scale), -qmax - 1.0, qmax) * scale

        def fixed_qdq_u16(x):
            scale = 1.0 / 65536.0
            return jnp.clip(jnp.round(x / scale), 0.0, 65535.0) * scale

        def lpbq_dequant(w):
            O, I = w.shape
            qmax = 2.0 ** (W_BITS - 1) - 1.0
            wb = w.reshape(O, I // BLOCK, BLOCK)
            s = jnp.maximum(jnp.max(jnp.abs(wb), axis=-1, keepdims=True) / qmax, 1e-12)
            wq = jnp.clip(jnp.round(wb / s), -qmax - 1.0, qmax) * s
            return wq.reshape(O, I)
        key = jax.random.key(seed)
        k1, k2, k3, k4 = jax.random.split(key, 4)
        B, S, H, I = (2, 512, 128, 384)
        x = jax.random.normal(k1, (B, S, H), jnp.float32)
        w_gate = jax.random.normal(k2, (I, H), jnp.float32) * 0.02
        w_up = jax.random.normal(k3, (I, H), jnp.float32) * 0.02
        w_down = jax.random.normal(k4, (H, I), jnp.float32) * 0.02
        return {'x': x, 'w_gate': w_gate, 'w_up': w_up, 'w_down': w_down}
    _L2_ffn_all = _L2_ffn_setup()
    _L2_ffn_in = {k: v for k, v in _L2_ffn_all.items() if k in ('w_gate', 'w_up', 'w_down')}
    del _L2_ffn_all

    def _L3_xattn_setup():
        import jax, jax.numpy as jnp
        import numpy as np
        B, S, D = (4, 256, 128)
        H = 16
        DK = D // H

        def _split_heads(x):
            b, s, _ = x.shape
            return x.reshape(b, s, H, DK).transpose(0, 2, 1, 3)
        key = jax.random.key(seed)
        ks = jax.random.split(key, 8)
        scale = 1.0 / np.sqrt(D)
        return {'q': jax.random.normal(ks[0], (B, S, D), dtype=jnp.float32), 'k': jax.random.normal(ks[1], (B, S, D), dtype=jnp.float32), 'v': jax.random.normal(ks[2], (B, S, D), dtype=jnp.float32), 'mask': jnp.ones((B, 1, S, S), dtype=jnp.int32), 'Wq': jax.random.normal(ks[3], (D, D), dtype=jnp.float32) * scale, 'bq': jnp.zeros((D,), dtype=jnp.float32), 'Wo': jax.random.normal(ks[4], (D, D), dtype=jnp.float32) * scale, 'bo': jnp.zeros((D,), dtype=jnp.float32)}
    _L3_xattn_all = _L3_xattn_setup()
    _L3_xattn_in = {k: v for k, v in _L3_xattn_all.items() if k in ('Wq', 'bq', 'Wo', 'bo')}
    del _L3_xattn_all

    def _L3_attn_setup():
        import jax, jax.numpy as jnp
        import numpy as np
        N_HEAD = 16
        N_EMBD = 128
        LOCAL_WINDOW = 32
        GLOBAL_IDX = np.array([0, 1, 2, 3], dtype=np.int64)

        def build_mask(T):
            i = np.arange(T)[:, None]
            j = np.arange(T)[None, :]
            causal = j <= i
            local = causal & (j >= i - LOCAL_WINDOW + 1)
            g_row = np.isin(np.arange(T), GLOBAL_IDX)[:, None]
            g_col = np.isin(np.arange(T), GLOBAL_IDX)[None, :]
            mask = local | g_row & causal | g_col & causal
            return jnp.asarray(mask)
        key = jax.random.key(seed)
        k1, k2, k3 = jax.random.split(key, 3)
        B, T, C = (2, 256, N_EMBD)
        x = jax.random.normal(k1, (B, T, C), dtype=jnp.float32)
        w_attn = jax.random.normal(k2, (3 * C, C), dtype=jnp.float32) * (1.0 / np.sqrt(C))
        w_proj = jax.random.normal(k3, (C, C), dtype=jnp.float32) * (1.0 / np.sqrt(C))
        return {'x': x, 'w_attn': w_attn, 'w_proj': w_proj}
    _L3_attn_all = _L3_attn_setup()
    _L3_attn_in = {k: v for k, v in _L3_attn_all.items() if k in ('w_attn', 'w_proj')}
    del _L3_attn_all

    def _L3_ffn_setup():
        import jax, jax.numpy as jnp
        import numpy as np
        D_MODEL = 128
        EXPANSION = 4
        D_HIDDEN = D_MODEL * EXPANSION
        NUM_STAGES = int(np.log2(D_HIDDEN))

        def butterfly(y, weights, dim):
            lead = y.shape[:-1]
            for stage in range(weights.shape[0]):
                s = 2 ** stage
                nb = dim // (2 * s)
                yr = y.reshape(*lead, nb, 2, s)
                a = yr[..., 0, :]
                b = yr[..., 1, :]
                w = weights[stage].reshape(nb, s, 2, 2)
                na = w[..., 0, 0] * a + w[..., 0, 1] * b
                nb2 = w[..., 1, 0] * a + w[..., 1, 1] * b
                y = jnp.stack([na, nb2], axis=-2).reshape(*lead, dim)
            return y
        key = jax.random.key(seed)
        ks = jax.random.split(key, 6)
        B, S = (4, 256)
        x = jax.random.normal(ks[0], (B, S, D_MODEL), jnp.float32)
        W_exp = jax.random.normal(ks[1], (D_MODEL, D_HIDDEN), jnp.float32) * 0.02
        b_exp = jnp.zeros((D_HIDDEN,), jnp.float32)
        up_weights = jax.random.normal(ks[2], (NUM_STAGES, D_HIDDEN // 2, 2, 2), jnp.float32) * 0.02
        up_bias = jnp.zeros((D_HIDDEN,), jnp.float32)
        down_weights = jax.random.normal(ks[3], (NUM_STAGES, D_HIDDEN // 2, 2, 2), jnp.float32) * 0.02
        W_con = jax.random.normal(ks[4], (D_HIDDEN, D_MODEL), jnp.float32) * 0.02
        b_con = jnp.zeros((D_MODEL,), jnp.float32)
        down_bias = jnp.zeros((D_MODEL,), jnp.float32)
        return dict(x=x, W_exp=W_exp, b_exp=b_exp, up_weights=up_weights, up_bias=up_bias, down_weights=down_weights, W_con=W_con, b_con=b_con, down_bias=down_bias)
    _L3_ffn_all = _L3_ffn_setup()
    _L3_ffn_in = {k: v for k, v in _L3_ffn_all.items() if k in ('W_exp', 'b_exp', 'up_weights', 'up_bias', 'down_weights', 'W_con', 'b_con', 'down_bias')}
    del _L3_ffn_all
    return {'x': x, 'ctx_1024': ctx_1024, 'mask_Bx1xSxS2_bf0': mask_Bx1xSxS2_bf0, 'mask_Bx1xSxS2_if1': mask_Bx1xSxS2_if1, 'L0_xattn_Wq': _L0_xattn_in['Wq'], 'L0_xattn_Wkv': _L0_xattn_in['Wkv'], 'L0_xattn_Wc': _L0_xattn_in['Wc'], 'L0_attn_Wq': _L0_attn_in['Wq'], 'L0_attn_bq': _L0_attn_in['bq'], 'L0_attn_Wk': _L0_attn_in['Wk'], 'L0_attn_bk': _L0_attn_in['bk'], 'L0_attn_Wv': _L0_attn_in['Wv'], 'L0_attn_bv': _L0_attn_in['bv'], 'L0_attn_Wo': _L0_attn_in['Wo'], 'L0_attn_bo': _L0_attn_in['bo'], 'L0_ffn_Wg': _L0_ffn_in['Wg'], 'L0_ffn_W1': _L0_ffn_in['W1'], 'L0_ffn_W2': _L0_ffn_in['W2'], 'L1_xattn_wq_w': _L1_xattn_in['wq_w'], 'L1_xattn_wq_b': _L1_xattn_in['wq_b'], 'L1_xattn_wk_w': _L1_xattn_in['wk_w'], 'L1_xattn_wk_b': _L1_xattn_in['wk_b'], 'L1_xattn_wv_w': _L1_xattn_in['wv_w'], 'L1_xattn_wv_b': _L1_xattn_in['wv_b'], 'L1_xattn_wo_w': _L1_xattn_in['wo_w'], 'L1_xattn_wo_b': _L1_xattn_in['wo_b'], 'L1_xattn_ln_g': _L1_xattn_in['ln_g'], 'L1_xattn_ln_b': _L1_xattn_in['ln_b'], 'L1_attn_w_qkv': _L1_attn_in['w_qkv'], 'L1_attn_w_proj': _L1_attn_in['w_proj'], 'L1_attn_b_proj': _L1_attn_in['b_proj'], 'L1_attn_w_dwc': _L1_attn_in['w_dwc'], 'L1_attn_b_dwc': _L1_attn_in['b_dwc'], 'L1_ffn_Wr': _L1_ffn_in['Wr'], 'L1_ffn_W1': _L1_ffn_in['W1'], 'L1_ffn_b1': _L1_ffn_in['b1'], 'L1_ffn_W2': _L1_ffn_in['W2'], 'L1_ffn_b2': _L1_ffn_in['b2'], 'L2_xattn_w_cq': _L2_xattn_in['w_cq'], 'L2_xattn_b_cq': _L2_xattn_in['b_cq'], 'L2_xattn_w_c': _L2_xattn_in['w_c'], 'L2_xattn_b_c': _L2_xattn_in['b_c'], 'L2_xattn_w_q': _L2_xattn_in['w_q'], 'L2_xattn_b_q': _L2_xattn_in['b_q'], 'L2_xattn_W_l': _L2_xattn_in['W_l'], 'L2_xattn_b_l': _L2_xattn_in['b_l'], 'L2_attn_Wq': _L2_attn_in['Wq'], 'L2_attn_Wk': _L2_attn_in['Wk'], 'L2_attn_Wv': _L2_attn_in['Wv'], 'L2_attn_Wu': _L2_attn_in['Wu'], 'L2_attn_bu': _L2_attn_in['bu'], 'L2_ffn_w_gate': _L2_ffn_in['w_gate'], 'L2_ffn_w_up': _L2_ffn_in['w_up'], 'L2_ffn_w_down': _L2_ffn_in['w_down'], 'L3_xattn_Wq': _L3_xattn_in['Wq'], 'L3_xattn_bq': _L3_xattn_in['bq'], 'L3_xattn_Wo': _L3_xattn_in['Wo'], 'L3_xattn_bo': _L3_xattn_in['bo'], 'L3_attn_w_attn': _L3_attn_in['w_attn'], 'L3_attn_w_proj': _L3_attn_in['w_proj'], 'L3_ffn_W_exp': _L3_ffn_in['W_exp'], 'L3_ffn_b_exp': _L3_ffn_in['b_exp'], 'L3_ffn_up_weights': _L3_ffn_in['up_weights'], 'L3_ffn_up_bias': _L3_ffn_in['up_bias'], 'L3_ffn_down_weights': _L3_ffn_in['down_weights'], 'L3_ffn_W_con': _L3_ffn_in['W_con'], 'L3_ffn_b_con': _L3_ffn_in['b_con'], 'L3_ffn_down_bias': _L3_ffn_in['down_bias']}

def reference(x, ctx_1024, mask_Bx1xSxS2_bf0, mask_Bx1xSxS2_if1, L0_xattn_Wq, L0_xattn_Wkv, L0_xattn_Wc, L0_attn_Wq, L0_attn_bq, L0_attn_Wk, L0_attn_bk, L0_attn_Wv, L0_attn_bv, L0_attn_Wo, L0_attn_bo, L0_ffn_Wg, L0_ffn_W1, L0_ffn_W2, L1_xattn_wq_w, L1_xattn_wq_b, L1_xattn_wk_w, L1_xattn_wk_b, L1_xattn_wv_w, L1_xattn_wv_b, L1_xattn_wo_w, L1_xattn_wo_b, L1_xattn_ln_g, L1_xattn_ln_b, L1_attn_w_qkv, L1_attn_w_proj, L1_attn_b_proj, L1_attn_w_dwc, L1_attn_b_dwc, L1_ffn_Wr, L1_ffn_W1, L1_ffn_b1, L1_ffn_W2, L1_ffn_b2, L2_xattn_w_cq, L2_xattn_b_cq, L2_xattn_w_c, L2_xattn_b_c, L2_xattn_w_q, L2_xattn_b_q, L2_xattn_W_l, L2_xattn_b_l, L2_attn_Wq, L2_attn_Wk, L2_attn_Wv, L2_attn_Wu, L2_attn_bu, L2_ffn_w_gate, L2_ffn_w_up, L2_ffn_w_down, L3_xattn_Wq, L3_xattn_bq, L3_xattn_Wo, L3_xattn_bo, L3_attn_w_attn, L3_attn_w_proj, L3_ffn_W_exp, L3_ffn_b_exp, L3_ffn_up_weights, L3_ffn_up_bias, L3_ffn_down_weights, L3_ffn_W_con, L3_ffn_b_con, L3_ffn_down_bias):
    import jax
    import jax.numpy as jnp

    def _L0_xattn_ref(q, kv, Wq, Wkv, Wc):
        import jax, jax.numpy as jnp
        import numpy as np
        N_HEAD = 16
        b, l, d = q.shape
        h = N_HEAD
        dh = d // h
        qp = jnp.einsum('bld,ed->ble', q, Wq)
        scores = jnp.einsum('bld,bmd->blm', qp, kv)
        idx = jnp.argmax(scores, axis=-1)
        mem = jnp.take_along_axis(kv, idx[..., None], axis=1)
        mkv = jnp.einsum('bld,ed->ble', mem, Wkv)
        mk, mv = jnp.split(mkv, 2, axis=-1)
        qh = qp.reshape(b, l, h, dh).transpose(0, 2, 1, 3)
        scale = 1.0 / np.sqrt(dh).astype(np.float32)
        logits = jnp.einsum('bhld,bmd->bhlm', qh, mk) * scale
        attn = jax.nn.softmax(logits, axis=-1)
        out = jnp.einsum('bhlm,bmd->bhld', attn, mv)
        out = out.transpose(0, 2, 1, 3).reshape(b, l, d)
        return jnp.einsum('bld,ed->ble', out, Wc)

    def _L0_attn_ref(x, Wq, bq, Wk, bk, Wv, bv, Wo, bo):
        import jax, jax.numpy as jnp
        import numpy as np
        D_MODEL = 128
        N_HEADS = 16
        HEAD_DIM = D_MODEL // N_HEADS
        WINDOW = 128

        def _window_starts(seq_len, window):
            starts = []
            for i in range(0, seq_len, window // 2):
                end = min(i + window, seq_len)
                starts.append(max(0, end - window))
                if end == seq_len:
                    break
            return np.asarray(starts, dtype=np.int32)
        B, S, D = x.shape
        q = x @ Wq + bq
        k = x @ Wk + bk
        v = x @ Wv + bv
        starts = _window_starts(S, WINDOW)
        idx = starts[:, None] + np.arange(WINDOW)[None, :]
        idx_j = jnp.asarray(idx)
        qw = q[:, idx_j]
        kw = k[:, idx_j]
        vw = v[:, idx_j]
        scores = jnp.einsum('bwqd,bwkd->bwqk', qw, kw) / np.sqrt(HEAD_DIM)
        attn = jax.nn.softmax(scores, axis=-1)
        out_w = jnp.einsum('bwqk,bwkd->bwqd', attn, vw)
        flat_idx = idx.reshape(-1)
        out = jnp.zeros((B, S, D), x.dtype).at[:, flat_idx].add(out_w.reshape(B, -1, D))
        counts = jnp.zeros((S,), x.dtype).at[flat_idx].add(1.0)
        out = out / counts[None, :, None]
        return out @ Wo + bo

    def _L0_ffn_ref(token_inputs, Wg, W1, W2):
        import jax, jax.numpy as jnp
        import numpy as np
        CAPACITY_FACTOR = 1.0

        def _route(token_inputs, Wg, capacity):
            dt = token_inputs.dtype
            logits = jnp.einsum('bnd,de->bne', token_inputs, Wg)
            gates = jax.nn.softmax(logits, axis=-1)
            expert_idx = jnp.argmax(gates, axis=-1)
            mask = jax.nn.one_hot(expert_idx, Wg.shape[1], dtype=dt)
            gate = jnp.sum(gates * mask, axis=-1)
            pos = jnp.cumsum(mask, axis=1) * mask - mask
            keep = mask * (pos < capacity).astype(dt)
            pos_oh = jax.nn.one_hot(pos.astype(jnp.int32), capacity, dtype=dt)
            dispatch = keep[..., None] * pos_oh
            combine = dispatch * gate[:, :, None, None]
            return (dispatch, combine)
        B, N, D = token_inputs.shape
        E = Wg.shape[1]
        capacity = int(N * CAPACITY_FACTOR // E)
        dispatch, combine = _route(token_inputs, Wg, capacity)
        expert_inputs = jnp.einsum('bnd,bnec->becd', token_inputs, dispatch)
        h = jax.nn.gelu(jnp.einsum('becd,edh->bech', expert_inputs, W1))
        expert_outputs = jnp.einsum('bech,ehd->becd', h, W2)
        output = jnp.einsum('becd,bnec->bnd', expert_outputs, combine)
        return output

    def _L1_xattn_ref(q, k, v, mask, training, wq_w, wq_b, wk_w, wk_b, wv_w, wv_b, wo_w, wo_b, ln_g, ln_b):
        import jax, jax.numpy as jnp
        import numpy as np
        B, S, D, H = (2, 256, 128, 16)
        HD = D // H
        LN_EPS = 1e-05

        def _linear(x, w, b):
            return jnp.einsum('bsd,od->bso', x, w) + b

        def _split_heads(x):
            b, s, _ = x.shape
            return x.reshape(b, s, H, HD).transpose(0, 2, 1, 3)
        residual = q
        Q = _split_heads(_linear(q, wq_w, wq_b))
        K = _split_heads(_linear(k, wk_w, wk_b))
        V = _split_heads(_linear(v, wv_w, wv_b))
        dk = jnp.sqrt(jnp.asarray(HD, jnp.float16)).astype(jnp.float32) + 1e-08
        score = jnp.einsum('bhqd,bhkd->bhqk', Q, K) / dk
        attn = jnp.where(mask, -jnp.inf, score)
        ctx = jnp.einsum('bhqk,bhkd->bhqd', attn, V)
        b, _, s, _ = ctx.shape
        ctx = ctx.transpose(0, 2, 1, 3).reshape(b, s, D)
        o = _linear(ctx, wo_w, wo_b)
        x = residual + o
        mu = jnp.mean(x, axis=-1, keepdims=True)
        var = jnp.mean(jnp.square(x - mu), axis=-1, keepdims=True)
        return ln_g * (x - mu) * jax.lax.rsqrt(var + LN_EPS) + ln_b

    def _L1_attn_ref(x, w_qkv, w_proj, b_proj, w_dwc, b_dwc):
        import jax, jax.numpy as jnp
        import numpy as np
        FOCUS = 3
        EPS = 1e-06

        def _norm_last(t):
            return t / jnp.sum(t, axis=-1, keepdims=True)
        B, N, C = x.shape
        H = 16
        d = C // H
        qkv = jnp.einsum('bnc,oc->bno', x, w_qkv).reshape(B, N, 3, H, d)
        qkv = jnp.transpose(qkv, (2, 0, 3, 1, 4))
        q, k, v = (qkv[0], qkv[1], qkv[2])
        q = _norm_last(jax.nn.relu(q) + EPS)
        k = _norm_last(jax.nn.relu(k) + EPS)
        q = _norm_last(q ** FOCUS)
        k = _norm_last(k ** FOCUS)
        kv = jnp.einsum('bhnd,bhne->bhde', k, v)
        z = 1.0 / (jnp.einsum('bhnd,bhd->bhn', q, k.sum(axis=2)) + EPS)
        out = jnp.einsum('bhnd,bhde,bhn->bhne', q, kv, z)
        out = jnp.transpose(out, (0, 2, 1, 3)).reshape(B, N, C)
        xp = jnp.pad(out, ((0, 0), (1, 1), (0, 0)))
        conv = xp[:, 0:N, :] * w_dwc[:, 0] + xp[:, 1:N + 1, :] * w_dwc[:, 1] + xp[:, 2:N + 2, :] * w_dwc[:, 2] + b_dwc
        out = out + conv
        return jnp.einsum('bnc,oc->bno', out, w_proj) + b_proj

    def _L1_ffn_ref(x, Wr, W1, b1, W2, b2):
        import jax, jax.numpy as jnp
        import numpy as np
        CAP_FACTOR = 1.5
        orig_shape = x.shape
        D = x.shape[-1]
        E = Wr.shape[0]
        xf = x.reshape(-1, D)
        T = xf.shape[0]
        cap = int(CAP_FACTOR * T / E)
        logits = xf @ Wr.T
        vals, idx = jax.lax.top_k(logits.T, cap)
        w = jax.nn.softmax(vals, axis=-1)
        xg = xf[idx]
        h = jax.nn.gelu(jnp.einsum('ecd,esdm->ecsm', xg, W1) + b1[:, None], approximate=False)
        y = jnp.einsum('ecsm,esmk->ecsk', h, W2) + b2[:, None]
        y = y.reshape(E, cap, D) * w[..., None]
        out = jnp.zeros_like(xf).at[idx.reshape(-1)].add(y.reshape(-1, D))
        return out.reshape(orig_shape)

    def _L2_xattn_ref(c, q, w_cq, b_cq, w_c, b_c, w_q, b_q, W_l, b_l):
        import jax, jax.numpy as jnp
        import numpy as np
        B, C_LEN, Q_LEN, D = (8, 256, 64, 128)
        cq = jnp.einsum('bcd,bqd,d->bcq', c, q, w_cq) + b_cq
        s = (c @ w_c + b_c)[:, :, None] + (q @ w_q + b_q)[:, None, :] + cq
        a = jax.nn.softmax(s, axis=2)
        c2q_att = jnp.einsum('bcq,bqd->bcd', a, q)
        b_att = jax.nn.softmax(jnp.max(s, axis=2), axis=1)
        q2c_att = jnp.einsum('bc,bcd->bd', b_att, c)[:, None, :]
        x = jnp.concatenate([c, c2q_att, c * c2q_att, c * q2c_att], axis=-1)
        z = x @ W_l.T + b_l
        return z

    def _L2_attn_ref(x, Wq, Wk, Wv, Wu, bu):
        import jax, jax.numpy as jnp
        import numpy as np
        B, T, EMB, HEADS = (4, 256, 128, 16)
        CHUNK = EMB // HEADS
        b, t, d = x.shape
        h = HEADS
        c = d // h
        xh = x.reshape(b, t, h, c)
        scale = d ** (-0.25)
        q = jnp.einsum('bthc,oc->btho', xh, Wq) * scale
        k = jnp.einsum('bthc,oc->btho', xh, Wk) * scale
        v = jnp.einsum('bthc,oc->btho', xh, Wv)
        scores = jnp.einsum('bihc,bjhc->bhij', q, k)
        i = jnp.arange(t)[:, None]
        j = jnp.arange(t)[None, :]
        scores = jnp.where(j > i, -jnp.inf, scores)
        attn = jax.nn.softmax(scores, axis=-1)
        y = jnp.einsum('bhij,bjhc->bihc', attn, v).reshape(b, t, d)
        return y @ Wu.T + bu

    def _L2_ffn_ref(x, w_gate, w_up, w_down):
        import jax, jax.numpy as jnp
        import numpy as np
        BLOCK = 32
        W_BITS = 4
        ACT_BITS = 16

        def act_qdq(x):
            qmax = 2.0 ** (ACT_BITS - 1) - 1.0
            scale = jnp.maximum(jnp.max(jnp.abs(x)) / qmax, 1e-12)
            return jnp.clip(jnp.round(x / scale), -qmax - 1.0, qmax) * scale

        def fixed_qdq_u16(x):
            scale = 1.0 / 65536.0
            return jnp.clip(jnp.round(x / scale), 0.0, 65535.0) * scale

        def lpbq_dequant(w):
            O, I = w.shape
            qmax = 2.0 ** (W_BITS - 1) - 1.0
            wb = w.reshape(O, I // BLOCK, BLOCK)
            s = jnp.maximum(jnp.max(jnp.abs(wb), axis=-1, keepdims=True) / qmax, 1e-12)
            wq = jnp.clip(jnp.round(wb / s), -qmax - 1.0, qmax) * s
            return wq.reshape(O, I)
        x = act_qdq(x)
        up = act_qdq(x @ lpbq_dequant(w_up).T)
        gate = act_qdq(x @ lpbq_dequant(w_gate).T)
        sig = fixed_qdq_u16(jax.nn.sigmoid(gate))
        gate = act_qdq(gate * sig)
        o = act_qdq(gate * up)
        return o @ lpbq_dequant(w_down).T

    def _L3_xattn_ref(q, k, v, mask, Wq, bq, Wo, bo):
        import jax, jax.numpy as jnp
        import numpy as np
        B, S, D = (4, 256, 128)
        H = 16
        DK = D // H

        def _split_heads(x):
            b, s, _ = x.shape
            return x.reshape(b, s, H, DK).transpose(0, 2, 1, 3)
        qh = _split_heads(q @ Wq.T + bq)
        kh = _split_heads(k @ Wq.T + bq)
        vh = _split_heads(v @ Wq.T + bq)
        scores = jnp.einsum('bhqd,bhkd->bhqk', qh, kh) / jnp.sqrt(jnp.float32(DK))
        scores = jnp.where(mask == 0, jnp.float32(-1000000000.0), scores)
        p_attn = jax.nn.softmax(scores, axis=-1)
        x = jnp.einsum('bhqk,bhkd->bhqd', p_attn, vh)
        x = x.transpose(0, 2, 1, 3).reshape(q.shape[0], -1, H * DK)
        return x @ Wo.T + bo

    def _L3_attn_ref(x, w_attn, w_proj):
        import jax, jax.numpy as jnp
        import numpy as np
        N_HEAD = 16
        N_EMBD = 128
        LOCAL_WINDOW = 32
        GLOBAL_IDX = np.array([0, 1, 2, 3], dtype=np.int64)

        def build_mask(T):
            i = np.arange(T)[:, None]
            j = np.arange(T)[None, :]
            causal = j <= i
            local = causal & (j >= i - LOCAL_WINDOW + 1)
            g_row = np.isin(np.arange(T), GLOBAL_IDX)[:, None]
            g_col = np.isin(np.arange(T), GLOBAL_IDX)[None, :]
            mask = local | g_row & causal | g_col & causal
            return jnp.asarray(mask)
        B, T, C = x.shape
        H, D = (N_HEAD, C // N_HEAD)
        qkv = jnp.einsum('btc,fc->btf', x, w_attn)
        q, k, v = jnp.split(qkv, 3, axis=-1)
        q = q.reshape(B, T, H, D).transpose(0, 2, 1, 3)
        k = k.reshape(B, T, H, D).transpose(0, 2, 1, 3)
        v = v.reshape(B, T, H, D).transpose(0, 2, 1, 3)
        mask = build_mask(T)
        scale = 1.0 / np.sqrt(D)
        att = jnp.einsum('bhqd,bhkd->bhqk', q, k) * scale
        att = jnp.where(mask, att, jnp.finfo(att.dtype).min)
        att = jax.nn.softmax(att, axis=-1)
        y = jnp.einsum('bhqk,bhkd->bhqd', att, v)
        y = y.transpose(0, 2, 1, 3).reshape(B, T, C)
        return jnp.einsum('btc,oc->bto', y, w_proj)

    def _L3_ffn_ref(x, W_exp, b_exp, up_weights, up_bias, down_weights, W_con, b_con, down_bias):
        import jax, jax.numpy as jnp
        import numpy as np
        D_MODEL = 128
        EXPANSION = 4
        D_HIDDEN = D_MODEL * EXPANSION
        NUM_STAGES = int(np.log2(D_HIDDEN))

        def butterfly(y, weights, dim):
            lead = y.shape[:-1]
            for stage in range(weights.shape[0]):
                s = 2 ** stage
                nb = dim // (2 * s)
                yr = y.reshape(*lead, nb, 2, s)
                a = yr[..., 0, :]
                b = yr[..., 1, :]
                w = weights[stage].reshape(nb, s, 2, 2)
                na = w[..., 0, 0] * a + w[..., 0, 1] * b
                nb2 = w[..., 1, 0] * a + w[..., 1, 1] * b
                y = jnp.stack([na, nb2], axis=-2).reshape(*lead, dim)
            return y
        h = jnp.einsum('bsd,dh->bsh', x, W_exp) + b_exp
        h = butterfly(h, up_weights, D_HIDDEN)
        h = jax.nn.gelu(h + up_bias, approximate=False)
        h = butterfly(h, down_weights, D_HIDDEN)
        y = jnp.einsum('bsh,hd->bsd', h, W_con) + b_con
        return y + down_bias
    x = x + _L0_xattn_ref(_layernorm(x, axis=-1), ctx_1024, L0_xattn_Wq, L0_xattn_Wkv, L0_xattn_Wc)
    x = x + _L0_attn_ref(_layernorm(x, axis=-1), L0_attn_Wq, L0_attn_bq, L0_attn_Wk, L0_attn_bk, L0_attn_Wv, L0_attn_bv, L0_attn_Wo, L0_attn_bo)
    x = x + _L0_ffn_ref(_layernorm(x, axis=-1), L0_ffn_Wg, L0_ffn_W1, L0_ffn_W2)
    x = x + _L1_xattn_ref(_layernorm(x, axis=-1), ctx_1024, ctx_1024, mask_Bx1xSxS2_bf0, 0, L1_xattn_wq_w, L1_xattn_wq_b, L1_xattn_wk_w, L1_xattn_wk_b, L1_xattn_wv_w, L1_xattn_wv_b, L1_xattn_wo_w, L1_xattn_wo_b, L1_xattn_ln_g, L1_xattn_ln_b)
    x = x + _L1_attn_ref(_layernorm(x, axis=-1), L1_attn_w_qkv, L1_attn_w_proj, L1_attn_b_proj, L1_attn_w_dwc, L1_attn_b_dwc)
    x = x + _L1_ffn_ref(_layernorm(x, axis=-1), L1_ffn_Wr, L1_ffn_W1, L1_ffn_b1, L1_ffn_W2, L1_ffn_b2)
    x = x + _L2_xattn_ref(_layernorm(x, axis=-1), ctx_1024, L2_xattn_w_cq, L2_xattn_b_cq, L2_xattn_w_c, L2_xattn_b_c, L2_xattn_w_q, L2_xattn_b_q, L2_xattn_W_l, L2_xattn_b_l)
    x = x + _L2_attn_ref(_layernorm(x, axis=-1), L2_attn_Wq, L2_attn_Wk, L2_attn_Wv, L2_attn_Wu, L2_attn_bu)
    x = x + _L2_ffn_ref(_layernorm(x, axis=-1), L2_ffn_w_gate, L2_ffn_w_up, L2_ffn_w_down)
    x = x + _L3_xattn_ref(_layernorm(x, axis=-1), ctx_1024, ctx_1024, mask_Bx1xSxS2_if1, L3_xattn_Wq, L3_xattn_bq, L3_xattn_Wo, L3_xattn_bo)
    x = x + _L3_attn_ref(_layernorm(x, axis=-1), L3_attn_w_attn, L3_attn_w_proj)
    x = x + _L3_ffn_ref(_layernorm(x, axis=-1), L3_ffn_W_exp, L3_ffn_b_exp, L3_ffn_up_weights, L3_ffn_up_bias, L3_ffn_down_weights, L3_ffn_W_con, L3_ffn_b_con, L3_ffn_down_bias)
    return x

_drawn_inputs = setup_inputs


def setup_inputs(seed=0):
    import zlib

    import numpy as np

    out = dict(_drawn_inputs(seed))
    spreads = {'L1_xattn_wq_b': (0.0, 0.1),
     'L1_xattn_wk_b': (0.0, 0.1),
     'L1_xattn_wv_b': (0.0, 0.1),
     'L1_xattn_wo_b': (0.0, 0.1),
     'L1_xattn_ln_g': (1.0, 0.2),
     'L1_xattn_ln_b': (0.0, 0.1),
     'L1_ffn_b1': (0.0, 0.8),
     'L1_ffn_b2': (0.0, 2.0),
     'L2_attn_bu': (0.0, 0.1),
     'L3_xattn_bq': (0.0, 0.444),
     'L3_xattn_bo': (0.0, 0.645),
     'L3_ffn_b_exp': (0.0, 0.1),
     'L3_ffn_up_bias': (0.0, 0.1),
     'L3_ffn_b_con': (0.0, 0.67),
     'L3_ffn_down_bias': (0.0, 0.701)}
    factors = {'L0_xattn_Wq': 3.034,
     'L0_attn_bq': 2.78,
     'L0_attn_bk': 64.0,
     'L0_attn_bo': 3.183,
     'L0_ffn_Wg': 8.0,
     'L0_ffn_W1': 8.0,
     'L0_ffn_W2': 8.0,
     'L1_attn_w_qkv': 5.716,
     'L1_attn_w_proj': 5.534,
     'L1_attn_b_proj': 4.902,
     'L1_attn_w_dwc': 8.0,
     'L1_attn_b_dwc': 8.0,
     'L1_ffn_Wr': 8.0,
     'L1_ffn_W1': 8.0,
     'L1_ffn_W2': 8.0,
     'L2_ffn_w_gate': 8.0,
     'L2_ffn_w_up': 8.0,
     'L2_ffn_w_down': 8.0,
     'L2_xattn_b_l': 2.934}
    for name, (base, spread) in spreads.items():
        noise = np.random.default_rng([zlib.crc32(name.encode()), seed]).standard_normal(out[name].shape)
        drawn = base * np.exp(spread * noise) if base else spread * noise
        out[name] = jnp.asarray(drawn.astype(out[name].dtype))
    for name, factor in factors.items():
        out[name] = (out[name] * factor).astype(out[name].dtype)
    return out
```

```python
import concourse.bass as bass
from concourse import mybir
from concourse.alu_op_type import AluOpType as ALU
from contextlib import ExitStack
import numpy as np

P = 128
D = 128
NB = 128
L = 32
S2 = 257
TOKENS = NB * L
T = 4
GT = T * P
GB = GT // L
GROUPS = TOKENS // GT
BPT = P // L
H, DH = 16, 8
HC = H // 4
E0, HID0 = 8, 512
CAP0 = L // E0
WINDOW = 128
E1, S1 = 48, 4
CAP1 = int(1.5 * TOKENS / E1)
KW = D // S1
I2 = 384
HID3, STAGES = 512, 9
NEG = -1e30
LOWEST = -3.0e38

F32 = mybir.dt.float32
I32 = mybir.dt.int32
U32 = mybir.dt.uint32
U8 = mybir.dt.uint8
ACT = mybir.ActivationFunctionType
X = mybir.AxisListType.X
MUL, ADD, SUB, MAX, MIN, EQ = ALU.mult, ALU.add, ALU.subtract, ALU.max, ALU.min, ALU.is_equal


class Steps:

    def __init__(self, engine, own):
        self.engine, self.own, self.counts = engine, own, {}

    def __call__(self, instruction, signal=None):
        signal = self.own if signal is None else signal
        n = self.counts[id(signal)] = self.counts.get(id(signal), 0) + 1
        instruction.then_inc(signal, 1)
        self.engine.wait_ge(signal, n)


class Kit:

    def __init__(self, nc):
        self.nc = nc
        self.numbers = []
        self.tiles = 0

    def signals(self, stack, layer, *names):
        sems = {n: stack.enter_context(self.nc.semaphore(f"{layer}_{n}"))
                for n in ("vector_step", "scalar_step", "pool_step") + names}
        self.numbers += [sem.num for sem in sems.values()]
        return sems

    def clear_signals(self):
        lo, hi = min(self.numbers), max(self.numbers)
        self.nc.gpsimd.dma_reset(range(lo, hi + 1))
        self.nc.gpsimd.sem_clear(range(lo, hi + 1))
        self.nc.all_engine_barrier()


def tile(k, stack, name, *shape, dtype=F32):
    k.tiles += 1
    return stack.enter_context(k.nc.sbuf_tensor(f"{name}_{k.tiles}", list(shape), dtype))


def over(ap, shape):
    return ap.broadcast_to(list(shape))


NORM = ("xn_ready", "xt_psum", "xt_ready")


def norm_tiles(k, stack):
    k.stat = tile(k, stack, "stat", P, 4, T)
    k.xc = tile(k, stack, "x_centred", P, T, D)
    k.sq = tile(k, stack, "x_squared", P, T, D)


def normalise(k, step, x, out, signal=None):
    nc = k.nc
    mean, var, rstd, half = (k.stat[:, i, :] for i in range(4))
    step(nc.vector.reduce_sum(mean, x, X))
    step(nc.vector.tensor_scalar(mean, mean, 1.0 / D, None, MUL))
    step(nc.vector.tensor_tensor(k.xc[:], x, over(mean.unsqueeze(2), (P, T, D)), SUB))
    step(nc.vector.tensor_tensor(k.sq[:], k.xc[:], k.xc[:], MUL))
    step(nc.vector.reduce_sum(var, k.sq[:], X))
    step(nc.vector.tensor_scalar(var, var, 1.0 / D, 1e-5, MUL, ADD))
    step(nc.vector.tensor_scalar(half.bitcast(I32), var.bitcast(I32), 1, None, ALU.logical_shift_right))
    step(nc.vector.tensor_scalar(rstd.bitcast(I32), half.bitcast(I32), -1.0, float(0x5F3759DF), MUL, ADD))
    for _ in range(3):
        step(nc.vector.tensor_tensor(half, rstd, rstd, MUL))
        step(nc.vector.scalar_tensor_tensor(half, half, -0.5, var, MUL, MUL))
        step(nc.vector.scalar_tensor_tensor(rstd, half, 1.5, rstd, ADD, MUL))
    step(nc.vector.tensor_tensor(out, k.xc[:], over(rstd.unsqueeze(2), (P, T, D)), MUL), signal)


def norm_vector(k, vec, step, s):
    normalise(k, step, k.xg[:], k.xn[:], s["xn_ready"])


def norm_tensor(k, pe, s, bank=0):
    pe.wait_ge(s["xn_ready"], 1)
    for t in range(T):
        last = k.nc.tensor.transpose(k.ps[:, bank, t * P:(t + 1) * P], k.xn[:, t, :], k.ident)
    last.then_inc(s["xt_psum"], 1)


def norm_scalar(k, act, step, s, bank=0):
    act.wait_ge(s["xt_psum"], 1)
    step(k.nc.scalar.activation(k.xt[:], k.ps[:, bank, :], ACT.Copy), s["xt_ready"])


CORE = ("qx_ready", "k_psum", "k_ready", "q_psum", "rep_ready", "v_psum", "vx_ready", "scores", "shifted",
        "exps", "pt_ready", "o_psum", "o_ready", "z_psum", "residual")


def core_tiles(k, stack):
    k.qx = tile(k, stack, "q_by_head", P, GB, 4, L)
    k.kt = tile(k, stack, "k_t", P, GT)
    k.rep = tile(k, stack, "source_four_times", P, GB, 4, L)
    k.vx = tile(k, stack, "v_by_head", P, GB, D)
    k.pr = tile(k, stack, "probabilities", P, HC, GB, L)
    k.pt = tile(k, stack, "probabilities_t", P, HC, GB, L)
    k.mx = tile(k, stack, "row_max", P, HC, GB)
    k.rs = tile(k, stack, "row_sum", P, HC, GB)
    k.ot = tile(k, stack, "o_t", P, GT)


def core_tensor(k, pe, s, wv, wo, q_bank=1):
    nc, ps = k.nc, k.ps
    pe.wait_ge(s["rep_ready"], 1)
    for b in range(GB):
        last = nc.tensor.matmul(ps[:, 4 + b // 4, (b % 4) * D:(b % 4 + 1) * D], k.rep[:, b, :, :].rearrange("p a b -> p (a b)"),
                                wv, start=True, stop=True)
    last.then_inc(s["v_psum"], 1)
    pe.wait_ge(s["qx_ready"], 4)
    pe.wait_ge(s["k_ready"], 1)
    for b in range(GB):
        for c in range(HC):
            rows = slice(L * c, L * c + L)
            last = nc.tensor.matmul(ps[:, c, b * L:(b + 1) * L], k.qx[rows, b, :, :].rearrange("p a b -> p (a b)"),
                                    k.kt[rows, b * L:(b + 1) * L], start=True, stop=True)
    last.then_inc(s["scores"], 1)
    pe.wait_ge(s["vx_ready"], 1)
    for c in range(HC):
        pe.wait_ge(s["pt_ready"], c + 1)
        for b in range(GB):
            last = nc.tensor.matmul(ps[L * c:L * c + L, 4, b * L:(b + 1) * L], k.vx[:, b, L * c:L * c + L],
                                    k.pt[:, c, b, :], start=True, stop=True)
    last.then_inc(s["o_psum"], 1)
    project(k, pe, s, wo)


def project(k, pe, s, wo):
    pe.wait_ge(s["o_ready"], 1)
    for t in range(T):
        last = k.nc.tensor.matmul(k.ps[:, 5, t * D:(t + 1) * D], k.ot[:, t * P:(t + 1) * P], wo, start=True, stop=True)
    last.then_inc(s["z_psum"], 1)


def q_by_head(k, vec, step, s, bank=1, bias=None):
    nc = k.nc
    vec.wait_ge(s["q_psum"], 1)
    q = k.ps[:, bank, :].rearrange("p (b n) -> p b n", n=L)
    for h in range(4):
        if bias is None:
            step(nc.vector.tensor_scalar(k.qx[:, :, h, :], q, k.quad_head[:, h:h + 1], None, MUL), s["qx_ready"])
        else:
            step(nc.vector.tensor_scalar(k.qx[:, :, h, :], q, bias, k.quad_head[:, h:h + 1], ADD, MUL), s["qx_ready"])


def v_by_head(k, vec, step, s):
    vec.wait_ge(s["v_psum"], 1)
    step(k.nc.vector.tensor_tensor(k.vx[:].rearrange("p b d -> p b d"),
                                   k.ps[:, 4:8, :].rearrange("p c (b d) -> p (c b) d", d=D),
                                   over(k.v_heads.unsqueeze(1), (P, GB, D)), MUL), s["vx_ready"])


def core_vector(k, vec, step, s, scale, causal, bias=None):
    nc = k.nc
    vec.wait_ge(s["scores"], 1)
    for c in range(HC):
        sc = k.ps[:, c, :].rearrange("p (b j) -> p b j", j=L)
        if causal:
            step(nc.vector.scalar_tensor_tensor(k.pr[:, c, :, :], sc, scale, over(k.causal.unsqueeze(1), (P, GB, L)), MUL, ADD))
            sc = k.pr[:, c, :, :]
        step(nc.vector.reduce_max(k.mx[:, c, :], sc, X))
        step(nc.vector.tensor_tensor(k.pr[:, c, :, :], sc, over(k.mx[:, c, :].unsqueeze(2), (P, GB, L)), SUB), s["shifted"])
    for c in range(HC):
        vec.wait_ge(s["exps"], c + 1)
        pr, rs = k.pr[:, c, :, :], k.rs[:, c, :]
        step(nc.vector.reduce_sum(rs, pr, X))
        step(nc.vector.reciprocal(rs, rs))
        step(nc.vector.tensor_tensor(pr, pr, over(rs.unsqueeze(2), (P, GB, L)), MUL))
        step(nc.vector.transpose(k.pt[:, c, :, :], pr), s["pt_ready"])
    add_projection(k, vec, step, s, bias)


def add_projection(k, vec, step, s, bias=None):
    nc = k.nc
    if bias is not None:
        step(nc.vector.tensor_tensor(k.xg[:], k.xg[:], over(bias.unsqueeze(1), (P, T, D)), ADD))
    vec.wait_ge(s["z_psum"], 1)
    step(nc.vector.tensor_tensor(k.xg[:], k.xg[:], k.ps[:, 5, :].rearrange("p (t d) -> p t d", d=D), ADD), s["residual"])


def core_scalar(k, act, step, s, scale, causal):
    nc = k.nc
    for c in range(HC):
        act.wait_ge(s["shifted"], c + 1)
        step(nc.scalar.activation(k.pr[:, c, :, :], k.pr[:, c, :, :], ACT.Exp, scale=1.0 if causal else scale), s["exps"])
    act.wait_ge(s["o_psum"], 1)
    step(nc.scalar.activation(k.ot[:], k.ps[:, 4, :], ACT.Copy), s["o_ready"])


def four_times(k, source):
    return over(source.rearrange("p (b n) -> p b n", n=L).unsqueeze(2), (P, GB, 4, L))


def l0_xattn(k, phase, w, ctx_rows):
    nc, ps = k.nc, k.ps
    s = k.signals(phase, "l0x", *NORM, *CORE, "qt_ready", "found_scores", "rows_found", "rows_loaded", "mem_psum", "mem_ready")
    with ExitStack() as own, nc.Block() as block:
        norm_tiles(k, own)
        core_tiles(k, own)
        qt = tile(k, own, "l0x_qt", P, GT)
        best = tile(k, own, "best", P, T, 8)
        best_at = tile(k, own, "best_at", P, T, 8, dtype=U32)
        rows = tile(k, own, "rows", P, T, dtype=I32)
        mem = tile(k, own, "mem", P, T, D)
        mt = tile(k, own, "mem_t", P, GT)

        @block.vector
        def _(vec):
            step = Steps(vec, s["vector_step"])
            norm_vector(k, vec, step, s)
            q_by_head(k, vec, step, s)
            for t in range(T):
                vec.wait_ge(s["found_scores"], t + 1)
                step(nc.vector.max(best[:, t, :], ps[:, 4 + t, 0:S2]))
                step(nc.vector.max_index(best_at[:, t, :], best[:, t, :], ps[:, 4 + t, 0:S2]))
            step(nc.vector.tensor_tensor(rows[:], best_at[:, :, 0], k.row_base, ADD), s["rows_found"])
            step(nc.vector.tensor_scalar(k.row_base, k.row_base, float(GB * S2), None, ADD))
            v_by_head(k, vec, step, s)
            core_vector(k, vec, step, s, DH ** -0.5, False)

        @block.gpsimd
        def _(pool):
            pool.wait_ge(s["rows_found"], 1)
            for t in range(T):
                nc.gpsimd.indirect_dma_start(out=mem[:, t, :], out_offset=None, in_=ctx_rows,
                                             in_offset=bass.IndirectOffsetOnAxis(ap=rows[:, t:t + 1], axis=0)).then_inc(s["rows_loaded"], 16)
            pool.wait_ge(s["rows_loaded"], 16 * T)
            pool.wait_ge(s["mem_ready"], 1)
            nc.gpsimd.tensor_copy(k.rep[:], four_times(k, mt[:])).then_inc(s["rep_ready"], 1)

        @block.scalar
        def _(act):
            step = Steps(act, s["scalar_step"])
            norm_scalar(k, act, step, s)
            act.wait_ge(s["q_psum"], 1)
            act.wait_ge(s["qx_ready"], 4)
            step(nc.scalar.activation(qt[:], ps[:, 1, :], ACT.Copy), s["qt_ready"])
            act.wait_ge(s["mem_psum"], 1)
            step(nc.scalar.activation(mt[:], ps[:, 2, :], ACT.Copy), s["mem_ready"])
            act.wait_ge(s["k_psum"], 1)
            step(nc.scalar.activation(k.kt[:], ps[:, 3, :], ACT.Copy), s["k_ready"])
            core_scalar(k, act, step, s, DH ** -0.5, False)

        @block.tensor
        def _(pe):
            norm_tensor(k, pe, s)
            pe.wait_ge(s["xt_ready"], 1)
            nc.tensor.matmul(ps[:, 1, :], w["l0x_q"], k.xt[:], start=True, stop=True).then_inc(s["q_psum"], 1)
            pe.wait_ge(s["qt_ready"], 1)
            pe.wait_ge(k.ctxt_loaded, 16)
            for t in range(T):
                for j in range(BPT):
                    b = t * BPT + j
                    last = nc.tensor.matmul(ps[L * j:L * j + L, 4 + t, 0:S2], qt[:, b * L:(b + 1) * L], k.ctxt[:, b, :], start=True, stop=True)
                last.then_inc(s["found_scores"], 1)
            pe.wait_ge(s["rows_loaded"], 16 * T)
            for t in range(T):
                last = nc.tensor.transpose(ps[:, 2, t * P:(t + 1) * P], mem[:, t, :], k.ident)
            last.then_inc(s["mem_psum"], 1)
            pe.wait_ge(s["mem_ready"], 1)
            nc.tensor.matmul(ps[:, 3, :], w["l0x_k"], mt[:], start=True, stop=True).then_inc(s["k_psum"], 1)
            core_tensor(k, pe, s, w["l0x_v"], w["l0x_c"])


def l0_attn(k, phase, w, rowv, colv):
    nc, ps = k.nc, k.ps
    s = k.signals(phase, "l0a", *NORM, "q_psum", "k_psum", "v_psum", "q_ready", "k_ready", "v_ready", "scores", "shifted", "exps",
                  "pt_ready", "o_psum", "o_ready", "z_psum", "residual")
    scale = DH ** -0.5
    with ExitStack() as own, nc.Block() as block:
        norm_tiles(k, own)
        qt, kt = tile(k, own, "l0a_qt", P, GT), tile(k, own, "l0a_kt", P, GT)
        v = tile(k, own, "l0a_v", P, T, D)
        pr, pt = tile(k, own, "l0a_p", P, T, L), tile(k, own, "l0a_pt", P, T, L)
        mx = tile(k, own, "l0a_mx", P, T)
        k.ot = tile(k, own, "l0a_ot", P, GT)

        @block.vector
        def _(vec):
            step = Steps(vec, s["vector_step"])
            norm_vector(k, vec, step, s)
            vec.wait_ge(s["v_psum"], 1)
            step(nc.vector.tensor_tensor(v[:], ps[:, 3, :].rearrange("p (t d) -> p t d", d=D), over(rowv["l0a_bv"].unsqueeze(1), (P, T, D)), ADD), s["v_ready"])
            vec.wait_ge(s["scores"], 1)
            sc = ps[:, 4, 0:T * L].rearrange("p (t j) -> p t j", j=L)
            step(nc.vector.reduce_max(mx[:], sc, X))
            step(nc.vector.tensor_tensor(pr[:], sc, over(mx[:].unsqueeze(2), (P, T, L)), SUB), s["shifted"])
            vec.wait_ge(s["exps"], 1)
            step(nc.vector.tensor_scalar(pr[:, :, L - 1:L], pr[:, :, L - 1:L], float(WINDOW - L + 1), None, MUL))
            step(nc.vector.reduce_sum(mx[:], pr[:], X))
            step(nc.vector.reciprocal(mx[:], mx[:]))
            step(nc.vector.tensor_tensor(pr[:], pr[:], over(mx[:].unsqueeze(2), (P, T, L)), MUL))
            step(nc.vector.transpose(pt[:], pr[:]), s["pt_ready"])
            add_projection(k, vec, step, s, rowv["l0a_bo"])

        @block.scalar
        def _(act):
            step = Steps(act, s["scalar_step"])
            norm_scalar(k, act, step, s)
            act.wait_ge(s["q_psum"], 1)
            step(nc.scalar.activation(qt[:], ps[:, 1, :], ACT.Identity, bias=colv["l0a_bq"]), s["q_ready"])
            act.wait_ge(s["k_psum"], 1)
            step(nc.scalar.activation(kt[:], ps[:, 2, :], ACT.Identity, bias=colv["l0a_bk"]), s["k_ready"])
            act.wait_ge(s["shifted"], 1)
            step(nc.scalar.activation(pr[:], pr[:], ACT.Exp, scale=scale), s["exps"])
            act.wait_ge(s["o_psum"], 1)
            step(nc.scalar.activation(k.ot[:].rearrange("p (t j n) -> p j t n", j=BPT, n=L),
                                      ps[:, 0:4, 0:T * L].rearrange("p j (t n) -> p j t n", n=L), ACT.Copy), s["o_ready"])

        @block.tensor
        def _(pe):
            norm_tensor(k, pe, s)
            pe.wait_ge(s["xt_ready"], 1)
            nc.tensor.matmul(ps[:, 1, :], w["l0a_q"], k.xt[:], start=True, stop=True).then_inc(s["q_psum"], 1)
            nc.tensor.matmul(ps[:, 2, :], w["l0a_k"], k.xt[:], start=True, stop=True).then_inc(s["k_psum"], 1)
            for t in range(T):
                last = nc.tensor.matmul(ps[:, 3, t * D:(t + 1) * D], k.xt[:, t * P:(t + 1) * P], w["l0a_v"], start=True, stop=True)
            last.then_inc(s["v_psum"], 1)
            pe.wait_ge(s["q_ready"], 1)
            pe.wait_ge(s["k_ready"], 1)
            for t in range(T):
                for j in range(BPT):
                    b = slice((t * BPT + j) * L, (t * BPT + j + 1) * L)
                    last = nc.tensor.matmul(ps[L * j:L * j + L, 4, t * L:(t + 1) * L], qt[:, b], kt[:, b], start=True, stop=True)
            last.then_inc(s["scores"], 1)
            pe.wait_ge(s["pt_ready"], 1)
            pe.wait_ge(s["v_ready"], 1)
            for t in range(T):
                for j in range(BPT):
                    r = slice(L * j, L * j + L)
                    last = nc.tensor.matmul(ps[:, j, t * L:(t + 1) * L], v[r, t, :], pt[r, t, :], start=True, stop=True)
            last.then_inc(s["o_psum"], 1)
            project(k, pe, s, w["l0a_o"])


def l0_ffn(k, phase, w):
    nc, ps = k.nc, k.ps
    s = k.signals(phase, "l0f", *NORM, "logits", "shifted", "exps", "chosen", "places", "dispatch_ready", "slots_psum", "slots_ready",
                  "hidden_psum", "hidden_ready", "y_psum", "y_ready", "yt_psum", "yt_ready", "combine_ready", "z_psum", "residual")
    with ExitStack() as own, nc.Block() as block:
        norm_tiles(k, own)
        lg = tile(k, own, "l0f_logits", P, T, E0)
        ex = tile(k, own, "l0f_exps", P, T, E0)
        hot = tile(k, own, "l0f_onehot", P, T, E0)
        st = tile(k, own, "l0f_stats", P, 4, T)
        at = tile(k, own, "l0f_at", P, T, CAP0)
        disp = tile(k, own, "l0f_dispatch", P, T, E0, CAP0)
        comb = tile(k, own, "l0f_combine", P, T, L)
        combx = tile(k, own, "l0f_combine_x", P, T, BPT, L)
        xs = tile(k, own, "l0f_slots", P, E0, GB, CAP0)
        hid = tile(k, own, "l0f_hidden", P, E0 * 4, GB * CAP0)
        yt = tile(k, own, "l0f_yt", P, GB, E0, CAP0)
        y = tile(k, own, "l0f_y", P, T, D)

        @block.vector
        def _(vec):
            step = Steps(vec, s["vector_step"])
            norm_vector(k, vec, step, s)
            vec.wait_ge(s["logits"], 1)
            mx, gate, place, pick = (st[:, i, :] for i in range(4))
            step(nc.vector.tensor_copy(lg[:], ps[:, 1, 0:T * E0].rearrange("p (t e) -> p t e", e=E0)))
            step(nc.vector.reduce_max(mx, lg[:], X))
            step(nc.vector.tensor_tensor(ex[:], lg[:], over(mx.unsqueeze(2), (P, T, E0)), SUB), s["shifted"])
            step(nc.vector.tensor_tensor(hot[:], lg[:], over(mx.unsqueeze(2), (P, T, E0)), EQ))
            step(nc.vector.tensor_tensor(hot[:], hot[:], over(k.countdown.unsqueeze(1), (P, T, E0)), MUL))
            step(nc.vector.reduce_max(pick, hot[:], X))
            step(nc.vector.tensor_tensor(hot[:], over(pick.unsqueeze(2), (P, T, E0)), over(k.countdown.unsqueeze(1), (P, T, E0)), EQ), s["chosen"])
            vec.wait_ge(s["exps"], 1)
            step(nc.vector.reduce_sum(gate, ex[:], X))
            step(nc.vector.reciprocal(gate, gate))
            vec.wait_ge(s["places"], 1)
            step(nc.vector.tensor_tensor(lg[:], ps[:, 2, 0:T * E0].rearrange("p (t e) -> p t e", e=E0), hot[:], MUL))
            step(nc.vector.reduce_sum(place, lg[:], X))
            step(nc.vector.tensor_tensor(at[:], over(place.unsqueeze(2), (P, T, CAP0)), over(k.count4.unsqueeze(1), (P, T, CAP0)), EQ))
            step(nc.vector.tensor_tensor(disp[:], over(hot[:].unsqueeze(3), (P, T, E0, CAP0)), over(at[:].unsqueeze(2), (P, T, E0, CAP0)), MUL), s["dispatch_ready"])
            flat = disp[:].rearrange("p t e c -> p t (e c)")
            vec.wait_ge(s["slots_psum"], 1)
            step(nc.vector.tensor_tensor(flat, flat, over(gate.unsqueeze(2), (P, T, L)), MUL))
            step(nc.vector.transpose(comb[:], flat))
            step(nc.vector.tensor_tensor(combx[:], over(comb[:].unsqueeze(2), (P, T, BPT, L)), over(k.tile_batch.unsqueeze(1).unsqueeze(3), (P, T, BPT, L)), MUL), s["combine_ready"])
            add_projection(k, vec, step, s)

        @block.scalar
        def _(act):
            step = Steps(act, s["scalar_step"])
            norm_scalar(k, act, step, s)
            act.wait_ge(s["shifted"], 1)
            step(nc.scalar.activation(ex[:], ex[:], ACT.Exp), s["exps"])
            act.wait_ge(s["slots_psum"], 1)
            for j in range(BPT):
                step(nc.scalar.activation(xs[:].rearrange("p e (t j) c -> p j t e c", j=BPT)[:, j],
                                          ps[:, 4 + j, 0:P].rearrange("p (t e c) -> p t e c", t=T, e=E0), ACT.Copy), s["slots_ready"])
            for n in range(4):
                act.wait_ge(s["hidden_psum"], n + 1)
                step(nc.scalar.activation(hid[:, 8 * n:8 * n + 8, :].rearrange("p a b -> p (a b)"), ps[:, n, :], ACT.Gelu_apprx_tanh), s["hidden_ready"])
            act.wait_ge(s["y_psum"], 1)
            step(nc.scalar.activation(yt[:].rearrange("p b e c -> p e b c"), ps[:, 6, :].rearrange("p (e b c) -> p e b c", e=E0, c=CAP0), ACT.Copy), s["y_ready"])
            act.wait_ge(s["yt_psum"], 1)
            step(nc.scalar.activation(y[:].rearrange("p t d -> p (t d)"), ps[:, 7, :], ACT.Copy), s["yt_ready"])

        @block.tensor
        def _(pe):
            norm_tensor(k, pe, s)
            pe.wait_ge(s["xt_ready"], 1)
            for t in range(T):
                last = nc.tensor.matmul(ps[:, 1, t * E0:(t + 1) * E0], k.xt[:, t * P:(t + 1) * P], w["l0f_g"], start=True, stop=True)
            last.then_inc(s["logits"], 1)
            pe.wait_ge(s["chosen"], 1)
            nc.tensor.matmul(ps[:, 2, 0:T * E0], k.earlier, hot[:].rearrange("p t e -> p (t e)"), start=True, stop=True).then_inc(s["places"], 1)
            pe.wait_ge(s["dispatch_ready"], 1)
            for t in range(T):
                for j in range(BPT):
                    r = slice(L * j, L * j + L)
                    last = nc.tensor.matmul(ps[:, 4 + j, t * L:(t + 1) * L], k.xn[r, t, :], disp[r, t, :, :].rearrange("p e c -> p (e c)"), start=True, stop=True)
            last.then_inc(s["slots_psum"], 1)
            pe.wait_ge(s["slots_ready"], BPT)
            for e in range(E0):
                for c in range(4):
                    n = e * 4 + c
                    last = nc.tensor.matmul(ps[:, n // 8, (n % 8) * 64:(n % 8 + 1) * 64], w["l0f_w1"][:, e, c * P:(c + 1) * P],
                                            xs[:, e, :, :].rearrange("p b c -> p (b c)"), start=True, stop=True)
                    if n % 8 == 7:
                        last.then_inc(s["hidden_psum"], 1)
            for e in range(E0):
                if e % 2 == 0:
                    pe.wait_ge(s["hidden_ready"], e // 2 + 1)
                for c in range(4):
                    last = nc.tensor.matmul(ps[:, 6, e * 64:(e + 1) * 64], w["l0f_w2"][:, e, c, :], hid[:, e * 4 + c, :], start=c == 0, stop=c == 3)
            last.then_inc(s["y_psum"], 1)
            pe.wait_ge(s["y_ready"], 1)
            for t in range(T):
                last = nc.tensor.transpose(ps[:, 7, t * P:(t + 1) * P], yt[:, t * BPT:(t + 1) * BPT, :, :].rearrange("p b e c -> p (b e c)"), k.ident)
            last.then_inc(s["yt_psum"], 1)
            pe.wait_ge(s["yt_ready"], 1)
            pe.wait_ge(s["combine_ready"], 1)
            for t in range(T):
                last = nc.tensor.matmul(ps[:, 5, t * D:(t + 1) * D], combx[:, t, :, :].rearrange("p j n -> p (j n)"), y[:, t, :], start=True, stop=True)
            last.then_inc(s["z_psum"], 1)


def l1_xattn(k, phase, w, rowv, colv):
    nc, ps = k.nc, k.ps
    s = k.signals(phase, "l1x", *NORM, "q_psum", "q_ready", "g_psum", "g_ready", "t_psum", "t_ready", "m_psum", "m_ready",
                  "o_psum", "o_ready", "z_psum", "residual")
    inv_dk = 1.0 / (2.828125 + 1e-8)
    with ExitStack() as own, nc.Block() as block:
        norm_tiles(k, own)
        qt = tile(k, own, "l1x_qt", P, GT)
        gram = tile(k, own, "l1x_gram", P, 4, D + 1)
        t1 = tile(k, own, "l1x_t1", P, 4, D)
        sbk = tile(k, own, "l1x_sbk", P, 4, D)
        kv = tile(k, own, "l1x_kv", P, GB, D)
        k.ot = tile(k, own, "l1x_ot", P, GT)
        c0 = tile(k, own, "l1x_c0", P, D)
        masked = tile(k, own, "l1x_masked", P, 2, T)
        res = tile(k, own, "l1x_res", P, T, D)

        @block.vector
        def _(vec):
            step = Steps(vec, s["vector_step"])
            norm_vector(k, vec, step, s)
            step(nc.vector.tensor_scalar(c0[:], rowv["l1x_bv"], colv["l1x_bk"], float(S2), MUL, MUL))
            step(nc.vector.tensor_tensor(c0[:], c0[:], k.same_head, MUL))
            step(nc.vector.reduce_max(masked[:, 0, :], k.mask[:], X))
            step(nc.vector.tensor_scalar(masked[:, 1, :], masked[:, 0, :], LOWEST, 1e10, MUL, MUL))
            for b in range(GB):
                i = b % 4
                vec.wait_ge(s["g_ready"], b + 1)
                step(nc.vector.tensor_scalar(sbk[:, i, :], rowv["l1x_bk"], gram[:, i, D:D + 1], None, MUL))
                vec.wait_ge(s["t_psum"], b + 1)
                step(nc.vector.scalar_tensor_tensor(t1[:, i, :], rowv["l1x_bv"], gram[:, i, D:D + 1], ps[:, 4 + b % 2, 0:D], MUL, ADD), s["t_ready"])
                vec.wait_ge(s["m_psum"], b + 1)
                step(nc.vector.tensor_tensor(kv[:, b, :], ps[:, 6 + b % 2, 0:D], k.same_head, MUL))
                step(nc.vector.tensor_tensor(kv[:, b, :], kv[:, b, :], c0[:], ADD), s["m_ready"])
            vec.wait_ge(s["z_psum"], 1)
            step(nc.vector.tensor_tensor(res[:], k.xn[:], ps[:, 5, :].rearrange("p (t d) -> p t d", d=D), ADD))
            step(nc.vector.tensor_tensor(res[:], res[:], over(rowv["l1x_bo"].unsqueeze(1), (P, T, D)), ADD))
            step(nc.vector.tensor_tensor(res[:], res[:], over(masked[:, 1, :].unsqueeze(2), (P, T, D)), ADD))
            normalise(k, step, res[:], res[:])
            step(nc.vector.tensor_tensor(res[:], res[:], over(rowv["l1x_g"].unsqueeze(1), (P, T, D)), MUL))
            step(nc.vector.tensor_tensor(res[:], res[:], over(rowv["l1x_b"].unsqueeze(1), (P, T, D)), ADD))
            step(nc.vector.tensor_tensor(k.xg[:], k.xg[:], res[:], ADD), s["residual"])

        @block.scalar
        def _(act):
            step = Steps(act, s["scalar_step"])
            norm_scalar(k, act, step, s)
            act.wait_ge(s["q_psum"], 1)
            step(nc.scalar.activation(qt[:], ps[:, 1, :], ACT.Identity, bias=colv["l1x_bq"]))
            step(nc.scalar.activation(qt[:], qt[:], ACT.Copy, scale=inv_dk), s["q_ready"])
            for b in range(GB):
                act.wait_ge(s["g_psum"], b + 1)
                if b >= 4:
                    act.wait_ge(s["m_psum"], b - 3)
                step(nc.scalar.activation(gram[:, b % 4, :], ps[:, 2 + b % 2, 0:D + 1], ACT.Copy), s["g_ready"])
            act.wait_ge(s["o_psum"], 1)
            step(nc.scalar.activation(k.ot[:], ps[:, 0, :], ACT.Copy), s["o_ready"])

        @block.tensor
        def _(pe):
            norm_tensor(k, pe, s)
            pe.wait_ge(s["xt_ready"], 1)
            nc.tensor.matmul(ps[:, 1, :], w["l1x_q"], k.xt[:], start=True, stop=True).then_inc(s["q_psum"], 1)
            pe.wait_ge(k.ctx_loaded, 32)

            def moments(b):
                if b >= 2:
                    pe.wait_ge(s["g_ready"], b - 1)
                bank = ps[:, 2 + b % 2, 0:D + 1]
                nc.tensor.matmul(bank, k.ctx[:, b, 0, 0:D], k.ctx[:, b, 0, :], start=True, stop=False)
                nc.tensor.matmul(bank, k.ctx[:, b, 1, 0:D], k.ctx[:, b, 1, :], start=False, stop=False)
                nc.tensor.matmul(bank, k.last[:, b, 0:D], k.last[:, b, :], start=False, stop=True).then_inc(s["g_psum"], 1)

            def values(b):
                pe.wait_ge(s["g_ready"], b + 1)
                if b >= 2:
                    pe.wait_ge(s["t_ready"], b - 1)
                nc.tensor.matmul(ps[:, 4 + b % 2, 0:D], gram[:, b % 4, 0:D], w["l1x_v"], start=True, stop=True).then_inc(s["t_psum"], 1)

            def keys(b):
                pe.wait_ge(s["t_ready"], b + 1)
                if b >= 2:
                    pe.wait_ge(s["m_ready"], b - 1)
                nc.tensor.matmul(ps[:, 6 + b % 2, 0:D], w["l1x_k"], t1[:, b % 4, :], start=True, stop=False)
                nc.tensor.matmul(ps[:, 6 + b % 2, 0:D], sbk[:, b % 4, :], w["l1x_v"], start=False, stop=True).then_inc(s["m_psum"], 1)

            for b in range(GB + 2):
                if b < GB:
                    moments(b)
                if 1 <= b <= GB:
                    values(b - 1)
                if b >= 2:
                    keys(b - 2)
            pe.wait_ge(s["q_ready"], 1)
            pe.wait_ge(s["m_ready"], GB)
            for b in range(GB):
                last = nc.tensor.matmul(ps[:, 0, b * L:(b + 1) * L], kv[:, b, :], qt[:, b * L:(b + 1) * L], start=True, stop=True)
            last.then_inc(s["o_psum"], 1)
            project(k, pe, s, w["l1x_o"])


def l1_attn(k, phase, w, rowv, colv):
    nc, ps = k.nc, k.ps
    s = k.signals(phase, "l1a", *NORM, "qkv_psum", "qkv_ready", "v_ready", "qt_psum", "qt_ready", "kv_psum", "kv_ready", "ks_psum",
                  "ks_ready", "kz_ready", "num_psum", "den_psum", "o_ready", "z_psum", "residual")
    with ExitStack() as own, nc.Block() as block:
        norm_tiles(k, own)
        qk = tile(k, own, "l1a_qk", P, T, 2 * H, DH)
        pw = tile(k, own, "l1a_pw", P, T, 2 * H, DH)
        sm = tile(k, own, "l1a_sums", P, T, 2 * H)
        v = tile(k, own, "l1a_v", P, T, D)
        qt = tile(k, own, "l1a_qt", P, GT)
        kv = tile(k, own, "l1a_kv", P, GB, D)
        kz = tile(k, own, "l1a_kz", P, GB, D)
        ks = tile(k, own, "l1a_ks", P, GB)
        out = tile(k, own, "l1a_out", P, GB, L)
        den = tile(k, own, "l1a_den", P, GB, L)
        k.ot = tile(k, own, "l1a_ot", P, GT)

        @block.vector
        def _(vec):
            step = Steps(vec, s["vector_step"])
            norm_vector(k, vec, step, s)
            for t in range(T):
                vec.wait_ge(s["qkv_psum"], t + 1)
                step(nc.vector.tensor_scalar(qk[:, t, :, :].rearrange("p h d -> p (h d)"), ps[:, 1 + t, 0:2 * D], 0.0, 1e-6, MAX, ADD), s["qkv_ready"])
            wide = (P, T * 2 * H, DH)
            q3, p3 = (a[:].rearrange("p t h d -> p (t h) d") for a in (qk, pw))
            s3 = sm[:].rearrange("p t h -> p (t h)")
            for power in (1, 3):
                if power == 3:
                    step(nc.vector.tensor_tensor(p3, q3, q3, MUL))
                    step(nc.vector.tensor_tensor(q3, q3, p3, MUL))
                step(nc.vector.reduce_sum(s3, q3, X))
                step(nc.vector.reciprocal(s3, s3))
                step(nc.vector.tensor_tensor(q3, q3, over(s3.unsqueeze(2), wide), MUL), None if power == 1 else s["qkv_ready"])
            vec.wait_ge(s["kv_psum"], 1)
            for j in range(BPT):
                step(nc.vector.tensor_tensor(kv[:].rearrange("p (t j) d -> p j t d", j=BPT)[:, j], ps[:, 1 + j, :].rearrange("p (t d) -> p t d", d=D),
                                             over(k.same_head.unsqueeze(1), (P, T, D)), MUL), s["kv_ready"])
            vec.wait_ge(s["den_psum"], 1)
            o, dn = out[:], den[:]
            step(nc.vector.tensor_scalar(dn, ps[:, 7, :].rearrange("p (b n) -> p b n", n=L), 1e-6, None, ADD))
            step(nc.vector.reciprocal(dn, dn))
            step(nc.vector.tensor_tensor(o, dn, ps[:, 6, :].rearrange("p (b n) -> p b n", n=L), MUL))
            ot = k.ot[:].rearrange("p (b n) -> p b n", n=L)
            before, here, after = (colv[f"l1a_w{i}"] for i in range(3))
            step(nc.vector.tensor_scalar(ot, o, here, colv["l1a_bc"], MUL, ADD))
            step(nc.vector.tensor_tensor(ot, ot, o, ADD))
            step(nc.vector.scalar_tensor_tensor(ot[:, :, 1:L], o[:, :, 0:L - 1], before, ot[:, :, 1:L], MUL, ADD))
            step(nc.vector.scalar_tensor_tensor(ot[:, :, 0:L - 1], o[:, :, 1:L], after, ot[:, :, 0:L - 1], MUL, ADD), s["o_ready"])
            add_projection(k, vec, step, s, rowv["l1a_bp"])

        @block.gpsimd
        def _(pool):
            pool.wait_ge(s["ks_ready"], 1)
            nc.gpsimd.tensor_tensor(kz[:], over(k.same_head.unsqueeze(1), (P, GB, D)), over(ks[:].unsqueeze(2), (P, GB, D)), MUL).then_inc(s["kz_ready"], 1)

        @block.scalar
        def _(act):
            step = Steps(act, s["scalar_step"])
            norm_scalar(k, act, step, s)
            for t in range(T):
                act.wait_ge(s["qkv_ready"], t + 1)
                step(nc.scalar.activation(v[:, t, :], ps[:, 1 + t, 2 * D:3 * D], ACT.Copy), s["v_ready"])
            act.wait_ge(s["ks_psum"], 1)
            step(nc.scalar.activation(ks[:], ps[:, 5, 0:GB], ACT.Copy), s["ks_ready"])
            act.wait_ge(s["qt_psum"], 1)
            step(nc.scalar.activation(qt[:], ps[:, 0, :], ACT.Copy), s["qt_ready"])

        @block.tensor
        def _(pe):
            norm_tensor(k, pe, s)
            pe.wait_ge(s["xt_ready"], 1)
            for t in range(T):
                nc.tensor.matmul(ps[:, 1 + t, 0:3 * D], k.xt[:, t * P:(t + 1) * P], w["l1a_qkv"], start=True, stop=True).then_inc(s["qkv_psum"], 1)
            pe.wait_ge(s["qkv_ready"], T + 1)
            pe.wait_ge(s["v_ready"], T)
            for t in range(T):
                last = nc.tensor.matmul(ps[:, 5, t * BPT:(t + 1) * BPT], qk[:, t, H:2 * H, :].rearrange("p h d -> p (h d)"), k.tile_batch, start=True, stop=True)
            last.then_inc(s["ks_psum"], 1)
            for t in range(T):
                for j in range(BPT):
                    r = slice(L * j, L * j + L)
                    last = nc.tensor.matmul(ps[:, 1 + j, t * D:(t + 1) * D], qk[r, t, H:2 * H, :].rearrange("p h d -> p (h d)"), v[r, t, :], start=True, stop=True)
            last.then_inc(s["kv_psum"], 1)
            for t in range(T):
                last = nc.tensor.transpose(ps[:, 0, t * P:(t + 1) * P], qk[:, t, 0:H, :].rearrange("p h d -> p (h d)"), k.ident)
            last.then_inc(s["qt_psum"], 1)
            pe.wait_ge(s["qt_ready"], 1)
            pe.wait_ge(s["kv_ready"], BPT)
            for b in range(GB):
                last = nc.tensor.matmul(ps[:, 6, b * L:(b + 1) * L], kv[:, b, :], qt[:, b * L:(b + 1) * L], start=True, stop=True)
            last.then_inc(s["num_psum"], 1)
            pe.wait_ge(s["kz_ready"], 1)
            for b in range(GB):
                last = nc.tensor.matmul(ps[:, 7, b * L:(b + 1) * L], kz[:, b, :], qt[:, b * L:(b + 1) * L], start=True, stop=True)
            last.then_inc(s["den_psum"], 1)
            pe.wait_ge(s["o_ready"], 1)
            for t in range(T):
                last = nc.tensor.matmul(ps[:, 5, t * D:(t + 1) * D], k.ot[:, t * P:(t + 1) * P], w["l1a_p"], start=True, stop=True)
            last.then_inc(s["z_psum"], 1)


def l1_router(k, phase, w, store_x, store_xn, store_logits):
    nc, ps = k.nc, k.ps
    s = k.signals(phase, "l1r", *NORM, "logits", "logits_ready", "stored")
    with ExitStack() as own, nc.Block() as block:
        norm_tiles(k, own)
        lg = tile(k, own, "l1r_logits", E1, GT)

        @block.vector
        def _(vec):
            norm_vector(k, vec, Steps(vec, s["vector_step"]), s)

        @block.scalar
        def _(act):
            step = Steps(act, s["scalar_step"])
            norm_scalar(k, act, step, s)
            act.wait_ge(s["logits"], 1)
            step(nc.scalar.activation(lg[:], ps[0:E1, 1, :], ACT.Copy), s["logits_ready"])

        @block.tensor
        def _(pe):
            norm_tensor(k, pe, s)
            pe.wait_ge(s["xt_ready"], 1)
            nc.tensor.matmul(ps[0:E1, 1, :], w["l1f_r"], k.xt[:], start=True, stop=True).then_inc(s["logits"], 1)

        @block.sync
        def _(sp):
            sp.dma_start(store_x, k.xg[:]).then_inc(s["stored"], 16)
            sp.wait_ge(s["xn_ready"], 1)
            sp.dma_start(store_xn, k.xn[:]).then_inc(s["stored"], 16)
            sp.wait_ge(s["logits_ready"], 1)
            sp.dma_start(store_logits, lg[:]).then_inc(s["stored"], 16)
            sp.wait_ge(s["stored"], 48)
            sp.wait_ge(k.ctxt_loaded, 16)
            sp.wait_ge(k.ctx_loaded, 32)


def phase_a(k, dram, groups, layers):
    nc = k.nc
    with ExitStack() as phase:
        wp = tile(k, phase, "a_weights", P, len(A_MATS), D)
        rp = tile(k, phase, "a_rows", P, len(A_ROWS), D)
        cp = tile(k, phase, "a_cols", P, len(A_COLS))
        wg, wr = tile(k, phase, "a_wg", P, E0), tile(k, phase, "a_wr", P, E1)
        w1, w2 = tile(k, phase, "a_w1", P, E0, HID0), tile(k, phase, "a_w2", P, E0, 4, D)
        k.ctxt = tile(k, phase, "ctx_t", P, GB, S2)
        k.ctx = tile(k, phase, "ctx_rows", P, GB, 2, D + 1)
        k.last = tile(k, phase, "ctx_last_row", 1, GB, D + 1)
        k.mask = tile(k, phase, "mask", P, T, S2, dtype=U8)
        w = {n: wp[:, i, :] for i, n in enumerate(A_MATS)}
        w["l1a_qkv"] = wp[:, A_MATS.index("l1a_q"):A_MATS.index("l1a_q") + 3, :].rearrange("p a d -> p (a d)")
        w.update({"l0f_g": wg[:], "l1f_r": wr[:], "l0f_w1": w1, "l0f_w2": w2})
        rowv = {n: rp[:, i, :] for i, n in enumerate(A_ROWS)}
        colv = {n: cp[:, i:i + 1] for i, n in enumerate(A_COLS)}
        loaded = phase.enter_context(nc.semaphore("a_weights_loaded"))
        with nc.Block() as block:
            @block.sync
            def _(sp):
                for dst, name in ((wp, "a_mats"), (cp, "a_cols"), (wg, "l0f_g"), (wr, "l1f_r"), (w1, "l0f_w1"), (w2, "l0f_w2")):
                    sp.dma_start(dst[:], dram[name]).then_inc(loaded, 16)
                sp.dma_start(rp[:], dram["a_rows"].partition_broadcast(P)).then_inc(loaded, 16)
                sp.wait_ge(loaded, 16 * 7)

        with nc.Fori(0, groups) as g:
            k.numbers = []
            k.x_loaded, k.ctxt_loaded, k.ctx_loaded, k.mask_loaded = (
                phase.enter_context(nc.semaphore("a_" + n)) for n in ("x_loaded", "ctxt_loaded", "ctx_loaded", "mask_loaded"))
            k.numbers += [sem.num for sem in (k.x_loaded, k.ctxt_loaded, k.ctx_loaded, k.mask_loaded)]
            with nc.Block() as block:
                @block.sync
                def _(sp):
                    sp.dma_start(k.xg[:], dram["x"].rearrange("(g t p) d -> g p t d", g=GROUPS, p=P)[g]).then_inc(k.x_loaded, 16)
                    sp.dma_start(k.ctxt[:], dram["ctx_t"].rearrange("p (g b s) -> g p b s", g=GROUPS, b=GB)[g]).then_inc(k.ctxt_loaded, 16)
                    sp.dma_start(k.ctx[:], dram["ctx_rows"].rearrange("p (g b) i d -> g p b i d", g=GROUPS)[g]).then_inc(k.ctx_loaded, 16)
                    sp.dma_start(k.last[:], dram["ctx_last"].rearrange("p (g b) d -> g p b d", g=GROUPS)[g]).then_inc(k.ctx_loaded, 16)
                    sp.dma_start(k.mask[:], dram["mask_bool"].rearrange("(g t p) s -> g p t s", g=GROUPS, p=P)[g]).then_inc(k.mask_loaded, 16)
                    sp.wait_ge(k.x_loaded, 16)
                    sp.wait_ge(k.mask_loaded, 16)

            if "l0x" in layers:
                l0_xattn(k, phase, w, dram["ctx"])
            if "l0a" in layers:
                l0_attn(k, phase, w, rowv, colv)
            if "l0f" in layers:
                l0_ffn(k, phase, w)
            if "l1x" in layers:
                l1_xattn(k, phase, w, rowv, colv)
            if "l1a" in layers:
                l1_attn(k, phase, w, rowv, colv)
            group = lambda a: a.rearrange("(g t p) d -> g p t d", g=GROUPS, p=P)[g]
            l1_router(k, phase, w, group(dram["x_a"]), group(dram["xn_a"]), dram["logits"].rearrange("e (g n) -> g e n", g=GROUPS)[g])
            k.clear_signals()


TOP_ROUNDS = CAP1 // 8
HALF = TOKENS // 2
HALF_AT = 64
PER = 4


def choose_tokens(k, phase, dram, weight_of, token_of):
    nc, ps = k.nc, k.ps
    s = k.signals(phase, "l1t", "loaded", "filled", "shifted", "exps", "merged", "turned", "zeroed", "zeros_stored")
    with ExitStack() as own, nc.Block() as block:
        lg = tile(k, own, "l1t_logits", HALF_AT + E1, HALF)
        val = tile(k, own, "l1t_values", HALF_AT + E1, CAP1)
        at = tile(k, own, "l1t_at", HALF_AT + E1, CAP1, dtype=U32)
        atf = tile(k, own, "l1t_at_f", HALF_AT + E1, CAP1)
        second = tile(k, own, "l1t_second", E1, 2, CAP1)
        both = tile(k, own, "l1t_both", E1, 4, CAP1)
        st = tile(k, own, "l1t_stats", E1, 2)
        zeros = tile(k, own, "l1t_zeros", P, TOKENS)

        @block.sync
        def _(sp):
            sp.wait_ge(s["filled"], 1)
            sp.dma_start(lg[0:E1, :], dram["logits"][:, 0:HALF]).then_inc(s["loaded"], 16)
            sp.dma_start(lg[HALF_AT:HALF_AT + E1, :], dram["logits"][:, HALF:TOKENS]).then_inc(s["loaded"], 16)
            sp.wait_ge(s["zeroed"], 1)
            for j in range(PER):
                sp.dma_start(dram[f"sums_{j}"].rearrange("(p q) d -> p (q d)", p=P), zeros[:]).then_inc(s["zeros_stored"], 16)
            sp.wait_ge(s["zeros_stored"], 16 * PER)

        @block.gpsimd
        def _(pool):
            nc.gpsimd.memset(zeros[:], 0.0).then_inc(s["zeroed"], 1)

        @block.vector
        def _(vec):
            step = Steps(vec, s["vector_step"])
            step(nc.vector.memset(lg[:], LOWEST), s["filled"])
            vec.wait_ge(s["loaded"], 32)
            for r in range(TOP_ROUNDS):
                eight = slice(8 * r, 8 * r + 8)
                step(nc.vector.max(val[:, eight], lg[:]))
                step(nc.vector.max_index(at[:, eight], val[:, eight], lg[:]))
                step(nc.vector.match_replace(lg[:], val[:, eight], lg[:], LOWEST))
            step(nc.vector.tensor_copy(atf[:], at[:]))
            step(nc.vector.tensor_copy(second[:, 0, :], val[HALF_AT:HALF_AT + E1, ::-1]))
            step(nc.vector.tensor_scalar(second[:, 1, :], atf[HALF_AT:HALF_AT + E1, ::-1], float(HALF), None, ADD))
            first, best, token, weight = (both[:, i, :] for i in range(4))
            step(nc.vector.tensor_tensor(first, val[0:E1, :], second[:, 0, :], ALU.is_ge))
            step(nc.vector.tensor_tensor(best, val[0:E1, :], second[:, 0, :], MAX))
            step(nc.vector.tensor_tensor(token, atf[0:E1, :], second[:, 1, :], SUB))
            step(nc.vector.tensor_tensor(token, token, first, MUL))
            step(nc.vector.tensor_tensor(token, token, second[:, 1, :], ADD))
            step(nc.vector.reduce_max(st[:, 0:1], best, X))
            step(nc.vector.tensor_scalar(weight, best, st[:, 0:1], None, SUB), s["shifted"])
            vec.wait_ge(s["exps"], 1)
            step(nc.vector.reduce_sum(st[:, 1:2], weight, X))
            step(nc.vector.reciprocal(st[:, 1:2], st[:, 1:2]))
            step(nc.vector.tensor_scalar(weight, weight, st[:, 1:2], None, MUL), s["merged"])
            vec.wait_ge(s["turned"], 1)
            step(nc.vector.tensor_copy(weight_of[:], ps[:, 0, 0:E1]))
            step(nc.vector.tensor_copy(token_of[:], ps[:, 0, E1:2 * E1]))

        @block.scalar
        def _(act):
            act.wait_ge(s["shifted"], 1)
            nc.scalar.activation(both[:, 3, :], both[:, 3, :], ACT.Exp).then_inc(s["exps"], 1)

        @block.tensor
        def _(pe):
            pe.wait_ge(s["merged"], 1)
            nc.tensor.transpose(ps[:, 0, 0:E1], both[:, 3, :], k.ident[0:E1, 0:E1])
            nc.tensor.transpose(ps[:, 0, E1:2 * E1], both[:, 2, :], k.ident[0:E1, 0:E1]).then_inc(s["turned"], 1)


def l1_experts(k, phase, dram, weight_of, token_of, b1):
    nc, ps = k.nc, k.ps
    with nc.Fori(0, E1 // PER) as n:
        k.numbers = []
        s = k.signals(phase, "l1e", "picked", "weights_loaded", "gathered", "xt_psum", "xt_ready", "hidden_psum", "hidden_ready", "y_psum",
                      "y_ready", "scattered")
        with ExitStack() as own, nc.Block() as block:
            rows = tile(k, own, "l1e_rows", P, PER, dtype=I32)
            wt = tile(k, own, "l1e_weight", P, PER)
            b1n = tile(k, own, "l1e_b1", P, PER * S1)
            w1 = tile(k, own, "l1e_w1", P, PER, S1, P)
            w2 = tile(k, own, "l1e_w2", P, PER, S1, KW)
            b2 = tile(k, own, "l1e_b2", P, PER, D)
            xe = tile(k, own, "l1e_x", P, PER, D)
            xet = tile(k, own, "l1e_xt", P, PER, P)
            hid = tile(k, own, "l1e_hidden", P, PER, S1, P)
            y = tile(k, own, "l1e_y", P, PER, D)

            @block.sync
            def _(sp):
                sp.dma_start(w1[:], dram["l1f_w1"].rearrange("p (n e) s m -> n p e s m", e=PER)[n]).then_inc(s["weights_loaded"], 16)
                sp.dma_start(w2[:], dram["l1f_w2"].rearrange("p (n e) s m -> n p e s m", e=PER)[n]).then_inc(s["weights_loaded"], 16)
                sp.dma_start(b2[:], dram["l1f_b2"].rearrange("(n e) d -> n e d", e=PER)[n].partition_broadcast(P)).then_inc(s["weights_loaded"], 16)

            @block.vector
            def _(vec):
                step = Steps(vec, s["vector_step"])
                step(nc.vector.tensor_copy(rows[:], token_of[:, bass.ts(n, PER)]), s["picked"])
                step(nc.vector.tensor_copy(wt[:], weight_of[:, bass.ts(n, PER)]))
                step(nc.vector.tensor_copy(b1n[:], b1[:, bass.ts(n, PER * S1)]), s["picked"])
                vec.wait_ge(s["weights_loaded"], 48)
                vec.wait_ge(s["y_psum"], 1)
                step(nc.vector.tensor_tensor(y[:], b2[:], ps[:, 5, :].rearrange("p (e d) -> p e d", d=D), ADD))
                step(nc.vector.tensor_tensor(y[:], y[:], over(wt[:].unsqueeze(2), (P, PER, D)), MUL), s["y_ready"])

            @block.gpsimd
            def _(pool):
                pool.wait_ge(s["picked"], 1)
                for e in range(PER):
                    nc.gpsimd.indirect_dma_start(out=xe[:, e, :], out_offset=None, in_=dram["xn_a"],
                                                 in_offset=bass.IndirectOffsetOnAxis(ap=rows[:, e:e + 1], axis=0)).then_inc(s["gathered"], 16)
                pool.wait_ge(s["gathered"], 16 * PER)
                pool.wait_ge(s["y_ready"], 1)
                for e in range(PER):
                    nc.gpsimd.indirect_dma_start(out=dram[f"sums_{e}"], out_offset=bass.IndirectOffsetOnAxis(ap=rows[:, e:e + 1], axis=0),
                                                 in_=y[:, e, :], in_offset=None, compute_op=ADD).then_inc(s["scattered"], 16)
                pool.wait_ge(s["scattered"], 16 * PER)

            @block.scalar
            def _(act):
                step = Steps(act, s["scalar_step"])
                act.wait_ge(s["xt_psum"], 1)
                step(nc.scalar.activation(xet[:].rearrange("p e c -> p (e c)"), ps[:, 0, :], ACT.Copy), s["xt_ready"])
                act.wait_ge(s["picked"], 2)
                for e in range(PER):
                    act.wait_ge(s["hidden_psum"], e + 1)
                    for i in range(S1):
                        step(nc.scalar.activation(hid[:, e, i, :], ps[:, 1 + e, i * P:(i + 1) * P], ACT.Gelu,
                                                  bias=b1n[:, e * S1 + i:e * S1 + i + 1]), s["hidden_ready"])

            @block.tensor
            def _(pe):
                pe.wait_ge(s["gathered"], 16 * PER)
                for e in range(PER):
                    last = nc.tensor.transpose(ps[:, 0, e * P:(e + 1) * P], xe[:, e, :], k.ident)
                last.then_inc(s["xt_psum"], 1)
                pe.wait_ge(s["xt_ready"], 1)
                pe.wait_ge(s["weights_loaded"], 48)
                for e in range(PER):
                    for i in range(S1):
                        last = nc.tensor.matmul(ps[:, 1 + e, i * P:(i + 1) * P], w1[:, e, i, :], xet[:, e, :], start=True, stop=True)
                    last.then_inc(s["hidden_psum"], 1)
                for e in range(PER):
                    for i in range(S1):
                        pe.wait_ge(s["hidden_ready"], e * S1 + i + 1)
                        last = nc.tensor.matmul(ps[:, 5, e * D + i * KW:e * D + (i + 1) * KW], hid[:, e, i, :], w2[:, e, i, :], start=True, stop=True)
                last.then_inc(s["y_psum"], 1)
        k.clear_signals()


def phase_b(k, dram):
    nc = k.nc
    with ExitStack() as phase:
        weight_of = tile(k, phase, "l1_weight_of", P, E1)
        token_of = tile(k, phase, "l1_token_of", P, E1, dtype=I32)
        b1 = tile(k, phase, "l1_b1", P, E1 * S1)
        loaded = phase.enter_context(nc.semaphore("b_b1_loaded"))
        with nc.Block() as block:
            @block.sync
            def _(sp):
                sp.dma_start(b1[:], dram["l1f_b1"]).then_inc(loaded, 16)
                sp.wait_ge(loaded, 16)
        choose_tokens(k, phase, dram, weight_of, token_of)
        l1_experts(k, phase, dram, weight_of, token_of, b1)


def l2_xattn(k, phase, w, rowv, colv, biases):
    nc, ps = k.nc, k.ps
    s = k.signals(phase, "l2x", *NORM, "qw_ready", "scores", "neg_ready", "exps", "p_ready", "turned", "pt_ready", "c2q_psum", "c2q_ready",
                  "best_ready", "best_turned", "b_shifted", "b_exps", "b_ready", "b_back", "bd_ready", "q2c_psum", "cat_ready", "z_psum", "residual")
    ROW = 300
    with ExitStack() as own, nc.Block() as block:
        norm_tiles(k, own)
        qw = tile(k, own, "l2x_qw", P, GT)
        pr = tile(k, own, "l2x_p", P, T, S2)
        st = tile(k, own, "l2x_stats", P, 4, T)
        pt = tile(k, own, "l2x_pt", P, 2, GT)
        ptl = tile(k, own, "l2x_pt_last", 1, GT)
        ba = tile(k, own, "l2x_batch_att", T, BPT, L)
        bs = tile(k, own, "l2x_batch_stats", T, 2, BPT)
        bd = tile(k, own, "l2x_batch_att_x", P, T, BPT)
        q2c = tile(k, own, "l2x_q2c", P, GB)
        cat = tile(k, own, "l2x_cat", P, 3, GT)
        total = tile(k, own, "l2x_bias", P, 1)

        @block.vector
        def _(vec):
            step = Steps(vec, s["vector_step"])
            norm_vector(k, vec, step, s)
            step(nc.vector.reduce_sum(total[:], biases, X))
            vec.wait_ge(s["xt_ready"], 1)
            step(nc.vector.tensor_scalar(qw[:], k.xt[:], colv["l2x_wcq"], colv["l2x_wq"], MUL, ADD), s["qw_ready"])
            mx, neg, best, rs = (st[:, i, :] for i in range(4))
            vec.wait_ge(s["scores"], 1)
            step(nc.vector.reduce_max(mx, ps[:, 0:T, 0:S2], X))
            step(nc.vector.tensor_scalar(best, ps[:, 0, ROW:ROW + T], total[:], None, ADD))
            step(nc.vector.tensor_tensor(best, best, mx, ADD), s["best_ready"])
            step(nc.vector.tensor_scalar(neg, mx, -1.0, None, MUL), s["neg_ready"])
            vec.wait_ge(s["exps"], T)
            step(nc.vector.reciprocal(rs, rs))
            step(nc.vector.tensor_tensor(pr[:], pr[:], over(rs.unsqueeze(2), (P, T, S2)), MUL), s["p_ready"])
            bmx, bsum = bs[:, 0, :], bs[:, 1, :]
            vec.wait_ge(s["best_turned"], 1)
            got = ps[0:T, 7, 0:P].rearrange("p (j n) -> p j n", n=L)
            step(nc.vector.reduce_max(bmx, got, X))
            step(nc.vector.tensor_tensor(ba[:], got, over(bmx.unsqueeze(2), (T, BPT, L)), SUB), s["b_shifted"])
            vec.wait_ge(s["b_exps"], 1)
            step(nc.vector.reduce_sum(bsum, ba[:], X))
            step(nc.vector.reciprocal(bsum, bsum))
            step(nc.vector.tensor_tensor(ba[:], ba[:], over(bsum.unsqueeze(2), (T, BPT, L)), MUL), s["b_ready"])
            vec.wait_ge(s["turned"], 1)
            step(nc.vector.tensor_copy(pt[:, 1, :], ps[:, 5, :]), s["pt_ready"])
            vec.wait_ge(s["b_back"], 1)
            step(nc.vector.tensor_tensor(bd[:], over(ps[:, 0, 0:T].unsqueeze(2), (P, T, BPT)), over(k.tile_batch.unsqueeze(1), (P, T, BPT)), MUL), s["bd_ready"])
            vec.wait_ge(s["q2c_psum"], 1)
            step(nc.vector.tensor_copy(q2c[:], ps[:, 1, 0:GB]))
            step(nc.vector.tensor_tensor(cat[:, 2, :].rearrange("p (b n) -> p b n", n=L), k.xt[:].rearrange("p (b n) -> p b n", n=L),
                                         over(q2c[:].unsqueeze(2), (P, GB, L)), MUL), s["cat_ready"])
            vec.wait_ge(s["c2q_ready"], 1)
            step(nc.vector.tensor_tensor(cat[:, 1, :], cat[:, 0, :], k.xt[:], MUL), s["cat_ready"])
            add_projection(k, vec, step, s, rowv["l2x_bl"])

        @block.scalar
        def _(act):
            step = Steps(act, s["scalar_step"])
            norm_scalar(k, act, step, s, bank=4)
            act.wait_ge(s["neg_ready"], 1)
            for t in range(T):
                step(nc.scalar.activation(pr[:, t, :], ps[:, t, 0:S2], ACT.Exp, bias=st[:, 1, t:t + 1], accum_out=st[:, 3, t:t + 1]), s["exps"])
            act.wait_ge(s["b_shifted"], 1)
            step(nc.scalar.activation(ba[:], ba[:], ACT.Exp), s["b_exps"])
            act.wait_ge(s["turned"], 1)
            step(nc.scalar.activation(pt[:, 0, :], ps[:, 4, :], ACT.Copy))
            step(nc.scalar.activation(ptl[:], ps[0:1, 6, :], ACT.Copy))
            act.wait_ge(s["pt_ready"], 1)
            act.wait_ge(s["c2q_psum"], 1)
            step(nc.scalar.activation(cat[:, 0, :], ps[:, 2, :], ACT.Copy), s["c2q_ready"])

        @block.tensor
        def _(pe):
            norm_tensor(k, pe, s, bank=4)
            pe.wait_ge(s["xt_ready"], 1)
            for t in range(T):
                nc.tensor.matmul(ps[:, 0, ROW + t:ROW + t + 1], k.xt[:, t * P:(t + 1) * P], colv["l2x_wc"], start=True, stop=True)
            pe.wait_ge(s["qw_ready"], 1)
            for t in range(T):
                for j in range(BPT):
                    b = t * BPT + j
                    last = nc.tensor.matmul(ps[L * j:L * j + L, t, 0:S2], qw[:, b * L:(b + 1) * L], k.ctxt[:, b, :], start=True, stop=True)
            last.then_inc(s["scores"], 1)
            pe.wait_ge(s["best_ready"], 1)
            nc.tensor.transpose(ps[0:T, 7, 0:P], st[:, 2, :], k.ident).then_inc(s["best_turned"], 1)
            pe.wait_ge(s["p_ready"], 1)
            for t in range(T):
                for i in range(2):
                    nc.tensor.transpose(ps[:, 4 + i, t * P:(t + 1) * P], pr[:, t, i * P:(i + 1) * P], k.ident)
                last = nc.tensor.transpose(ps[0:1, 6, t * P:(t + 1) * P], pr[:, t, 2 * P:S2], k.ident)
            last.then_inc(s["turned"], 1)
            pe.wait_ge(s["b_ready"], 1)
            nc.tensor.transpose(ps[:, 0, 0:T], ba[:].rearrange("t j n -> t (j n)"), k.ident[0:T, 0:T]).then_inc(s["b_back"], 1)
            pe.wait_ge(s["pt_ready"], 1)
            pe.wait_ge(s["scalar_step"], 2)
            for b in range(GB):
                c = slice(b * L, (b + 1) * L)
                nc.tensor.matmul(ps[:, 2, c], k.ctx[:, b, 0, 0:D], pt[:, 0, c], start=True, stop=False)
                nc.tensor.matmul(ps[:, 2, c], k.ctx[:, b, 1, 0:D], pt[:, 1, c], start=False, stop=False)
                last = nc.tensor.matmul(ps[:, 2, c], k.last[:, b, 0:D], ptl[:, c], start=False, stop=True)
            last.then_inc(s["c2q_psum"], 1)
            pe.wait_ge(s["bd_ready"], 1)
            for t in range(T):
                last = nc.tensor.matmul(ps[:, 1, t * BPT:(t + 1) * BPT], k.xn[:, t, :], bd[:, t, :], start=True, stop=True)
            last.then_inc(s["q2c_psum"], 1)
            pe.wait_ge(s["cat_ready"], 2)
            for t in range(T):
                c = slice(t * P, (t + 1) * P)
                for i, src in enumerate((k.xt[:, c], cat[:, 0, c], cat[:, 1, c], cat[:, 2, c])):
                    last = nc.tensor.matmul(ps[:, 5, t * D:(t + 1) * D], src, w["l2x_l"][:, i * D:(i + 1) * D], start=i == 0, stop=i == 3)
            last.then_inc(s["z_psum"], 1)


def self_attn(k, phase, name, wq, wk, wv, wo, scale, bias=None):
    nc, ps = k.nc, k.ps
    s = k.signals(phase, name, *NORM, *CORE)
    with ExitStack() as own, nc.Block() as block:
        norm_tiles(k, own)
        core_tiles(k, own)

        @block.vector
        def _(vec):
            step = Steps(vec, s["vector_step"])
            norm_vector(k, vec, step, s)
            q_by_head(k, vec, step, s)
            v_by_head(k, vec, step, s)
            core_vector(k, vec, step, s, scale, True, bias)

        @block.gpsimd
        def _(pool):
            pool.wait_ge(s["xt_ready"], 1)
            nc.gpsimd.tensor_copy(k.rep[:], four_times(k, k.xt[:])).then_inc(s["rep_ready"], 1)

        @block.scalar
        def _(act):
            step = Steps(act, s["scalar_step"])
            norm_scalar(k, act, step, s)
            act.wait_ge(s["k_psum"], 1)
            step(nc.scalar.activation(k.kt[:], ps[:, 2, :], ACT.Copy), s["k_ready"])
            core_scalar(k, act, step, s, scale, True)

        @block.tensor
        def _(pe):
            norm_tensor(k, pe, s)
            pe.wait_ge(s["xt_ready"], 1)
            nc.tensor.matmul(ps[:, 1, :], wq, k.xt[:], start=True, stop=True).then_inc(s["q_psum"], 1)
            nc.tensor.matmul(ps[:, 2, :], wk, k.xt[:], start=True, stop=True).then_inc(s["k_psum"], 1)
            core_tensor(k, pe, s, wv, wo)


def l2_norm_out(k, phase, store_x, store_xt, largest):
    nc = k.nc
    s = k.signals(phase, "l2n", *NORM, "stored")
    with ExitStack() as own, nc.Block() as block:
        norm_tiles(k, own)
        mx = tile(k, own, "l2n_mx", P, 1)

        @block.vector
        def _(vec):
            step = Steps(vec, s["vector_step"])
            norm_vector(k, vec, step, s)
            step(nc.vector.reduce_max(mx[:], k.xn[:].rearrange("p t d -> p (t d)"), X, apply_absolute_value=True))
            step(nc.vector.tensor_tensor(largest, largest, mx[:], MAX))

        @block.scalar
        def _(act):
            norm_scalar(k, act, Steps(act, s["scalar_step"]), s)

        @block.tensor
        def _(pe):
            norm_tensor(k, pe, s)

        @block.sync
        def _(sp):
            sp.dma_start(store_x, k.xg[:]).then_inc(s["stored"], 16)
            sp.wait_ge(s["xt_ready"], 1)
            sp.dma_start(store_xt, k.xt[:]).then_inc(s["stored"], 16)
            sp.wait_ge(s["stored"], 32)


def phase_c(k, dram, groups, layers, largest):
    nc = k.nc
    with ExitStack() as phase:
        wp = tile(k, phase, "c_weights", P, len(C_MATS), D)
        rp = tile(k, phase, "c_rows", P, len(C_ROWS), D)
        cp = tile(k, phase, "c_cols", P, len(C_COLS))
        wl = tile(k, phase, "c_wl", P, 4 * D)
        bc = tile(k, phase, "c_biases", P, 3)
        k.ctxt = tile(k, phase, "c_ctx_t", P, GB, S2)
        k.ctx = tile(k, phase, "c_ctx_rows", P, GB, 2, D + 1)
        k.last = tile(k, phase, "c_ctx_last_row", 1, GB, D + 1)
        sums = tile(k, phase, "c_sums", P, PER, T, D)
        w = {n: wp[:, i, :] for i, n in enumerate(C_MATS)}
        w["l2x_l"] = wl[:]
        rowv = {n: rp[:, i, :] for i, n in enumerate(C_ROWS)}
        colv = {n: cp[:, i:i + 1] for i, n in enumerate(C_COLS)}
        loaded = phase.enter_context(nc.semaphore("c_weights_loaded"))
        cleared = phase.enter_context(nc.semaphore("c_largest_cleared"))
        with nc.Block() as block:
            @block.sync
            def _(sp):
                for dst, name in ((wp, "c_mats"), (cp, "c_cols"), (wl, "l2x_l")):
                    sp.dma_start(dst[:], dram[name]).then_inc(loaded, 16)
                sp.dma_start(rp[:], dram["c_rows"].partition_broadcast(P)).then_inc(loaded, 16)
                sp.dma_start(bc[:], dram["l2x_biases"].partition_broadcast(P)).then_inc(loaded, 16)
                sp.wait_ge(loaded, 16 * 5)

            @block.vector
            def _(vec):
                nc.vector.memset(largest, 0.0).then_inc(cleared, 1)
                vec.wait_ge(cleared, 1)

        with nc.Fori(0, groups) as g:
            k.numbers = []
            s = k.signals(phase, "c_load", "x_loaded", "sums_loaded", "ctx_loaded")
            group = lambda a: a.rearrange("(g t p) d -> g p t d", g=GROUPS, p=P)[g]
            with nc.Block() as block:
                @block.sync
                def _(sp):
                    sp.dma_start(k.xg[:], group(dram["x_a"])).then_inc(s["x_loaded"], 16)
                    for j in range(PER):
                        sp.dma_start(sums[:, j, :, :], group(dram[f"sums_{j}"])).then_inc(s["sums_loaded"], 16)
                    sp.dma_start(k.ctxt[:], dram["ctx_t"].rearrange("p (g b s) -> g p b s", g=GROUPS, b=GB)[g]).then_inc(s["ctx_loaded"], 16)
                    sp.dma_start(k.ctx[:], dram["ctx_rows"].rearrange("p (g b) i d -> g p b i d", g=GROUPS)[g]).then_inc(s["ctx_loaded"], 16)
                    sp.dma_start(k.last[:], dram["ctx_last"].rearrange("p (g b) d -> g p b d", g=GROUPS)[g]).then_inc(s["ctx_loaded"], 16)
                    sp.wait_ge(s["ctx_loaded"], 48)

                @block.vector
                def _(vec):
                    step = Steps(vec, s["vector_step"])
                    vec.wait_ge(s["x_loaded"], 16)
                    vec.wait_ge(s["sums_loaded"], 16 * PER)
                    for j in range(PER if "l1f" in layers else 0):
                        step(nc.vector.tensor_tensor(k.xg[:], k.xg[:], sums[:, j, :, :], ADD))

            if "l2x" in layers:
                l2_xattn(k, phase, w, rowv, colv, bc[:])
            if "l2a" in layers:
                self_attn(k, phase, "l2a", w["l2a_q"], w["l2a_k"], w["l2a_v"], w["l2a_u"], D ** -0.5, rowv["l2a_bu"])
            l2_norm_out(k, phase, group(dram["x_c"]), dram["xt_c"].rearrange("p (g n) -> g p n", g=GROUPS)[g], largest)
            k.clear_signals()


ROUND = 1.5 * 2.0 ** 23
ACT_MAX = 2.0 ** 15 - 1.0
SIG_STEPS = 65536.0
BLOCK2, W_MAX = 32, 7.0
CH2 = I2 // P


def quantise(k, step, x, inverse, scale, low, high, signal=None):
    v = k.nc.vector
    step(v.tensor_scalar(x, x, inverse, ROUND, MUL, ADD))
    step(v.tensor_scalar(x, x, ROUND, high, SUB, MIN))
    step(v.tensor_scalar(x, x, low, scale, MAX, MUL), signal)


def quantise_weights(k, phase, dram, up, gate, down):
    nc, ps = k.nc, k.ps
    s = k.signals(phase, "l2w", "loaded", "quantised", "turned")
    with ExitStack() as own, nc.Block() as block:
        blocks = CH2 * P // BLOCK2
        wt = tile(k, own, "l2w", P, 3, blocks, BLOCK2)
        sc = tile(k, own, "l2w_scale", P, 3, blocks)
        inv = tile(k, own, "l2w_inverse", P, 3, blocks)

        @block.sync
        def _(sp):
            for i, name in enumerate(("l2f_up", "l2f_gate", "l2f_down")):
                sp.dma_start(wt[:, i, :, :].rearrange("p b i -> p (b i)"), dram[name]).then_inc(s["loaded"], 16)

        @block.vector
        def _(vec):
            step = Steps(vec, s["vector_step"])
            vec.wait_ge(s["loaded"], 48)
            w3 = wt[:].rearrange("p a b i -> p (a b) i")
            s2, i2 = sc[:].rearrange("p a b -> p (a b)"), inv[:].rearrange("p a b -> p (a b)")
            step(nc.vector.reduce_max(s2, w3, X, apply_absolute_value=True))
            step(nc.vector.tensor_scalar(s2, s2, 1.0 / W_MAX, 1e-12, MUL, MAX))
            step(nc.vector.reciprocal(i2, s2))
            wide = (P, 3 * blocks, BLOCK2)
            step(nc.vector.tensor_tensor(w3, w3, over(i2.unsqueeze(2), wide), MUL))
            step(nc.vector.tensor_scalar(w3, w3, ROUND, ROUND, ADD, SUB))
            step(nc.vector.tensor_scalar(w3, w3, -W_MAX - 1.0, W_MAX, MAX, MIN))
            step(nc.vector.tensor_tensor(w3, w3, over(s2.unsqueeze(2), wide), MUL), s["quantised"])
            vec.wait_ge(s["turned"], 1)
            for i, dst in enumerate((up, gate, down)):
                step(nc.vector.tensor_copy(dst, ps[:, i, 0:I2]))

        @block.tensor
        def _(pe):
            pe.wait_ge(s["quantised"], 1)
            for i in range(3):
                for c in range(CH2):
                    last = nc.tensor.transpose(ps[:, i, c * P:(c + 1) * P], wt[:, i, c * 4:(c + 1) * 4, :].rearrange("p b i -> p (b i)"), k.ident)
            last.then_inc(s["turned"], 1)


def scale_of_largest(k, phase, name, columns, scales):
    nc, ps = k.nc, k.ps
    s = k.signals(phase, name, "turned", "found", "spread")
    n = len(columns)
    with ExitStack() as own, nc.Block() as block:
        one = tile(k, own, name + "_one", 1, n)

        @block.tensor
        def _(pe):
            for i, column in enumerate(columns):
                last = nc.tensor.transpose(ps[0:1, 0, i * P:(i + 1) * P], column, k.ident)
            last.then_inc(s["turned"], 1)
            pe.wait_ge(s["found"], 1)
            nc.tensor.matmul(ps[:, 1, 0:n], k.ones[0:1, :], one[:], start=True, stop=True).then_inc(s["spread"], 1)

        @block.vector
        def _(vec):
            step = Steps(vec, s["vector_step"])
            vec.wait_ge(s["turned"], 1)
            step(nc.vector.reduce_max(one[:], ps[0:1, 0, 0:n * P].rearrange("p (n q) -> p n q", n=n), X), s["found"])
            vec.wait_ge(s["spread"], 1)
            step(nc.vector.tensor_scalar(scales[:, 0, 0:n], ps[:, 1, 0:n], 1.0 / ACT_MAX, 1e-12, MUL, MAX))
            step(nc.vector.reciprocal(scales[:, 1, 0:n], scales[:, 0, 0:n]))


def phase_d(k, dram, groups, largest):
    nc, ps = k.nc, k.ps
    with ExitStack() as phase:
        wup, wgate = tile(k, phase, "l2f_up_t", P, I2), tile(k, phase, "l2f_gate_t", P, I2)
        wdown = tile(k, phase, "l2f_down_t", P, CH2, D)
        up = tile(k, phase, "l2f_up", P, GROUPS, CH2 * GT)
        gate = tile(k, phase, "l2f_gate", P, GROUPS, CH2 * GT)
        big = tile(k, phase, "l2f_largest", P, 2)
        new = tile(k, phase, "l2f_largest_here", P, 2)
        scales = tile(k, phase, "l2f_scales", P, 4, 2, 2)
        quantise_weights(k, phase, dram, wup[:], wgate[:], wdown[:].rearrange("p c d -> p (c d)"))
        scale_of_largest(k, phase, "l2f_x_scale", (largest,), scales[:, 0, :, :])

        def clear_largest(name):
            s = k.signals(phase, name, "cleared")
            with nc.Block() as block:
                @block.vector
                def _(vec):
                    Steps(vec, s["vector_step"])(nc.vector.memset(big[:], 0.0), s["cleared"])

        def scale(n, kind, column):
            return scales[:, n, kind, column:column + 1]

        clear_largest("l2f_clear_ug")
        with nc.Fori(0, groups) as g:
            k.numbers = []
            s = k.signals(phase, "l2f_ug", "loaded", "xq_ready", "psum", "copied", "measured")
            with ExitStack() as own, nc.Block() as block:
                xq = tile(k, own, "l2f_xq", P, GT)

                @block.sync
                def _(sp):
                    sp.dma_start(xq[:], dram["xt_c"].rearrange("p (g n) -> g p n", g=GROUPS)[g]).then_inc(s["loaded"], 16)

                @block.vector
                def _(vec):
                    step = Steps(vec, s["vector_step"])
                    vec.wait_ge(s["loaded"], 16)
                    quantise(k, step, xq[:], scale(0, 1, 0), scale(0, 0, 0), -ACT_MAX - 1.0, ACT_MAX, s["xq_ready"])
                    vec.wait_ge(s["psum"], 2)
                    for i in range(2):
                        step(nc.vector.reduce_max(new[:, i:i + 1], ps[:, i * CH2:(i + 1) * CH2, :].rearrange("p c n -> p (c n)"), X, apply_absolute_value=True), s["measured"])
                    step(nc.vector.tensor_tensor(big[:], big[:], new[:], MAX))

                @block.scalar
                def _(act):
                    step = Steps(act, s["scalar_step"])
                    for i, dst in enumerate((up, gate)):
                        act.wait_ge(s["measured"], i + 1)
                        step(nc.scalar.activation(dst[:, bass.ds(g, 1), :].rearrange("p a n -> p (a n)"),
                                                  ps[:, i * CH2:(i + 1) * CH2, :].rearrange("p c n -> p (c n)"), ACT.Copy), s["copied"])

                @block.tensor
                def _(pe):
                    pe.wait_ge(s["xq_ready"], 1)
                    for i, wt in enumerate((wup, wgate)):
                        for c in range(CH2):
                            last = nc.tensor.matmul(ps[:, i * CH2 + c, :], wt[:, c * P:(c + 1) * P], xq[:], start=True, stop=True)
                        last.then_inc(s["psum"], 1)
            k.clear_signals()
        scale_of_largest(k, phase, "l2f_ug_scale", (big[:, 0:1], big[:, 1:2]), scales[:, 1, :, :])

        clear_largest("l2f_clear_act")
        with nc.Fori(0, groups) as g:
            k.numbers = []
            s = k.signals(phase, "l2f_act", "gate_ready", "sig_ready")
            with ExitStack() as own, nc.Block() as block:
                sig = tile(k, own, "l2f_sigmoid", P, CH2 * GT)
                u, gt = (a[:, bass.ds(g, 1), :].rearrange("p a n -> p (a n)") for a in (up, gate))

                @block.vector
                def _(vec):
                    step = Steps(vec, s["vector_step"])
                    quantise(k, step, gt, scale(1, 1, 1), scale(1, 0, 1), -ACT_MAX - 1.0, ACT_MAX, s["gate_ready"])
                    quantise(k, step, u, scale(1, 1, 0), scale(1, 0, 0), -ACT_MAX - 1.0, ACT_MAX)
                    vec.wait_ge(s["sig_ready"], 1)
                    step(nc.vector.tensor_scalar(sig[:], sig[:], SIG_STEPS, ROUND, MUL, ADD))
                    step(nc.vector.tensor_scalar(sig[:], sig[:], ROUND, SIG_STEPS - 1.0, SUB, MIN))
                    step(nc.vector.tensor_scalar(sig[:], sig[:], 0.0, 1.0 / SIG_STEPS, MAX, MUL))
                    step(nc.vector.tensor_tensor(gt, gt, sig[:], MUL))
                    step(nc.vector.reduce_max(new[:, 0:1], gt, X, apply_absolute_value=True))
                    step(nc.vector.tensor_tensor(big[:, 0:1], big[:, 0:1], new[:, 0:1], MAX))

                @block.scalar
                def _(act):
                    act.wait_ge(s["gate_ready"], 1)
                    nc.scalar.activation(sig[:], gt, ACT.Sigmoid).then_inc(s["sig_ready"], 1)
            k.clear_signals()
        scale_of_largest(k, phase, "l2f_act_scale", (big[:, 0:1],), scales[:, 2, :, :])

        clear_largest("l2f_clear_o")
        with nc.Fori(0, groups) as g:
            k.numbers = []
            s = k.signals(phase, "l2f_mul")
            with nc.Block() as block:
                u, gt = (a[:, bass.ds(g, 1), :].rearrange("p a n -> p (a n)") for a in (up, gate))

                @block.vector
                def _(vec):
                    step = Steps(vec, s["vector_step"])
                    quantise(k, step, gt, scale(2, 1, 0), scale(2, 0, 0), -ACT_MAX - 1.0, ACT_MAX)
                    step(nc.vector.tensor_tensor(gt, gt, u, MUL))
                    step(nc.vector.reduce_max(new[:, 0:1], gt, X, apply_absolute_value=True))
                    step(nc.vector.tensor_tensor(big[:, 0:1], big[:, 0:1], new[:, 0:1], MAX))
            k.clear_signals()
        scale_of_largest(k, phase, "l2f_o_scale", (big[:, 0:1],), scales[:, 3, :, :])

        with nc.Fori(0, groups) as g:
            k.numbers = []
            s = k.signals(phase, "l2f_down", "loaded", "oq_ready", "psum", "x_ready", "stored")
            group = lambda a: a.rearrange("(g t p) d -> g p t d", g=GROUPS, p=P)[g]
            with ExitStack() as own, nc.Block() as block:
                oq = tile(k, own, "l2f_oq", P, CH2, GT)
                gt = gate[:, bass.ds(g, 1), :].rearrange("p a n -> p (a n)")

                @block.sync
                def _(sp):
                    sp.dma_start(k.xg[:], group(dram["x_c"])).then_inc(s["loaded"], 16)
                    sp.wait_ge(s["x_ready"], 1)
                    sp.dma_start(group(dram["x_d"]), k.xg[:]).then_inc(s["stored"], 16)
                    sp.wait_ge(s["stored"], 16)

                @block.vector
                def _(vec):
                    step = Steps(vec, s["vector_step"])
                    flat = oq[:].rearrange("p c n -> p (c n)")
                    step(nc.vector.tensor_copy(flat, gt))
                    quantise(k, step, flat, scale(3, 1, 0), scale(3, 0, 0), -ACT_MAX - 1.0, ACT_MAX, s["oq_ready"])
                    vec.wait_ge(s["loaded"], 16)
                    vec.wait_ge(s["psum"], 1)
                    step(nc.vector.tensor_tensor(k.xg[:], k.xg[:], ps[:, 0, :].rearrange("p (t d) -> p t d", d=D), ADD), s["x_ready"])

                @block.tensor
                def _(pe):
                    pe.wait_ge(s["oq_ready"], 1)
                    for t in range(T):
                        for c in range(CH2):
                            last = nc.tensor.matmul(ps[:, 0, t * D:(t + 1) * D], oq[:, c, t * P:(t + 1) * P], wdown[:, c, :], start=c == 0, stop=c == CH2 - 1)
                    last.then_inc(s["psum"], 1)
            k.clear_signals()


CHUNKS = GB * S2
Q = 4


def l3_xattn(k, phase, w, rowv, colv):
    nc, ps = k.nc, k.ps
    s = k.signals(phase, "l3x", *NORM, "q_psum", "qx_ready", "kt_psum", "kt_ready", "v_psum", "v_ready", "last_psum", "last_ready", "masks_ready",
                  "scores", "top_ready", "exps", "turned", "pt0_ready", "pt1_ready", "o_psum", "om_ready", "ot_psum", "o_ready", "z_psum", "residual")
    scale = DH ** -0.5
    with ExitStack() as own, nc.Block() as block:
        norm_tiles(k, own)
        k.qx = tile(k, own, "l3x_q_by_head", P, GB, 4, L)
        kt = tile(k, own, "l3x_kt", P, GB, S2)
        v = tile(k, own, "l3x_v", P, GB, 2, D)
        vl = tile(k, own, "l3x_v_last", Q, GB, D)
        sc = tile(k, own, "l3x_scores", P, 2, Q, S2)
        st = tile(k, own, "l3x_stats", P, 2, 3, Q)
        pt = tile(k, own, "l3x_pt", P, 2, Q, P)
        ptl = tile(k, own, "l3x_pt_last", Q, P)
        om = tile(k, own, "l3x_om", P, 2, D)
        vm = tile(k, own, "l3x_vm", P, Q, 4 * DH)
        k.ot = tile(k, own, "l3x_ot", P, GT)
        ktf = kt[:].rearrange("p b s -> p (b s)")
        ctf = k.ctxt[:].rearrange("p b s -> p (b s)")
        strips = [(i, min(512, CHUNKS - i)) for i in range(0, CHUNKS, 512)]

        @block.gpsimd
        def _(pool):
            nc.gpsimd.tensor_scalar(k.maskf[:], k.maski[:], 0.0, -1e9 / scale, EQ, MUL).then_inc(s["masks_ready"], 1)

        @block.vector
        def _(vec):
            step = Steps(vec, s["vector_step"])
            norm_vector(k, vec, step, s)
            q_by_head(k, vec, step, s, bank=1, bias=colv["l3x_bq"])
            for i in range(4):
                vec.wait_ge(s["v_psum"], 2 * i + 2)
                step(nc.vector.tensor_copy(v[:, 4 * i:4 * i + 4, :, :].rearrange("p b c d -> p (b c d)"), ps[:, 4 + 2 * (i % 2):6 + 2 * (i % 2), :].rearrange("p a n -> p (a n)")), s["v_ready"])
            vec.wait_ge(s["last_psum"], 1)
            step(nc.vector.tensor_tensor(vl[:], ps[0:Q, 0:4, :].rearrange("p a (b d) -> p (a b) d", d=D), over(k.quad_cols[0:Q, :].unsqueeze(1), (Q, GB, D)), MUL), s["last_ready"])
            vec.wait_ge(s["masks_ready"], 1)
            for i in range(GB + 1):
                if i < GB:
                    vec.wait_ge(s["scores"], i + 1)
                    for c in range(Q):
                        step(nc.vector.tensor_tensor_reduce(out=sc[:, i % 2, c, :], in0=ps[:, c, 0:S2], in1=k.maskf[:, i, :], scale=scale, scalar=LOWEST,
                                                            op0=ADD, op1=MAX, accum_out=st[:, i % 2, 0, c:c + 1]))
                    step(nc.vector.tensor_scalar(st[:, i % 2, 0, :], st[:, i % 2, 0, :], -1.0, None, MUL), s["top_ready"])
                if i > 0:
                    b, h = i - 1, (i - 1) % 2
                    vec.wait_ge(s["exps"], Q * (b + 1))
                    step(nc.vector.reciprocal(st[:, h, 2, :], st[:, h, 1, :]))
                    step(nc.vector.tensor_tensor(vm[:], k.v_heads.rearrange("p (c d) -> p c d", c=Q), over(st[:, h, 2, :].unsqueeze(2), (P, Q, 4 * DH)), MUL))
                    vec.wait_ge(s["turned"], b + 1)
                    step(nc.vector.tensor_copy(pt[:, 0, :, :].rearrange("p c n -> p (c n)"), ps[:, 4, :]), s["pt0_ready"])
                    vec.wait_ge(s["o_psum"], b + 1)
                    step(nc.vector.tensor_tensor(om[:, h, :], ps[:, 6, 0:D], vm[:].rearrange("p c d -> p (c d)"), MUL), s["om_ready"])
            add_projection(k, vec, step, s, rowv["l3x_bo"])

        @block.scalar
        def _(act):
            step = Steps(act, s["scalar_step"])
            norm_scalar(k, act, step, s)
            for n, (at, width) in enumerate(strips):
                act.wait_ge(s["kt_psum"], n + 1)
                step(nc.scalar.activation(ktf[:, at:at + width], ps[:, 2 + n % 2, 0:width], ACT.Identity, bias=colv["l3x_bq"]), s["kt_ready"])
            for i in range(GB + 1):
                if i < GB:
                    act.wait_ge(s["top_ready"], i + 1)
                    for c in range(Q):
                        step(nc.scalar.activation(sc[:, i % 2, c, :], sc[:, i % 2, c, :], ACT.Exp, bias=st[:, i % 2, 0, c:c + 1],
                                                  accum_out=st[:, i % 2, 1, c:c + 1]), s["exps"])
                if i > 0:
                    act.wait_ge(s["turned"], i)
                    step(nc.scalar.activation(pt[:, 1, :, :].rearrange("p c n -> p (c n)"), ps[:, 5, :], ACT.Copy))
                    step(nc.scalar.activation(ptl[:], ps[0:Q, 6, P:2 * P], ACT.Copy), s["pt1_ready"])
            act.wait_ge(s["ot_psum"], GB)
            step(nc.scalar.activation(k.ot[:], ps[:, 7, :], ACT.Copy), s["o_ready"])

        @block.tensor
        def _(pe):
            norm_tensor(k, pe, s)
            pe.wait_ge(s["xt_ready"], 1)
            nc.tensor.matmul(ps[:, 1, :], w["l3x_q"], k.xt[:], start=True, stop=True).then_inc(s["q_psum"], 1)
            for n, (at, width) in enumerate(strips):
                if n >= 2:
                    pe.wait_ge(s["kt_ready"], n - 1)
                nc.tensor.matmul(ps[:, 2 + n % 2, 0:width], w["l3x_q"], ctf[:, at:at + width], start=True, stop=True).then_inc(s["kt_psum"], 1)
            pe.wait_ge(s["kt_ready"], len(strips))
            for n in range(GB // 2):
                if n >= 4 and n % 2 == 0:
                    pe.wait_ge(s["v_ready"], n // 2 - 1)
                for j in range(2):
                    for i in range(2):
                        last = nc.tensor.transpose(ps[:, 4 + n % 4, (2 * j + i) * P:(2 * j + i + 1) * P], kt[:, 2 * n + j, i * P:(i + 1) * P], k.ident)
                last.then_inc(s["v_psum"], 1)
            pe.wait_ge(s["qx_ready"], 4)
            for b in range(GB):
                last = nc.tensor.matmul(ps[0:Q, b // 4, (b % 4) * D:(b % 4 + 1) * D], over(kt[:, b, S2 - 1:S2], (P, Q)), k.ident, start=True, stop=True)
            last.then_inc(s["last_psum"], 1)
            pe.wait_ge(s["last_ready"], 1)
            pe.wait_ge(s["v_ready"], 4)

            def scores(b):
                if b > 0:
                    pe.wait_ge(s["top_ready"], b)
                for c in range(Q):
                    r = slice(L * c, L * c + L)
                    last = nc.tensor.matmul(ps[:, c, 0:S2], k.qx[r, b, :, :].rearrange("p h n -> p (h n)"), kt[r, b, :], start=True, stop=True)
                last.then_inc(s["scores"], 1)

            def fold(b):
                pe.wait_ge(s["om_ready"], b + 1)
                nc.tensor.matmul(ps[:, 7, b * L:(b + 1) * L], om[:, b % 2, :], k.fold, start=True, stop=True).then_inc(s["ot_psum"], 1)

            scores(0)
            for b in range(GB):
                if b + 1 < GB:
                    scores(b + 1)
                pe.wait_ge(s["exps"], Q * (b + 1))
                if b > 0:
                    pe.wait_ge(s["pt0_ready"], b)
                    pe.wait_ge(s["om_ready"], b)
                    pe.wait_ge(s["pt1_ready"], b)
                for c in range(Q):
                    for i in range(2):
                        nc.tensor.transpose(ps[:, 4 + i, c * P:(c + 1) * P], sc[:, b % 2, c, i * P:(i + 1) * P], k.ident)
                nc.tensor.transpose(ps[0:Q, 6, P:2 * P], sc[:, b % 2, :, 2 * P], k.ident).then_inc(s["turned"], 1)
                if b > 0:
                    fold(b - 1)
                pe.wait_ge(s["pt0_ready"], b + 1)
                pe.wait_ge(s["pt1_ready"], b + 1)
                nc.tensor.matmul(ps[:, 6, 0:D], ptl[:], vl[:, b, :], start=True, stop=False)
                for c in range(Q):
                    cols = slice(c * 4 * DH, (c + 1) * 4 * DH)
                    for i in range(2):
                        last = nc.tensor.matmul(ps[:, 6, cols], pt[:, i, c, :], v[:, b, i, cols], start=False, stop=c == Q - 1 and i == 1)
                last.then_inc(s["o_psum"], 1)
            fold(GB - 1)
            project(k, pe, s, w["l3x_o"])


def butterflies(k, phase, dram, up_w, up_b, down_w):
    nc, ps = k.nc, k.ps
    s = k.signals(phase, "fly", "loaded", "down_loaded", "up_done", "done", "b_psum", "w_psum")
    pairs = HID3 // 2
    with ExitStack() as own, nc.Block() as block:
        fw = tile(k, own, "fly_weights", P, STAGES, pairs * 4)
        y = tile(k, own, "fly_rows", P, 2, 2, HID3)
        t = tile(k, own, "fly_terms", P, 4, 2, pairs)
        ub = tile(k, own, "fly_up_bias", 1, HID3)

        @block.sync
        def _(sp):
            sp.dma_start(fw[:], dram["l3f_up"].partition_broadcast(P)).then_inc(s["loaded"], 16)
            sp.dma_start(y[:, 0, 0, :], dram["l3f_exp"]).then_inc(s["loaded"], 16)
            sp.dma_start(y[:, 0, 1, :], dram["l3f_b_exp"].partition_broadcast(P)).then_inc(s["loaded"], 16)
            sp.dma_start(ub[:], dram["l3f_up_bias"]).then_inc(s["loaded"], 16)
            sp.wait_ge(s["up_done"], 1)
            sp.dma_start(fw[:], dram["l3f_down"].partition_broadcast(P)).then_inc(s["down_loaded"], 16)
            sp.dma_start(y[:, 0, 0, :], dram["l3f_con"]).then_inc(s["down_loaded"], 16)

        @block.vector
        def _(vec):
            step = Steps(vec, s["vector_step"])

            def stages(order, rows, flipped):
                at = 0
                for stage in order:
                    st = 2 ** stage
                    nb = HID3 // (2 * st)
                    shape = (P, rows, nb, st)
                    old, new = (y[:, i, 0:rows, :].rearrange("p r (b two s) -> p r b two s", two=2, s=st) for i in (at, 1 - at))
                    wq = fw[:, stage, :].rearrange("p (b s q) -> p b s q", s=st, q=4)
                    tt = [t[:, i, 0:rows, :].rearrange("p r (b s) -> p r b s", s=st) for i in range(4)]
                    for i in range(4):
                        q = (i % 2) * 2 + i // 2 if flipped else i
                        for r in range(rows):
                            step(nc.vector.tensor_tensor(tt[i][:, r], old[:, r, :, i % 2, :], wq[:, :, :, q], MUL))
                    for i in range(2):
                        for r in range(rows):
                            step(nc.vector.tensor_tensor(new[:, r, :, i, :], tt[2 * i][:, r], tt[2 * i + 1][:, r], ADD))
                    at = 1 - at
                return at

            vec.wait_ge(s["loaded"], 64)
            at = stages(range(STAGES), 2, False)
            step(nc.vector.tensor_copy(up_w[:], y[:, at, 0, :]))
            step(nc.vector.tensor_tensor(ub[:], ub[:], y[0:1, at, 1, :], ADD), s["up_done"])
            vec.wait_ge(s["b_psum"], 1)
            step(nc.vector.tensor_copy(up_b[:], ps[:, 0, 0:4]))
            vec.wait_ge(s["down_loaded"], 32)
            at = stages(reversed(range(STAGES)), 1, True)
            step(nc.vector.tensor_copy(y[:, at, 1, :], y[:, at, 0, :]), s["done"])
            vec.wait_ge(s["w_psum"], 1)
            step(nc.vector.tensor_copy(down_w[:].rearrange("p c d -> p (c d)"), ps[:, 1, :]))

        @block.tensor
        def _(pe):
            pe.wait_ge(s["up_done"], 1)
            for c in range(4):
                last = nc.tensor.transpose(ps[:, 0, c:c + 1], ub[:, c * P:(c + 1) * P], k.ident[0:1, 0:1])
            last.then_inc(s["b_psum"], 1)
            pe.wait_ge(s["done"], 1)
            for c in range(4):
                last = nc.tensor.transpose(ps[:, 1, c * P:(c + 1) * P], y[:, STAGES % 2, 1, c * P:(c + 1) * P], k.ident)
            last.then_inc(s["w_psum"], 1)


def l3_ffn(k, phase, up_w, up_b, down_w, rowv, store):
    nc, ps = k.nc, k.ps
    s = k.signals(phase, "l3f", *NORM, "hidden_psum", "hidden_ready", "z_psum", "residual", "stored")
    with ExitStack() as own, nc.Block() as block:
        norm_tiles(k, own)
        hid = tile(k, own, "l3f_hidden", P, 4, GT)

        @block.vector
        def _(vec):
            step = Steps(vec, s["vector_step"])
            norm_vector(k, vec, step, s)
            step(nc.vector.tensor_tensor(k.xg[:], k.xg[:], over(rowv["l3f_bd"].unsqueeze(1), (P, T, D)), ADD))
            add_projection(k, vec, step, s, rowv["l3f_bc"])

        @block.scalar
        def _(act):
            step = Steps(act, s["scalar_step"])
            norm_scalar(k, act, step, s)
            for c in range(4):
                act.wait_ge(s["hidden_psum"], c + 1)
                step(nc.scalar.activation(hid[:, c, :], ps[:, 1 + c, :], ACT.Gelu, bias=up_b[:, c:c + 1]), s["hidden_ready"])

        @block.tensor
        def _(pe):
            norm_tensor(k, pe, s)
            pe.wait_ge(s["xt_ready"], 1)
            for c in range(4):
                nc.tensor.matmul(ps[:, 1 + c, :], up_w[:, c * P:(c + 1) * P], k.xt[:], start=True, stop=True).then_inc(s["hidden_psum"], 1)
            pe.wait_ge(s["hidden_ready"], 4)
            for t in range(T):
                for c in range(4):
                    last = nc.tensor.matmul(ps[:, 5, t * D:(t + 1) * D], hid[:, c, t * P:(t + 1) * P], down_w[:, c, :], start=c == 0, stop=c == 3)
            last.then_inc(s["z_psum"], 1)

        @block.sync
        def _(sp):
            sp.wait_ge(s["residual"], 1)
            sp.dma_start(store, k.xg[:]).then_inc(s["stored"], 16)
            sp.wait_ge(s["stored"], 16)


def phase_e(k, dram, groups, layers):
    nc = k.nc
    with ExitStack() as phase:
        wp = tile(k, phase, "e_weights", P, len(E_MATS), D)
        rp = tile(k, phase, "e_rows", P, len(E_ROWS), D)
        cp = tile(k, phase, "e_cols", P, len(E_COLS))
        up_w, up_b, down_w = tile(k, phase, "e_up_w", P, HID3), tile(k, phase, "e_up_b", P, 4), tile(k, phase, "e_down_w", P, 4, D)
        w = {n: wp[:, i, :] for i, n in enumerate(E_MATS)}
        rowv = {n: rp[:, i, :] for i, n in enumerate(E_ROWS)}
        colv = {n: cp[:, i:i + 1] for i, n in enumerate(E_COLS)}
        loaded = phase.enter_context(nc.semaphore("e_weights_loaded"))
        with nc.Block() as block:
            @block.sync
            def _(sp):
                for dst, name in ((wp, "e_mats"), (cp, "e_cols")):
                    sp.dma_start(dst[:], dram[name]).then_inc(loaded, 16)
                sp.dma_start(rp[:], dram["e_rows"].partition_broadcast(P)).then_inc(loaded, 16)
                sp.wait_ge(loaded, 48)
        if "l3f" in layers:
            butterflies(k, phase, dram, up_w, up_b, down_w)
        k.ctxt = tile(k, phase, "e_ctx_t", P, GB, S2)
        k.maski = tile(k, phase, "e_mask", P, GB, S2, dtype=I32)
        k.maskf = tile(k, phase, "e_mask_added", P, GB, S2)
        with nc.Fori(0, groups) as g:
            k.numbers = []
            s = k.signals(phase, "e_load", "loaded")
            group = lambda a: a.rearrange("(g t p) d -> g p t d", g=GROUPS, p=P)[g]
            with nc.Block() as block:
                @block.sync
                def _(sp):
                    sp.dma_start(k.xg[:], group(dram["x_d"])).then_inc(s["loaded"], 16)
                    sp.dma_start(k.ctxt[:], dram["ctx_t"].rearrange("p (g b s) -> g p b s", g=GROUPS, b=GB)[g]).then_inc(s["loaded"], 16)
                    for h in range(4):
                        sp.dma_start(k.maski[L * h:L * h + L, :, :], dram["mask_i32"].rearrange("q (g b s) -> g q b s", g=GROUPS, b=GB)[g]).then_inc(s["loaded"], 16)
                    sp.wait_ge(s["loaded"], 96)
            if "l3x" in layers:
                l3_xattn(k, phase, w, rowv, colv)
            if "l3a" in layers:
                self_attn(k, phase, "l3a", w["l3a_q"], w["l3a_k"], w["l3a_v"], w["l3a_p"], DH ** -0.5)
            if "l3f" in layers:
                l3_ffn(k, phase, up_w, up_b, down_w, rowv, group(dram["out"]))
            else:
                store_group(k, phase, group(dram["out"]))
            k.clear_signals()


def store_group(k, phase, store):
    s = k.signals(phase, "store", "stored")
    with k.nc.Block() as block:
        @block.sync
        def _(sp):
            sp.dma_start(store, k.xg[:]).then_inc(s["stored"], 16)
            sp.wait_ge(s["stored"], 16)


A_MATS = ["l0x_q", "l0x_k", "l0x_v", "l0x_c", "l0a_q", "l0a_k", "l0a_v", "l0a_o", "l1x_q", "l1x_k", "l1x_v", "l1x_o",
          "l1a_q", "l1a_k", "l1a_v", "l1a_p"]
A_ROWS = ["l0a_bv", "l0a_bo", "l1x_bk", "l1x_bv", "l1x_bo", "l1x_g", "l1x_b", "l1a_bp"]
A_COLS = ["l0a_bq", "l0a_bk", "l1x_bq", "l1x_bk", "l1a_w0", "l1a_w1", "l1a_w2", "l1a_bc"]
C_MATS = ["l2a_q", "l2a_k", "l2a_v", "l2a_u"]
C_ROWS = ["l2x_bl", "l2a_bu"]
C_COLS = ["l2x_wcq", "l2x_wq", "l2x_wc"]
E_MATS = ["l3x_q", "l3x_o", "l3a_q", "l3a_k", "l3a_v", "l3a_p"]
E_ROWS = ["l3x_bo", "l3f_bc", "l3f_bd"]
E_COLS = ["l3x_bq"]
CONSTS = {"ident": P, "same_head": P, "v_heads": P, "earlier": P, "causal": L, "quad_head": 4, "tile_batch": 4, "countdown": E0,
          "count4": CAP0, "row_base": T, "fold": L, "quad_cols": P, "ones": P}


def constants():
    p = np.arange(P)[:, None]
    c = np.arange(P)[None, :]
    made = {
        "ident": p == c,
        "same_head": p // DH == c // DH,
        "v_heads": p // L == (c // DH) % 4,
        "earlier": (p // L == c // L) & (p < c),
        "causal": np.where(np.arange(L)[None, :] > p % L, NEG, 0.0),
        "quad_head": (p // DH) % 4 == np.arange(4)[None, :],
        "tile_batch": p // L == np.arange(4)[None, :],
        "countdown": np.broadcast_to(E0 - np.arange(E0)[None, :], (P, E0)),
        "count4": np.broadcast_to(np.arange(CAP0)[None, :], (P, CAP0)),
        "row_base": (np.arange(T)[None, :] * BPT + p // L) * S2,
        "quad_cols": p == c // L,
        "ones": np.ones((P, P)),
        "fold": p % L == np.arange(L)[None, :],
    }
    return np.concatenate([made[n].astype(np.float32) for n in CONSTS], axis=1)


def layout(i):
    st = lambda a: np.ascontiguousarray(a)
    ctx = i["ctx_1024"].reshape(NB * S2, D)
    with_one = np.concatenate([i["ctx_1024"], np.ones((NB, S2, 1), np.float32)], axis=2)
    wkv = i["L0_xattn_Wkv"]
    w5 = i["L1_attn_w_qkv"]
    def by_head(a):
        out = np.zeros((H, DH, H, DH), np.float32)
        for h in range(H):
            out[h, :, h, :] = a.T
        return out.reshape(D, D)

    wa = i["L3_attn_w_attn"]
    mats = {"l3x_q": i["L3_xattn_Wq"].T, "l3x_o": i["L3_xattn_Wo"].T, "l3a_q": wa[:D].T, "l3a_k": wa[D:2 * D].T, "l3a_v": wa[2 * D:].T,
            "l3a_p": i["L3_attn_w_proj"].T,
            "l2a_q": by_head(i["L2_attn_Wq"]), "l2a_k": by_head(i["L2_attn_Wk"]), "l2a_v": by_head(i["L2_attn_Wv"]), "l2a_u": i["L2_attn_Wu"].T,
            "l0x_q": i["L0_xattn_Wq"].T, "l0x_k": np.tile(wkv[:DH].T, (1, H)), "l0x_v": np.tile(wkv[DH:].T, (1, H)), "l0x_c": i["L0_xattn_Wc"].T,
            "l0a_q": i["L0_attn_Wq"], "l0a_k": i["L0_attn_Wk"], "l0a_v": i["L0_attn_Wv"], "l0a_o": i["L0_attn_Wo"],
            "l1x_q": i["L1_xattn_wq_w"].T, "l1x_k": i["L1_xattn_wk_w"].T, "l1x_v": i["L1_xattn_wv_w"].T, "l1x_o": i["L1_xattn_wo_w"].T,
            "l1a_q": w5[:D].T, "l1a_k": w5[D:2 * D].T, "l1a_v": w5[2 * D:].T, "l1a_p": i["L1_attn_w_proj"].T}
    rows = {"l3x_bo": i["L3_xattn_bo"], "l3f_bc": i["L3_ffn_b_con"], "l3f_bd": i["L3_ffn_down_bias"],
            "l2x_bl": i["L2_xattn_b_l"], "l2a_bu": i["L2_attn_bu"],
            "l0a_bv": i["L0_attn_bv"], "l0a_bo": i["L0_attn_bo"], "l1x_bk": i["L1_xattn_wk_b"], "l1x_bv": i["L1_xattn_wv_b"],
            "l1x_bo": i["L1_xattn_wo_b"], "l1x_g": i["L1_xattn_ln_g"], "l1x_b": i["L1_xattn_ln_b"], "l1a_bp": i["L1_attn_b_proj"]}
    cols = {"l3x_bq": i["L3_xattn_bq"],
            "l2x_wcq": i["L2_xattn_w_cq"], "l2x_wq": i["L2_xattn_w_q"], "l2x_wc": i["L2_xattn_w_c"],
            "l0a_bq": i["L0_attn_bq"], "l0a_bk": i["L0_attn_bk"], "l1x_bq": i["L1_xattn_wq_b"], "l1x_bk": i["L1_xattn_wk_b"],
            "l1a_w0": i["L1_attn_w_dwc"][:, 0], "l1a_w1": i["L1_attn_w_dwc"][:, 1], "l1a_w2": i["L1_attn_w_dwc"][:, 2], "l1a_bc": i["L1_attn_b_dwc"]}
    return {
        "x": st(i["x"].reshape(TOKENS, D)), "ctx": st(ctx), "ctx_t": st(ctx.T),
        "mask_bool": st(i["mask_Bx1xSxS2_bf0"].reshape(TOKENS, S2)),
        "ctx_rows": st(with_one[:, :2 * P].reshape(NB, 2, P, D + 1).transpose(2, 0, 1, 3)), "ctx_last": st(with_one[None, :, 2 * P]),
        "consts": constants(),
        "a_mats": st(np.stack([mats[n] for n in A_MATS], axis=1)),
        "a_rows": st(np.stack([rows[n] for n in A_ROWS])),
        "a_cols": st(np.stack([cols[n] for n in A_COLS], axis=1)),
        "c_mats": st(np.stack([mats[n] for n in C_MATS], axis=1)),
        "c_rows": st(np.stack([rows[n] for n in C_ROWS])),
        "c_cols": st(np.stack([cols[n] for n in C_COLS], axis=1)),
        "l2x_l": st(i["L2_xattn_W_l"].reshape(D, 4, D).transpose(2, 1, 0).reshape(D, 4 * D)),
        "l2x_biases": st(np.stack([i["L2_xattn_b_c"], i["L2_xattn_b_q"], i["L2_xattn_b_cq"]])),
        "l1f_w1": st(i["L1_ffn_W1"].transpose(2, 0, 1, 3)), "l1f_w2": st(i["L1_ffn_W2"].transpose(2, 0, 1, 3)),
        "l1f_b1": st(i["L1_ffn_b1"].reshape(E1 * S1, P).T), "l1f_b2": st(i["L1_ffn_b2"].reshape(E1, D)),
        "e_mats": st(np.stack([mats[n] for n in E_MATS], axis=1)),
        "e_rows": st(np.stack([rows[n] for n in E_ROWS])),
        "e_cols": st(np.stack([cols[n] for n in E_COLS], axis=1)),
        "mask_i32": st(i["mask_Bx1xSxS2_if1"].reshape(NB, L, S2).transpose(1, 0, 2).reshape(L, NB * S2)),
        "l3f_up": st(i["L3_ffn_up_weights"].reshape(STAGES, 2 * HID3)), "l3f_down": st(i["L3_ffn_down_weights"].reshape(STAGES, 2 * HID3)),
        "l3f_exp": st(i["L3_ffn_W_exp"]), "l3f_b_exp": st(i["L3_ffn_b_exp"]), "l3f_up_bias": st(i["L3_ffn_up_bias"].reshape(1, HID3)),
        "l3f_con": st(i["L3_ffn_W_con"].T),
        "l2f_up": st(i["L2_ffn_w_up"].reshape(CH2, P, D).transpose(1, 0, 2).reshape(P, I2)),
        "l2f_gate": st(i["L2_ffn_w_gate"].reshape(CH2, P, D).transpose(1, 0, 2).reshape(P, I2)), "l2f_down": st(i["L2_ffn_w_down"]),
        "l0f_g": st(i["L0_ffn_Wg"]), "l1f_r": st(i["L1_ffn_Wr"].T),
        "l0f_w1": st(i["L0_ffn_W1"].transpose(1, 0, 2)),
        "l0f_w2": st(i["L0_ffn_W2"].reshape(E0, 4, P, D).transpose(2, 0, 1, 3)),
    }


LAYERS = ("l0x", "l0a", "l0f", "l1x", "l1a", "l1f", "l2x", "l2a", "l3x", "l3a", "l3f")
SCRATCH = {"x_a": (TOKENS, D), "xn_a": (TOKENS, D), "logits": (E1, TOKENS), **{f"sums_{j}": (TOKENS, D) for j in range(PER)},
           "x_c": (TOKENS, D), "xt_c": (P, TOKENS), "x_d": (TOKENS, D)}


def build(nc, dram, groups=GROUPS, layers=LAYERS, phases="ABCDE"):
    k = Kit(nc)
    with ExitStack() as whole:
        consts = tile(k, whole, "const_tiles", P, sum(CONSTS.values()))
        ends = np.cumsum(list(CONSTS.values())).tolist()
        (k.ident, k.same_head, k.v_heads, k.earlier, k.causal, k.quad_head, k.tile_batch, k.countdown,
         k.count4, k.row_base, k.fold, k.quad_cols, k.ones) = (consts[:, end - n:end] for end, n in zip(ends, CONSTS.values()))
        k.xg = tile(k, whole, "x_group", P, T, D)
        k.xn = tile(k, whole, "xn_group", P, T, D)
        k.xt = tile(k, whole, "xn_group_t", P, GT)
        k.ps = whole.enter_context(nc.psum_tensor("ps", [P, 8, 512], F32))
        got = whole.enter_context(nc.semaphore("consts_loaded"))
        with nc.Block() as block:
            @block.sync
            def _(sp):
                sp.dma_start(consts[:], dram["consts"]).then_inc(got, 16)
                sp.wait_ge(got, 16)
        largest = tile(k, whole, "largest", P, 1)
        if "A" in phases:
            phase_a(k, dram, groups, layers)
        if "B" in phases:
            phase_b(k, dram)
        if "C" in phases:
            phase_c(k, dram, groups, layers, largest[:])
        if "D" in phases:
            phase_d(k, dram, groups, largest[:])
        if "E" in phases:
            phase_e(k, dram, groups, layers)


def kernel(**inputs):
    import numpy as np
    import concourse.bacc as bacc
    from concourse.bass_utils import run_bass_kernel_spmd

    nc = bacc.Bacc("TRN2", target_bir_lowering=False, num_devices=1)
    arrays = layout({n: np.asarray(a) for n, a in inputs.items()})
    dram = {n: nc.dram_tensor("in_" + n, a.shape, mybir.dt.from_np(a.dtype), kind="ExternalInput").ap() for n, a in arrays.items()}
    dram.update({n: nc.dram_tensor("scratch_" + n, shape, F32, kind="Internal").ap() for n, shape in SCRATCH.items()})
    dram["out"] = nc.dram_tensor("out_x", (TOKENS, D), F32, kind="ExternalOutput").ap()
    build(nc, dram)
    r = run_bass_kernel_spmd(nc, [{"in_" + n: a for n, a in arrays.items()}], core_ids=[0])
    return r.results[0]["out_x"].reshape(NB, L, D)
```

```python
import concourse.bass as bass
from concourse import mybir
from concourse.alu_op_type import AluOpType as ALU
from contextlib import ExitStack
import numpy as np

P = 128
D = 128
NB = 128
L = 32
S2 = 257
TOKENS = NB * L
T = 4
GT = T * P
GB = GT // L
GROUPS = TOKENS // GT
BPT = P // L
H, DH = 16, 8
HC = H // 4
E0, HID0 = 8, 512
CAP0 = L // E0
WINDOW = 128
E1, S1 = 48, 4
CAP1 = int(1.5 * TOKENS / E1)
KW = D // S1
I2 = 384
HID3, STAGES = 512, 9
NEG = -1e30
LOWEST = -3.0e38

F32 = mybir.dt.float32
I32 = mybir.dt.int32
U32 = mybir.dt.uint32
U8 = mybir.dt.uint8
ACT = mybir.ActivationFunctionType
X = mybir.AxisListType.X
MUL, ADD, SUB, MAX, MIN, EQ = ALU.mult, ALU.add, ALU.subtract, ALU.max, ALU.min, ALU.is_equal


class Steps:

    def __init__(self, engine, own):
        self.engine, self.own, self.counts = engine, own, {}

    def __call__(self, instruction, signal=None):
        signal = self.own if signal is None else signal
        n = self.counts[id(signal)] = self.counts.get(id(signal), 0) + 1
        instruction.then_inc(signal, 1)
        self.engine.wait_ge(signal, n)

    def free(self, instruction, signal=None):
        signal = self.own if signal is None else signal
        self.counts[id(signal)] = self.counts.get(id(signal), 0) + 1
        instruction.then_inc(signal, 1)

    def settled(self, signal=None):
        signal = self.own if signal is None else signal
        self.engine.wait_ge(signal, self.counts[id(signal)])


class Kit:

    def __init__(self, nc):
        self.nc = nc
        self.numbers = []
        self.tiles = 0

    def signals(self, stack, layer, *names):
        sems = {n: stack.enter_context(self.nc.semaphore(f"{layer}_{n}"))
                for n in ("vector_step", "scalar_step", "pool_step") + names}
        self.numbers += [sem.num for sem in sems.values()]
        return sems

    def flag(self, stack, name):
        sem = stack.enter_context(self.nc.semaphore(name))
        self.numbers.append(sem.num)
        return sem

    def clear_signals(self):
        ids = sorted(self.numbers)
        firsts = [n for n in ids if n - 1 not in ids]
        lasts = [n for n in ids if n + 1 not in ids]
        self.nc.all_engine_barrier()
        for lo, hi in zip(firsts, lasts):
            self.nc.gpsimd.dma_reset(range(lo, hi + 1))
            self.nc.gpsimd.sem_clear(range(lo, hi + 1))
        self.nc.all_engine_barrier()
        self.numbers = []


def tile(k, stack, name, *shape, dtype=F32):
    k.tiles += 1
    return stack.enter_context(k.nc.sbuf_tensor(f"{name}_{k.tiles}", list(shape), dtype))


def over(ap, shape):
    return ap.broadcast_to(list(shape))


NORM = ("xn_ready", "xt_psum", "xt_ready")


def norm_tiles(k, stack):
    k.stat = tile(k, stack, "stat", P, 2, T)
    k.parts = tile(k, stack, "stat_parts", P, T, 6)
    k.mv = tile(k, stack, "mean_variance", P, T, 2)


def normalise(k, step, x, out, signal=None):
    nc = k.nc
    rstd, half, var = k.stat[:, 0, :], k.stat[:, 1, :], k.mv[:, :, 1]
    for t in range(T):
        step.free(nc.vector.bn_stats(k.parts[:, t, :], x[:, t, :]))
    step.settled()
    for t in range(T):
        step.free(nc.vector.bn_aggr(k.mv[:, t, :], k.parts[:, t, :]))
    step.settled()
    step(nc.vector.tensor_scalar(var, var, 1e-5, None, ADD))
    step(nc.vector.tensor_scalar(half.bitcast(I32), var.bitcast(I32), 1, None, ALU.logical_shift_right))
    step(nc.vector.tensor_scalar(rstd.bitcast(I32), half.bitcast(I32), -1.0, float(0x5F3759DF), MUL, ADD))
    for _ in range(3):
        step(nc.vector.tensor_tensor(half, rstd, rstd, MUL))
        step(nc.vector.scalar_tensor_tensor(half, half, -0.5, var, MUL, MUL))
        step(nc.vector.scalar_tensor_tensor(rstd, half, 1.5, rstd, ADD, MUL))
    for t in range(T):
        step.free(nc.vector.tensor_scalar(out[:, t, :], x[:, t, :], k.mv[:, t, 0:1], rstd[:, t:t + 1], SUB, MUL), signal)
    step.settled(signal)


def norm_vector(k, vec, step, s):
    normalise(k, step, k.x_in[:], k.xn[:], s["xn_ready"])


def norm_tensor(k, pe, s, bank=0):
    for t in range(T):
        pe.wait_ge(s["xn_ready"], t + 1)
        last = k.nc.tensor.transpose(k.ps[:, bank, t * P:(t + 1) * P], k.xn[:, t, :], k.ident)
    last.then_inc(s["xt_psum"], 1)


def norm_scalar(k, act, step, s, bank=0):
    act.wait_ge(s["xt_psum"], 1)
    step(k.nc.scalar.activation(k.xt[:], k.ps[:, bank, :], ACT.Copy), s["xt_ready"])


CORE = ("qx_ready", "k_psum", "k_ready", "q_psum", "rep_ready", "v_psum", "vx_ready", "scores", "shifted",
        "exps", "sums_ready", "p_ready", "pt_ready", "o_psum", "o_ready", "z_psum", "residual")
CHUNK = 4
NCHUNK = GB // CHUNK


def core_tiles(k, stack):
    k.qx = tile(k, stack, "q_by_head", P, GB, 4, L)
    k.kt = tile(k, stack, "k_t", P, GT)
    k.rep = tile(k, stack, "source_four_times", P, GB, 4, L)
    k.vx = tile(k, stack, "v_by_head", P, GB, D)
    k.st = tile(k, stack, "scores_masked", P, NCHUNK, CHUNK * 4, L)
    k.pr = tile(k, stack, "probabilities", P, NCHUNK, CHUNK * 4, L)
    k.pt = tile(k, stack, "probabilities_t", P, GB, 4, L)
    k.mx = tile(k, stack, "row_max", P, NCHUNK, CHUNK * 4)
    k.rs = tile(k, stack, "row_sum", P, NCHUNK, CHUNK * 4)
    k.ot = tile(k, stack, "o_t", P, GT)


def core_tensor(k, pe, s, wv, wo, q_bank=1):
    nc, ps = k.nc, k.ps
    pe.wait_ge(s["rep_ready"], 1)
    for b in range(GB):
        last = nc.tensor.matmul(ps[:, 4 + b // 4, (b % 4) * D:(b % 4 + 1) * D], k.rep[:, b, :, :].rearrange("p a b -> p (a b)"),
                                wv, start=True, stop=True)
    last.then_inc(s["v_psum"], 1)
    pe.wait_ge(s["qx_ready"], 4)
    pe.wait_ge(s["k_ready"], 1)
    for n in range(NCHUNK):
        for b in range(CHUNK * n, CHUNK * n + CHUNK):
            for c in range(HC):
                rows = slice(L * c, L * c + L)
                last = nc.tensor.matmul(ps[rows, n, (b % CHUNK) * P:(b % CHUNK + 1) * P], k.kt[rows, b * L:(b + 1) * L],
                                        k.qx[rows, b, :, :].rearrange("p a b -> p (a b)"), start=True, stop=True)
        last.then_inc(s["scores"], 1)
    pe.wait_ge(s["vx_ready"], 1)
    for n in range(NCHUNK):
        pe.wait_ge(s["pt_ready"], n + 1)
        for a in range(4):
            for b in range(CHUNK * n, CHUNK * n + CHUNK):
                last = nc.tensor.matmul(ps[L * a:L * a + L, 4, b * L:(b + 1) * L], k.vx[:, b, L * a:L * a + L],
                                        k.pt[:, b, a, :], start=True, stop=True)
    last.then_inc(s["o_psum"], 1)
    project(k, pe, s, wo)


def project(k, pe, s, wo):
    pe.wait_ge(s["o_ready"], 1)
    for t in range(T):
        last = k.nc.tensor.matmul(k.ps[:, 5, t * D:(t + 1) * D], k.ot[:, t * P:(t + 1) * P], wo, start=True, stop=True)
    last.then_inc(s["z_psum"], 1)


def q_by_head(k, vec, step, s, bank=1, bias=None):
    nc = k.nc
    vec.wait_ge(s["q_psum"], 1)
    q = k.ps[:, bank, :].rearrange("p (b n) -> p b n", n=L)
    for h in range(4):
        if bias is None:
            step(nc.vector.tensor_scalar(k.qx[:, :, h, :], q, k.quad_head[:, h:h + 1], None, MUL), s["qx_ready"])
        else:
            step(nc.vector.tensor_scalar(k.qx[:, :, h, :], q, bias, k.quad_head[:, h:h + 1], ADD, MUL), s["qx_ready"])


def v_by_head(k, vec, step, s):
    vec.wait_ge(s["v_psum"], 1)
    step(k.nc.vector.tensor_tensor(k.vx[:].rearrange("p b d -> p b d"),
                                   k.ps[:, 4:8, :].rearrange("p c (b d) -> p (c b) d", d=D),
                                   over(k.v_heads.unsqueeze(1), (P, GB, D)), MUL), s["vx_ready"])


def core_vector(k, vec, step, s, scale, causal, bias=None):
    nc = k.nc
    for n in range(NCHUNK):
        vec.wait_ge(s["scores"], n + 1)
        sc, pr = k.ps[:, n, :], k.pr[:, n, :, :]
        if causal:
            step(nc.vector.scalar_tensor_tensor(k.st[:, n, :, :], sc.rearrange("p (m q) -> p m q", q=L), scale,
                                                over(k.causal.unsqueeze(1), (P, CHUNK * 4, L)), MUL, ADD))
            sc = k.st[:, n, :, :].rearrange("p m q -> p (m q)")
        step(nc.vector.transpose(pr.rearrange("p m q -> p (m q)"), sc))
        step(nc.vector.reduce_max(k.mx[:, n, :], pr, X))
        step(nc.vector.tensor_tensor(pr, pr, over(k.mx[:, n, :].unsqueeze(2), (P, CHUNK * 4, L)), SUB), s["shifted"])

    def turn(n):
        vec.wait_ge(s["p_ready"], n + 1)
        step(nc.vector.transpose(k.pt[:, CHUNK * n:CHUNK * n + CHUNK, :, :].rearrange("p b a q -> p (b a q)"),
                                 k.pr[:, n, :, :].rearrange("p m q -> p (m q)")), s["pt_ready"])

    for n in range(NCHUNK):
        vec.wait_ge(s["exps"], n + 1)
        step(nc.vector.reduce_sum(k.rs[:, n, :], k.pr[:, n, :, :], X))
        step(nc.vector.reciprocal(k.rs[:, n, :], k.rs[:, n, :]), s["sums_ready"])
        if n > 1:
            turn(n - 2)
    turn(NCHUNK - 2)
    turn(NCHUNK - 1)
    add_projection(k, vec, step, s, bias)


def core_pool(k, pool, s):
    for n in range(NCHUNK):
        pool.wait_ge(s["sums_ready"], n + 1)
        pr = k.pr[:, n, :, :]
        k.nc.gpsimd.tensor_tensor(pr, pr, over(k.rs[:, n, :].unsqueeze(2), (P, CHUNK * 4, L)), MUL).then_inc(s["p_ready"], 1)


def add_projection(k, vec, step, s, bias=None):
    nc, x = k.nc, k.x_in
    if bias is not None:
        step(nc.vector.tensor_tensor(k.xg[:], x[:], over(bias.unsqueeze(1), (P, T, D)), ADD))
        x = k.xg
    vec.wait_ge(s["z_psum"], 1)
    step(nc.vector.tensor_tensor(k.xg[:], x[:], k.ps[:, 5, :].rearrange("p (t d) -> p t d", d=D), ADD), s["residual"])


def core_scalar(k, act, step, s, scale, causal):
    nc = k.nc
    for n in range(NCHUNK):
        act.wait_ge(s["shifted"], n + 1)
        step(nc.scalar.activation(k.pr[:, n, :, :], k.pr[:, n, :, :], ACT.Exp, scale=1.0 if causal else scale), s["exps"])
    act.wait_ge(s["o_psum"], 1)
    step(nc.scalar.activation(k.ot[:], k.ps[:, 4, :], ACT.Copy), s["o_ready"])


def four_times(k, source):
    return over(source.rearrange("p (b n) -> p b n", n=L).unsqueeze(2), (P, GB, 4, L))


def l0_xattn(k, phase, w, ctx_rows, next_x, next_ctxt):
    nc, ps = k.nc, k.ps
    s = k.signals(phase, "l0x", *NORM, *CORE, "qt_ready", "found_scores", "rows_found", "rows_loaded", "mem_psum", "mem_ready")
    with ExitStack() as own, nc.Block() as block:
        norm_tiles(k, own)
        core_tiles(k, own)
        qt = tile(k, own, "l0x_qt", P, GT)
        best = tile(k, own, "best", P, T, 8)
        best_at = tile(k, own, "best_at", P, T, 8, dtype=U32)
        rows = tile(k, own, "rows", P, T, dtype=I32)
        mem = tile(k, own, "mem", P, T, D)
        mt = tile(k, own, "mem_t", P, GT)

        @block.vector
        def _(vec):
            step = Steps(vec, s["vector_step"])
            norm_vector(k, vec, step, s)
            q_by_head(k, vec, step, s)
            for t in range(T):
                vec.wait_ge(s["found_scores"], t + 1)
                step(nc.vector.max(best[:, t, :], ps[:, 4 + t, 0:S2]))
                step(nc.vector.max_index(best_at[:, t, :], best[:, t, :], ps[:, 4 + t, 0:S2]))
            step(nc.vector.tensor_tensor(rows[:], best_at[:, :, 0], k.row_base, ADD), s["rows_found"])
            step(nc.vector.tensor_scalar(k.row_base, k.row_base, float(GB * S2), None, ADD))
            v_by_head(k, vec, step, s)
            core_vector(k, vec, step, s, DH ** -0.5, False)

        @block.sync
        def _(sp):
            sp.wait_ge(s["found_scores"], T)
            sp.dma_start(k.ctxt[:], next_ctxt).then_inc(k.ctxt_loaded, 16)
            sp.wait_ge(s["residual"], 1)
            sp.dma_start(k.x_next[:], next_x).then_inc(k.x_loaded, 16)

        @block.gpsimd
        def _(pool):
            pool.wait_ge(s["rows_found"], 1)
            for t in range(T):
                nc.gpsimd.indirect_dma_start(out=mem[:, t, :], out_offset=None, in_=ctx_rows,
                                             in_offset=bass.IndirectOffsetOnAxis(ap=rows[:, t:t + 1], axis=0)).then_inc(s["rows_loaded"], 16)
            pool.wait_ge(s["rows_loaded"], 16 * T)
            core_pool(k, pool, s)

        @block.scalar
        def _(act):
            step = Steps(act, s["scalar_step"])
            norm_scalar(k, act, step, s)
            act.wait_ge(s["q_psum"], 1)
            act.wait_ge(s["qx_ready"], 4)
            step(nc.scalar.activation(qt[:], ps[:, 1, :], ACT.Copy), s["qt_ready"])
            act.wait_ge(s["mem_psum"], 1)
            step(nc.scalar.activation(mt[:], ps[:, 2, :], ACT.Copy), s["mem_ready"])
            step(nc.scalar.activation(k.rep[:], four_times(k, ps[:, 2, :]), ACT.Copy), s["rep_ready"])
            act.wait_ge(s["k_psum"], 1)
            step(nc.scalar.activation(k.kt[:], ps[:, 3, :], ACT.Copy), s["k_ready"])
            core_scalar(k, act, step, s, DH ** -0.5, False)

        @block.tensor
        def _(pe):
            norm_tensor(k, pe, s)
            pe.wait_ge(s["xt_ready"], 1)
            nc.tensor.matmul(ps[:, 1, :], w["l0x_q"], k.xt[:], start=True, stop=True).then_inc(s["q_psum"], 1)
            pe.wait_ge(s["qt_ready"], 1)
            for t in range(T):
                for j in range(BPT):
                    b = t * BPT + j
                    last = nc.tensor.matmul(ps[L * j:L * j + L, 4 + t, 0:S2], qt[:, b * L:(b + 1) * L], k.ctxt[:, b, :], start=True, stop=True)
                last.then_inc(s["found_scores"], 1)
            pe.wait_ge(s["rows_loaded"], 16 * T)
            for t in range(T):
                last = nc.tensor.transpose(ps[:, 2, t * P:(t + 1) * P], mem[:, t, :], k.ident)
            last.then_inc(s["mem_psum"], 1)
            pe.wait_ge(s["mem_ready"], 1)
            nc.tensor.matmul(ps[:, 3, :], w["l0x_k"], mt[:], start=True, stop=True).then_inc(s["k_psum"], 1)
            core_tensor(k, pe, s, w["l0x_v"], w["l0x_c"])


def l0_attn(k, phase, w, rowv, colv):
    nc, ps = k.nc, k.ps
    s = k.signals(phase, "l0a", *NORM, "q_psum", "k_psum", "v_psum", "q_ready", "k_ready", "v_ready", "scores", "shifted", "exps",
                  "pt_ready", "o_psum", "o_ready", "z_psum", "residual")
    scale = DH ** -0.5
    with ExitStack() as own, nc.Block() as block:
        norm_tiles(k, own)
        qt, kt = tile(k, own, "l0a_qt", P, GT), tile(k, own, "l0a_kt", P, GT)
        v = tile(k, own, "l0a_v", P, T, D)
        pr, pt = tile(k, own, "l0a_p", P, T, L), tile(k, own, "l0a_pt", P, T, L)
        mx = tile(k, own, "l0a_mx", P, T)
        k.ot = tile(k, own, "l0a_ot", P, GT)

        @block.vector
        def _(vec):
            step = Steps(vec, s["vector_step"])
            norm_vector(k, vec, step, s)
            vec.wait_ge(s["v_psum"], 1)
            step(nc.vector.tensor_tensor(v[:], ps[:, 3, :].rearrange("p (t d) -> p t d", d=D), over(rowv["l0a_bv"].unsqueeze(1), (P, T, D)), ADD), s["v_ready"])
            vec.wait_ge(s["scores"], 1)
            sc = ps[:, 4, 0:T * L].rearrange("p (t j) -> p t j", j=L)
            step(nc.vector.reduce_max(mx[:], sc, X))
            step(nc.vector.tensor_tensor(pr[:], sc, over(mx[:].unsqueeze(2), (P, T, L)), SUB), s["shifted"])
            vec.wait_ge(s["exps"], 1)
            step(nc.vector.tensor_scalar(pr[:, :, L - 1:L], pr[:, :, L - 1:L], float(WINDOW - L + 1), None, MUL))
            step(nc.vector.reduce_sum(mx[:], pr[:], X))
            step(nc.vector.reciprocal(mx[:], mx[:]))
            step(nc.vector.tensor_tensor(pr[:], pr[:], over(mx[:].unsqueeze(2), (P, T, L)), MUL))
            step(nc.vector.transpose(pt[:], pr[:]), s["pt_ready"])
            add_projection(k, vec, step, s, rowv["l0a_bo"])

        @block.scalar
        def _(act):
            step = Steps(act, s["scalar_step"])
            norm_scalar(k, act, step, s)
            act.wait_ge(s["q_psum"], 1)
            step(nc.scalar.activation(qt[:], ps[:, 1, :], ACT.Identity, bias=colv["l0a_bq"]), s["q_ready"])
            act.wait_ge(s["k_psum"], 1)
            step(nc.scalar.activation(kt[:], ps[:, 2, :], ACT.Identity, bias=colv["l0a_bk"]), s["k_ready"])
            act.wait_ge(s["shifted"], 1)
            step(nc.scalar.activation(pr[:], pr[:], ACT.Exp, scale=scale), s["exps"])
            act.wait_ge(s["o_psum"], 1)
            step(nc.scalar.activation(k.ot[:].rearrange("p (t j n) -> p j t n", j=BPT, n=L),
                                      ps[:, 0:4, 0:T * L].rearrange("p j (t n) -> p j t n", n=L), ACT.Copy), s["o_ready"])

        @block.tensor
        def _(pe):
            norm_tensor(k, pe, s)
            pe.wait_ge(s["xt_ready"], 1)
            nc.tensor.matmul(ps[:, 1, :], w["l0a_q"], k.xt[:], start=True, stop=True).then_inc(s["q_psum"], 1)
            nc.tensor.matmul(ps[:, 2, :], w["l0a_k"], k.xt[:], start=True, stop=True).then_inc(s["k_psum"], 1)
            for t in range(T):
                last = nc.tensor.matmul(ps[:, 3, t * D:(t + 1) * D], k.xt[:, t * P:(t + 1) * P], w["l0a_v"], start=True, stop=True)
            last.then_inc(s["v_psum"], 1)
            pe.wait_ge(s["q_ready"], 1)
            pe.wait_ge(s["k_ready"], 1)
            for t in range(T):
                for j in range(BPT):
                    b = slice((t * BPT + j) * L, (t * BPT + j + 1) * L)
                    last = nc.tensor.matmul(ps[L * j:L * j + L, 4, t * L:(t + 1) * L], qt[:, b], kt[:, b], start=True, stop=True)
            last.then_inc(s["scores"], 1)
            pe.wait_ge(s["pt_ready"], 1)
            pe.wait_ge(s["v_ready"], 1)
            for t in range(T):
                for j in range(BPT):
                    r = slice(L * j, L * j + L)
                    last = nc.tensor.matmul(ps[:, j, t * L:(t + 1) * L], v[r, t, :], pt[r, t, :], start=True, stop=True)
            last.then_inc(s["o_psum"], 1)
            project(k, pe, s, w["l0a_o"])


def l0_ffn(k, phase, w):
    nc, ps = k.nc, k.ps
    s = k.signals(phase, "l0f", *NORM, "logits", "shifted", "exps", "chosen", "places", "dispatch_ready", "slots_psum", "slots_ready",
                  "hidden_psum", "hidden_ready", "y_psum", "y_ready", "yt_psum", "yt_ready", "combine_ready", "z_psum", "residual")
    with ExitStack() as own, nc.Block() as block:
        norm_tiles(k, own)
        lg = tile(k, own, "l0f_logits", P, T, E0)
        ex = tile(k, own, "l0f_exps", P, T, E0)
        hot = tile(k, own, "l0f_onehot", P, T, E0)
        st = tile(k, own, "l0f_stats", P, 4, T)
        at = tile(k, own, "l0f_at", P, T, CAP0)
        disp = tile(k, own, "l0f_dispatch", P, T, E0, CAP0)
        comb = tile(k, own, "l0f_combine", P, T, L)
        combx = tile(k, own, "l0f_combine_x", P, T, BPT, L)
        xs = tile(k, own, "l0f_slots", P, E0, GB, CAP0)
        hid = tile(k, own, "l0f_hidden", P, E0 * 4, GB * CAP0)
        yt = tile(k, own, "l0f_yt", P, GB, E0, CAP0)
        y = tile(k, own, "l0f_y", P, T, D)

        @block.vector
        def _(vec):
            step = Steps(vec, s["vector_step"])
            norm_vector(k, vec, step, s)
            vec.wait_ge(s["logits"], 1)
            mx, gate, place, pick = (st[:, i, :] for i in range(4))
            step(nc.vector.tensor_copy(lg[:], ps[:, 1, 0:T * E0].rearrange("p (t e) -> p t e", e=E0)))
            step(nc.vector.reduce_max(mx, lg[:], X))
            step(nc.vector.tensor_tensor(ex[:], lg[:], over(mx.unsqueeze(2), (P, T, E0)), SUB), s["shifted"])
            step(nc.vector.tensor_tensor(hot[:], lg[:], over(mx.unsqueeze(2), (P, T, E0)), EQ))
            step(nc.vector.tensor_tensor(hot[:], hot[:], over(k.countdown.unsqueeze(1), (P, T, E0)), MUL))
            step(nc.vector.reduce_max(pick, hot[:], X))
            step(nc.vector.tensor_tensor(hot[:], over(pick.unsqueeze(2), (P, T, E0)), over(k.countdown.unsqueeze(1), (P, T, E0)), EQ), s["chosen"])
            vec.wait_ge(s["exps"], 1)
            step(nc.vector.reduce_sum(gate, ex[:], X))
            step(nc.vector.reciprocal(gate, gate))
            vec.wait_ge(s["places"], 1)
            step(nc.vector.tensor_tensor(lg[:], ps[:, 2, 0:T * E0].rearrange("p (t e) -> p t e", e=E0), hot[:], MUL))
            step(nc.vector.reduce_sum(place, lg[:], X))
            step(nc.vector.tensor_tensor(at[:], over(place.unsqueeze(2), (P, T, CAP0)), over(k.count4.unsqueeze(1), (P, T, CAP0)), EQ))
            step(nc.vector.tensor_tensor(disp[:], over(hot[:].unsqueeze(3), (P, T, E0, CAP0)), over(at[:].unsqueeze(2), (P, T, E0, CAP0)), MUL), s["dispatch_ready"])
            flat = disp[:].rearrange("p t e c -> p t (e c)")
            vec.wait_ge(s["slots_psum"], 1)
            step(nc.vector.tensor_tensor(flat, flat, over(gate.unsqueeze(2), (P, T, L)), MUL))
            step(nc.vector.transpose(comb[:], flat))
            step(nc.vector.tensor_tensor(combx[:], over(comb[:].unsqueeze(2), (P, T, BPT, L)), over(k.tile_batch.unsqueeze(1).unsqueeze(3), (P, T, BPT, L)), MUL), s["combine_ready"])
            add_projection(k, vec, step, s)

        @block.scalar
        def _(act):
            step = Steps(act, s["scalar_step"])
            norm_scalar(k, act, step, s)
            act.wait_ge(s["shifted"], 1)
            step(nc.scalar.activation(ex[:], ex[:], ACT.Exp), s["exps"])
            act.wait_ge(s["slots_psum"], 1)
            for j in range(BPT):
                step(nc.scalar.activation(xs[:].rearrange("p e (t j) c -> p j t e c", j=BPT)[:, j],
                                          ps[:, 4 + j, 0:P].rearrange("p (t e c) -> p t e c", t=T, e=E0), ACT.Copy), s["slots_ready"])
            for n in range(4):
                act.wait_ge(s["hidden_psum"], n + 1)
                step(nc.scalar.activation(hid[:, 8 * n:8 * n + 8, :].rearrange("p a b -> p (a b)"), ps[:, n, :], ACT.Gelu_apprx_tanh), s["hidden_ready"])
            act.wait_ge(s["y_psum"], 1)
            step(nc.scalar.activation(yt[:].rearrange("p b e c -> p e b c"), ps[:, 6, :].rearrange("p (e b c) -> p e b c", e=E0, c=CAP0), ACT.Copy), s["y_ready"])
            act.wait_ge(s["yt_psum"], 1)
            step(nc.scalar.activation(y[:].rearrange("p t d -> p (t d)"), ps[:, 7, :], ACT.Copy), s["yt_ready"])

        @block.tensor
        def _(pe):
            norm_tensor(k, pe, s)
            pe.wait_ge(s["xt_ready"], 1)
            for t in range(T):
                last = nc.tensor.matmul(ps[:, 1, t * E0:(t + 1) * E0], k.xt[:, t * P:(t + 1) * P], w["l0f_g"], start=True, stop=True)
            last.then_inc(s["logits"], 1)
            pe.wait_ge(s["chosen"], 1)
            nc.tensor.matmul(ps[:, 2, 0:T * E0], k.earlier, hot[:].rearrange("p t e -> p (t e)"), start=True, stop=True).then_inc(s["places"], 1)
            pe.wait_ge(s["dispatch_ready"], 1)
            for t in range(T):
                for j in range(BPT):
                    r = slice(L * j, L * j + L)
                    last = nc.tensor.matmul(ps[:, 4 + j, t * L:(t + 1) * L], k.xn[r, t, :], disp[r, t, :, :].rearrange("p e c -> p (e c)"), start=True, stop=True)
            last.then_inc(s["slots_psum"], 1)
            pe.wait_ge(s["slots_ready"], BPT)
            pe.wait_ge(k.ffn_loaded, 32)
            for e in range(E0):
                for c in range(4):
                    n = e * 4 + c
                    last = nc.tensor.matmul(ps[:, n // 8, (n % 8) * 64:(n % 8 + 1) * 64], w["l0f_w1"][:, e, c * P:(c + 1) * P],
                                            xs[:, e, :, :].rearrange("p b c -> p (b c)"), start=True, stop=True)
                    if n % 8 == 7:
                        last.then_inc(s["hidden_psum"], 1)
            for e in range(E0):
                if e % 2 == 0:
                    pe.wait_ge(s["hidden_ready"], e // 2 + 1)
                for c in range(4):
                    last = nc.tensor.matmul(ps[:, 6, e * 64:(e + 1) * 64], w["l0f_w2"][:, e, c, :], hid[:, e * 4 + c, :], start=c == 0, stop=c == 3)
            last.then_inc(s["y_psum"], 1)
            pe.wait_ge(s["y_ready"], 1)
            for t in range(T):
                last = nc.tensor.transpose(ps[:, 7, t * P:(t + 1) * P], yt[:, t * BPT:(t + 1) * BPT, :, :].rearrange("p b e c -> p (b e c)"), k.ident)
            last.then_inc(s["yt_psum"], 1)
            pe.wait_ge(s["yt_ready"], 1)
            pe.wait_ge(s["combine_ready"], 1)
            for t in range(T):
                last = nc.tensor.matmul(ps[:, 5, t * D:(t + 1) * D], combx[:, t, :, :].rearrange("p j n -> p (j n)"), y[:, t, :], start=True, stop=True)
            last.then_inc(s["z_psum"], 1)


def l1_xattn(k, phase, w, rowv, colv, next_ctx, next_last, next_mask):
    nc, ps = k.nc, k.ps
    s = k.signals(phase, "l1x", *NORM, "q_psum", "q_ready", "g_psum", "g_ready", "t_psum", "t_ready", "m_psum", "m_ready",
                  "o_psum", "o_ready", "z_psum", "residual")
    inv_dk = 1.0 / (2.828125 + 1e-8)
    with ExitStack() as own, nc.Block() as block:
        norm_tiles(k, own)
        qt = tile(k, own, "l1x_qt", P, GT)
        gram = tile(k, own, "l1x_gram", P, 4, D + 1)
        t1 = tile(k, own, "l1x_t1", P, 4, D)
        sbk = tile(k, own, "l1x_sbk", P, 4, D)
        kv = tile(k, own, "l1x_kv", P, GB, D)
        k.ot = tile(k, own, "l1x_ot", P, GT)
        c0 = tile(k, own, "l1x_c0", P, D)
        masked = tile(k, own, "l1x_masked", P, 2, T)
        res = tile(k, own, "l1x_res", P, T, D)

        @block.sync
        def _(sp):
            sp.wait_ge(s["g_psum"], GB)
            sp.dma_start(k.ctx[:], next_ctx).then_inc(k.ctx_loaded, 16)
            sp.dma_start(k.last[:], next_last).then_inc(k.ctx_loaded, 16)
            sp.wait_ge(s["t_ready"], 1)
            sp.dma_start(k.mask[:], next_mask).then_inc(k.mask_loaded, 16)

        @block.vector
        def _(vec):
            step = Steps(vec, s["vector_step"])
            norm_vector(k, vec, step, s)
            step(nc.vector.tensor_scalar(c0[:], rowv["l1x_bv"], colv["l1x_bk"], float(S2), MUL, MUL))
            step(nc.vector.tensor_tensor(c0[:], c0[:], k.same_head, MUL))
            step(nc.vector.reduce_max(masked[:, 0, :], k.mask[:], X))
            step(nc.vector.tensor_scalar(masked[:, 1, :], masked[:, 0, :], LOWEST, 1e10, MUL, MUL))
            for b in range(GB):
                i = b % 4
                vec.wait_ge(s["g_ready"], b + 1)
                step(nc.vector.tensor_scalar(sbk[:, i, :], rowv["l1x_bk"], gram[:, i, D:D + 1], None, MUL))
                vec.wait_ge(s["t_psum"], b + 1)
                step(nc.vector.scalar_tensor_tensor(t1[:, i, :], rowv["l1x_bv"], gram[:, i, D:D + 1], ps[:, 4 + b % 2, 0:D], MUL, ADD), s["t_ready"])
                vec.wait_ge(s["m_psum"], b + 1)
                step(nc.vector.tensor_tensor(kv[:, b, :], ps[:, 6 + b % 2, 0:D], k.same_head, MUL))
                step(nc.vector.tensor_tensor(kv[:, b, :], kv[:, b, :], c0[:], ADD), s["m_ready"])
            vec.wait_ge(s["z_psum"], 1)
            step(nc.vector.tensor_tensor(res[:], k.xn[:], ps[:, 5, :].rearrange("p (t d) -> p t d", d=D), ADD))
            step(nc.vector.tensor_tensor(res[:], res[:], over(rowv["l1x_bo"].unsqueeze(1), (P, T, D)), ADD))
            step(nc.vector.tensor_tensor(res[:], res[:], over(masked[:, 1, :].unsqueeze(2), (P, T, D)), ADD))
            normalise(k, step, res[:], res[:])
            step(nc.vector.tensor_tensor(res[:], res[:], over(rowv["l1x_g"].unsqueeze(1), (P, T, D)), MUL))
            step(nc.vector.tensor_tensor(res[:], res[:], over(rowv["l1x_b"].unsqueeze(1), (P, T, D)), ADD))
            step(nc.vector.tensor_tensor(k.xg[:], k.xg[:], res[:], ADD), s["residual"])

        @block.scalar
        def _(act):
            step = Steps(act, s["scalar_step"])
            norm_scalar(k, act, step, s)
            act.wait_ge(s["q_psum"], 1)
            step(nc.scalar.activation(qt[:], ps[:, 1, :], ACT.Identity, bias=colv["l1x_bq"]))
            step(nc.scalar.activation(qt[:], qt[:], ACT.Copy, scale=inv_dk), s["q_ready"])
            for b in range(GB):
                act.wait_ge(s["g_psum"], b + 1)
                if b >= 4:
                    act.wait_ge(s["m_psum"], b - 3)
                step(nc.scalar.activation(gram[:, b % 4, :], ps[:, 2 + b % 2, 0:D + 1], ACT.Copy), s["g_ready"])
            act.wait_ge(s["o_psum"], 1)
            step(nc.scalar.activation(k.ot[:], ps[:, 0, :], ACT.Copy), s["o_ready"])

        @block.tensor
        def _(pe):
            norm_tensor(k, pe, s)
            pe.wait_ge(s["xt_ready"], 1)
            nc.tensor.matmul(ps[:, 1, :], w["l1x_q"], k.xt[:], start=True, stop=True).then_inc(s["q_psum"], 1)

            def moments(b):
                if b >= 2:
                    pe.wait_ge(s["g_ready"], b - 1)
                bank = ps[:, 2 + b % 2, 0:D + 1]
                nc.tensor.matmul(bank, k.ctx[:, b, 0, 0:D], k.ctx[:, b, 0, :], start=True, stop=False)
                nc.tensor.matmul(bank, k.ctx[:, b, 1, 0:D], k.ctx[:, b, 1, :], start=False, stop=False)
                nc.tensor.matmul(bank, k.last[:, b, 0:D], k.last[:, b, :], start=False, stop=True).then_inc(s["g_psum"], 1)

            def values(b):
                pe.wait_ge(s["g_ready"], b + 1)
                if b >= 2:
                    pe.wait_ge(s["t_ready"], b - 1)
                nc.tensor.matmul(ps[:, 4 + b % 2, 0:D], gram[:, b % 4, 0:D], w["l1x_v"], start=True, stop=True).then_inc(s["t_psum"], 1)

            def keys(b):
                pe.wait_ge(s["t_ready"], b + 1)
                if b >= 2:
                    pe.wait_ge(s["m_ready"], b - 1)
                nc.tensor.matmul(ps[:, 6 + b % 2, 0:D], w["l1x_k"], t1[:, b % 4, :], start=True, stop=False)
                nc.tensor.matmul(ps[:, 6 + b % 2, 0:D], sbk[:, b % 4, :], w["l1x_v"], start=False, stop=True).then_inc(s["m_psum"], 1)

            for b in range(GB + 2):
                if b < GB:
                    moments(b)
                if 1 <= b <= GB:
                    values(b - 1)
                if b >= 2:
                    keys(b - 2)
            pe.wait_ge(s["q_ready"], 1)
            pe.wait_ge(s["m_ready"], GB)
            for b in range(GB):
                last = nc.tensor.matmul(ps[:, 0, b * L:(b + 1) * L], kv[:, b, :], qt[:, b * L:(b + 1) * L], start=True, stop=True)
            last.then_inc(s["o_psum"], 1)
            project(k, pe, s, w["l1x_o"])


def l1_attn(k, phase, w, rowv, colv):
    nc, ps = k.nc, k.ps
    s = k.signals(phase, "l1a", *NORM, "qkv_psum", "qkv_ready", "v_ready", "qt_psum", "qt_ready", "kv_psum", "kv_ready", "ks_psum",
                  "q_ready", "num_psum", "o_ready", "z_psum", "residual")
    with ExitStack() as own, nc.Block() as block:
        norm_tiles(k, own)
        qk = tile(k, own, "l1a_qk", P, T, 2 * H, DH)
        pw = tile(k, own, "l1a_pw", P, T, 2 * H, DH)
        sm = tile(k, own, "l1a_sums", P, T, 2 * H)
        v = tile(k, own, "l1a_v", P, T, D)
        qt = tile(k, own, "l1a_qt", P, GT)
        kv = tile(k, own, "l1a_kv", P, GB, D)
        out = tile(k, own, "l1a_out", P, GB, L)
        den = tile(k, own, "l1a_den", P, T, H)
        k.ot = tile(k, own, "l1a_ot", P, GT)

        @block.vector
        def _(vec):
            step = Steps(vec, s["vector_step"])
            norm_vector(k, vec, step, s)
            for t in range(T):
                vec.wait_ge(s["qkv_psum"], t + 1)
                step(nc.vector.tensor_scalar(qk[:, t, :, :].rearrange("p h d -> p (h d)"), ps[:, 1 + t, 0:2 * D], 0.0, 1e-6, MAX, ADD), s["qkv_ready"])
            wide = (P, T * 2 * H, DH)
            q3, p3 = (a[:].rearrange("p t h d -> p (t h) d") for a in (qk, pw))
            s3 = sm[:].rearrange("p t h -> p (t h)")
            for power in (1, 3):
                if power == 3:
                    step(nc.vector.tensor_tensor(p3, q3, q3, MUL))
                    step(nc.vector.tensor_tensor(q3, q3, p3, MUL))
                step(nc.vector.reduce_sum(s3, q3, X))
                step(nc.vector.reciprocal(s3, s3))
                step(nc.vector.tensor_tensor(q3, q3, over(s3.unsqueeze(2), wide), MUL), None if power == 1 else s["qkv_ready"])
            vec.wait_ge(s["ks_psum"], 1)
            q4, p4 = qk[:, :, 0:H, :], pw[:, :, 0:H, :]
            for t in range(T):
                step.free(nc.vector.tensor_tensor(p4[:, t], q4[:, t], ps[:, 5, t * D:(t + 1) * D].rearrange("p (h d) -> p h d", d=DH), MUL))
            step.settled()
            step(nc.vector.reduce_sum(den[:], p4, X))
            step(nc.vector.tensor_scalar(den[:], den[:], 1e-6, None, ADD))
            step(nc.vector.reciprocal(den[:], den[:]))
            for t in range(T):
                step.free(nc.vector.tensor_tensor(q4[:, t], q4[:, t], over(den[:, t].unsqueeze(2), (P, H, DH)), MUL), s["q_ready"])
            step.settled(s["q_ready"])
            vec.wait_ge(s["kv_psum"], 1)
            for j in range(BPT):
                step(nc.vector.tensor_tensor(kv[:].rearrange("p (t j) d -> p j t d", j=BPT)[:, j], ps[:, 1 + j, :].rearrange("p (t d) -> p t d", d=D),
                                             over(k.same_head.unsqueeze(1), (P, T, D)), MUL), s["kv_ready"])
            vec.wait_ge(s["num_psum"], 1)
            o = out[:]
            step(nc.vector.tensor_copy(o, ps[:, 6, :].rearrange("p (b n) -> p b n", n=L)))
            ot = k.ot[:].rearrange("p (b n) -> p b n", n=L)
            before, here, after = (colv[f"l1a_w{i}"] for i in range(3))
            step(nc.vector.tensor_scalar(ot, o, here, colv["l1a_bc"], MUL, ADD))
            step(nc.vector.tensor_tensor(ot, ot, o, ADD))
            step(nc.vector.scalar_tensor_tensor(ot[:, :, 1:L], o[:, :, 0:L - 1], before, ot[:, :, 1:L], MUL, ADD))
            step(nc.vector.scalar_tensor_tensor(ot[:, :, 0:L - 1], o[:, :, 1:L], after, ot[:, :, 0:L - 1], MUL, ADD), s["o_ready"])
            add_projection(k, vec, step, s, rowv["l1a_bp"])

        @block.scalar
        def _(act):
            step = Steps(act, s["scalar_step"])
            norm_scalar(k, act, step, s)
            for t in range(T):
                act.wait_ge(s["qkv_ready"], t + 1)
                step(nc.scalar.activation(v[:, t, :], ps[:, 1 + t, 2 * D:3 * D], ACT.Copy), s["v_ready"])
            act.wait_ge(s["qt_psum"], 1)
            step(nc.scalar.activation(qt[:], ps[:, 0, :], ACT.Copy), s["qt_ready"])

        @block.tensor
        def _(pe):
            norm_tensor(k, pe, s)
            pe.wait_ge(s["xt_ready"], 1)
            for t in range(T):
                nc.tensor.matmul(ps[:, 1 + t, 0:3 * D], k.xt[:, t * P:(t + 1) * P], w["l1a_qkv"], start=True, stop=True).then_inc(s["qkv_psum"], 1)
            pe.wait_ge(s["qkv_ready"], T + 1)
            pe.wait_ge(s["v_ready"], T)
            for t in range(T):
                last = nc.tensor.matmul(ps[:, 5, t * D:(t + 1) * D], k.same_batch, qk[:, t, H:2 * H, :].rearrange("p h d -> p (h d)"), start=True, stop=True)
            last.then_inc(s["ks_psum"], 1)
            for t in range(T):
                for j in range(BPT):
                    r = slice(L * j, L * j + L)
                    last = nc.tensor.matmul(ps[:, 1 + j, t * D:(t + 1) * D], qk[r, t, H:2 * H, :].rearrange("p h d -> p (h d)"), v[r, t, :], start=True, stop=True)
            last.then_inc(s["kv_psum"], 1)
            pe.wait_ge(s["q_ready"], T)
            for t in range(T):
                last = nc.tensor.transpose(ps[:, 0, t * P:(t + 1) * P], qk[:, t, 0:H, :].rearrange("p h d -> p (h d)"), k.ident)
            last.then_inc(s["qt_psum"], 1)
            pe.wait_ge(s["qt_ready"], 1)
            pe.wait_ge(s["kv_ready"], BPT)
            for b in range(GB):
                last = nc.tensor.matmul(ps[:, 6, b * L:(b + 1) * L], kv[:, b, :], qt[:, b * L:(b + 1) * L], start=True, stop=True)
            last.then_inc(s["num_psum"], 1)
            pe.wait_ge(s["o_ready"], 1)
            for t in range(T):
                last = nc.tensor.matmul(ps[:, 5, t * D:(t + 1) * D], k.ot[:, t * P:(t + 1) * P], w["l1a_p"], start=True, stop=True)
            last.then_inc(s["z_psum"], 1)


def l1_router(k, phase, w, store_x, store_xn, store_logits):
    nc, ps = k.nc, k.ps
    s = k.signals(phase, "l1r", *NORM, "logits", "logits_ready", "stored")
    with ExitStack() as own, nc.Block() as block:
        norm_tiles(k, own)
        lg = tile(k, own, "l1r_logits", E1, GT)

        @block.vector
        def _(vec):
            norm_vector(k, vec, Steps(vec, s["vector_step"]), s)

        @block.scalar
        def _(act):
            step = Steps(act, s["scalar_step"])
            norm_scalar(k, act, step, s)
            act.wait_ge(s["logits"], 1)
            step(nc.scalar.activation(lg[:], ps[0:E1, 1, :], ACT.Copy), s["logits_ready"])

        @block.tensor
        def _(pe):
            norm_tensor(k, pe, s)
            pe.wait_ge(s["xt_ready"], 1)
            nc.tensor.matmul(ps[0:E1, 1, :], w["l1f_r"], k.xt[:], start=True, stop=True).then_inc(s["logits"], 1)

        @block.sync
        def _(sp):
            sp.dma_start(store_x, k.xg[:]).then_inc(s["stored"], 16)
            sp.wait_ge(s["xn_ready"], T)
            sp.dma_start(store_xn, k.xn[:]).then_inc(s["stored"], 16)
            sp.wait_ge(s["logits_ready"], 1)
            sp.dma_start(store_logits, lg[:]).then_inc(s["stored"], 16)
            sp.wait_ge(s["stored"], 48)
            sp.wait_ge(k.x_loaded, 16)
            sp.wait_ge(k.ctxt_loaded, 16)
            sp.wait_ge(k.ctx_loaded, 32)
            sp.wait_ge(k.mask_loaded, 16)


def token_group(a, g):
    return a.rearrange("(g t p) d -> g p t d", g=GROUPS, p=P)[g]


def context_group(dram, g):
    return (dram["ctx_t"].rearrange("p (g b s) -> g p b s", g=GROUPS, b=GB)[g],
            dram["ctx_rows"].rearrange("p (g b) i d -> g p b i d", g=GROUPS)[g],
            dram["ctx_last"].rearrange("p (g b) d -> g p b d", g=GROUPS)[g])


def phase_a(k, dram, groups, layers):
    nc = k.nc
    with ExitStack() as phase:
        wp = tile(k, phase, "a_weights", P, len(A_MATS), D)
        rp = tile(k, phase, "a_rows", P, len(A_ROWS), D)
        cp = tile(k, phase, "a_cols", P, len(A_COLS))
        wg, wr = tile(k, phase, "a_wg", P, E0), tile(k, phase, "a_wr", P, E1)
        w1, w2 = tile(k, phase, "a_w1", P, E0, HID0), tile(k, phase, "a_w2", P, E0, 4, D)
        k.ctxt = tile(k, phase, "ctx_t", P, GB, S2)
        k.ctx = tile(k, phase, "ctx_rows", P, GB, 2, D + 1)
        k.last = tile(k, phase, "ctx_last_row", 1, GB, D + 1)
        k.mask = tile(k, phase, "mask", P, T, S2, dtype=U8)
        w = {n: wp[:, i, :] for i, n in enumerate(A_MATS)}
        w["l1a_qkv"] = wp[:, A_MATS.index("l1a_q"):A_MATS.index("l1a_q") + 3, :].rearrange("p a d -> p (a d)")
        w.update({"l0f_g": wg[:], "l1f_r": wr[:], "l0f_w1": w1, "l0f_w2": w2})
        rowv = {n: rp[:, i, :] for i, n in enumerate(A_ROWS)}
        colv = {n: cp[:, i:i + 1] for i, n in enumerate(A_COLS)}
        mask_group = lambda g: dram["mask_bool"].rearrange("(g t p) s -> g p t s", g=GROUPS, p=P)[g]
        loaded = k.flag(phase, "a_weights_loaded")
        k.ffn_loaded = k.flag(phase, "a_ffn_weights_loaded")
        with nc.Block() as block:
            @block.sync
            def _(sp):
                ctxt, ctx, last = context_group(dram, 0)
                for dst, src in ((wp, dram["a_mats"]), (cp, dram["a_cols"]), (rp, dram["a_rows"].partition_broadcast(P)), (k.x_next, token_group(dram["x"], 0)),
                                 (wg, dram["l0f_g"]), (wr, dram["l1f_r"]), (k.mask, mask_group(0)), (k.ctxt, ctxt), (k.ctx, ctx), (k.last, last)):
                    sp.dma_start(dst[:], src).then_inc(loaded, 16)
                sp.dma_start(w1[:], dram["l0f_w1"]).then_inc(k.ffn_loaded, 16)
                sp.dma_start(w2[:], dram["l0f_w2"]).then_inc(k.ffn_loaded, 16)
                sp.wait_ge(loaded, 16 * 10)

        k.numbers.remove(k.ffn_loaded.num)
        k.clear_signals()
        with nc.Fori(0, groups) as g:
            k.x_loaded, k.ctxt_loaded, k.ctx_loaded, k.mask_loaded = (
                k.flag(phase, "a_" + n) for n in ("x_loaded", "ctxt_loaded", "ctx_loaded", "mask_loaded"))
            after = (g + 1) % GROUPS
            ctxt, ctx, last = context_group(dram, after)
            k.x_in = k.x_next
            l0_xattn(k, phase, w, dram["ctx"], token_group(dram["x"], after), ctxt)
            k.x_in = k.xg
            if "l0a" in layers:
                l0_attn(k, phase, w, rowv, colv)
            if "l0f" in layers:
                l0_ffn(k, phase, w)
            l1_xattn(k, phase, w, rowv, colv, ctx, last, mask_group(after))
            if "l1a" in layers:
                l1_attn(k, phase, w, rowv, colv)
            l1_router(k, phase, w, token_group(dram["x_a"], g), token_group(dram["xn_a"], g), dram["logits"].rearrange("e (g n) -> g e n", g=GROUPS)[g])
            k.clear_signals()
        k.numbers.append(k.ffn_loaded.num)


TOP_ROUNDS = CAP1 // 8
HALF = TOKENS // 2
HALF_AT = 64
PER = 4


def choose_tokens(k, phase, dram, weight_of, token_of):
    nc, ps = k.nc, k.ps
    s = k.signals(phase, "l1t", "loaded", "filled", "shifted", "exps", "merged", "turned", "zeroed", "zeros_stored")
    with ExitStack() as own, nc.Block() as block:
        lg = tile(k, own, "l1t_logits", HALF_AT + E1, HALF)
        val = tile(k, own, "l1t_values", HALF_AT + E1, CAP1)
        at = tile(k, own, "l1t_at", HALF_AT + E1, CAP1, dtype=U32)
        atf = tile(k, own, "l1t_at_f", HALF_AT + E1, CAP1)
        second = tile(k, own, "l1t_second", E1, 2, CAP1)
        both = tile(k, own, "l1t_both", E1, 4, CAP1)
        st = tile(k, own, "l1t_stats", E1, 2)
        zeros = tile(k, own, "l1t_zeros", P, TOKENS)

        @block.sync
        def _(sp):
            sp.wait_ge(s["filled"], 1)
            sp.dma_start(lg[0:E1, :], dram["logits"][:, 0:HALF]).then_inc(s["loaded"], 16)
            sp.dma_start(lg[HALF_AT:HALF_AT + E1, :], dram["logits"][:, HALF:TOKENS]).then_inc(s["loaded"], 16)
            sp.wait_ge(s["zeroed"], 1)
            for j in range(PER):
                sp.dma_start(dram[f"sums_{j}"].rearrange("(p q) d -> p (q d)", p=P), zeros[:]).then_inc(s["zeros_stored"], 16)
            sp.wait_ge(s["zeros_stored"], 16 * PER)

        @block.gpsimd
        def _(pool):
            nc.gpsimd.memset(zeros[:], 0.0).then_inc(s["zeroed"], 1)

        @block.vector
        def _(vec):
            step = Steps(vec, s["vector_step"])
            step(nc.vector.memset(lg[:], LOWEST), s["filled"])
            vec.wait_ge(s["loaded"], 32)
            for r in range(TOP_ROUNDS):
                eight = slice(8 * r, 8 * r + 8)
                step(nc.vector.max(val[:, eight], lg[:]))
                step(nc.vector.max_index(at[:, eight], val[:, eight], lg[:]))
                step(nc.vector.match_replace(lg[:], val[:, eight], lg[:], LOWEST))
            step(nc.vector.tensor_copy(atf[:], at[:]))
            step(nc.vector.tensor_copy(second[:, 0, :], val[HALF_AT:HALF_AT + E1, ::-1]))
            step(nc.vector.tensor_scalar(second[:, 1, :], atf[HALF_AT:HALF_AT + E1, ::-1], float(HALF), None, ADD))
            first, best, token, weight = (both[:, i, :] for i in range(4))
            step(nc.vector.tensor_tensor(first, val[0:E1, :], second[:, 0, :], ALU.is_ge))
            step(nc.vector.tensor_tensor(best, val[0:E1, :], second[:, 0, :], MAX))
            step(nc.vector.tensor_tensor(token, atf[0:E1, :], second[:, 1, :], SUB))
            step(nc.vector.tensor_tensor(token, token, first, MUL))
            step(nc.vector.tensor_tensor(token, token, second[:, 1, :], ADD))
            step(nc.vector.reduce_max(st[:, 0:1], best, X))
            step(nc.vector.tensor_scalar(weight, best, st[:, 0:1], None, SUB), s["shifted"])
            vec.wait_ge(s["exps"], 1)
            step(nc.vector.reduce_sum(st[:, 1:2], weight, X))
            step(nc.vector.reciprocal(st[:, 1:2], st[:, 1:2]))
            step(nc.vector.tensor_scalar(weight, weight, st[:, 1:2], None, MUL), s["merged"])
            vec.wait_ge(s["turned"], 1)
            step(nc.vector.tensor_copy(weight_of[:], ps[:, 0, 0:E1]))
            step(nc.vector.tensor_copy(token_of[:], ps[:, 0, E1:2 * E1]))

        @block.scalar
        def _(act):
            act.wait_ge(s["shifted"], 1)
            nc.scalar.activation(both[:, 3, :], both[:, 3, :], ACT.Exp).then_inc(s["exps"], 1)

        @block.tensor
        def _(pe):
            pe.wait_ge(s["merged"], 1)
            nc.tensor.transpose(ps[:, 0, 0:E1], both[:, 3, :], k.ident[0:E1, 0:E1])
            nc.tensor.transpose(ps[:, 0, E1:2 * E1], both[:, 2, :], k.ident[0:E1, 0:E1]).then_inc(s["turned"], 1)


def l1_experts(k, phase, dram, weight_of, token_of, b1):
    nc, ps = k.nc, k.ps
    k.clear_signals()
    with nc.Fori(0, E1 // PER) as n:
        s = k.signals(phase, "l1e", "picked", "weights_loaded", "gathered", "xt_psum", "xt_ready", "hidden_psum", "hidden_ready", "y_psum",
                      "y_ready", "scattered")
        with ExitStack() as own, nc.Block() as block:
            rows = tile(k, own, "l1e_rows", P, PER, dtype=I32)
            wt = tile(k, own, "l1e_weight", P, PER)
            b1n = tile(k, own, "l1e_b1", P, PER * S1)
            w1 = tile(k, own, "l1e_w1", P, PER, S1, P)
            w2 = tile(k, own, "l1e_w2", P, PER, S1, KW)
            b2 = tile(k, own, "l1e_b2", P, PER, D)
            xe = tile(k, own, "l1e_x", P, PER, D)
            xet = tile(k, own, "l1e_xt", P, PER, P)
            hid = tile(k, own, "l1e_hidden", P, PER, S1, P)
            y = tile(k, own, "l1e_y", P, PER, D)

            @block.sync
            def _(sp):
                sp.dma_start(w1[:], dram["l1f_w1"].rearrange("p (n e) s m -> n p e s m", e=PER)[n]).then_inc(s["weights_loaded"], 16)
                sp.dma_start(w2[:], dram["l1f_w2"].rearrange("p (n e) s m -> n p e s m", e=PER)[n]).then_inc(s["weights_loaded"], 16)
                sp.dma_start(b2[:], dram["l1f_b2"].rearrange("(n e) d -> n e d", e=PER)[n].partition_broadcast(P)).then_inc(s["weights_loaded"], 16)

            @block.vector
            def _(vec):
                step = Steps(vec, s["vector_step"])
                step(nc.vector.tensor_copy(rows[:], token_of[:, bass.ts(n, PER)]), s["picked"])
                step(nc.vector.tensor_copy(wt[:], weight_of[:, bass.ts(n, PER)]))
                step(nc.vector.tensor_copy(b1n[:], b1[:, bass.ts(n, PER * S1)]), s["picked"])
                vec.wait_ge(s["weights_loaded"], 48)
                vec.wait_ge(s["y_psum"], 1)
                step(nc.vector.tensor_tensor(y[:], b2[:], ps[:, 5, :].rearrange("p (e d) -> p e d", d=D), ADD))
                step(nc.vector.tensor_tensor(y[:], y[:], over(wt[:].unsqueeze(2), (P, PER, D)), MUL), s["y_ready"])

            @block.gpsimd
            def _(pool):
                pool.wait_ge(s["picked"], 1)
                for e in range(PER):
                    nc.gpsimd.indirect_dma_start(out=xe[:, e, :], out_offset=None, in_=dram["xn_a"],
                                                 in_offset=bass.IndirectOffsetOnAxis(ap=rows[:, e:e + 1], axis=0)).then_inc(s["gathered"], 16)
                pool.wait_ge(s["gathered"], 16 * PER)
                pool.wait_ge(s["y_ready"], 1)
                for e in range(PER):
                    nc.gpsimd.indirect_dma_start(out=dram[f"sums_{e}"], out_offset=bass.IndirectOffsetOnAxis(ap=rows[:, e:e + 1], axis=0),
                                                 in_=y[:, e, :], in_offset=None, compute_op=ADD).then_inc(s["scattered"], 16)
                pool.wait_ge(s["scattered"], 16 * PER)

            @block.scalar
            def _(act):
                step = Steps(act, s["scalar_step"])
                act.wait_ge(s["xt_psum"], 1)
                step(nc.scalar.activation(xet[:].rearrange("p e c -> p (e c)"), ps[:, 0, :], ACT.Copy), s["xt_ready"])
                act.wait_ge(s["picked"], 2)
                for e in range(PER):
                    act.wait_ge(s["hidden_psum"], e + 1)
                    for i in range(S1):
                        step(nc.scalar.activation(hid[:, e, i, :], ps[:, 1 + e, i * P:(i + 1) * P], ACT.Gelu,
                                                  bias=b1n[:, e * S1 + i:e * S1 + i + 1]), s["hidden_ready"])

            @block.tensor
            def _(pe):
                pe.wait_ge(s["gathered"], 16 * PER)
                for e in range(PER):
                    last = nc.tensor.transpose(ps[:, 0, e * P:(e + 1) * P], xe[:, e, :], k.ident)
                last.then_inc(s["xt_psum"], 1)
                pe.wait_ge(s["xt_ready"], 1)
                pe.wait_ge(s["weights_loaded"], 48)
                for e in range(PER):
                    for i in range(S1):
                        last = nc.tensor.matmul(ps[:, 1 + e, i * P:(i + 1) * P], w1[:, e, i, :], xet[:, e, :], start=True, stop=True)
                    last.then_inc(s["hidden_psum"], 1)
                for e in range(PER):
                    for i in range(S1):
                        pe.wait_ge(s["hidden_ready"], e * S1 + i + 1)
                        last = nc.tensor.matmul(ps[:, 5, e * D + i * KW:e * D + (i + 1) * KW], hid[:, e, i, :], w2[:, e, i, :], start=True, stop=True)
                last.then_inc(s["y_psum"], 1)
        k.clear_signals()


def phase_b(k, dram):
    nc = k.nc
    with ExitStack() as phase:
        weight_of = tile(k, phase, "l1_weight_of", P, E1)
        token_of = tile(k, phase, "l1_token_of", P, E1, dtype=I32)
        b1 = tile(k, phase, "l1_b1", P, E1 * S1)
        loaded = k.flag(phase, "b_b1_loaded")
        with nc.Block() as block:
            @block.sync
            def _(sp):
                sp.dma_start(b1[:], dram["l1f_b1"]).then_inc(loaded, 16)
                sp.wait_ge(loaded, 16)
        choose_tokens(k, phase, dram, weight_of, token_of)
        l1_experts(k, phase, dram, weight_of, token_of, b1)


def l2_xattn(k, phase, w, rowv, colv, biases, next_context):
    nc, ps = k.nc, k.ps
    s = k.signals(phase, "l2x", *NORM, "qw_ready", "scores", "neg_ready", "exps", "p_ready", "turned", "pt_ready", "c2q_psum", "c2q_rows", "c2q_turned", "c2q_ready",
                  "best_ready", "best_turned", "b_shifted", "b_exps", "b_ready", "b_back", "bd_ready", "q2c_psum", "cat_ready", "z_psum", "residual")
    ROW = 300
    with ExitStack() as own, nc.Block() as block:
        norm_tiles(k, own)
        qw = tile(k, own, "l2x_qw", P, GT)
        pr = tile(k, own, "l2x_p", P, T, S2)
        st = tile(k, own, "l2x_stats", P, 4, T)
        pt = tile(k, own, "l2x_pt", P, 2, GT)
        ptl = tile(k, own, "l2x_pt_last", 1, GT)
        ba = tile(k, own, "l2x_batch_att", T, BPT, L)
        bs = tile(k, own, "l2x_batch_stats", T, 2, BPT)
        bd = tile(k, own, "l2x_batch_att_x", P, T, BPT)
        q2c = tile(k, own, "l2x_q2c", P, GB)
        cat = tile(k, own, "l2x_cat", P, 3, GT)
        c2q = tile(k, own, "l2x_c2q", P, T, D)
        total = tile(k, own, "l2x_bias", P, 1)
        next_ctxt, next_ctx, next_last = next_context

        @block.sync
        def _(sp):
            sp.wait_ge(s["scores"], 1)
            sp.dma_start(k.ctxt[:], next_ctxt).then_inc(k.next_loaded, 16)
            sp.wait_ge(s["c2q_psum"], 1)
            sp.dma_start(k.ctx[:], next_ctx).then_inc(k.next_loaded, 16)
            sp.dma_start(k.last[:], next_last).then_inc(k.next_loaded, 16)

        @block.vector
        def _(vec):
            step = Steps(vec, s["vector_step"])
            norm_vector(k, vec, step, s)
            step(nc.vector.reduce_sum(total[:], biases, X))
            vec.wait_ge(s["xt_ready"], 1)
            step(nc.vector.tensor_scalar(qw[:], k.xt[:], colv["l2x_wcq"], colv["l2x_wq"], MUL, ADD), s["qw_ready"])
            mx, neg, best, rs = (st[:, i, :] for i in range(4))
            vec.wait_ge(s["scores"], 1)
            step(nc.vector.reduce_max(mx, ps[:, 0:T, 0:S2], X))
            step(nc.vector.tensor_scalar(best, ps[:, 0, ROW:ROW + T], total[:], None, ADD))
            step(nc.vector.tensor_tensor(best, best, mx, ADD), s["best_ready"])
            step(nc.vector.tensor_scalar(neg, mx, -1.0, None, MUL), s["neg_ready"])
            vec.wait_ge(s["exps"], T)
            step(nc.vector.reciprocal(rs, rs))
            step(nc.vector.tensor_tensor(pr[:], pr[:], over(rs.unsqueeze(2), (P, T, S2)), MUL), s["p_ready"])
            bmx, bsum = bs[:, 0, :], bs[:, 1, :]
            vec.wait_ge(s["best_turned"], 1)
            got = ps[0:T, 7, 0:P].rearrange("p (j n) -> p j n", n=L)
            step(nc.vector.reduce_max(bmx, got, X))
            step(nc.vector.tensor_tensor(ba[:], got, over(bmx.unsqueeze(2), (T, BPT, L)), SUB), s["b_shifted"])
            vec.wait_ge(s["b_exps"], 1)
            step(nc.vector.reduce_sum(bsum, ba[:], X))
            step(nc.vector.reciprocal(bsum, bsum))
            step(nc.vector.tensor_tensor(ba[:], ba[:], over(bsum.unsqueeze(2), (T, BPT, L)), MUL), s["b_ready"])
            vec.wait_ge(s["turned"], 1)
            step(nc.vector.tensor_copy(pt[:, 1, :], ps[:, 5, :]), s["pt_ready"])
            vec.wait_ge(s["b_back"], 1)
            step(nc.vector.tensor_tensor(bd[:], over(ps[:, 0, 0:T].unsqueeze(2), (P, T, BPT)), over(k.tile_batch.unsqueeze(1), (P, T, BPT)), MUL), s["bd_ready"])
            vec.wait_ge(s["q2c_psum"], 1)
            step(nc.vector.tensor_copy(q2c[:], ps[:, 1, 0:GB]))
            step(nc.vector.tensor_tensor(cat[:, 2, :].rearrange("p (b n) -> p b n", n=L), k.xt[:].rearrange("p (b n) -> p b n", n=L),
                                         over(q2c[:].unsqueeze(2), (P, GB, L)), MUL), s["cat_ready"])
            vec.wait_ge(s["c2q_ready"], 1)
            step(nc.vector.tensor_tensor(cat[:, 1, :], cat[:, 0, :], k.xt[:], MUL), s["cat_ready"])
            add_projection(k, vec, step, s, rowv["l2x_bl"])

        @block.scalar
        def _(act):
            step = Steps(act, s["scalar_step"])
            norm_scalar(k, act, step, s, bank=4)
            act.wait_ge(s["neg_ready"], 1)
            for t in range(T):
                step(nc.scalar.activation(pr[:, t, :], ps[:, t, 0:S2], ACT.Exp, bias=st[:, 1, t:t + 1], accum_out=st[:, 3, t:t + 1]), s["exps"])
            act.wait_ge(s["b_shifted"], 1)
            step(nc.scalar.activation(ba[:], ba[:], ACT.Exp), s["b_exps"])
            act.wait_ge(s["turned"], 1)
            step(nc.scalar.activation(pt[:, 0, :], ps[:, 4, :], ACT.Copy))
            step(nc.scalar.activation(ptl[:], ps[0:1, 6, :], ACT.Copy))
            act.wait_ge(s["pt_ready"], 1)
            act.wait_ge(s["c2q_psum"], 1)
            step(nc.scalar.activation(c2q[:].rearrange("p t d -> p (t d)"), ps[:, 2, :], ACT.Copy), s["c2q_rows"])
            act.wait_ge(s["c2q_turned"], 1)
            step(nc.scalar.activation(cat[:, 0, :], ps[:, 3, :], ACT.Copy), s["c2q_ready"])

        @block.tensor
        def _(pe):
            norm_tensor(k, pe, s, bank=4)
            pe.wait_ge(s["xt_ready"], 1)
            for t in range(T):
                nc.tensor.matmul(ps[:, 0, ROW + t:ROW + t + 1], k.xt[:, t * P:(t + 1) * P], colv["l2x_wc"], start=True, stop=True)
            pe.wait_ge(s["qw_ready"], 1)
            for t in range(T):
                for j in range(BPT):
                    b = t * BPT + j
                    last = nc.tensor.matmul(ps[L * j:L * j + L, t, 0:S2], qw[:, b * L:(b + 1) * L], k.ctxt[:, b, :], start=True, stop=True)
            last.then_inc(s["scores"], 1)
            pe.wait_ge(s["best_ready"], 1)
            nc.tensor.transpose(ps[0:T, 7, 0:P], st[:, 2, :], k.ident).then_inc(s["best_turned"], 1)
            pe.wait_ge(s["p_ready"], 1)
            for t in range(T):
                for i in range(2):
                    nc.tensor.transpose(ps[:, 4 + i, t * P:(t + 1) * P], pr[:, t, i * P:(i + 1) * P], k.ident)
                last = nc.tensor.transpose(ps[0:1, 6, t * P:(t + 1) * P], pr[:, t, 2 * P:S2], k.ident)
            last.then_inc(s["turned"], 1)
            pe.wait_ge(s["b_ready"], 1)
            nc.tensor.transpose(ps[:, 0, 0:T], ba[:].rearrange("t j n -> t (j n)"), k.ident[0:T, 0:T]).then_inc(s["b_back"], 1)
            pe.wait_ge(s["pt_ready"], 1)
            pe.wait_ge(s["scalar_step"], 2)
            for b in range(GB):
                c = slice(b * L, (b + 1) * L)
                out = ps[L * (b % BPT):L * (b % BPT) + L, 2, (b // BPT) * D:(b // BPT + 1) * D]
                nc.tensor.matmul(out, pt[:, 0, c], k.ctx[:, b, 0, 0:D], start=True, stop=False)
                nc.tensor.matmul(out, pt[:, 1, c], k.ctx[:, b, 1, 0:D], start=False, stop=False)
                last = nc.tensor.matmul(out, ptl[:, c], k.last[:, b, 0:D], start=False, stop=True)
            last.then_inc(s["c2q_psum"], 1)
            pe.wait_ge(s["bd_ready"], 1)
            for t in range(T):
                last = nc.tensor.matmul(ps[:, 1, t * BPT:(t + 1) * BPT], k.xn[:, t, :], bd[:, t, :], start=True, stop=True)
            last.then_inc(s["q2c_psum"], 1)
            pe.wait_ge(s["c2q_rows"], 1)
            for t in range(T):
                last = nc.tensor.transpose(ps[:, 3, t * P:(t + 1) * P], c2q[:, t, :], k.ident)
            last.then_inc(s["c2q_turned"], 1)
            pe.wait_ge(s["cat_ready"], 2)
            for t in range(T):
                c = slice(t * P, (t + 1) * P)
                for i, src in enumerate((k.xt[:, c], cat[:, 0, c], cat[:, 1, c], cat[:, 2, c])):
                    last = nc.tensor.matmul(ps[:, 5, t * D:(t + 1) * D], src, w["l2x_l"][:, i * D:(i + 1) * D], start=i == 0, stop=i == 3)
            last.then_inc(s["z_psum"], 1)


def self_attn(k, phase, name, wq, wk, wv, wo, scale, bias=None):
    nc, ps = k.nc, k.ps
    s = k.signals(phase, name, *NORM, *CORE)
    with ExitStack() as own, nc.Block() as block:
        norm_tiles(k, own)
        core_tiles(k, own)

        @block.vector
        def _(vec):
            step = Steps(vec, s["vector_step"])
            norm_vector(k, vec, step, s)
            q_by_head(k, vec, step, s)
            v_by_head(k, vec, step, s)
            core_vector(k, vec, step, s, scale, True, bias)

        @block.gpsimd
        def _(pool):
            core_pool(k, pool, s)

        @block.scalar
        def _(act):
            step = Steps(act, s["scalar_step"])
            norm_scalar(k, act, step, s)
            step(nc.scalar.activation(k.rep[:], four_times(k, ps[:, 0, :]), ACT.Copy), s["rep_ready"])
            act.wait_ge(s["k_psum"], 1)
            step(nc.scalar.activation(k.kt[:], ps[:, 2, :], ACT.Copy), s["k_ready"])
            core_scalar(k, act, step, s, scale, True)

        @block.tensor
        def _(pe):
            norm_tensor(k, pe, s)
            pe.wait_ge(s["xt_ready"], 1)
            nc.tensor.matmul(ps[:, 1, :], wq, k.xt[:], start=True, stop=True).then_inc(s["q_psum"], 1)
            nc.tensor.matmul(ps[:, 2, :], wk, k.xt[:], start=True, stop=True).then_inc(s["k_psum"], 1)
            core_tensor(k, pe, s, wv, wo)


def l2_norm_out(k, phase, store_x, store_xt, largest):
    nc = k.nc
    s = k.signals(phase, "l2n", *NORM, "stored")
    with ExitStack() as own, nc.Block() as block:
        norm_tiles(k, own)
        mx = tile(k, own, "l2n_mx", P, 1)

        @block.vector
        def _(vec):
            step = Steps(vec, s["vector_step"])
            norm_vector(k, vec, step, s)
            step(nc.vector.reduce_max(mx[:], k.xn[:].rearrange("p t d -> p (t d)"), X, apply_absolute_value=True))
            step(nc.vector.tensor_tensor(largest, largest, mx[:], MAX))

        @block.scalar
        def _(act):
            norm_scalar(k, act, Steps(act, s["scalar_step"]), s)

        @block.tensor
        def _(pe):
            norm_tensor(k, pe, s)

        @block.sync
        def _(sp):
            sp.dma_start(store_x, k.xg[:]).then_inc(s["stored"], 16)
            sp.wait_ge(s["xt_ready"], 1)
            sp.dma_start(store_xt, k.xt[:]).then_inc(s["stored"], 16)
            sp.wait_ge(s["stored"], 32)
            sp.wait_ge(k.next_loaded, 16 * (4 + PER))


def phase_c(k, dram, groups, layers, largest):
    nc = k.nc
    with ExitStack() as phase:
        wp = tile(k, phase, "c_weights", P, len(C_MATS), D)
        rp = tile(k, phase, "c_rows", P, len(C_ROWS), D)
        cp = tile(k, phase, "c_cols", P, len(C_COLS))
        wl = tile(k, phase, "c_wl", P, 4 * D)
        bc = tile(k, phase, "c_biases", P, 3)
        k.ctxt = tile(k, phase, "c_ctx_t", P, GB, S2)
        k.ctx = tile(k, phase, "c_ctx_rows", P, GB, 2, D + 1)
        k.last = tile(k, phase, "c_ctx_last_row", 1, GB, D + 1)
        sums = tile(k, phase, "c_sums", P, PER, T, D)
        w = {n: wp[:, i, :] for i, n in enumerate(C_MATS)}
        w["l2x_l"] = wl[:]
        rowv = {n: rp[:, i, :] for i, n in enumerate(C_ROWS)}
        colv = {n: cp[:, i:i + 1] for i, n in enumerate(C_COLS)}
        loaded = k.flag(phase, "c_weights_loaded")
        cleared = k.flag(phase, "c_largest_cleared")
        with nc.Block() as block:
            @block.sync
            def _(sp):
                for dst, name in ((wp, "c_mats"), (cp, "c_cols"), (wl, "l2x_l")):
                    sp.dma_start(dst[:], dram[name]).then_inc(loaded, 16)
                sp.dma_start(rp[:], dram["c_rows"].partition_broadcast(P)).then_inc(loaded, 16)
                sp.dma_start(bc[:], dram["l2x_biases"].partition_broadcast(P)).then_inc(loaded, 16)
                ctxt, ctx, last = context_group(dram, 0)
                for dst, src in ((k.ctxt, ctxt), (k.ctx, ctx), (k.last, last), (k.x_next, token_group(dram["x_a"], 0))):
                    sp.dma_start(dst[:], src).then_inc(loaded, 16)
                for j in range(PER):
                    sp.dma_start(sums[:, j, :, :], token_group(dram[f"sums_{j}"], 0)).then_inc(loaded, 16)
                sp.wait_ge(loaded, 16 * (9 + PER))

            @block.vector
            def _(vec):
                nc.vector.memset(largest, 0.0).then_inc(cleared, 1)
                vec.wait_ge(cleared, 1)

        k.clear_signals()
        with nc.Fori(0, groups) as g:
            s = k.signals(phase, "c_add", "added")
            k.next_loaded = k.flag(phase, "c_next_loaded")
            after = (g + 1) % GROUPS
            with nc.Block() as block:
                @block.vector
                def _(vec):
                    step = Steps(vec, s["vector_step"])
                    step(nc.vector.tensor_tensor(k.xg[:], k.x_next[:], sums[:, 0, :, :], ADD))
                    for j in range(1, PER):
                        step(nc.vector.tensor_tensor(k.xg[:], k.xg[:], sums[:, j, :, :], ADD), s["added"] if j == PER - 1 else None)

                @block.sync
                def _(sp):
                    sp.wait_ge(s["added"], 1)
                    sp.dma_start(k.x_next[:], token_group(dram["x_a"], after)).then_inc(k.next_loaded, 16)
                    for j in range(PER):
                        sp.dma_start(sums[:, j, :, :], token_group(dram[f"sums_{j}"], after)).then_inc(k.next_loaded, 16)

            l2_xattn(k, phase, w, rowv, colv, bc[:], context_group(dram, after))
            if "l2a" in layers:
                self_attn(k, phase, "l2a", w["l2a_q"], w["l2a_k"], w["l2a_v"], w["l2a_u"], D ** -0.5, rowv["l2a_bu"])
            l2_norm_out(k, phase, token_group(dram["x_c"], g), dram["xt_c"].rearrange("p (g n) -> g p n", g=GROUPS)[g], largest)
            k.clear_signals()


ROUND = 1.5 * 2.0 ** 23
ACT_MAX = 2.0 ** 15 - 1.0
SIG_STEPS = 65536.0
BLOCK2, W_MAX = 32, 7.0
CH2 = I2 // P


def quantise(k, step, x, inverse, scale, low, high, signal=None):
    v = k.nc.vector
    step(v.tensor_scalar(x, x, inverse, ROUND, MUL, ADD))
    step(v.tensor_scalar(x, x, ROUND, high, SUB, MIN))
    step(v.tensor_scalar(x, x, low, scale, MAX, MUL), signal)


def quantise_weights(k, phase, dram, up, gate, down):
    nc, ps = k.nc, k.ps
    s = k.signals(phase, "l2w", "loaded", "quantised", "turned")
    with ExitStack() as own, nc.Block() as block:
        blocks = CH2 * P // BLOCK2
        wt = tile(k, own, "l2w", P, 3, blocks, BLOCK2)
        sc = tile(k, own, "l2w_scale", P, 3, blocks)
        inv = tile(k, own, "l2w_inverse", P, 3, blocks)

        @block.sync
        def _(sp):
            for i, name in enumerate(("l2f_up", "l2f_gate", "l2f_down")):
                sp.dma_start(wt[:, i, :, :].rearrange("p b i -> p (b i)"), dram[name]).then_inc(s["loaded"], 16)

        @block.vector
        def _(vec):
            step = Steps(vec, s["vector_step"])
            vec.wait_ge(s["loaded"], 48)
            w3 = wt[:].rearrange("p a b i -> p (a b) i")
            s2, i2 = sc[:].rearrange("p a b -> p (a b)"), inv[:].rearrange("p a b -> p (a b)")
            step(nc.vector.reduce_max(s2, w3, X, apply_absolute_value=True))
            step(nc.vector.tensor_scalar(s2, s2, 1.0 / W_MAX, 1e-12, MUL, MAX))
            step(nc.vector.reciprocal(i2, s2))
            wide = (P, 3 * blocks, BLOCK2)
            step(nc.vector.tensor_tensor(w3, w3, over(i2.unsqueeze(2), wide), MUL))
            step(nc.vector.tensor_scalar(w3, w3, ROUND, ROUND, ADD, SUB))
            step(nc.vector.tensor_scalar(w3, w3, -W_MAX - 1.0, W_MAX, MAX, MIN))
            step(nc.vector.tensor_tensor(w3, w3, over(s2.unsqueeze(2), wide), MUL), s["quantised"])
            vec.wait_ge(s["turned"], 1)
            for i, dst in enumerate((up, gate, down)):
                step(nc.vector.tensor_copy(dst, ps[:, i, 0:I2]))

        @block.tensor
        def _(pe):
            pe.wait_ge(s["quantised"], 1)
            for i in range(3):
                for c in range(CH2):
                    last = nc.tensor.transpose(ps[:, i, c * P:(c + 1) * P], wt[:, i, c * 4:(c + 1) * 4, :].rearrange("p b i -> p (b i)"), k.ident)
            last.then_inc(s["turned"], 1)


def scale_of_largest(k, phase, name, columns, scales):
    nc, ps = k.nc, k.ps
    s = k.signals(phase, name, "turned", "found", "spread")
    n = len(columns)
    with ExitStack() as own, nc.Block() as block:
        one = tile(k, own, name + "_one", 1, n)

        @block.tensor
        def _(pe):
            for i, column in enumerate(columns):
                last = nc.tensor.transpose(ps[0:1, 0, i * P:(i + 1) * P], column, k.ident)
            last.then_inc(s["turned"], 1)
            pe.wait_ge(s["found"], 1)
            nc.tensor.matmul(ps[:, 1, 0:n], k.ones[0:1, :], one[:], start=True, stop=True).then_inc(s["spread"], 1)

        @block.vector
        def _(vec):
            step = Steps(vec, s["vector_step"])
            vec.wait_ge(s["turned"], 1)
            step(nc.vector.reduce_max(one[:], ps[0:1, 0, 0:n * P].rearrange("p (n q) -> p n q", n=n), X), s["found"])
            vec.wait_ge(s["spread"], 1)
            step(nc.vector.tensor_scalar(scales[:, 0, 0:n], ps[:, 1, 0:n], 1.0 / ACT_MAX, 1e-12, MUL, MAX))
            step(nc.vector.reciprocal(scales[:, 1, 0:n], scales[:, 0, 0:n]))


def phase_d(k, dram, groups, largest):
    nc, ps = k.nc, k.ps
    with ExitStack() as phase:
        wup, wgate = tile(k, phase, "l2f_up_t", P, I2), tile(k, phase, "l2f_gate_t", P, I2)
        wdown = tile(k, phase, "l2f_down_t", P, CH2, D)
        up = tile(k, phase, "l2f_up", P, GROUPS, CH2 * GT)
        gate = tile(k, phase, "l2f_gate", P, GROUPS, CH2 * GT)
        big = tile(k, phase, "l2f_largest", P, 2)
        new = tile(k, phase, "l2f_largest_here", P, 2)
        scales = tile(k, phase, "l2f_scales", P, 4, 2, 2)
        quantise_weights(k, phase, dram, wup[:], wgate[:], wdown[:].rearrange("p c d -> p (c d)"))
        scale_of_largest(k, phase, "l2f_x_scale", (largest,), scales[:, 0, :, :])

        def clear_largest(name):
            s = k.signals(phase, name, "cleared")
            with nc.Block() as block:
                @block.vector
                def _(vec):
                    Steps(vec, s["vector_step"])(nc.vector.memset(big[:], 0.0), s["cleared"])

        def scale(n, kind, column):
            return scales[:, n, kind, column:column + 1]

        clear_largest("l2f_clear_ug")
        k.clear_signals()
        with nc.Fori(0, groups) as g:
            s = k.signals(phase, "l2f_ug", "loaded", "xq_ready", "psum", "copied", "measured")
            with ExitStack() as own, nc.Block() as block:
                xq = tile(k, own, "l2f_xq", P, GT)

                @block.sync
                def _(sp):
                    sp.dma_start(xq[:], dram["xt_c"].rearrange("p (g n) -> g p n", g=GROUPS)[g]).then_inc(s["loaded"], 16)

                @block.vector
                def _(vec):
                    step = Steps(vec, s["vector_step"])
                    vec.wait_ge(s["loaded"], 16)
                    quantise(k, step, xq[:], scale(0, 1, 0), scale(0, 0, 0), -ACT_MAX - 1.0, ACT_MAX, s["xq_ready"])
                    vec.wait_ge(s["psum"], 2)
                    for i in range(2):
                        step(nc.vector.reduce_max(new[:, i:i + 1], ps[:, i * CH2:(i + 1) * CH2, :].rearrange("p c n -> p (c n)"), X, apply_absolute_value=True), s["measured"])
                    step(nc.vector.tensor_tensor(big[:], big[:], new[:], MAX))

                @block.scalar
                def _(act):
                    step = Steps(act, s["scalar_step"])
                    for i, dst in enumerate((up, gate)):
                        act.wait_ge(s["measured"], i + 1)
                        step(nc.scalar.activation(dst[:, bass.ds(g, 1), :].rearrange("p a n -> p (a n)"),
                                                  ps[:, i * CH2:(i + 1) * CH2, :].rearrange("p c n -> p (c n)"), ACT.Copy), s["copied"])

                @block.tensor
                def _(pe):
                    pe.wait_ge(s["xq_ready"], 1)
                    for i, wt in enumerate((wup, wgate)):
                        for c in range(CH2):
                            last = nc.tensor.matmul(ps[:, i * CH2 + c, :], wt[:, c * P:(c + 1) * P], xq[:], start=True, stop=True)
                        last.then_inc(s["psum"], 1)
            k.clear_signals()
        scale_of_largest(k, phase, "l2f_ug_scale", (big[:, 0:1], big[:, 1:2]), scales[:, 1, :, :])

        clear_largest("l2f_clear_act")
        k.clear_signals()
        with nc.Fori(0, groups) as g:
            s = k.signals(phase, "l2f_act", "gate_ready", "sig_ready")
            with ExitStack() as own, nc.Block() as block:
                sig = tile(k, own, "l2f_sigmoid", P, CH2 * GT)
                u, gt = (a[:, bass.ds(g, 1), :].rearrange("p a n -> p (a n)") for a in (up, gate))

                @block.vector
                def _(vec):
                    step = Steps(vec, s["vector_step"])
                    quantise(k, step, gt, scale(1, 1, 1), scale(1, 0, 1), -ACT_MAX - 1.0, ACT_MAX, s["gate_ready"])
                    quantise(k, step, u, scale(1, 1, 0), scale(1, 0, 0), -ACT_MAX - 1.0, ACT_MAX)
                    vec.wait_ge(s["sig_ready"], 1)
                    step(nc.vector.tensor_scalar(sig[:], sig[:], SIG_STEPS, ROUND, MUL, ADD))
                    step(nc.vector.tensor_scalar(sig[:], sig[:], ROUND, SIG_STEPS - 1.0, SUB, MIN))
                    step(nc.vector.tensor_scalar(sig[:], sig[:], 0.0, 1.0 / SIG_STEPS, MAX, MUL))
                    step(nc.vector.tensor_tensor(gt, gt, sig[:], MUL))
                    step(nc.vector.reduce_max(new[:, 0:1], gt, X, apply_absolute_value=True))
                    step(nc.vector.tensor_tensor(big[:, 0:1], big[:, 0:1], new[:, 0:1], MAX))

                @block.scalar
                def _(act):
                    act.wait_ge(s["gate_ready"], 1)
                    nc.scalar.activation(sig[:], gt, ACT.Sigmoid).then_inc(s["sig_ready"], 1)
            k.clear_signals()
        scale_of_largest(k, phase, "l2f_act_scale", (big[:, 0:1],), scales[:, 2, :, :])

        clear_largest("l2f_clear_o")
        k.clear_signals()
        with nc.Fori(0, groups) as g:
            s = k.signals(phase, "l2f_mul")
            with nc.Block() as block:
                u, gt = (a[:, bass.ds(g, 1), :].rearrange("p a n -> p (a n)") for a in (up, gate))

                @block.vector
                def _(vec):
                    step = Steps(vec, s["vector_step"])
                    quantise(k, step, gt, scale(2, 1, 0), scale(2, 0, 0), -ACT_MAX - 1.0, ACT_MAX)
                    step(nc.vector.tensor_tensor(gt, gt, u, MUL))
                    step(nc.vector.reduce_max(new[:, 0:1], gt, X, apply_absolute_value=True))
                    step(nc.vector.tensor_tensor(big[:, 0:1], big[:, 0:1], new[:, 0:1], MAX))
            k.clear_signals()
        scale_of_largest(k, phase, "l2f_o_scale", (big[:, 0:1],), scales[:, 3, :, :])

        k.clear_signals()
        with nc.Fori(0, groups) as g:
            s = k.signals(phase, "l2f_down", "loaded", "oq_ready", "psum", "x_ready", "stored")
            group = lambda a: a.rearrange("(g t p) d -> g p t d", g=GROUPS, p=P)[g]
            with ExitStack() as own, nc.Block() as block:
                oq = tile(k, own, "l2f_oq", P, CH2, GT)
                gt = gate[:, bass.ds(g, 1), :].rearrange("p a n -> p (a n)")

                @block.sync
                def _(sp):
                    sp.dma_start(k.xg[:], group(dram["x_c"])).then_inc(s["loaded"], 16)
                    sp.wait_ge(s["x_ready"], 1)
                    sp.dma_start(group(dram["x_d"]), k.xg[:]).then_inc(s["stored"], 16)
                    sp.wait_ge(s["stored"], 16)

                @block.vector
                def _(vec):
                    step = Steps(vec, s["vector_step"])
                    flat = oq[:].rearrange("p c n -> p (c n)")
                    step(nc.vector.tensor_copy(flat, gt))
                    quantise(k, step, flat, scale(3, 1, 0), scale(3, 0, 0), -ACT_MAX - 1.0, ACT_MAX, s["oq_ready"])
                    vec.wait_ge(s["loaded"], 16)
                    vec.wait_ge(s["psum"], 1)
                    step(nc.vector.tensor_tensor(k.xg[:], k.xg[:], ps[:, 0, :].rearrange("p (t d) -> p t d", d=D), ADD), s["x_ready"])

                @block.tensor
                def _(pe):
                    pe.wait_ge(s["oq_ready"], 1)
                    for t in range(T):
                        for c in range(CH2):
                            last = nc.tensor.matmul(ps[:, 0, t * D:(t + 1) * D], oq[:, c, t * P:(t + 1) * P], wdown[:, c, :], start=c == 0, stop=c == CH2 - 1)
                    last.then_inc(s["psum"], 1)
            k.clear_signals()


CHUNKS = GB * S2
Q = 4


def l3_xattn(k, phase, w, rowv, colv, next_x, next_ctxt, next_mask):
    nc, ps = k.nc, k.ps
    s = k.signals(phase, "l3x", *NORM, "q_psum", "qx_ready", "kt_psum", "kt_ready", "v_psum", "v_ready", "last_psum", "last_ready", "masks_ready",
                  "scores", "top_ready", "exps", "p_ready", "last_turned", "turned", "ptl_ready", "pt_ready", "o_psum", "om_ready", "o_ready", "z_psum", "residual")
    scale = DH ** -0.5
    with ExitStack() as own, nc.Block() as block:
        norm_tiles(k, own)
        k.qx = tile(k, own, "l3x_q_by_head", P, GB, 4, L)
        kt = tile(k, own, "l3x_kt", P, GB, S2)
        v = tile(k, own, "l3x_v", P, GB, 2, D)
        vl = tile(k, own, "l3x_v_last", Q, GB, D)
        sc = tile(k, own, "l3x_scores", P, 2, Q, S2)
        st = tile(k, own, "l3x_stats", P, 2, 3, Q)
        pt = tile(k, own, "l3x_pt", P, 2, 2, Q, P)
        ptl = tile(k, own, "l3x_pt_last", Q, 2, P)
        om = tile(k, own, "l3x_om", P, 4, L)
        k.ot = tile(k, own, "l3x_ot", P, GT)
        ktf = kt[:].rearrange("p b s -> p (b s)")
        ctf = k.ctxt[:].rearrange("p b s -> p (b s)")
        strips = [(i, min(512, CHUNKS - i)) for i in range(0, CHUNKS, 512)]

        @block.sync
        def _(sp):
            sp.wait_ge(s["masks_ready"], 1)
            for h in range(4):
                sp.dma_start(k.maski[L * h:L * h + L, :, :], next_mask).then_inc(k.next_loaded, 16)
            sp.wait_ge(s["kt_psum"], len(strips))
            sp.dma_start(k.ctxt[:], next_ctxt).then_inc(k.next_loaded, 16)
            sp.wait_ge(s["residual"], 1)
            sp.dma_start(k.x_next[:], next_x).then_inc(k.next_loaded, 16)

        @block.gpsimd
        def _(pool):
            nc.gpsimd.tensor_scalar(k.maskf[:], k.maski[:], 0.0, -1e9 / scale, EQ, MUL).then_inc(s["masks_ready"], 1)

        @block.vector
        def _(vec):
            step = Steps(vec, s["vector_step"])
            norm_vector(k, vec, step, s)
            q_by_head(k, vec, step, s, bank=1, bias=colv["l3x_bq"])
            for i in range(4):
                vec.wait_ge(s["v_psum"], 2 * i + 2)
                step(nc.vector.tensor_copy(v[:, 4 * i:4 * i + 4, :, :].rearrange("p b c d -> p (b c d)"), ps[:, 4 + 2 * (i % 2):6 + 2 * (i % 2), :].rearrange("p a n -> p (a n)")), s["v_ready"])
            vec.wait_ge(s["last_psum"], 1)
            step(nc.vector.tensor_tensor(vl[:], ps[0:Q, 0:4, :].rearrange("p a (b d) -> p (a b) d", d=D), over(k.quad_cols[0:Q, :].unsqueeze(1), (Q, GB, D)), MUL), s["last_ready"])
            vec.wait_ge(s["masks_ready"], 1)
            for i in range(GB + 2):
                if 1 <= i <= GB:
                    h = (i - 1) % 2
                    vec.wait_ge(s["exps"], Q * i)
                    step(nc.vector.reciprocal(st[:, h, 2, :], st[:, h, 1, :]))
                    step(nc.vector.tensor_tensor(sc[:, h, :, :], sc[:, h, :, :], over(st[:, h, 2, :].unsqueeze(2), (P, Q, S2)), MUL), s["p_ready"])
                if i < GB:
                    vec.wait_ge(s["scores"], i + 1)
                    for c in range(Q):
                        step.free(nc.vector.tensor_tensor_reduce(out=sc[:, i % 2, c, :], in0=ps[:, c, 0:S2], in1=k.maskf[:, i, :], scale=scale, scalar=LOWEST,
                                                                 op0=ADD, op1=MAX, accum_out=st[:, i % 2, 0, c:c + 1]))
                    step.settled()
                    step(nc.vector.tensor_scalar(st[:, i % 2, 0, :], st[:, i % 2, 0, :], -1.0, None, MUL), s["top_ready"])
                if i >= 2:
                    vec.wait_ge(s["o_psum"], i - 1)
                    step(nc.vector.tensor_tensor(om[:], ps[:, 6, 0:D].rearrange("p (h n) -> p h n", n=L), over(k.quad_head.unsqueeze(2), (P, 4, L)), MUL), s["om_ready"])
                    step(nc.vector.reduce_sum(k.ot[:, (i - 2) * L:(i - 1) * L], om[:].rearrange("p h n -> p n h"), X), s["o_ready"])
            add_projection(k, vec, step, s, rowv["l3x_bo"])

        @block.scalar
        def _(act):
            step = Steps(act, s["scalar_step"])
            norm_scalar(k, act, step, s)
            for n, (at, width) in enumerate(strips):
                act.wait_ge(s["kt_psum"], n + 1)
                step(nc.scalar.activation(ktf[:, at:at + width], ps[:, 2 + n % 2, 0:width], ACT.Identity, bias=colv["l3x_bq"]), s["kt_ready"])
            for i in range(GB + 1):
                if i > 0:
                    h = (i - 1) % 2
                    act.wait_ge(s["last_turned"], i)
                    step(nc.scalar.activation(ptl[:, h, :], ps[0:Q, 6, P:2 * P], ACT.Copy), s["ptl_ready"])
                    act.wait_ge(s["turned"], i)
                    step(nc.scalar.activation(pt[:, h, :, :, :].rearrange("p i c n -> p (i c n)"), ps[:, 4:6, :].rearrange("p i n -> p (i n)"), ACT.Copy), s["pt_ready"])
                if i < GB:
                    act.wait_ge(s["top_ready"], i + 1)
                    for c in range(Q):
                        step.free(nc.scalar.activation(sc[:, i % 2, c, :], sc[:, i % 2, c, :], ACT.Exp, bias=st[:, i % 2, 0, c:c + 1],
                                                       accum_out=st[:, i % 2, 1, c:c + 1]), s["exps"])
                    step.settled(s["exps"])

        @block.tensor
        def _(pe):
            norm_tensor(k, pe, s)
            pe.wait_ge(s["xt_ready"], 1)
            nc.tensor.matmul(ps[:, 1, :], w["l3x_q"], k.xt[:], start=True, stop=True).then_inc(s["q_psum"], 1)
            for n, (at, width) in enumerate(strips):
                if n >= 2:
                    pe.wait_ge(s["kt_ready"], n - 1)
                nc.tensor.matmul(ps[:, 2 + n % 2, 0:width], w["l3x_q"], ctf[:, at:at + width], start=True, stop=True).then_inc(s["kt_psum"], 1)
            pe.wait_ge(s["kt_ready"], len(strips))
            for n in range(GB // 2):
                if n >= 4 and n % 2 == 0:
                    pe.wait_ge(s["v_ready"], n // 2 - 1)
                for j in range(2):
                    for i in range(2):
                        last = nc.tensor.transpose(ps[:, 4 + n % 4, (2 * j + i) * P:(2 * j + i + 1) * P], kt[:, 2 * n + j, i * P:(i + 1) * P], k.ident)
                last.then_inc(s["v_psum"], 1)
            pe.wait_ge(s["qx_ready"], 4)
            for b in range(GB):
                last = nc.tensor.matmul(ps[0:Q, b // 4, (b % 4) * D:(b % 4 + 1) * D], over(kt[:, b, S2 - 1:S2], (P, Q)), k.ident, start=True, stop=True)
            last.then_inc(s["last_psum"], 1)
            pe.wait_ge(s["last_ready"], 1)
            pe.wait_ge(s["v_ready"], 4)

            def scores(b):
                if b > 0:
                    pe.wait_ge(s["top_ready"], b)
                for c in range(Q):
                    r = slice(L * c, L * c + L)
                    last = nc.tensor.matmul(ps[:, c, 0:S2], k.qx[r, b, :, :].rearrange("p h n -> p (h n)"), kt[r, b, :], start=True, stop=True)
                last.then_inc(s["scores"], 1)

            def turn(b):
                pe.wait_ge(s["p_ready"], b + 1)
                if b > 1:
                    pe.wait_ge(s["om_ready"], b - 1)
                nc.tensor.transpose(ps[0:Q, 6, P:2 * P], sc[:, b % 2, :, 2 * P], k.ident).then_inc(s["last_turned"], 1)
                if b > 0:
                    pe.wait_ge(s["pt_ready"], b)
                for c in range(Q):
                    for i in range(2):
                        last = nc.tensor.transpose(ps[:, 4 + i, c * P:(c + 1) * P], sc[:, b % 2, c, i * P:(i + 1) * P], k.ident)
                last.then_inc(s["turned"], 1)

            def outputs(b):
                pe.wait_ge(s["pt_ready"], b + 1)
                if b > 0:
                    pe.wait_ge(s["om_ready"], b)
                pe.wait_ge(s["ptl_ready"], min(b + 2, GB))
                nc.tensor.matmul(ps[:, 6, 0:D], vl[:, b, :], ptl[:, b % 2, :], start=True, stop=False)
                for i in range(2):
                    for c in range(Q):
                        r = slice(L * c, L * c + L)
                        last = nc.tensor.matmul(ps[r, 6, 0:D], v[:, b, i, r], pt[:, b % 2, i, c, :], start=False, stop=i == 1)
                last.then_inc(s["o_psum"], 1)

            scores(0)
            for b in range(GB):
                if b + 1 < GB:
                    scores(b + 1)
                turn(b)
                if b > 0:
                    outputs(b - 1)
            outputs(GB - 1)
            pe.wait_ge(s["o_ready"], GB)
            project(k, pe, s, w["l3x_o"])


def butterflies(k, phase, dram, up_w, up_b, down_w):
    nc, ps = k.nc, k.ps
    s = k.signals(phase, "fly", "loaded", "down_loaded", "up_done", "done", "b_psum", "w_psum")
    pairs = HID3 // 2
    with ExitStack() as own, nc.Block() as block:
        fw = tile(k, own, "fly_weights", P, STAGES, pairs * 4)
        y = tile(k, own, "fly_rows", P, 2, 2, HID3)
        t = tile(k, own, "fly_terms", P, 4, 2, pairs)
        ub = tile(k, own, "fly_up_bias", 1, HID3)

        @block.sync
        def _(sp):
            sp.dma_start(fw[:], dram["l3f_up"].partition_broadcast(P)).then_inc(s["loaded"], 16)
            sp.dma_start(y[:, 0, 0, :], dram["l3f_exp"]).then_inc(s["loaded"], 16)
            sp.dma_start(y[:, 0, 1, :], dram["l3f_b_exp"].partition_broadcast(P)).then_inc(s["loaded"], 16)
            sp.dma_start(ub[:], dram["l3f_up_bias"]).then_inc(s["loaded"], 16)
            sp.wait_ge(s["up_done"], 1)
            sp.dma_start(fw[:], dram["l3f_down"].partition_broadcast(P)).then_inc(s["down_loaded"], 16)
            sp.dma_start(y[:, 0, 0, :], dram["l3f_con"]).then_inc(s["down_loaded"], 16)

        @block.vector
        def _(vec):
            step = Steps(vec, s["vector_step"])

            def stages(order, rows, flipped):
                at = 0
                for stage in order:
                    st = 2 ** stage
                    nb = HID3 // (2 * st)
                    shape = (P, rows, nb, st)
                    old, new = (y[:, i, 0:rows, :].rearrange("p r (b two s) -> p r b two s", two=2, s=st) for i in (at, 1 - at))
                    wq = fw[:, stage, :].rearrange("p (b s q) -> p b s q", s=st, q=4)
                    tt = [t[:, i, 0:rows, :].rearrange("p r (b s) -> p r b s", s=st) for i in range(4)]
                    for i in range(4):
                        q = (i % 2) * 2 + i // 2 if flipped else i
                        for r in range(rows):
                            step(nc.vector.tensor_tensor(tt[i][:, r], old[:, r, :, i % 2, :], wq[:, :, :, q], MUL))
                    for i in range(2):
                        for r in range(rows):
                            step(nc.vector.tensor_tensor(new[:, r, :, i, :], tt[2 * i][:, r], tt[2 * i + 1][:, r], ADD))
                    at = 1 - at
                return at

            vec.wait_ge(s["loaded"], 64)
            at = stages(range(STAGES), 2, False)
            step(nc.vector.tensor_copy(up_w[:], y[:, at, 0, :]))
            step(nc.vector.tensor_tensor(ub[:], ub[:], y[0:1, at, 1, :], ADD), s["up_done"])
            vec.wait_ge(s["b_psum"], 1)
            step(nc.vector.tensor_copy(up_b[:], ps[:, 0, 0:4]))
            vec.wait_ge(s["down_loaded"], 32)
            at = stages(reversed(range(STAGES)), 1, True)
            step(nc.vector.tensor_copy(y[:, at, 1, :], y[:, at, 0, :]), s["done"])
            vec.wait_ge(s["w_psum"], 1)
            step(nc.vector.tensor_copy(down_w[:].rearrange("p c d -> p (c d)"), ps[:, 1, :]))

        @block.tensor
        def _(pe):
            pe.wait_ge(s["up_done"], 1)
            for c in range(4):
                last = nc.tensor.transpose(ps[:, 0, c:c + 1], ub[:, c * P:(c + 1) * P], k.ident[0:1, 0:1])
            last.then_inc(s["b_psum"], 1)
            pe.wait_ge(s["done"], 1)
            for c in range(4):
                last = nc.tensor.transpose(ps[:, 1, c * P:(c + 1) * P], y[:, STAGES % 2, 1, c * P:(c + 1) * P], k.ident)
            last.then_inc(s["w_psum"], 1)


def l3_ffn(k, phase, up_w, up_b, down_w, rowv, store):
    nc, ps = k.nc, k.ps
    s = k.signals(phase, "l3f", *NORM, "hidden_psum", "hidden_ready", "z_psum", "residual", "stored")
    with ExitStack() as own, nc.Block() as block:
        norm_tiles(k, own)
        hid = tile(k, own, "l3f_hidden", P, 4, GT)

        @block.vector
        def _(vec):
            step = Steps(vec, s["vector_step"])
            norm_vector(k, vec, step, s)
            step(nc.vector.tensor_tensor(k.xg[:], k.xg[:], over(rowv["l3f_bd"].unsqueeze(1), (P, T, D)), ADD))
            add_projection(k, vec, step, s, rowv["l3f_bc"])

        @block.scalar
        def _(act):
            step = Steps(act, s["scalar_step"])
            norm_scalar(k, act, step, s)
            for c in range(4):
                act.wait_ge(s["hidden_psum"], c + 1)
                step(nc.scalar.activation(hid[:, c, :], ps[:, 1 + c, :], ACT.Gelu, bias=up_b[:, c:c + 1]), s["hidden_ready"])

        @block.tensor
        def _(pe):
            norm_tensor(k, pe, s)
            pe.wait_ge(s["xt_ready"], 1)
            for c in range(4):
                nc.tensor.matmul(ps[:, 1 + c, :], up_w[:, c * P:(c + 1) * P], k.xt[:], start=True, stop=True).then_inc(s["hidden_psum"], 1)
            pe.wait_ge(s["hidden_ready"], 4)
            for t in range(T):
                for c in range(4):
                    last = nc.tensor.matmul(ps[:, 5, t * D:(t + 1) * D], hid[:, c, t * P:(t + 1) * P], down_w[:, c, :], start=c == 0, stop=c == 3)
            last.then_inc(s["z_psum"], 1)

        @block.sync
        def _(sp):
            sp.wait_ge(s["residual"], 1)
            sp.dma_start(store, k.xg[:]).then_inc(s["stored"], 16)
            sp.wait_ge(s["stored"], 16)
            sp.wait_ge(k.next_loaded, 16 * 6)


def phase_e(k, dram, groups, layers):
    nc = k.nc
    with ExitStack() as phase:
        wp = tile(k, phase, "e_weights", P, len(E_MATS), D)
        rp = tile(k, phase, "e_rows", P, len(E_ROWS), D)
        cp = tile(k, phase, "e_cols", P, len(E_COLS))
        up_w, up_b, down_w = tile(k, phase, "e_up_w", P, HID3), tile(k, phase, "e_up_b", P, 4), tile(k, phase, "e_down_w", P, 4, D)
        w = {n: wp[:, i, :] for i, n in enumerate(E_MATS)}
        rowv = {n: rp[:, i, :] for i, n in enumerate(E_ROWS)}
        colv = {n: cp[:, i:i + 1] for i, n in enumerate(E_COLS)}
        k.ctxt = tile(k, phase, "e_ctx_t", P, GB, S2)
        k.maski = tile(k, phase, "e_mask", P, GB, S2, dtype=I32)
        mask_group = lambda g: dram["mask_i32"].rearrange("q (g b s) -> g q b s", g=GROUPS, b=GB)[g]
        loaded = k.flag(phase, "e_weights_loaded")
        k.first_loaded = k.flag(phase, "e_first_loaded")
        with nc.Block() as block:
            @block.sync
            def _(sp):
                for dst, name in ((wp, "e_mats"), (cp, "e_cols")):
                    sp.dma_start(dst[:], dram[name]).then_inc(loaded, 16)
                sp.dma_start(rp[:], dram["e_rows"].partition_broadcast(P)).then_inc(loaded, 16)
                sp.wait_ge(loaded, 48)
        butterflies(k, phase, dram, up_w, up_b, down_w)
        with nc.Block() as block:
            @block.sync
            def _(sp):
                sp.dma_start(k.x_next[:], token_group(dram["x_d"], 0)).then_inc(k.first_loaded, 16)
                sp.dma_start(k.ctxt[:], context_group(dram, 0)[0]).then_inc(k.first_loaded, 16)
                for h in range(4):
                    sp.dma_start(k.maski[L * h:L * h + L, :, :], mask_group(0)).then_inc(k.first_loaded, 16)
                sp.wait_ge(k.first_loaded, 96)
        k.maskf = tile(k, phase, "e_mask_added", P, GB, S2)
        k.clear_signals()
        with nc.Fori(0, groups) as g:
            k.next_loaded = k.flag(phase, "e_next_loaded")
            after = (g + 1) % GROUPS
            k.x_in = k.x_next
            l3_xattn(k, phase, w, rowv, colv, token_group(dram["x_d"], after), context_group(dram, after)[0], mask_group(after))
            k.x_in = k.xg
            if "l3a" in layers:
                self_attn(k, phase, "l3a", w["l3a_q"], w["l3a_k"], w["l3a_v"], w["l3a_p"], DH ** -0.5)
            if "l3f" in layers:
                l3_ffn(k, phase, up_w, up_b, down_w, rowv, token_group(dram["out"], g))
            else:
                store_group(k, phase, token_group(dram["out"], g))
            k.clear_signals()


def store_group(k, phase, store):
    s = k.signals(phase, "store", "stored")
    with k.nc.Block() as block:
        @block.sync
        def _(sp):
            sp.dma_start(store, k.xg[:]).then_inc(s["stored"], 16)
            sp.wait_ge(s["stored"], 16)
            sp.wait_ge(k.next_loaded, 16 * 6)
A_MATS = ["l0x_q", "l0x_k", "l0x_v", "l0x_c", "l0a_q", "l0a_k", "l0a_v", "l0a_o", "l1x_q", "l1x_k", "l1x_v", "l1x_o",
          "l1a_q", "l1a_k", "l1a_v", "l1a_p"]
A_ROWS = ["l0a_bv", "l0a_bo", "l1x_bk", "l1x_bv", "l1x_bo", "l1x_g", "l1x_b", "l1a_bp"]
A_COLS = ["l0a_bq", "l0a_bk", "l1x_bq", "l1x_bk", "l1a_w0", "l1a_w1", "l1a_w2", "l1a_bc"]
C_MATS = ["l2a_q", "l2a_k", "l2a_v", "l2a_u"]
C_ROWS = ["l2x_bl", "l2a_bu"]
C_COLS = ["l2x_wcq", "l2x_wq", "l2x_wc"]
E_MATS = ["l3x_q", "l3x_o", "l3a_q", "l3a_k", "l3a_v", "l3a_p"]
E_ROWS = ["l3x_bo", "l3f_bc", "l3f_bd"]
E_COLS = ["l3x_bq"]
CONSTS = {"ident": P, "same_head": P, "v_heads": P, "earlier": P, "causal": L, "quad_head": 4, "tile_batch": 4, "countdown": E0,
          "count4": CAP0, "row_base": T, "fold": L, "quad_cols": P, "ones": P, "same_batch": P}


def constants():
    p = np.arange(P)[:, None]
    c = np.arange(P)[None, :]
    made = {
        "ident": p == c,
        "same_head": p // DH == c // DH,
        "v_heads": p // L == (c // DH) % 4,
        "earlier": (p // L == c // L) & (p < c),
        "causal": np.where(p % L > np.arange(L)[None, :], NEG, 0.0),
        "quad_head": (p // DH) % 4 == np.arange(4)[None, :],
        "tile_batch": p // L == np.arange(4)[None, :],
        "countdown": np.broadcast_to(E0 - np.arange(E0)[None, :], (P, E0)),
        "count4": np.broadcast_to(np.arange(CAP0)[None, :], (P, CAP0)),
        "row_base": (np.arange(T)[None, :] * BPT + p // L) * S2,
        "quad_cols": p == c // L,
        "ones": np.ones((P, P)),
        "same_batch": p // L == c // L,
        "fold": p % L == np.arange(L)[None, :],
    }
    return np.concatenate([made[n].astype(np.float32) for n in CONSTS], axis=1)


def layout(i):
    st = lambda a: np.ascontiguousarray(a)
    ctx = i["ctx_1024"].reshape(NB * S2, D)
    with_one = np.concatenate([i["ctx_1024"], np.ones((NB, S2, 1), np.float32)], axis=2)
    wkv = i["L0_xattn_Wkv"]
    w5 = i["L1_attn_w_qkv"]
    def by_head(a):
        out = np.zeros((H, DH, H, DH), np.float32)
        for h in range(H):
            out[h, :, h, :] = a.T
        return out.reshape(D, D)

    def by_place(a):
        return a.reshape(-1, 4, 4, DH).transpose(0, 2, 1, 3).reshape(-1, D)

    wa = i["L3_attn_w_attn"]
    mats = {"l3x_q": i["L3_xattn_Wq"].T, "l3x_o": i["L3_xattn_Wo"].T, "l3a_q": wa[:D].T, "l3a_k": wa[D:2 * D].T, "l3a_v": by_place(wa[2 * D:].T),
            "l3a_p": by_place(i["L3_attn_w_proj"]).T,
            "l2a_q": by_head(i["L2_attn_Wq"]), "l2a_k": by_head(i["L2_attn_Wk"]), "l2a_v": by_place(by_head(i["L2_attn_Wv"])), "l2a_u": by_place(i["L2_attn_Wu"]).T,
            "l0x_q": i["L0_xattn_Wq"].T, "l0x_k": np.tile(wkv[:DH].T, (1, H)), "l0x_v": by_place(np.tile(wkv[DH:].T, (1, H))), "l0x_c": by_place(i["L0_xattn_Wc"]).T,
            "l0a_q": i["L0_attn_Wq"], "l0a_k": i["L0_attn_Wk"], "l0a_v": i["L0_attn_Wv"], "l0a_o": i["L0_attn_Wo"],
            "l1x_q": i["L1_xattn_wq_w"].T, "l1x_k": i["L1_xattn_wk_w"].T, "l1x_v": i["L1_xattn_wv_w"].T, "l1x_o": i["L1_xattn_wo_w"].T,
            "l1a_q": w5[:D].T, "l1a_k": w5[D:2 * D].T, "l1a_v": w5[2 * D:].T, "l1a_p": i["L1_attn_w_proj"].T}
    rows = {"l3x_bo": i["L3_xattn_bo"], "l3f_bc": i["L3_ffn_b_con"], "l3f_bd": i["L3_ffn_down_bias"],
            "l2x_bl": i["L2_xattn_b_l"], "l2a_bu": i["L2_attn_bu"],
            "l0a_bv": i["L0_attn_bv"], "l0a_bo": i["L0_attn_bo"], "l1x_bk": i["L1_xattn_wk_b"], "l1x_bv": i["L1_xattn_wv_b"],
            "l1x_bo": i["L1_xattn_wo_b"], "l1x_g": i["L1_xattn_ln_g"], "l1x_b": i["L1_xattn_ln_b"], "l1a_bp": i["L1_attn_b_proj"]}
    cols = {"l3x_bq": i["L3_xattn_bq"],
            "l2x_wcq": i["L2_xattn_w_cq"], "l2x_wq": i["L2_xattn_w_q"], "l2x_wc": i["L2_xattn_w_c"],
            "l0a_bq": i["L0_attn_bq"], "l0a_bk": i["L0_attn_bk"], "l1x_bq": i["L1_xattn_wq_b"], "l1x_bk": i["L1_xattn_wk_b"],
            "l1a_w0": i["L1_attn_w_dwc"][:, 0], "l1a_w1": i["L1_attn_w_dwc"][:, 1], "l1a_w2": i["L1_attn_w_dwc"][:, 2], "l1a_bc": i["L1_attn_b_dwc"]}
    return {
        "x": st(i["x"].reshape(TOKENS, D)), "ctx": st(ctx), "ctx_t": st(ctx.T),
        "mask_bool": st(i["mask_Bx1xSxS2_bf0"].reshape(TOKENS, S2)),
        "ctx_rows": st(with_one[:, :2 * P].reshape(NB, 2, P, D + 1).transpose(2, 0, 1, 3)), "ctx_last": st(with_one[None, :, 2 * P]),
        "consts": constants(),
        "a_mats": st(np.stack([mats[n] for n in A_MATS], axis=1)),
        "a_rows": st(np.stack([rows[n] for n in A_ROWS])),
        "a_cols": st(np.stack([cols[n] for n in A_COLS], axis=1)),
        "c_mats": st(np.stack([mats[n] for n in C_MATS], axis=1)),
        "c_rows": st(np.stack([rows[n] for n in C_ROWS])),
        "c_cols": st(np.stack([cols[n] for n in C_COLS], axis=1)),
        "l2x_l": st(i["L2_xattn_W_l"].reshape(D, 4, D).transpose(2, 1, 0).reshape(D, 4 * D)),
        "l2x_biases": st(np.stack([i["L2_xattn_b_c"], i["L2_xattn_b_q"], i["L2_xattn_b_cq"]])),
        "l1f_w1": st(i["L1_ffn_W1"].transpose(2, 0, 1, 3)), "l1f_w2": st(i["L1_ffn_W2"].transpose(2, 0, 1, 3)),
        "l1f_b1": st(i["L1_ffn_b1"].reshape(E1 * S1, P).T), "l1f_b2": st(i["L1_ffn_b2"].reshape(E1, D)),
        "e_mats": st(np.stack([mats[n] for n in E_MATS], axis=1)),
        "e_rows": st(np.stack([rows[n] for n in E_ROWS])),
        "e_cols": st(np.stack([cols[n] for n in E_COLS], axis=1)),
        "mask_i32": st(i["mask_Bx1xSxS2_if1"].reshape(NB, L, S2).transpose(1, 0, 2).reshape(L, NB * S2)),
        "l3f_up": st(i["L3_ffn_up_weights"].reshape(STAGES, 2 * HID3)), "l3f_down": st(i["L3_ffn_down_weights"].reshape(STAGES, 2 * HID3)),
        "l3f_exp": st(i["L3_ffn_W_exp"]), "l3f_b_exp": st(i["L3_ffn_b_exp"]), "l3f_up_bias": st(i["L3_ffn_up_bias"].reshape(1, HID3)),
        "l3f_con": st(i["L3_ffn_W_con"].T),
        "l2f_up": st(i["L2_ffn_w_up"].reshape(CH2, P, D).transpose(1, 0, 2).reshape(P, I2)),
        "l2f_gate": st(i["L2_ffn_w_gate"].reshape(CH2, P, D).transpose(1, 0, 2).reshape(P, I2)), "l2f_down": st(i["L2_ffn_w_down"]),
        "l0f_g": st(i["L0_ffn_Wg"]), "l1f_r": st(i["L1_ffn_Wr"].T),
        "l0f_w1": st(i["L0_ffn_W1"].transpose(1, 0, 2)),
        "l0f_w2": st(i["L0_ffn_W2"].reshape(E0, 4, P, D).transpose(2, 0, 1, 3)),
    }


LAYERS = ("l0x", "l0a", "l0f", "l1x", "l1a", "l1f", "l2x", "l2a", "l3x", "l3a", "l3f")
SCRATCH = {"x_a": (TOKENS, D), "xn_a": (TOKENS, D), "logits": (E1, TOKENS), **{f"sums_{j}": (TOKENS, D) for j in range(PER)},
           "x_c": (TOKENS, D), "xt_c": (P, TOKENS), "x_d": (TOKENS, D)}


def build(nc, dram, groups=GROUPS, layers=LAYERS, phases="ABCDE"):
    k = Kit(nc)
    with ExitStack() as whole:
        consts = tile(k, whole, "const_tiles", P, sum(CONSTS.values()))
        ends = np.cumsum(list(CONSTS.values())).tolist()
        (k.ident, k.same_head, k.v_heads, k.earlier, k.causal, k.quad_head, k.tile_batch, k.countdown,
         k.count4, k.row_base, k.fold, k.quad_cols, k.ones, k.same_batch) = (consts[:, end - n:end] for end, n in zip(ends, CONSTS.values()))
        k.xg = tile(k, whole, "x_group", P, T, D)
        k.x_next = tile(k, whole, "x_group_next", P, T, D)
        k.x_in = k.xg
        k.xn = tile(k, whole, "xn_group", P, T, D)
        k.xt = tile(k, whole, "xn_group_t", P, GT)
        k.ps = whole.enter_context(nc.psum_tensor("ps", [P, 8, 512], F32))
        got = k.flag(whole, "consts_loaded")
        with nc.Block() as block:
            @block.sync
            def _(sp):
                sp.dma_start(consts[:], dram["consts"]).then_inc(got, 16)
                sp.wait_ge(got, 16)
        largest = tile(k, whole, "largest", P, 1)
        if "A" in phases:
            phase_a(k, dram, groups, layers)
        if "B" in phases:
            phase_b(k, dram)
        if "C" in phases:
            phase_c(k, dram, groups, layers, largest[:])
        if "D" in phases:
            phase_d(k, dram, groups, largest[:])
        if "E" in phases:
            phase_e(k, dram, groups, layers)


def kernel(**inputs):
    import numpy as np
    import concourse.bacc as bacc
    from concourse.bass_utils import run_bass_kernel_spmd

    nc = bacc.Bacc("TRN2", target_bir_lowering=False, num_devices=1)
    arrays = layout({n: np.asarray(a) for n, a in inputs.items()})
    dram = {n: nc.dram_tensor("in_" + n, a.shape, mybir.dt.from_np(a.dtype), kind="ExternalInput").ap() for n, a in arrays.items()}
    dram.update({n: nc.dram_tensor("scratch_" + n, shape, F32, kind="Internal").ap() for n, shape in SCRATCH.items()})
    dram["out"] = nc.dram_tensor("out_x", (TOKENS, D), F32, kind="ExternalOutput").ap()
    build(nc, dram)
    r = run_bass_kernel_spmd(nc, [{"in_" + n: a for n, a in arrays.items()}], core_ids=[0])
    return r.results[0]["out_x"].reshape(NB, L, D)
```

```python
import concourse.bass as bass
from concourse import mybir
from concourse.alu_op_type import AluOpType as ALU
from contextlib import ExitStack
import numpy as np

P = 128
D = 128
NB = 128
L = 32
S2 = 257
TOKENS = NB * L
T = 4
GT = T * P
GB = GT // L
GROUPS = TOKENS // GT
BPT = P // L
H, DH = 16, 8
HC = H // 4
E0, HID0 = 8, 512
PAIRS0 = E0 // 2
CAP0 = L // E0
WINDOW = 128
E1, S1 = 48, 4
CAP1 = int(1.5 * TOKENS / E1)
KW = D // S1
I2 = 384
HID3, STAGES = 512, 9
NEG = -1e30
LOWEST = -3.0e38

F32 = mybir.dt.float32
I32 = mybir.dt.int32
U32 = mybir.dt.uint32
U8 = mybir.dt.uint8
ACT = mybir.ActivationFunctionType
X = mybir.AxisListType.X
MUL, ADD, SUB, MAX, MIN, EQ = ALU.mult, ALU.add, ALU.subtract, ALU.max, ALU.min, ALU.is_equal


class Steps:

    def __init__(self, engine, own):
        self.engine, self.own, self.counts = engine, own, {}

    def __call__(self, instruction, signal=None):
        signal = self.own if signal is None else signal
        n = self.counts[id(signal)] = self.counts.get(id(signal), 0) + 1
        instruction.then_inc(signal, 1)
        self.engine.wait_ge(signal, n)

    def free(self, instruction, signal=None):
        signal = self.own if signal is None else signal
        self.counts[id(signal)] = self.counts.get(id(signal), 0) + 1
        instruction.then_inc(signal, 1)

    def settled(self, signal=None):
        signal = self.own if signal is None else signal
        self.engine.wait_ge(signal, self.counts[id(signal)])


class Kit:

    def __init__(self, nc):
        self.nc = nc
        self.numbers = []
        self.tiles = 0

    def signals(self, stack, layer, *names):
        sems = {n: stack.enter_context(self.nc.semaphore(f"{layer}_{n}"))
                for n in ("vector_step", "scalar_step", "pool_step") + names}
        self.numbers += [sem.num for sem in sems.values()]
        return sems

    def flag(self, stack, name):
        sem = stack.enter_context(self.nc.semaphore(name))
        self.numbers.append(sem.num)
        return sem

    def clear_signals(self):
        ids = sorted(self.numbers)
        firsts = [n for n in ids if n - 1 not in ids]
        lasts = [n for n in ids if n + 1 not in ids]
        self.nc.all_engine_barrier()
        for lo, hi in zip(firsts, lasts):
            self.nc.gpsimd.dma_reset(range(lo, hi + 1))
            self.nc.gpsimd.sem_clear(range(lo, hi + 1))
        self.nc.all_engine_barrier()
        self.numbers = []


def tile(k, stack, name, *shape, dtype=F32):
    k.tiles += 1
    return stack.enter_context(k.nc.sbuf_tensor(f"{name}_{k.tiles}", list(shape), dtype))


def over(ap, shape):
    return ap.broadcast_to(list(shape))


NORM = ("xn_ready", "xt_psum", "xt_ready")


def normalise(k, step, x, out, signal=None, parts_known=False):
    nc = k.nc
    rstd, half, var = k.stat[:, 0, :], k.stat[:, 1, :], k.mv[:, :, 1]
    if not parts_known:
        for t in range(T):
            step.free(nc.vector.bn_stats(k.parts[:, t, :], x[:, t, :]))
        step.settled()
    for t in range(T):
        step.free(nc.vector.bn_aggr(k.mv[:, t, :], k.parts[:, t, :]))
    step.settled()
    step(nc.vector.tensor_scalar(var, var, 1e-5, None, ADD))
    step(nc.vector.tensor_scalar(half.bitcast(I32), var.bitcast(I32), 1, None, ALU.logical_shift_right))
    step(nc.vector.tensor_scalar(rstd.bitcast(I32), half.bitcast(I32), -1.0, float(0x5F3759DF), MUL, ADD))
    for _ in range(3):
        step(nc.vector.tensor_tensor(half, rstd, rstd, MUL))
        step(nc.vector.scalar_tensor_tensor(half, half, -0.5, var, MUL, MUL))
        step(nc.vector.scalar_tensor_tensor(rstd, half, 1.5, rstd, ADD, MUL))
    for t in range(T):
        step.free(nc.vector.tensor_scalar(out[:, t, :], x[:, t, :], k.mv[:, t, 0:1], rstd[:, t:t + 1], SUB, MUL), signal)
    step.settled(signal)


def norm_vector(k, vec, step, s):
    normalise(k, step, k.x_in[:], k.xn[:], s["xn_ready"], k.parts_known)
    k.parts_known = False


def norm_tensor(k, pe, s, bank=0):
    for t in range(T):
        pe.wait_ge(s["xn_ready"], t + 1)
        last = k.nc.tensor.transpose(k.ps[:, bank, t * P:(t + 1) * P], k.xn[:, t, :], k.ident)
    last.then_inc(s["xt_psum"], 1)


def norm_scalar(k, act, step, s, bank=0):
    act.wait_ge(s["xt_psum"], 1)
    step(k.nc.scalar.activation(k.xt[:], k.ps[:, bank, :], ACT.Copy), s["xt_ready"])


CORE = ("qx_ready", "k_psum", "k_ready", "q_psum", "rep_ready", "v_psum", "vx_ready", "scores", "max_ready", "shifted",
        "exps", "sums_ready", "p_ready", "pt_ready", "o_psum", "o_ready", "z_psum", "residual")
CORE_BANKS = (0, 1, 2, 3)
CHUNK = 4
NCHUNK = GB // CHUNK


def core_tiles(k, stack):
    k.qx = tile(k, stack, "q_by_head", P, GB, 4, L)
    k.kt = tile(k, stack, "k_t", P, GT)
    k.rep = tile(k, stack, "source_four_times", P, GB, 4, L)
    k.vx = tile(k, stack, "v_by_head", P, GB, D)
    k.st = tile(k, stack, "scores_masked", P, NCHUNK, CHUNK * 4, L)
    k.pr = tile(k, stack, "probabilities", P, NCHUNK, CHUNK * 4, L)
    k.pt = tile(k, stack, "probabilities_t", P, GB, 4, L)
    k.mx = tile(k, stack, "row_max", P, NCHUNK, CHUNK * 4)
    k.rs = tile(k, stack, "row_sum", P, NCHUNK, CHUNK * 4)
    k.ot = tile(k, stack, "o_t", P, GT)


def core_tensor(k, pe, s, wv, wo, q_bank=1):
    nc, ps = k.nc, k.ps
    pe.wait_ge(s["rep_ready"], 1)
    for b in range(GB):
        last = nc.tensor.matmul(ps[:, 4 + b // 4, (b % 4) * D:(b % 4 + 1) * D], k.rep[:, b, :, :].rearrange("p a b -> p (a b)"),
                                wv, start=True, stop=True)
    last.then_inc(s["v_psum"], 1)
    pe.wait_ge(s["qx_ready"], 4)
    pe.wait_ge(s["k_ready"], 1)
    for n in range(NCHUNK):
        for b in range(CHUNK * n, CHUNK * n + CHUNK):
            for c in range(HC):
                rows = slice(L * c, L * c + L)
                last = nc.tensor.matmul(ps[rows, n, (b % CHUNK) * P:(b % CHUNK + 1) * P], k.kt[rows, b * L:(b + 1) * L],
                                        k.qx[rows, b, :, :].rearrange("p a b -> p (a b)"), start=True, stop=True)
        last.then_inc(s["scores"], 1)
    pe.wait_ge(s["vx_ready"], HC)
    for n in range(NCHUNK):
        pe.wait_ge(s["pt_ready"], n + 1)
        for a in range(4):
            for b in range(CHUNK * n, CHUNK * n + CHUNK):
                last = nc.tensor.matmul(ps[L * a:L * a + L, 4, b * L:(b + 1) * L], k.vx[:, b, L * a:L * a + L],
                                        k.pt[:, b, a, :], start=True, stop=True)
    last.then_inc(s["o_psum"], 1)
    project(k, pe, s, wo, CORE_BANKS)


def project(k, pe, s, wo, banks):
    pe.wait_ge(s["o_ready"], 1)
    for t in range(T):
        k.nc.tensor.matmul(k.ps[:, banks[t], 0:D], k.ot[:, t * P:(t + 1) * P], wo, start=True, stop=True).then_inc(s["z_psum"], 1)


def q_by_head(k, vec, step, s, source=None, bias=None):
    nc = k.nc
    if source is None:
        vec.wait_ge(s["q_psum"], 1)
        source = k.ps[:, 1, :]
    q = source.rearrange("p (b n) -> p b n", n=L)
    for h in range(4):
        if bias is None:
            step(nc.vector.tensor_scalar(k.qx[:, :, h, :], q, k.quad_head[:, h:h + 1], None, MUL), s["qx_ready"])
        else:
            step(nc.vector.tensor_scalar(k.qx[:, :, h, :], q, bias, k.quad_head[:, h:h + 1], ADD, MUL), s["qx_ready"])


def v_by_head(k, act, step, s):
    act.wait_ge(s["v_psum"], 1)
    for c in range(HC):
        step.free(k.nc.scalar.activation(k.vx[:].rearrange("p b (a c d) -> p c b a d", a=4, c=HC)[:, c],
                                         k.ps[:, 4:8, :].rearrange("p n (b a c d) -> p c (n b) a d", a=4, c=HC, d=DH)[:, c],
                                         ACT.Copy, scale=k.tile_batch[:, c:c + 1]), s["vx_ready"])
    step.settled(s["vx_ready"])


def core_vector(k, vec, step, s, scale, causal, bias=None):
    nc = k.nc
    for n in range(NCHUNK):
        vec.wait_ge(s["scores"], n + 1)
        sc, pr = k.ps[:, n, :], k.pr[:, n, :, :]
        if causal:
            step(nc.vector.scalar_tensor_tensor(k.st[:, n, :, :], sc.rearrange("p (m q) -> p m q", q=L), scale,
                                                over(k.causal.unsqueeze(1), (P, CHUNK * 4, L)), MUL, ADD))
            sc = k.st[:, n, :, :].rearrange("p m q -> p (m q)")
        step(nc.vector.transpose(pr.rearrange("p m q -> p (m q)"), sc))
        step.free(nc.vector.reduce_max(k.mx[:, n, :], pr, X), s["max_ready"])

    def turn(n):
        vec.wait_ge(s["p_ready"], n + 1)
        step(nc.vector.transpose(k.pt[:, CHUNK * n:CHUNK * n + CHUNK, :, :].rearrange("p b a q -> p (b a q)"),
                                 k.pr[:, n, :, :].rearrange("p m q -> p (m q)")), s["pt_ready"])

    for n in range(NCHUNK):
        vec.wait_ge(s["exps"], n + 1)
        step(nc.vector.reduce_sum(k.rs[:, n, :], k.pr[:, n, :, :], X))
        step(nc.vector.reciprocal(k.rs[:, n, :], k.rs[:, n, :]), s["sums_ready"])
        if n > 1:
            turn(n - 2)
    turn(NCHUNK - 2)
    turn(NCHUNK - 1)
    add_projection(k, vec, step, s, CORE_BANKS, bias)


def core_pool(k, pool, s):
    for n in range(NCHUNK):
        pool.wait_ge(s["max_ready"], n + 1)
        pr = k.pr[:, n, :, :]
        k.nc.gpsimd.tensor_tensor(pr, pr, over(k.mx[:, n, :].unsqueeze(2), (P, CHUNK * 4, L)), SUB).then_inc(s["shifted"], 1)
    for n in range(NCHUNK):
        pool.wait_ge(s["sums_ready"], n + 1)
        pr = k.pr[:, n, :, :]
        k.nc.gpsimd.tensor_tensor(pr, pr, over(k.rs[:, n, :].unsqueeze(2), (P, CHUNK * 4, L)), MUL).then_inc(s["p_ready"], 1)


def add_projection(k, vec, step, s, banks, bias=None, parts=True):
    nc, x = k.nc, k.x_in
    if bias is not None:
        step(nc.vector.tensor_tensor(k.xg[:], x[:], over(bias.unsqueeze(1), (P, T, D)), ADD))
        x = k.xg

    def part(t):
        vec.wait_ge(s["residual"], t + 1)
        if parts:
            step.free(nc.vector.bn_stats(k.parts[:, t, :], k.xg[:, t, :]))

    for t in range(T):
        vec.wait_ge(s["z_psum"], t + 1)
        step.free(nc.vector.tensor_tensor(k.xg[:, t, :], x[:, t, :], k.ps[:, banks[t], 0:D], ADD), s["residual"])
        if t > 0:
            part(t - 1)
    part(T - 1)
    step.settled()
    k.parts_known = parts


def core_scalar(k, act, step, s, scale, causal):
    nc = k.nc
    for n in range(NCHUNK):
        act.wait_ge(s["shifted"], n + 1)
        step(nc.scalar.activation(k.pr[:, n, :, :], k.pr[:, n, :, :], ACT.Exp, scale=1.0 if causal else scale), s["exps"])
    act.wait_ge(s["o_psum"], 1)
    step(nc.scalar.activation(k.ot[:], k.ps[:, 4, :], ACT.Copy), s["o_ready"])


def four_times(k, source):
    return over(source.rearrange("p (b n) -> p b n", n=L).unsqueeze(2), (P, GB, 4, L))


def l0_xattn(k, phase, w, ctx_rows, next_x, next_ctxt):
    nc, ps = k.nc, k.ps
    s = k.signals(phase, "l0x", *NORM, *CORE, "qt_ready", "found_scores", "rows_found", "rows_loaded", "mem_psum", "mem_ready")
    with ExitStack() as own, nc.Block() as block:
        core_tiles(k, own)
        qt = tile(k, own, "l0x_qt", P, GT)
        best = tile(k, own, "best", P, T, 8)
        best_at = tile(k, own, "best_at", P, T, 8, dtype=U32)
        rows = tile(k, own, "rows", P, T, dtype=I32)
        mem = tile(k, own, "mem", P, T, D)
        mt = tile(k, own, "mem_t", P, GT)

        @block.vector
        def _(vec):
            step = Steps(vec, s["vector_step"])
            norm_vector(k, vec, step, s)
            for t in range(T):
                vec.wait_ge(s["found_scores"], t + 1)
                step(nc.vector.max(best[:, t, :], ps[:, 4 + t, 0:S2]))
                step(nc.vector.max_index(best_at[:, t, :], best[:, t, :], ps[:, 4 + t, 0:S2]))
                step(nc.vector.tensor_tensor(rows[:, t:t + 1], best_at[:, t, 0:1], k.row_base[:, t:t + 1], ADD), s["rows_found"])
            step(nc.vector.tensor_scalar(k.row_base, k.row_base, float(GB * S2), None, ADD))
            vec.wait_ge(s["qt_ready"], 1)
            q_by_head(k, vec, step, s, source=qt[:])
            core_vector(k, vec, step, s, DH ** -0.5, False)

        @block.sync
        def _(sp):
            sp.wait_ge(s["found_scores"], T)
            sp.dma_start(k.ctxt[:], next_ctxt).then_inc(k.ctxt_loaded, 16)
            sp.wait_ge(s["residual"], T)
            sp.dma_start(k.x_next[:], next_x).then_inc(k.x_loaded, 16)

        @block.gpsimd
        def _(pool):
            for t in range(T):
                pool.wait_ge(s["rows_found"], t + 1)
                nc.gpsimd.indirect_dma_start(out=mem[:, t, :], out_offset=None, in_=ctx_rows,
                                             in_offset=bass.IndirectOffsetOnAxis(ap=rows[:, t:t + 1], axis=0)).then_inc(s["rows_loaded"], 16)
            pool.wait_ge(s["rows_loaded"], 16 * T)
            core_pool(k, pool, s)

        @block.scalar
        def _(act):
            step = Steps(act, s["scalar_step"])
            norm_scalar(k, act, step, s)
            act.wait_ge(s["q_psum"], 1)
            step(nc.scalar.activation(qt[:], ps[:, 1, :], ACT.Copy), s["qt_ready"])
            act.wait_ge(s["mem_psum"], 1)
            step(nc.scalar.activation(mt[:], ps[:, 2, :], ACT.Copy), s["mem_ready"])
            step(nc.scalar.activation(k.rep[:], four_times(k, ps[:, 2, :]), ACT.Copy), s["rep_ready"])
            act.wait_ge(s["k_psum"], 1)
            step(nc.scalar.activation(k.kt[:], ps[:, 3, :], ACT.Copy), s["k_ready"])
            v_by_head(k, act, step, s)
            core_scalar(k, act, step, s, DH ** -0.5, False)

        @block.tensor
        def _(pe):
            norm_tensor(k, pe, s)
            pe.wait_ge(s["xt_ready"], 1)
            nc.tensor.matmul(ps[:, 1, :], w["l0x_q"], k.xt[:], start=True, stop=True).then_inc(s["q_psum"], 1)
            pe.wait_ge(s["qt_ready"], 1)
            for t in range(T):
                for j in range(BPT):
                    b = t * BPT + j
                    last = nc.tensor.matmul(ps[L * j:L * j + L, 4 + t, 0:S2], qt[:, b * L:(b + 1) * L], k.ctxt[:, b, :], start=True, stop=True)
                last.then_inc(s["found_scores"], 1)
            pe.wait_ge(s["rows_loaded"], 16 * T)
            for t in range(T):
                last = nc.tensor.transpose(ps[:, 2, t * P:(t + 1) * P], mem[:, t, :], k.ident)
            last.then_inc(s["mem_psum"], 1)
            pe.wait_ge(s["mem_ready"], 1)
            nc.tensor.matmul(ps[:, 3, :], w["l0x_k"], mt[:], start=True, stop=True).then_inc(s["k_psum"], 1)
            core_tensor(k, pe, s, w["l0x_v"], w["l0x_c"])


def l0_attn(k, phase, w, rowv, colv):
    nc, ps = k.nc, k.ps
    s = k.signals(phase, "l0a", *NORM, "q_psum", "k_psum", "v_psum", "q_ready", "k_ready", "v_ready", "scores", "shifted", "exps",
                  "pt_ready", "o_psum", "o_ready", "z_psum", "residual")
    scale = DH ** -0.5
    with ExitStack() as own, nc.Block() as block:
        qt, kt = tile(k, own, "l0a_qt", P, GT), tile(k, own, "l0a_kt", P, GT)
        v = tile(k, own, "l0a_v", P, T, D)
        pr, pt = tile(k, own, "l0a_p", P, T, L), tile(k, own, "l0a_pt", P, T, L)
        mx = tile(k, own, "l0a_mx", P, T)
        k.ot = tile(k, own, "l0a_ot", P, GT)

        @block.vector
        def _(vec):
            step = Steps(vec, s["vector_step"])
            norm_vector(k, vec, step, s)
            vec.wait_ge(s["v_psum"], 1)
            step(nc.vector.tensor_tensor(v[:], ps[:, 3, :].rearrange("p (t d) -> p t d", d=D), over(rowv["l0a_bv"].unsqueeze(1), (P, T, D)), ADD), s["v_ready"])
            vec.wait_ge(s["scores"], 1)
            sc = ps[:, 4, 0:T * L].rearrange("p (t j) -> p t j", j=L)
            step(nc.vector.reduce_max(mx[:], sc, X))
            step(nc.vector.tensor_tensor(pr[:], sc, over(mx[:].unsqueeze(2), (P, T, L)), SUB), s["shifted"])
            vec.wait_ge(s["exps"], 1)
            step(nc.vector.tensor_scalar(pr[:, :, L - 1:L], pr[:, :, L - 1:L], float(WINDOW - L + 1), None, MUL))
            step(nc.vector.reduce_sum(mx[:], pr[:], X))
            step(nc.vector.reciprocal(mx[:], mx[:]))
            step(nc.vector.tensor_tensor(pr[:], pr[:], over(mx[:].unsqueeze(2), (P, T, L)), MUL))
            step(nc.vector.transpose(pt[:], pr[:]), s["pt_ready"])
            add_projection(k, vec, step, s, (4, 5, 6, 7), rowv["l0a_bo"])

        @block.scalar
        def _(act):
            step = Steps(act, s["scalar_step"])
            norm_scalar(k, act, step, s)
            act.wait_ge(s["q_psum"], 1)
            step(nc.scalar.activation(qt[:], ps[:, 1, :], ACT.Identity, bias=colv["l0a_bq"]), s["q_ready"])
            act.wait_ge(s["k_psum"], 1)
            step(nc.scalar.activation(kt[:], ps[:, 2, :], ACT.Identity, bias=colv["l0a_bk"]), s["k_ready"])
            act.wait_ge(s["shifted"], 1)
            step(nc.scalar.activation(pr[:], pr[:], ACT.Exp, scale=scale), s["exps"])
            act.wait_ge(s["o_psum"], 1)
            step(nc.scalar.activation(k.ot[:].rearrange("p (t j n) -> p j t n", j=BPT, n=L),
                                      ps[:, 0:4, 0:T * L].rearrange("p j (t n) -> p j t n", n=L), ACT.Copy), s["o_ready"])

        @block.tensor
        def _(pe):
            norm_tensor(k, pe, s)
            pe.wait_ge(s["xt_ready"], 1)
            nc.tensor.matmul(ps[:, 1, :], w["l0a_q"], k.xt[:], start=True, stop=True).then_inc(s["q_psum"], 1)
            nc.tensor.matmul(ps[:, 2, :], w["l0a_k"], k.xt[:], start=True, stop=True).then_inc(s["k_psum"], 1)
            for t in range(T):
                last = nc.tensor.matmul(ps[:, 3, t * D:(t + 1) * D], k.xt[:, t * P:(t + 1) * P], w["l0a_v"], start=True, stop=True)
            last.then_inc(s["v_psum"], 1)
            pe.wait_ge(s["q_ready"], 1)
            pe.wait_ge(s["k_ready"], 1)
            for t in range(T):
                for j in range(BPT):
                    b = slice((t * BPT + j) * L, (t * BPT + j + 1) * L)
                    last = nc.tensor.matmul(ps[L * j:L * j + L, 4, t * L:(t + 1) * L], qt[:, b], kt[:, b], start=True, stop=True)
            last.then_inc(s["scores"], 1)
            pe.wait_ge(s["pt_ready"], 1)
            pe.wait_ge(s["v_ready"], 1)
            for t in range(T):
                for j in range(BPT):
                    r = slice(L * j, L * j + L)
                    last = nc.tensor.matmul(ps[:, j, t * L:(t + 1) * L], v[r, t, :], pt[r, t, :], start=True, stop=True)
            last.then_inc(s["o_psum"], 1)
            project(k, pe, s, w["l0a_o"], (4, 5, 6, 7))


def l0_ffn(k, phase, w):
    nc, ps = k.nc, k.ps
    s = k.signals(phase, "l0f", *NORM, "logits", "shifted", "exps", "chosen", "places", "dispatch_ready", "slots_psum", "slots_ready",
                  "hidden_psum", "hidden_ready", "turned", "turned_ready", "y_psum", "y_ready", "ypt_psum", "ypt_ready", "yt_psum", "yt_ready", "combine_ready", "z_psum", "residual")
    with ExitStack() as own, nc.Block() as block:
        lg = tile(k, own, "l0f_logits", P, T, E0)
        ex = tile(k, own, "l0f_exps", P, T, E0)
        hot = tile(k, own, "l0f_onehot", P, T, E0)
        st = tile(k, own, "l0f_stats", P, 4, T)
        at = tile(k, own, "l0f_at", P, T, CAP0)
        disp = tile(k, own, "l0f_dispatch", P, T, E0, CAP0)
        comb = tile(k, own, "l0f_combine", P, T, L)
        combx = tile(k, own, "l0f_combine_x", P, T, BPT, L)
        xs = tile(k, own, "l0f_slots", P, E0, GB, CAP0)
        hid = tile(k, own, "l0f_hidden", P, PAIRS0, HID0)
        hidt = tile(k, own, "l0f_hidden_t", P, PAIRS0, 4, P)
        yp = tile(k, own, "l0f_y_by_pair", P, PAIRS0, D)
        yt = tile(k, own, "l0f_yt", P, GB, E0, CAP0)
        y = tile(k, own, "l0f_y", P, T, D)

        @block.vector
        def _(vec):
            step = Steps(vec, s["vector_step"])
            norm_vector(k, vec, step, s)
            vec.wait_ge(s["logits"], 1)
            mx, gate, place, pick = (st[:, i, :] for i in range(4))
            step(nc.vector.tensor_copy(lg[:], ps[:, 1, 0:T * E0].rearrange("p (t e) -> p t e", e=E0)))
            step(nc.vector.reduce_max(mx, lg[:], X))
            step(nc.vector.tensor_tensor(ex[:], lg[:], over(mx.unsqueeze(2), (P, T, E0)), SUB), s["shifted"])
            step(nc.vector.tensor_tensor(hot[:], lg[:], over(mx.unsqueeze(2), (P, T, E0)), EQ))
            step(nc.vector.tensor_tensor(hot[:], hot[:], over(k.countdown.unsqueeze(1), (P, T, E0)), MUL))
            step(nc.vector.reduce_max(pick, hot[:], X))
            step(nc.vector.tensor_tensor(hot[:], over(pick.unsqueeze(2), (P, T, E0)), over(k.countdown.unsqueeze(1), (P, T, E0)), EQ), s["chosen"])
            vec.wait_ge(s["exps"], 1)
            step(nc.vector.reduce_sum(gate, ex[:], X))
            step(nc.vector.reciprocal(gate, gate))
            vec.wait_ge(s["places"], 1)
            step(nc.vector.tensor_tensor(lg[:], ps[:, 2, 0:T * E0].rearrange("p (t e) -> p t e", e=E0), hot[:], MUL))
            step(nc.vector.reduce_sum(place, lg[:], X))
            step(nc.vector.tensor_tensor(at[:], over(place.unsqueeze(2), (P, T, CAP0)), over(k.count4.unsqueeze(1), (P, T, CAP0)), EQ))
            step(nc.vector.tensor_tensor(disp[:], over(hot[:].unsqueeze(3), (P, T, E0, CAP0)), over(at[:].unsqueeze(2), (P, T, E0, CAP0)), MUL), s["dispatch_ready"])
            flat = disp[:].rearrange("p t e c -> p t (e c)")
            vec.wait_ge(s["slots_psum"], 1)
            step(nc.vector.tensor_tensor(flat, flat, over(gate.unsqueeze(2), (P, T, L)), MUL))
            step(nc.vector.transpose(comb[:], flat))
            step(nc.vector.tensor_tensor(combx[:], over(comb[:].unsqueeze(2), (P, T, BPT, L)), over(k.tile_batch.unsqueeze(1).unsqueeze(3), (P, T, BPT, L)), MUL), s["combine_ready"])
            for n in range(PAIRS0):
                vec.wait_ge(s["turned"], n + 1)
                step(nc.vector.tensor_copy(hidt[:, n, :, :].rearrange("p c m -> p (c m)"), ps[:, 4 + n, :]), s["turned_ready"])
            add_projection(k, vec, step, s, (2, 3, 4, 5))

        @block.scalar
        def _(act):
            step = Steps(act, s["scalar_step"])
            norm_scalar(k, act, step, s)
            act.wait_ge(s["shifted"], 1)
            step(nc.scalar.activation(ex[:], ex[:], ACT.Exp), s["exps"])
            act.wait_ge(s["slots_psum"], 1)
            for j in range(BPT):
                step(nc.scalar.activation(xs[:].rearrange("p e (t j) c -> p j t e c", j=BPT)[:, j],
                                          ps[:, 4 + j, 0:P].rearrange("p (t e c) -> p t e c", t=T, e=E0), ACT.Copy), s["slots_ready"])
            for n in range(PAIRS0):
                act.wait_ge(s["hidden_psum"], n + 1)
                step(nc.scalar.activation(hid[:, n, :], ps[:, n, :], ACT.Gelu_apprx_tanh), s["hidden_ready"])
            act.wait_ge(s["y_psum"], 1)
            step(nc.scalar.activation(yp[:].rearrange("p n d -> p (n d)"), ps[:, 0, :], ACT.Copy), s["y_ready"])
            act.wait_ge(s["ypt_psum"], 1)
            step(nc.scalar.activation(yt[:].rearrange("p b e c -> p e b c"), ps[:, 1, :].rearrange("p (e b c) -> p e b c", e=E0, c=CAP0), ACT.Copy), s["ypt_ready"])
            act.wait_ge(s["yt_psum"], 1)
            step(nc.scalar.activation(y[:].rearrange("p t d -> p (t d)"), ps[:, 7, :], ACT.Copy), s["yt_ready"])

        @block.tensor
        def _(pe):
            norm_tensor(k, pe, s)
            pe.wait_ge(s["xt_ready"], 1)
            for t in range(T):
                last = nc.tensor.matmul(ps[:, 1, t * E0:(t + 1) * E0], k.xt[:, t * P:(t + 1) * P], w["l0f_g"], start=True, stop=True)
            last.then_inc(s["logits"], 1)
            pe.wait_ge(s["chosen"], 1)
            nc.tensor.matmul(ps[:, 2, 0:T * E0], k.earlier, hot[:].rearrange("p t e -> p (t e)"), start=True, stop=True).then_inc(s["places"], 1)
            pe.wait_ge(s["dispatch_ready"], 1)
            for t in range(T):
                for j in range(BPT):
                    r = slice(L * j, L * j + L)
                    last = nc.tensor.matmul(ps[:, 4 + j, t * L:(t + 1) * L], k.xn[r, t, :], disp[r, t, :, :].rearrange("p e c -> p (e c)"), start=True, stop=True)
            last.then_inc(s["slots_psum"], 1)
            pe.wait_ge(s["slots_ready"], BPT)
            pe.wait_ge(k.ffn_loaded, 32)
            for n in range(PAIRS0):
                for i in range(2):
                    e = 2 * n + i
                    last = nc.tensor.matmul(ps[64 * i:64 * i + 64, n, :], xs[:, e, :, :].rearrange("p b c -> p (b c)"), w["l0f_w1"][:, e, :], start=True, stop=True)
                last.then_inc(s["hidden_psum"], 1)
            for n in range(PAIRS0):
                pe.wait_ge(s["hidden_ready"], n + 1)
                for c in range(4):
                    last = nc.tensor.transpose(ps[:, 4 + n, c * P:(c + 1) * P], hid[:, n, c * P:(c + 1) * P], k.ident)
                last.then_inc(s["turned"], 1)
            for n in range(PAIRS0):
                pe.wait_ge(s["turned_ready"], n + 1)
                for c in range(4):
                    for i in range(2):
                        last = nc.tensor.matmul(ps[64 * i:64 * i + 64, 0, n * D:(n + 1) * D], hidt[:, n, c, 64 * i:64 * i + 64], w["l0f_w2"][:, 2 * n + i, c, :], start=c == 0, stop=c == 3)
            last.then_inc(s["y_psum"], 1)
            pe.wait_ge(s["y_ready"], 1)
            for n in range(PAIRS0):
                last = nc.tensor.transpose(ps[:, 1, n * P:(n + 1) * P], yp[:, n, :], k.ident)
            last.then_inc(s["ypt_psum"], 1)
            pe.wait_ge(s["ypt_ready"], 1)
            for t in range(T):
                last = nc.tensor.transpose(ps[:, 7, t * P:(t + 1) * P], yt[:, t * BPT:(t + 1) * BPT, :, :].rearrange("p b e c -> p (b e c)"), k.ident)
            last.then_inc(s["yt_psum"], 1)
            pe.wait_ge(s["yt_ready"], 1)
            pe.wait_ge(s["combine_ready"], 1)
            for t in range(T):
                nc.tensor.matmul(ps[:, 2 + t, 0:D], combx[:, t, :, :].rearrange("p j n -> p (j n)"), y[:, t, :], start=True, stop=True).then_inc(s["z_psum"], 1)


def l1_xattn(k, phase, w, rowv, colv, next_ctx, next_last, next_mask):
    nc, ps = k.nc, k.ps
    s = k.signals(phase, "l1x", *NORM, "q_psum", "q_ready", "g_psum", "g_ready", "t_psum", "sbk_ready", "t_ready", "m_psum", "m_ready",
                  "o_psum", "o_ready", "z_psum", "residual", "masked_ready", "xb_ready", "base_ready")
    inv_dk = 1.0 / (2.828125 + 1e-8)
    with ExitStack() as own, nc.Block() as block:
        qt = tile(k, own, "l1x_qt", P, GT)
        gram = tile(k, own, "l1x_gram", P, 4, D + 1)
        t1 = tile(k, own, "l1x_t1", P, 4, D)
        sbk = tile(k, own, "l1x_sbk", P, 4, D)
        kv = tile(k, own, "l1x_kv", P, GB, D)
        k.ot = tile(k, own, "l1x_ot", P, GT)
        c0 = tile(k, own, "l1x_c0", P, D)
        masked = tile(k, own, "l1x_masked", P, 2, T)
        res = tile(k, own, "l1x_res", P, T, D)
        base = tile(k, own, "l1x_res_base", P, T, D)
        xb = tile(k, own, "l1x_x_and_bias", P, T, D)

        @block.gpsimd
        def _(pool):
            step = Steps(pool, s["pool_step"])
            step(nc.gpsimd.tensor_tensor(xb[:], k.xg[:], over(rowv["l1x_b"].unsqueeze(1), (P, T, D)), ADD), s["xb_ready"])
            pool.wait_ge(s["xn_ready"], T)
            step(nc.gpsimd.tensor_tensor(base[:], k.xn[:], over(rowv["l1x_bo"].unsqueeze(1), (P, T, D)), ADD))
            pool.wait_ge(s["masked_ready"], 1)
            step(nc.gpsimd.tensor_tensor(base[:], base[:], over(masked[:, 1, :].unsqueeze(2), (P, T, D)), ADD), s["base_ready"])

        @block.sync
        def _(sp):
            sp.wait_ge(s["g_psum"], GB)
            sp.dma_start(k.ctx[:], next_ctx).then_inc(k.ctx_loaded, 16)
            sp.dma_start(k.last[:], next_last).then_inc(k.ctx_loaded, 16)
            sp.wait_ge(s["t_ready"], 1)
            sp.dma_start(k.mask[:], next_mask).then_inc(k.mask_loaded, 16)

        @block.vector
        def _(vec):
            step = Steps(vec, s["vector_step"])
            norm_vector(k, vec, step, s)
            step(nc.vector.tensor_scalar(c0[:], rowv["l1x_bv"], colv["l1x_bk"], float(S2), MUL, MUL))
            step(nc.vector.tensor_tensor(c0[:], c0[:], k.same_head, MUL))
            step(nc.vector.reduce_max(masked[:, 0, :], k.mask[:], X))
            step(nc.vector.tensor_scalar(masked[:, 1, :], masked[:, 0, :], LOWEST, 1e10, MUL, MUL), s["masked_ready"])
            for b in range(GB + 1):
                if b < GB:
                    i = b % 4
                    vec.wait_ge(s["g_ready"], b + 1)
                    step.free(nc.vector.tensor_scalar(sbk[:, i, :], rowv["l1x_bk"], gram[:, i, D:D + 1], None, MUL), s["sbk_ready"])
                    vec.wait_ge(s["t_psum"], b + 1)
                    step.free(nc.vector.scalar_tensor_tensor(t1[:, i, :], rowv["l1x_bv"], gram[:, i, D:D + 1], ps[:, 4 + b % 2, 0:D], MUL, ADD), s["t_ready"])
                if b > 0:
                    n = b - 1
                    vec.wait_ge(s["m_psum"], n + 1)
                    step(nc.vector.tensor_tensor(kv[:, n, :], ps[:, 6 + n % 2, 0:D], k.same_head, MUL))
                    step.free(nc.vector.tensor_tensor(kv[:, n, :], kv[:, n, :], c0[:], ADD), s["m_ready"])
            vec.wait_ge(s["base_ready"], 1)
            for t in range(T):
                vec.wait_ge(s["z_psum"], t + 1)
                step(nc.vector.tensor_tensor(res[:, t, :], base[:, t, :], ps[:, 2 + t, 0:D], ADD))
                step.free(nc.vector.bn_stats(k.parts[:, t, :], res[:, t, :]))
            step.settled()
            normalise(k, step, res[:], res[:], parts_known=True)
            vec.wait_ge(s["xb_ready"], 1)
            for t in range(T):
                step.free(nc.vector.tensor_tensor(res[:, t, :], res[:, t, :], rowv["l1x_g"], MUL), s["residual"])
            for t in range(T):
                vec.wait_ge(s["residual"], t + 1)
                step.free(nc.vector.tensor_tensor(k.xg[:, t, :], xb[:, t, :], res[:, t, :], ADD), s["residual"])
            for t in range(T):
                vec.wait_ge(s["residual"], T + t + 1)
                step.free(nc.vector.bn_stats(k.parts[:, t, :], k.xg[:, t, :]))
            step.settled()
            k.parts_known = True

        @block.scalar
        def _(act):
            step = Steps(act, s["scalar_step"])
            norm_scalar(k, act, step, s)
            act.wait_ge(s["q_psum"], 1)
            step(nc.scalar.activation(qt[:], ps[:, 1, :], ACT.Identity, bias=colv["l1x_bq"]))
            step(nc.scalar.activation(qt[:], qt[:], ACT.Copy, scale=inv_dk), s["q_ready"])
            for b in range(GB):
                act.wait_ge(s["g_psum"], b + 1)
                if b >= 4:
                    act.wait_ge(s["m_psum"], b - 3)
                step(nc.scalar.activation(gram[:, b % 4, :], ps[:, 2 + b % 2, 0:D + 1], ACT.Copy), s["g_ready"])
            act.wait_ge(s["o_psum"], 1)
            step(nc.scalar.activation(k.ot[:], ps[:, 0, :], ACT.Copy), s["o_ready"])

        @block.tensor
        def _(pe):
            norm_tensor(k, pe, s)
            pe.wait_ge(s["xt_ready"], 1)
            nc.tensor.matmul(ps[:, 1, :], w["l1x_q"], k.xt[:], start=True, stop=True).then_inc(s["q_psum"], 1)

            def moments(b):
                if b >= 2:
                    pe.wait_ge(s["g_ready"], b - 1)
                bank = ps[:, 2 + b % 2, 0:D + 1]
                nc.tensor.matmul(bank, k.ctx[:, b, 0, 0:D], k.ctx[:, b, 0, :], start=True, stop=False)
                nc.tensor.matmul(bank, k.ctx[:, b, 1, 0:D], k.ctx[:, b, 1, :], start=False, stop=False)
                nc.tensor.matmul(bank, k.last[:, b, 0:D], k.last[:, b, :], start=False, stop=True).then_inc(s["g_psum"], 1)

            def values(b):
                pe.wait_ge(s["g_ready"], b + 1)
                if b >= 2:
                    pe.wait_ge(s["t_ready"], b - 1)
                nc.tensor.matmul(ps[:, 4 + b % 2, 0:D], gram[:, b % 4, 0:D], w["l1x_v"], start=True, stop=True).then_inc(s["t_psum"], 1)

            def keys(b):
                pe.wait_ge(s["sbk_ready"], b + 1)
                pe.wait_ge(s["t_ready"], b + 1)
                if b >= 2:
                    pe.wait_ge(s["m_ready"], b - 1)
                nc.tensor.matmul(ps[:, 6 + b % 2, 0:D], w["l1x_k"], t1[:, b % 4, :], start=True, stop=False)
                nc.tensor.matmul(ps[:, 6 + b % 2, 0:D], sbk[:, b % 4, :], w["l1x_v"], start=False, stop=True).then_inc(s["m_psum"], 1)

            for b in range(GB + 2):
                if b < GB:
                    moments(b)
                if 1 <= b <= GB:
                    values(b - 1)
                if b >= 2:
                    keys(b - 2)
            pe.wait_ge(s["q_ready"], 1)
            pe.wait_ge(s["m_ready"], GB)
            for b in range(GB):
                last = nc.tensor.matmul(ps[:, 0, b * L:(b + 1) * L], kv[:, b, :], qt[:, b * L:(b + 1) * L], start=True, stop=True)
            last.then_inc(s["o_psum"], 1)
            project(k, pe, s, w["l1x_o"], (2, 3, 4, 5))


def l1_attn(k, phase, w, rowv, colv):
    nc, ps = k.nc, k.ps
    s = k.signals(phase, "l1a", *NORM, "qkv_psum", "qkv_ready", "v_ready", "qt_psum", "qt_ready", "kv_psum", "kv_ready", "ks_psum",
                  "q_ready", "num_psum", "o_ready", "z_psum", "residual")
    with ExitStack() as own, nc.Block() as block:
        qk = tile(k, own, "l1a_qk", P, T, 2 * H, DH)
        pw = tile(k, own, "l1a_pw", P, T, 2 * H, DH)
        sm = tile(k, own, "l1a_sums", P, T, 2 * H)
        v = tile(k, own, "l1a_v", P, T, D)
        qt = tile(k, own, "l1a_qt", P, GT)
        kv = tile(k, own, "l1a_kv", P, GB, D)
        out = tile(k, own, "l1a_out", P, GB, L)
        den = tile(k, own, "l1a_den", P, T, H)
        k.ot = tile(k, own, "l1a_ot", P, GT)

        @block.vector
        def _(vec):
            step = Steps(vec, s["vector_step"])
            norm_vector(k, vec, step, s)
            for t in range(T):
                vec.wait_ge(s["qkv_psum"], t + 1)
                step(nc.vector.tensor_scalar(qk[:, t, :, :].rearrange("p h d -> p (h d)"), ps[:, 1 + t, 0:2 * D], 0.0, 1e-6, MAX, ADD), s["qkv_ready"])
            wide = (P, T * 2 * H, DH)
            q3, p3 = (a[:].rearrange("p t h d -> p (t h) d") for a in (qk, pw))
            s3 = sm[:].rearrange("p t h -> p (t h)")
            for power in (1, 3):
                if power == 3:
                    step(nc.vector.tensor_tensor(p3, q3, q3, MUL))
                    step(nc.vector.tensor_tensor(q3, q3, p3, MUL))
                step(nc.vector.reduce_sum(s3, q3, X))
                step(nc.vector.reciprocal(s3, s3))
                step(nc.vector.tensor_tensor(q3, q3, over(s3.unsqueeze(2), wide), MUL), None if power == 1 else s["qkv_ready"])
            vec.wait_ge(s["ks_psum"], 1)
            q4, p4 = qk[:, :, 0:H, :], pw[:, :, 0:H, :]
            for t in range(T):
                step.free(nc.vector.tensor_tensor(p4[:, t], q4[:, t], ps[:, 5, t * D:(t + 1) * D].rearrange("p (h d) -> p h d", d=DH), MUL))
            step.settled()
            step(nc.vector.reduce_sum(den[:], p4, X))
            step(nc.vector.tensor_scalar(den[:], den[:], 1e-6, None, ADD))
            step(nc.vector.reciprocal(den[:], den[:]))
            for t in range(T):
                step.free(nc.vector.tensor_tensor(q4[:, t], q4[:, t], over(den[:, t].unsqueeze(2), (P, H, DH)), MUL), s["q_ready"])
            step.settled(s["q_ready"])
            vec.wait_ge(s["kv_psum"], 1)
            for j in range(BPT):
                step(nc.vector.tensor_tensor(kv[:].rearrange("p (t j) d -> p j t d", j=BPT)[:, j], ps[:, 1 + j, :].rearrange("p (t d) -> p t d", d=D),
                                             over(k.same_head.unsqueeze(1), (P, T, D)), MUL), s["kv_ready"])
            vec.wait_ge(s["num_psum"], 1)
            o = out[:]
            step(nc.vector.tensor_copy(o, ps[:, 6, :].rearrange("p (b n) -> p b n", n=L)))
            ot = k.ot[:].rearrange("p (b n) -> p b n", n=L)
            before, here, after = (colv[f"l1a_w{i}"] for i in range(3))
            step(nc.vector.tensor_scalar(ot, o, here, colv["l1a_bc"], MUL, ADD))
            step(nc.vector.tensor_tensor(ot, ot, o, ADD))
            step(nc.vector.scalar_tensor_tensor(ot[:, :, 1:L], o[:, :, 0:L - 1], before, ot[:, :, 1:L], MUL, ADD))
            step(nc.vector.scalar_tensor_tensor(ot[:, :, 0:L - 1], o[:, :, 1:L], after, ot[:, :, 0:L - 1], MUL, ADD), s["o_ready"])
            add_projection(k, vec, step, s, (1, 2, 3, 4), rowv["l1a_bp"])

        @block.scalar
        def _(act):
            step = Steps(act, s["scalar_step"])
            norm_scalar(k, act, step, s)
            for t in range(T):
                act.wait_ge(s["qkv_ready"], t + 1)
                step(nc.scalar.activation(v[:, t, :], ps[:, 1 + t, 2 * D:3 * D], ACT.Copy), s["v_ready"])
            act.wait_ge(s["qt_psum"], 1)
            step(nc.scalar.activation(qt[:], ps[:, 0, :], ACT.Copy), s["qt_ready"])

        @block.tensor
        def _(pe):
            norm_tensor(k, pe, s)
            pe.wait_ge(s["xt_ready"], 1)
            for t in range(T):
                nc.tensor.matmul(ps[:, 1 + t, 0:3 * D], k.xt[:, t * P:(t + 1) * P], w["l1a_qkv"], start=True, stop=True).then_inc(s["qkv_psum"], 1)
            pe.wait_ge(s["qkv_ready"], T + 1)
            pe.wait_ge(s["v_ready"], T)
            for t in range(T):
                last = nc.tensor.matmul(ps[:, 5, t * D:(t + 1) * D], k.same_batch, qk[:, t, H:2 * H, :].rearrange("p h d -> p (h d)"), start=True, stop=True)
            last.then_inc(s["ks_psum"], 1)
            for t in range(T):
                for j in range(BPT):
                    r = slice(L * j, L * j + L)
                    last = nc.tensor.matmul(ps[:, 1 + j, t * D:(t + 1) * D], qk[r, t, H:2 * H, :].rearrange("p h d -> p (h d)"), v[r, t, :], start=True, stop=True)
            last.then_inc(s["kv_psum"], 1)
            pe.wait_ge(s["q_ready"], T)
            for t in range(T):
                last = nc.tensor.transpose(ps[:, 0, t * P:(t + 1) * P], qk[:, t, 0:H, :].rearrange("p h d -> p (h d)"), k.ident)
            last.then_inc(s["qt_psum"], 1)
            pe.wait_ge(s["qt_ready"], 1)
            pe.wait_ge(s["kv_ready"], BPT)
            for b in range(GB):
                last = nc.tensor.matmul(ps[:, 6, b * L:(b + 1) * L], kv[:, b, :], qt[:, b * L:(b + 1) * L], start=True, stop=True)
            last.then_inc(s["num_psum"], 1)
            project(k, pe, s, w["l1a_p"], (1, 2, 3, 4))


def l1_router(k, phase, w, keep_x, store_xn, store_logits):
    nc, ps = k.nc, k.ps
    s = k.signals(phase, "l1r", *NORM, "logits", "logits_ready", "stored")
    with ExitStack() as own, nc.Block() as block:
        lg = tile(k, own, "l1r_logits", E1, GT)

        @block.vector
        def _(vec):
            norm_vector(k, vec, Steps(vec, s["vector_step"]), s)

        @block.scalar
        def _(act):
            step = Steps(act, s["scalar_step"])
            norm_scalar(k, act, step, s)
            step(nc.scalar.activation(keep_x, k.xg[:].rearrange("p t d -> p (t d)"), ACT.Copy))
            act.wait_ge(s["logits"], 1)
            step(nc.scalar.activation(lg[:], ps[0:E1, 1, :], ACT.Copy), s["logits_ready"])

        @block.tensor
        def _(pe):
            norm_tensor(k, pe, s)
            pe.wait_ge(s["xt_ready"], 1)
            nc.tensor.matmul(ps[0:E1, 1, :], w["l1f_r"], k.xt[:], start=True, stop=True).then_inc(s["logits"], 1)

        @block.sync
        def _(sp):
            sp.wait_ge(s["xn_ready"], T)
            sp.dma_start(store_xn, k.xn[:]).then_inc(s["stored"], 16)
            sp.wait_ge(s["logits_ready"], 1)
            sp.dma_start(store_logits, lg[:]).then_inc(s["stored"], 16)
            sp.wait_ge(s["stored"], 32)
            sp.wait_ge(k.x_loaded, 16)
            sp.wait_ge(k.ctxt_loaded, 16)
            sp.wait_ge(k.ctx_loaded, 32)
            sp.wait_ge(k.mask_loaded, 16)


def token_group(a, g):
    return a.rearrange("(g t p) d -> g p t d", g=GROUPS, p=P)[g]


def kept_group(a, g):
    return a[:, bass.ds(g, 1), :].rearrange("p a n -> p (a n)")


def context_group(dram, g):
    return (dram["ctx_t"].rearrange("p (g b s) -> g p b s", g=GROUPS, b=GB)[g],
            dram["ctx_rows"].rearrange("p (g b) i d -> g p b i d", g=GROUPS)[g],
            dram["ctx_last"].rearrange("p (g b) d -> g p b d", g=GROUPS)[g])


def phase_a(k, dram):
    nc = k.nc
    with ExitStack() as phase:
        wp = tile(k, phase, "a_weights", P, len(A_MATS), D)
        rp = tile(k, phase, "a_rows", P, len(A_ROWS), D)
        cp = tile(k, phase, "a_cols", P, len(A_COLS))
        wg, wr = tile(k, phase, "a_wg", P, E0), tile(k, phase, "a_wr", P, E1)
        w1, w2 = tile(k, phase, "a_w1", P, E0, HID0), tile(k, phase, "a_w2", P, E0, 4, D)
        k.ctxt = tile(k, phase, "ctx_t", P, GB, S2)
        k.ctx = tile(k, phase, "ctx_rows", P, GB, 2, D + 1)
        k.last = tile(k, phase, "ctx_last_row", 1, GB, D + 1)
        k.mask = tile(k, phase, "mask", P, T, S2, dtype=U8)
        w = {n: wp[:, i, :] for i, n in enumerate(A_MATS)}
        w["l1a_qkv"] = wp[:, A_MATS.index("l1a_q"):A_MATS.index("l1a_q") + 3, :].rearrange("p a d -> p (a d)")
        w.update({"l0f_g": wg[:], "l1f_r": wr[:], "l0f_w1": w1, "l0f_w2": w2})
        rowv = {n: rp[:, i, :] for i, n in enumerate(A_ROWS)}
        colv = {n: cp[:, i:i + 1] for i, n in enumerate(A_COLS)}
        mask_group = lambda g: dram["mask_bool"].rearrange("(g t p) s -> g p t s", g=GROUPS, p=P)[g]
        loaded = k.flag(phase, "a_weights_loaded")
        k.ffn_loaded = k.flag(phase, "a_ffn_weights_loaded")
        with nc.Block() as block:
            @block.sync
            def _(sp):
                ctxt, ctx, last = context_group(dram, 0)
                for dst, src in ((wp, dram["a_mats"]), (cp, dram["a_cols"]), (rp, dram["a_rows"].partition_broadcast(P)), (k.x_next, token_group(dram["x"], 0)),
                                 (wg, dram["l0f_g"]), (wr, dram["l1f_r"]), (k.mask, mask_group(0)), (k.ctxt, ctxt), (k.ctx, ctx), (k.last, last)):
                    sp.dma_start(dst[:], src).then_inc(loaded, 16)
                sp.dma_start(w1[:], dram["l0f_w1"]).then_inc(k.ffn_loaded, 16)
                sp.dma_start(w2[:], dram["l0f_w2"]).then_inc(k.ffn_loaded, 16)
                sp.wait_ge(loaded, 16 * 10)

        k.numbers.remove(k.ffn_loaded.num)
        k.clear_signals()
        with nc.Fori(0, GROUPS) as g:
            k.x_loaded, k.ctxt_loaded, k.ctx_loaded, k.mask_loaded = (
                k.flag(phase, "a_" + n) for n in ("x_loaded", "ctxt_loaded", "ctx_loaded", "mask_loaded"))
            after = (g + 1) % GROUPS
            ctxt, ctx, last = context_group(dram, after)
            k.x_in = k.x_next
            l0_xattn(k, phase, w, dram["ctx"], token_group(dram["x"], after), ctxt)
            k.x_in = k.xg
            l0_attn(k, phase, w, rowv, colv)
            l0_ffn(k, phase, w)
            l1_xattn(k, phase, w, rowv, colv, ctx, last, mask_group(after))
            l1_attn(k, phase, w, rowv, colv)
            l1_router(k, phase, w, kept_group(k.x_all, g), token_group(dram["xn_a"], g), dram["logits"].rearrange("e (g n) -> g e n", g=GROUPS)[g])
            k.clear_signals()
        k.numbers.append(k.ffn_loaded.num)


TOP_ROUNDS = CAP1 // 8
HALF = TOKENS // 2
HALF_AT = 64
PER = 4


def butterfly(k, step, eng, fw, y, t, order, rows, flipped):
    at = 0
    for stage in order:
        st = 2 ** stage
        old, new = (y[:, i, 0:rows, :].rearrange("p r (b two s) -> p r b two s", two=2, s=st) for i in (at, 1 - at))
        wq = fw[:, stage, :].rearrange("p (b s q) -> p b s q", s=st, q=4)
        tt = [t[:, i, 0:rows, :].rearrange("p r (b s) -> p r b s", s=st) for i in range(4)]
        for i in range(4):
            q = (i % 2) * 2 + i // 2 if flipped else i
            for r in range(rows):
                step.free(eng.tensor_tensor(tt[i][:, r], old[:, r, :, i % 2, :], wq[:, :, :, q], MUL))
        step.settled()
        for i in range(2):
            for r in range(rows):
                step.free(eng.tensor_tensor(new[:, r, :, i, :], tt[2 * i][:, r], tt[2 * i + 1][:, r], ADD))
        step.settled()
        at = 1 - at
    return at


def butterfly_tiles(k, stack, rows):
    return (tile(k, stack, "fly_weights", P, STAGES, HID3 * 2), tile(k, stack, "fly_rows", P, 2, rows, HID3),
            tile(k, stack, "fly_terms", P, 4, rows, HID3 // 2))


def choose_tokens(k, phase, dram, weight_of, token_of):
    nc, ps = k.nc, k.ps
    s = k.signals(phase, "l1t", "loaded", "filled", "shifted", "exps", "merged", "turned", "zeroed", "zeros_stored",
                  "fly_loaded", "fly_done", "bias_turned")
    with ExitStack() as own, nc.Block() as block:
        lg = tile(k, own, "l1t_logits", HALF_AT + E1, HALF)
        val = tile(k, own, "l1t_values", HALF_AT + E1, CAP1)
        at = tile(k, own, "l1t_at", HALF_AT + E1, CAP1, dtype=U32)
        atf = tile(k, own, "l1t_at_f", HALF_AT + E1, CAP1)
        second = tile(k, own, "l1t_second", E1, 2, CAP1)
        both = tile(k, own, "l1t_both", E1, 4, CAP1)
        st = tile(k, own, "l1t_stats", E1, 2)
        zeros = tile(k, own, "l1t_zeros", P, TOKENS)
        fw, fy, ft = butterfly_tiles(k, own, 2)
        ub = tile(k, own, "fly_up_bias", 1, HID3)

        @block.sync
        def _(sp):
            sp.wait_ge(s["filled"], 1)
            sp.dma_start(lg[0:E1, :], dram["logits"][:, 0:HALF]).then_inc(s["loaded"], 16)
            sp.dma_start(lg[HALF_AT:HALF_AT + E1, :], dram["logits"][:, HALF:TOKENS]).then_inc(s["loaded"], 16)
            sp.dma_start(fw[:], dram["l3f_up"].partition_broadcast(P)).then_inc(s["fly_loaded"], 16)
            sp.dma_start(fy[:, 0, 0, :], dram["l3f_exp"]).then_inc(s["fly_loaded"], 16)
            sp.dma_start(fy[:, 0, 1, :], dram["l3f_b_exp"].partition_broadcast(P)).then_inc(s["fly_loaded"], 16)
            sp.dma_start(ub[:], dram["l3f_up_bias"]).then_inc(s["fly_loaded"], 16)
            sp.wait_ge(s["zeroed"], 1)
            for j in range(PER):
                sp.dma_start(dram[f"sums_{j}"].rearrange("(p q) d -> p (q d)", p=P), zeros[:]).then_inc(s["zeros_stored"], 16)
            sp.wait_ge(s["zeros_stored"], 16 * PER)

        @block.gpsimd
        def _(pool):
            nc.gpsimd.memset(zeros[:], 0.0).then_inc(s["zeroed"], 1)
            step = Steps(pool, s["pool_step"])
            pool.wait_ge(s["fly_loaded"], 64)
            got = butterfly(k, step, nc.gpsimd, fw, fy, ft, range(STAGES), 2, False)
            step(nc.gpsimd.tensor_copy(k.up_w[:], fy[:, got, 0, :]))
            step(nc.gpsimd.tensor_tensor(ub[:], ub[:], fy[0:1, got, 1, :], ADD), s["fly_done"])

        @block.vector
        def _(vec):
            step = Steps(vec, s["vector_step"])
            step(nc.vector.memset(lg[:], LOWEST), s["filled"])
            vec.wait_ge(s["loaded"], 32)
            for r in range(TOP_ROUNDS):
                eight = slice(8 * r, 8 * r + 8)
                step(nc.vector.max(val[:, eight], lg[:]))
                step(nc.vector.max_index(at[:, eight], val[:, eight], lg[:]))
                step(nc.vector.match_replace(lg[:], val[:, eight], lg[:], LOWEST))
            step(nc.vector.tensor_copy(atf[:], at[:]))
            step(nc.vector.tensor_copy(second[:, 0, :], val[HALF_AT:HALF_AT + E1, ::-1]))
            step(nc.vector.tensor_scalar(second[:, 1, :], atf[HALF_AT:HALF_AT + E1, ::-1], float(HALF), None, ADD))
            first, best, token, weight = (both[:, i, :] for i in range(4))
            step(nc.vector.tensor_tensor(first, val[0:E1, :], second[:, 0, :], ALU.is_ge))
            step(nc.vector.tensor_tensor(best, val[0:E1, :], second[:, 0, :], MAX))
            step(nc.vector.tensor_tensor(token, atf[0:E1, :], second[:, 1, :], SUB))
            step(nc.vector.tensor_tensor(token, token, first, MUL))
            step(nc.vector.tensor_tensor(token, token, second[:, 1, :], ADD))
            step(nc.vector.reduce_max(st[:, 0:1], best, X))
            step(nc.vector.tensor_scalar(weight, best, st[:, 0:1], None, SUB), s["shifted"])
            vec.wait_ge(s["exps"], 1)
            step(nc.vector.reduce_sum(st[:, 1:2], weight, X))
            step(nc.vector.reciprocal(st[:, 1:2], st[:, 1:2]))
            step(nc.vector.tensor_scalar(weight, weight, st[:, 1:2], None, MUL), s["merged"])
            vec.wait_ge(s["turned"], 1)
            step(nc.vector.tensor_copy(weight_of[:], ps[:, 0, 0:E1]))
            step(nc.vector.tensor_copy(token_of[:], ps[:, 0, E1:2 * E1]))

        @block.scalar
        def _(act):
            act.wait_ge(s["shifted"], 1)
            nc.scalar.activation(both[:, 3, :], both[:, 3, :], ACT.Exp).then_inc(s["exps"], 1)
            act.wait_ge(s["bias_turned"], 1)
            nc.scalar.activation(k.up_b[:], ps[:, 2, 0:4], ACT.Copy).then_inc(s["scalar_step"], 1)

        @block.tensor
        def _(pe):
            pe.wait_ge(s["merged"], 1)
            nc.tensor.transpose(ps[:, 0, 0:E1], both[:, 3, :], k.ident[0:E1, 0:E1])
            nc.tensor.transpose(ps[:, 0, E1:2 * E1], both[:, 2, :], k.ident[0:E1, 0:E1]).then_inc(s["turned"], 1)
            pe.wait_ge(s["fly_done"], 1)
            for c in range(4):
                last = nc.tensor.transpose(ps[:, 2, c:c + 1], ub[:, c * P:(c + 1) * P], k.ident[0:1, 0:1])
            last.then_inc(s["bias_turned"], 1)


def l1_experts(k, phase, dram, weight_of, token_of, b1):
    nc, ps = k.nc, k.ps
    steps = E1 // PER
    s = k.signals(phase, "l1e", "weights_loaded_0", "weights_loaded_1", "gathered_0", "gathered_1", *(f"scattered_{e}" for e in range(PER)),
                  "rows_ready", "waits_taken", "picked", "xt_psum", "xt_ready", "hidden_psum", "hidden_ready", "y_psum", "y_ready", "y_vector")
    weights_loaded, gathered = ([s[f"{n}_{u}"] for u in range(2)] for n in ("weights_loaded", "gathered"))
    scattered = [s[f"scattered_{e}"] for e in range(PER)]
    with ExitStack() as own, nc.Block() as block:
        rows = tile(k, own, "l1e_rows_to_gather", P, 2, PER, dtype=I32)
        rows_out = tile(k, own, "l1e_rows_to_add", P, 2, PER, dtype=I32)
        wt = tile(k, own, "l1e_weight", P, 2, PER)
        b1n = tile(k, own, "l1e_b1", P, 2, PER * S1)
        w1 = tile(k, own, "l1e_w1", P, 2, PER, S1, P)
        w2 = tile(k, own, "l1e_w2", P, 2, PER, S1, KW)
        b2 = tile(k, own, "l1e_b2", P, 2, PER, D)
        xe = tile(k, own, "l1e_x", P, 2, PER, D)
        waits, first = tile(k, own, "l1e_waits", 1, 1), tile(k, own, "l1e_first", 1, 1)
        xet = tile(k, own, "l1e_xt", P, PER, P)
        hid = tile(k, own, "l1e_hidden", P, PER, S1, P)
        y = tile(k, own, "l1e_y", P, 2, PER, D)

        @block.sync
        def _(sp):
            def load(m, u):
                sp.dma_start(w1[:, u], dram["l1f_w1"].rearrange("p (n e) s m -> n p e s m", e=PER)[m]).then_inc(weights_loaded[u], 16)
                sp.dma_start(w2[:, u], dram["l1f_w2"].rearrange("p (n e) s m -> n p e s m", e=PER)[m]).then_inc(weights_loaded[u], 16)
                sp.dma_start(b2[:, u], dram["l1f_b2"].rearrange("(n e) d -> n e d", e=PER)[m].partition_broadcast(P)).then_inc(weights_loaded[u], 16)

            load(0, 0)
            load(1, 1)
            with sp.Fori(1, steps // 2) as i:
                for u in range(2):
                    sp.wait_ge(s["y_ready"], 2 * i + u)
                    load(2 * i + u, u)

        @block.gpsimd
        def _(pool):
            def row_numbers(dst, m):
                nc.gpsimd.tensor_copy(dst, token_of[:, bass.ts(m, PER)]).then_inc(s["rows_ready"], 1)

            def take_waits(before):
                pool.wait_ge(s["waits_taken"], before)
                nc.gpsimd.tensor_tensor(waits[:], k.ones[0:1, 0:1], k.ones[0:1, 0:1], MUL).then_inc(s["waits_taken"], 1)

            def gather(u):
                for e in range(PER):
                    nc.gpsimd.indirect_dma_start(out=xe[:, u, e, :], out_offset=None, in_=dram["xn_a"],
                                                 in_offset=bass.IndirectOffsetOnAxis(ap=rows[:, u, e:e + 1], axis=0)).then_inc(gathered[u], 16)

            nc.gpsimd.tensor_tensor(waits[:], k.ones[0:1, 0:1], k.ones[0:1, 0:1], MUL).then_inc(s["waits_taken"], 1)
            for m in range(3):
                if m == 2:
                    pool.wait_ge(s["xt_psum"], 1)
                row_numbers(rows[:, m % 2], m)
                pool.wait_ge(s["rows_ready"], m + 1)
                gather(m % 2)
            with pool.Fori(0, steps // 2) as i:
                for u in range(2):
                    m = 2 * i + u
                    row_numbers(rows_out[:, u], m)
                    pool.wait_ge(s["rows_ready"], 2 * m + 4)
                    pool.wait_ge(s["y_ready"], m + 2)
                    take_waits(2 * m + 1)
                    for e in range(PER):
                        nc.gpsimd.indirect_dma_start(out=dram[f"sums_{e}"], out_offset=bass.IndirectOffsetOnAxis(ap=rows_out[:, u, e:e + 1], axis=0),
                                                     in_=y[:, u, e, :], in_offset=None, compute_op=ADD).then_inc(scattered[e], 16)
                    pool.wait_ge(s["xt_psum"], m + 2)
                    row_numbers(rows[:, 1 - u], (m + 3) % steps)
                    pool.wait_ge(s["rows_ready"], 2 * m + 5)
                    take_waits(2 * m + 2)
                    gather(1 - u)
                    for e in range(PER):
                        pool.wait_ge(scattered[e], 16 * m + 16)
            pool.wait_ge(gathered[0], 16 * PER * (steps // 2 + 2))
            pool.wait_ge(gathered[1], 16 * PER * (steps // 2 + 1))

        @block.vector
        def _(vec):
            def pick(m, u):
                nc.vector.tensor_copy(wt[:, u], weight_of[:, bass.ts(m, PER)]).then_inc(s["picked"], 1)
                nc.vector.tensor_copy(b1n[:, u], b1[:, bass.ts(m, PER * S1)]).then_inc(s["picked"], 1)

            pick(0, 0)
            nc.vector.tensor_copy(first[:], k.ones[0:1, 0:1]).then_inc(s["y_ready"], 1)
            with vec.Fori(0, steps // 2) as i:
                for u in range(2):
                    m = 2 * i + u
                    pick((m + 1) % steps, 1 - u)
                    vec.wait_ge(s["picked"], 2 * m + 2)
                    vec.wait_ge(weights_loaded[u], 48 * (i + 1))
                    vec.wait_ge(s["rows_ready"], 2 * m + 2)
                    vec.wait_ge(s["y_psum"], m + 1)
                    nc.vector.tensor_tensor(y[:, u], b2[:, u], ps[:, 5, :].rearrange("p (e d) -> p e d", d=D), ADD).then_inc(s["y_vector"], 1)
                    vec.wait_ge(s["y_vector"], m + 1)
                    nc.vector.tensor_tensor(y[:, u], y[:, u], over(wt[:, u].unsqueeze(2), (P, PER, D)), MUL).then_inc(s["y_ready"], 1)
                    vec.wait_ge(s["y_ready"], m + 2)

        @block.scalar
        def _(act):
            def turned(m):
                act.wait_ge(s["xt_psum"], m + 1)
                nc.scalar.activation(xet[:].rearrange("p e c -> p (e c)"), ps[:, 0, :], ACT.Copy).then_inc(s["xt_ready"], 1)

            turned(0)
            with act.Fori(0, steps // 2) as i:
                for u in range(2):
                    m = 2 * i + u
                    act.wait_ge(s["picked"], 2 * m + 2)
                    for e in range(PER):
                        act.wait_ge(s["hidden_psum"], PER * m + e + 1)
                        for n in range(S1):
                            nc.scalar.activation(hid[:, e, n, :], ps[:, 1 + e, n * P:(n + 1) * P], ACT.Gelu,
                                                 bias=b1n[:, u, e * S1 + n:e * S1 + n + 1]).then_inc(s["hidden_ready"], 1)
                    turned(m + 1)

        @block.tensor
        def _(pe):
            def turn(u, need):
                pe.wait_ge(gathered[u], 16 * PER * need)
                for e in range(PER):
                    last = nc.tensor.transpose(ps[:, 0, e * P:(e + 1) * P], xe[:, u, e, :], k.ident)
                last.then_inc(s["xt_psum"], 1)

            turn(0, 1)
            with pe.Fori(0, steps // 2) as i:
                for u in range(2):
                    m = 2 * i + u
                    pe.wait_ge(s["xt_ready"], m + 1)
                    pe.wait_ge(weights_loaded[u], 48 * (i + 1))
                    for e in range(PER):
                        for n in range(S1):
                            last = nc.tensor.matmul(ps[:, 1 + e, n * P:(n + 1) * P], w1[:, u, e, n, :], xet[:, e, :], start=True, stop=True)
                        last.then_inc(s["hidden_psum"], 1)
                    turn(1 - u, i + 1 + u)
                    pe.wait_ge(s["y_ready"], m + 1)
                    for e in range(PER):
                        for n in range(S1):
                            pe.wait_ge(s["hidden_ready"], PER * S1 * m + e * S1 + n + 1)
                            last = nc.tensor.matmul(ps[:, 5, e * D + n * KW:e * D + (n + 1) * KW], hid[:, e, n, :], w2[:, u, e, n, :], start=True, stop=True)
                    last.then_inc(s["y_psum"], 1)
            pe.wait_ge(s["xt_ready"], steps + 1)


def phase_b(k, dram):
    nc = k.nc
    with ExitStack() as phase:
        weight_of = tile(k, phase, "l1_weight_of", P, E1)
        token_of = tile(k, phase, "l1_token_of", P, E1, dtype=I32)
        b1 = tile(k, phase, "l1_b1", P, E1 * S1)
        loaded = k.flag(phase, "b_b1_loaded")
        with nc.Block() as block:
            @block.sync
            def _(sp):
                sp.dma_start(b1[:], dram["l1f_b1"]).then_inc(loaded, 16)
                sp.wait_ge(loaded, 16)
        choose_tokens(k, phase, dram, weight_of, token_of)
        l1_experts(k, phase, dram, weight_of, token_of, b1)


def l2_xattn(k, phase, w, rowv, colv, biases, next_context):
    nc, ps = k.nc, k.ps
    s = k.signals(phase, "l2x", *NORM, "qw_ready", "scores", "neg_ready", "exps", "p_ready", "turned", "pt_ready", "c2q_psum", "c2q_rows", "c2q_turned", "c2q_ready",
                  "best_ready", "best_turned", "b_shifted", "b_exps", "b_ready", "b_back", "bd_ready", "q2c_psum", "cat_ready", "z_psum", "residual")
    ROW = 300
    with ExitStack() as own, nc.Block() as block:
        qw = tile(k, own, "l2x_qw", P, GT)
        pr = tile(k, own, "l2x_p", P, T, S2)
        st = tile(k, own, "l2x_stats", P, 4, T)
        pt = tile(k, own, "l2x_pt", P, 2, GT)
        ptl = tile(k, own, "l2x_pt_last", 1, GT)
        ba = tile(k, own, "l2x_batch_att", T, BPT, L)
        bs = tile(k, own, "l2x_batch_stats", T, 2, BPT)
        bd = tile(k, own, "l2x_batch_att_x", P, T, BPT)
        q2c = tile(k, own, "l2x_q2c", P, GB)
        cat = tile(k, own, "l2x_cat", P, 3, GT)
        c2q = tile(k, own, "l2x_c2q", P, T, D)
        total = tile(k, own, "l2x_bias", P, 1)
        next_ctxt, next_ctx, next_last = next_context

        @block.sync
        def _(sp):
            sp.wait_ge(s["scores"], 1)
            sp.dma_start(k.ctxt[:], next_ctxt).then_inc(k.next_loaded, 16)
            sp.wait_ge(s["c2q_psum"], 1)
            sp.dma_start(k.ctx[:], next_ctx).then_inc(k.next_loaded, 16)
            sp.dma_start(k.last[:], next_last).then_inc(k.next_loaded, 16)

        @block.vector
        def _(vec):
            step = Steps(vec, s["vector_step"])
            norm_vector(k, vec, step, s)
            step(nc.vector.reduce_sum(total[:], biases, X))
            vec.wait_ge(s["xt_ready"], 1)
            step(nc.vector.tensor_scalar(qw[:], k.xt[:], colv["l2x_wcq"], colv["l2x_wq"], MUL, ADD), s["qw_ready"])
            mx, neg, best, rs = (st[:, i, :] for i in range(4))
            vec.wait_ge(s["scores"], 1)
            step(nc.vector.reduce_max(mx, ps[:, 0:T, 0:S2], X))
            step(nc.vector.tensor_scalar(best, ps[:, 0, ROW:ROW + T], total[:], None, ADD))
            step(nc.vector.tensor_tensor(best, best, mx, ADD), s["best_ready"])
            step(nc.vector.tensor_scalar(neg, mx, -1.0, None, MUL), s["neg_ready"])
            vec.wait_ge(s["exps"], T)
            step(nc.vector.reciprocal(rs, rs))
            step(nc.vector.tensor_tensor(pr[:], pr[:], over(rs.unsqueeze(2), (P, T, S2)), MUL), s["p_ready"])
            bmx, bsum = bs[:, 0, :], bs[:, 1, :]
            vec.wait_ge(s["best_turned"], 1)
            got = ps[0:T, 7, 0:P].rearrange("p (j n) -> p j n", n=L)
            step(nc.vector.reduce_max(bmx, got, X))
            step(nc.vector.tensor_tensor(ba[:], got, over(bmx.unsqueeze(2), (T, BPT, L)), SUB), s["b_shifted"])
            vec.wait_ge(s["b_exps"], 1)
            step(nc.vector.reduce_sum(bsum, ba[:], X))
            step(nc.vector.reciprocal(bsum, bsum))
            step(nc.vector.tensor_tensor(ba[:], ba[:], over(bsum.unsqueeze(2), (T, BPT, L)), MUL), s["b_ready"])
            vec.wait_ge(s["turned"], 1)
            step(nc.vector.tensor_copy(pt[:, 1, :], ps[:, 5, :]), s["pt_ready"])
            vec.wait_ge(s["b_back"], 1)
            step(nc.vector.tensor_tensor(bd[:], over(ps[:, 0, 0:T].unsqueeze(2), (P, T, BPT)), over(k.tile_batch.unsqueeze(1), (P, T, BPT)), MUL), s["bd_ready"])
            vec.wait_ge(s["q2c_psum"], 1)
            step(nc.vector.tensor_copy(q2c[:], ps[:, 1, 0:GB]))
            step(nc.vector.tensor_tensor(cat[:, 2, :].rearrange("p (b n) -> p b n", n=L), k.xt[:].rearrange("p (b n) -> p b n", n=L),
                                         over(q2c[:].unsqueeze(2), (P, GB, L)), MUL), s["cat_ready"])
            vec.wait_ge(s["c2q_ready"], 1)
            step(nc.vector.tensor_tensor(cat[:, 1, :], cat[:, 0, :], k.xt[:], MUL), s["cat_ready"])
            add_projection(k, vec, step, s, (4, 5, 6, 7), rowv["l2x_bl"])

        @block.scalar
        def _(act):
            step = Steps(act, s["scalar_step"])
            norm_scalar(k, act, step, s, bank=4)
            act.wait_ge(s["neg_ready"], 1)
            for t in range(T):
                step(nc.scalar.activation(pr[:, t, :], ps[:, t, 0:S2], ACT.Exp, bias=st[:, 1, t:t + 1], accum_out=st[:, 3, t:t + 1]), s["exps"])
            act.wait_ge(s["b_shifted"], 1)
            step(nc.scalar.activation(ba[:], ba[:], ACT.Exp), s["b_exps"])
            act.wait_ge(s["turned"], 1)
            step(nc.scalar.activation(pt[:, 0, :], ps[:, 4, :], ACT.Copy))
            step(nc.scalar.activation(ptl[:], ps[0:1, 6, :], ACT.Copy))
            act.wait_ge(s["pt_ready"], 1)
            act.wait_ge(s["c2q_psum"], 1)
            step(nc.scalar.activation(c2q[:].rearrange("p t d -> p (t d)"), ps[:, 2, :], ACT.Copy), s["c2q_rows"])
            act.wait_ge(s["c2q_turned"], 1)
            step(nc.scalar.activation(cat[:, 0, :], ps[:, 3, :], ACT.Copy), s["c2q_ready"])

        @block.tensor
        def _(pe):
            norm_tensor(k, pe, s, bank=4)
            pe.wait_ge(s["xt_ready"], 1)
            for t in range(T):
                nc.tensor.matmul(ps[:, 0, ROW + t:ROW + t + 1], k.xt[:, t * P:(t + 1) * P], colv["l2x_wc"], start=True, stop=True)
            pe.wait_ge(s["qw_ready"], 1)
            for t in range(T):
                for j in range(BPT):
                    b = t * BPT + j
                    last = nc.tensor.matmul(ps[L * j:L * j + L, t, 0:S2], qw[:, b * L:(b + 1) * L], k.ctxt[:, b, :], start=True, stop=True)
            last.then_inc(s["scores"], 1)
            pe.wait_ge(s["best_ready"], 1)
            nc.tensor.transpose(ps[0:T, 7, 0:P], st[:, 2, :], k.ident).then_inc(s["best_turned"], 1)
            pe.wait_ge(s["p_ready"], 1)
            for t in range(T):
                for i in range(2):
                    nc.tensor.transpose(ps[:, 4 + i, t * P:(t + 1) * P], pr[:, t, i * P:(i + 1) * P], k.ident)
                last = nc.tensor.transpose(ps[0:1, 6, t * P:(t + 1) * P], pr[:, t, 2 * P:S2], k.ident)
            last.then_inc(s["turned"], 1)
            pe.wait_ge(s["b_ready"], 1)
            nc.tensor.transpose(ps[:, 0, 0:T], ba[:].rearrange("t j n -> t (j n)"), k.ident[0:T, 0:T]).then_inc(s["b_back"], 1)
            pe.wait_ge(s["pt_ready"], 1)
            pe.wait_ge(s["scalar_step"], 2)
            for b in range(GB):
                c = slice(b * L, (b + 1) * L)
                out = ps[L * (b % BPT):L * (b % BPT) + L, 2, (b // BPT) * D:(b // BPT + 1) * D]
                nc.tensor.matmul(out, pt[:, 0, c], k.ctx[:, b, 0, 0:D], start=True, stop=False)
                nc.tensor.matmul(out, pt[:, 1, c], k.ctx[:, b, 1, 0:D], start=False, stop=False)
                last = nc.tensor.matmul(out, ptl[:, c], k.last[:, b, 0:D], start=False, stop=True)
            last.then_inc(s["c2q_psum"], 1)
            pe.wait_ge(s["bd_ready"], 1)
            for t in range(T):
                last = nc.tensor.matmul(ps[:, 1, t * BPT:(t + 1) * BPT], k.xn[:, t, :], bd[:, t, :], start=True, stop=True)
            last.then_inc(s["q2c_psum"], 1)
            pe.wait_ge(s["c2q_rows"], 1)
            for t in range(T):
                last = nc.tensor.transpose(ps[:, 3, t * P:(t + 1) * P], c2q[:, t, :], k.ident)
            last.then_inc(s["c2q_turned"], 1)
            pe.wait_ge(s["cat_ready"], 2)
            for t in range(T):
                c = slice(t * P, (t + 1) * P)
                for i, src in enumerate((k.xt[:, c], cat[:, 0, c], cat[:, 1, c], cat[:, 2, c])):
                    last = nc.tensor.matmul(ps[:, 4 + t, 0:D], src, w["l2x_l"][:, i * D:(i + 1) * D], start=i == 0, stop=i == 3)
                last.then_inc(s["z_psum"], 1)


def self_attn(k, phase, name, wq, wk, wv, wo, scale, bias=None):
    nc, ps = k.nc, k.ps
    s = k.signals(phase, name, *NORM, *CORE)
    with ExitStack() as own, nc.Block() as block:
        core_tiles(k, own)

        @block.vector
        def _(vec):
            step = Steps(vec, s["vector_step"])
            norm_vector(k, vec, step, s)
            q_by_head(k, vec, step, s)
            core_vector(k, vec, step, s, scale, True, bias)

        @block.gpsimd
        def _(pool):
            core_pool(k, pool, s)

        @block.scalar
        def _(act):
            step = Steps(act, s["scalar_step"])
            norm_scalar(k, act, step, s)
            step(nc.scalar.activation(k.rep[:], four_times(k, ps[:, 0, :]), ACT.Copy), s["rep_ready"])
            act.wait_ge(s["k_psum"], 1)
            step(nc.scalar.activation(k.kt[:], ps[:, 2, :], ACT.Copy), s["k_ready"])
            v_by_head(k, act, step, s)
            core_scalar(k, act, step, s, scale, True)

        @block.tensor
        def _(pe):
            norm_tensor(k, pe, s)
            pe.wait_ge(s["xt_ready"], 1)
            nc.tensor.matmul(ps[:, 1, :], wq, k.xt[:], start=True, stop=True).then_inc(s["q_psum"], 1)
            nc.tensor.matmul(ps[:, 2, :], wk, k.xt[:], start=True, stop=True).then_inc(s["k_psum"], 1)
            core_tensor(k, pe, s, wv, wo)


def l2_norm_out(k, phase, keep_x, keep_xt, largest):
    nc = k.nc
    s = k.signals(phase, "l2n", *NORM)
    with ExitStack() as own, nc.Block() as block:
        mx = tile(k, own, "l2n_mx", P, 1)

        @block.vector
        def _(vec):
            step = Steps(vec, s["vector_step"])
            norm_vector(k, vec, step, s)
            step(nc.vector.reduce_max(mx[:], k.xn[:].rearrange("p t d -> p (t d)"), X, apply_absolute_value=True))
            step(nc.vector.tensor_tensor(largest, largest, mx[:], MAX))

        @block.scalar
        def _(act):
            step = Steps(act, s["scalar_step"])
            step(nc.scalar.activation(keep_x, k.xg[:].rearrange("p t d -> p (t d)"), ACT.Copy))
            act.wait_ge(s["xt_psum"], 1)
            step(nc.scalar.activation(keep_xt, k.ps[:, 0, :], ACT.Copy), s["xt_ready"])

        @block.tensor
        def _(pe):
            norm_tensor(k, pe, s)

        @block.sync
        def _(sp):
            sp.wait_ge(k.next_loaded, 16 * (3 + PER))


def phase_c(k, dram, largest):
    nc = k.nc
    with ExitStack() as phase:
        wp = tile(k, phase, "c_weights", P, len(C_MATS), D)
        rp = tile(k, phase, "c_rows", P, len(C_ROWS), D)
        cp = tile(k, phase, "c_cols", P, len(C_COLS))
        wl = tile(k, phase, "c_wl", P, 4 * D)
        bc = tile(k, phase, "c_biases", P, 3)
        k.ctxt = tile(k, phase, "c_ctx_t", P, GB, S2)
        k.ctx = tile(k, phase, "c_ctx_rows", P, GB, 2, D + 1)
        k.last = tile(k, phase, "c_ctx_last_row", 1, GB, D + 1)
        sums = tile(k, phase, "c_sums", P, PER, T, D)
        w = {n: wp[:, i, :] for i, n in enumerate(C_MATS)}
        w["l2x_l"] = wl[:]
        rowv = {n: rp[:, i, :] for i, n in enumerate(C_ROWS)}
        colv = {n: cp[:, i:i + 1] for i, n in enumerate(C_COLS)}
        loaded = k.flag(phase, "c_weights_loaded")
        cleared = k.flag(phase, "c_largest_cleared")
        s = k.signals(phase, "fly_down", "loaded", "done", "turned")
        with ExitStack() as own, nc.Block() as block:
            fw, fy, ft = butterfly_tiles(k, own, 1)

            @block.sync
            def _(sp):
                sp.dma_start(fw[:], dram["l3f_down"].partition_broadcast(P)).then_inc(s["loaded"], 16)
                sp.dma_start(fy[:, 0, 0, :], dram["l3f_con"]).then_inc(s["loaded"], 16)
                for dst, name in ((wp, "c_mats"), (cp, "c_cols"), (wl, "l2x_l")):
                    sp.dma_start(dst[:], dram[name]).then_inc(loaded, 16)
                sp.dma_start(rp[:], dram["c_rows"].partition_broadcast(P)).then_inc(loaded, 16)
                sp.dma_start(bc[:], dram["l2x_biases"].partition_broadcast(P)).then_inc(loaded, 16)
                ctxt, ctx, last = context_group(dram, 0)
                for dst, src in ((k.ctxt, ctxt), (k.ctx, ctx), (k.last, last)):
                    sp.dma_start(dst[:], src).then_inc(loaded, 16)
                for j in range(PER):
                    sp.dma_start(sums[:, j, :, :], token_group(dram[f"sums_{j}"], 0)).then_inc(loaded, 16)
                sp.wait_ge(loaded, 16 * (8 + PER))

            @block.vector
            def _(vec):
                step = Steps(vec, s["vector_step"])
                step(nc.vector.memset(largest, 0.0), cleared)
                vec.wait_ge(s["loaded"], 32)
                got = butterfly(k, step, nc.vector, fw, fy, ft, reversed(range(STAGES)), 1, True)
                step(nc.vector.tensor_copy(fy[:, 0, 0, :], fy[:, got, 0, :]), s["done"])
                vec.wait_ge(s["turned"], 1)
                step(nc.vector.tensor_copy(k.down_w[:].rearrange("p c d -> p (c d)"), k.ps[:, 0, :]))

            @block.tensor
            def _(pe):
                pe.wait_ge(s["done"], 1)
                for c in range(4):
                    last = nc.tensor.transpose(k.ps[:, 0, c * P:(c + 1) * P], fy[:, 0, 0, c * P:(c + 1) * P], k.ident)
                last.then_inc(s["turned"], 1)

        k.clear_signals()
        with nc.Fori(0, GROUPS) as g:
            s = k.signals(phase, "c_add", "added")
            k.next_loaded = k.flag(phase, "c_next_loaded")
            after = (g + 1) % GROUPS
            with nc.Block() as block:
                @block.vector
                def _(vec):
                    step = Steps(vec, s["vector_step"])
                    step(nc.vector.tensor_tensor(k.xg[:].rearrange("p t d -> p (t d)"), kept_group(k.x_all, g), sums[:, 0, :, :].rearrange("p t d -> p (t d)"), ADD))
                    for j in range(1, PER):
                        step(nc.vector.tensor_tensor(k.xg[:], k.xg[:], sums[:, j, :, :], ADD), s["added"] if j == PER - 1 else None)

                @block.sync
                def _(sp):
                    sp.wait_ge(s["added"], 1)
                    for j in range(PER):
                        sp.dma_start(sums[:, j, :, :], token_group(dram[f"sums_{j}"], after)).then_inc(k.next_loaded, 16)

            l2_xattn(k, phase, w, rowv, colv, bc[:], context_group(dram, after))
            self_attn(k, phase, "l2a", w["l2a_q"], w["l2a_k"], w["l2a_v"], w["l2a_u"], D ** -0.5, rowv["l2a_bu"])
            l2_norm_out(k, phase, kept_group(k.x_all, g), kept_group(k.xt_all, g), largest)
            k.clear_signals()


ROUND = 1.5 * 2.0 ** 23
ACT_MAX = 2.0 ** 15 - 1.0
SIG_STEPS = 65536.0
BLOCK2, W_MAX = 32, 7.0
CH2 = I2 // P
STEP = 4


def quantise(k, step, out, x, inverse, scale, signal=None):
    v = k.nc.vector
    step(v.tensor_scalar(out, x, inverse, ROUND, MUL, ADD))
    step(v.tensor_scalar(out, out, ROUND, scale, SUB, MUL), signal)


def quantise_weights(k, phase, dram, up, gate, down):
    nc, ps = k.nc, k.ps
    s = k.signals(phase, "l2w", "loaded", "quantised", "turned")
    with ExitStack() as own, nc.Block() as block:
        blocks = CH2 * P // BLOCK2
        wt = tile(k, own, "l2w", P, 3, blocks, BLOCK2)
        sc = tile(k, own, "l2w_scale", P, 3, blocks)
        inv = tile(k, own, "l2w_inverse", P, 3, blocks)

        @block.sync
        def _(sp):
            for i, name in enumerate(("l2f_up", "l2f_gate", "l2f_down")):
                sp.dma_start(wt[:, i, :, :].rearrange("p b i -> p (b i)"), dram[name]).then_inc(s["loaded"], 16)

        @block.vector
        def _(vec):
            step = Steps(vec, s["vector_step"])
            vec.wait_ge(s["loaded"], 48)
            w3 = wt[:].rearrange("p a b i -> p (a b) i")
            s2, i2 = sc[:].rearrange("p a b -> p (a b)"), inv[:].rearrange("p a b -> p (a b)")
            step(nc.vector.reduce_max(s2, w3, X, apply_absolute_value=True))
            step(nc.vector.tensor_scalar(s2, s2, 1.0 / W_MAX, 1e-12, MUL, MAX))
            step(nc.vector.reciprocal(i2, s2))
            wide = (P, 3 * blocks, BLOCK2)
            step(nc.vector.tensor_tensor(w3, w3, over(i2.unsqueeze(2), wide), MUL))
            step(nc.vector.tensor_scalar(w3, w3, ROUND, ROUND, ADD, SUB))
            step(nc.vector.tensor_scalar(w3, w3, -W_MAX - 1.0, W_MAX, MAX, MIN))
            step(nc.vector.tensor_tensor(w3, w3, over(s2.unsqueeze(2), wide), MUL), s["quantised"])
            vec.wait_ge(s["turned"], 1)
            for i, dst in enumerate((up, gate, down)):
                step(nc.vector.tensor_copy(dst, ps[:, i, 0:I2]))

        @block.tensor
        def _(pe):
            pe.wait_ge(s["quantised"], 1)
            for i in range(3):
                for c in range(CH2):
                    last = nc.tensor.transpose(ps[:, i, c * P:(c + 1) * P], wt[:, i, c * 4:(c + 1) * 4, :].rearrange("p b i -> p (b i)"), k.ident)
            last.then_inc(s["turned"], 1)


def scale_of_largest(k, phase, name, columns, scales):
    nc, ps = k.nc, k.ps
    s = k.signals(phase, name, "turned", "found", "spread")
    n = len(columns)
    with ExitStack() as own, nc.Block() as block:
        one = tile(k, own, name + "_one", 1, n)

        @block.tensor
        def _(pe):
            for i, column in enumerate(columns):
                last = nc.tensor.transpose(ps[0:1, 0, i * P:(i + 1) * P], column, k.ident)
            last.then_inc(s["turned"], 1)
            pe.wait_ge(s["found"], 1)
            nc.tensor.matmul(ps[:, 1, 0:n], k.ones[0:1, :], one[:], start=True, stop=True).then_inc(s["spread"], 1)

        @block.vector
        def _(vec):
            step = Steps(vec, s["vector_step"])
            vec.wait_ge(s["turned"], 1)
            step(nc.vector.reduce_max(one[:], ps[0:1, 0, 0:n * P].rearrange("p (n q) -> p n q", n=n), X), s["found"])
            vec.wait_ge(s["spread"], 1)
            step(nc.vector.tensor_scalar(scales[:, 0, 0:n], ps[:, 1, 0:n], 1.0 / ACT_MAX, 1e-12, MUL, MAX))
            step(nc.vector.reciprocal(scales[:, 1, 0:n], scales[:, 0, 0:n]))


def phase_d(k, dram, largest):
    nc, ps = k.nc, k.ps
    with ExitStack() as phase:
        wup, wgate = tile(k, phase, "l2f_up_t", P, I2), tile(k, phase, "l2f_gate_t", P, I2)
        wdown = tile(k, phase, "l2f_down_t", P, CH2, D)
        up = tile(k, phase, "l2f_up", P, GROUPS, CH2 * GT)
        gate = tile(k, phase, "l2f_gate", P, GROUPS, CH2 * GT)
        big = tile(k, phase, "l2f_largest", P, 2)
        new = tile(k, phase, "l2f_largest_here", P, 2)
        scales = tile(k, phase, "l2f_scales", P, 4, 2, 2)
        quantise_weights(k, phase, dram, wup[:], wgate[:], wdown[:].rearrange("p c d -> p (c d)"))
        scale_of_largest(k, phase, "l2f_x_scale", (largest,), scales[:, 0, :, :])

        def clear_largest(name):
            s = k.signals(phase, name, "cleared")
            with nc.Block() as block:
                @block.vector
                def _(vec):
                    Steps(vec, s["vector_step"])(nc.vector.memset(big[:], 0.0), s["cleared"])

        def scale(n, kind, column):
            return scales[:, n, kind, column:column + 1]

        clear_largest("l2f_clear_ug")
        k.clear_signals()
        with nc.Fori(0, GROUPS // STEP) as n:
            s = k.signals(phase, "l2f_ug", "xq_ready", "psum", "copied", "measured")
            with ExitStack() as own, nc.Block() as block:
                xq = tile(k, own, "l2f_xq", P, STEP, GT)
                one = [kept_group(k.xt_all, n * STEP + g) for g in range(STEP)]
                sides = [(g, i) for g in range(STEP) for i in range(2)]

                @block.vector
                def _(vec):
                    step = Steps(vec, s["vector_step"])
                    for g in range(STEP):
                        quantise(k, step, xq[:, g, :], one[g], scale(0, 1, 0), scale(0, 0, 0), s["xq_ready"])
                    for m, (g, i) in enumerate(sides):
                        vec.wait_ge(s["psum"], m + 1)
                        step(nc.vector.reduce_max(new[:, i:i + 1], ps[:, i * CH2:(i + 1) * CH2, :].rearrange("p c n -> p (c n)"), X, apply_absolute_value=True), s["measured"])
                        step(nc.vector.tensor_tensor(big[:, i:i + 1], big[:, i:i + 1], new[:, i:i + 1], MAX))

                @block.scalar
                def _(act):
                    step = Steps(act, s["scalar_step"])
                    for m, (g, i) in enumerate(sides):
                        act.wait_ge(s["measured"], m + 1)
                        step(nc.scalar.activation(kept_group((up, gate)[i], n * STEP + g),
                                                  ps[:, i * CH2:(i + 1) * CH2, :].rearrange("p c n -> p (c n)"), ACT.Copy), s["copied"])

                @block.tensor
                def _(pe):
                    for m, (g, i) in enumerate(sides):
                        pe.wait_ge(s["xq_ready"], g + 1)
                        if m >= 2:
                            pe.wait_ge(s["copied"], m - 1)
                        for c in range(CH2):
                            last = nc.tensor.matmul(ps[:, i * CH2 + c, :], (wup, wgate)[i][:, c * P:(c + 1) * P], xq[:, g, :], start=True, stop=True)
                        last.then_inc(s["psum"], 1)
            k.clear_signals()
        scale_of_largest(k, phase, "l2f_ug_scale", (big[:, 0:1], big[:, 1:2]), scales[:, 1, :, :])

        clear_largest("l2f_clear_act")
        k.clear_signals()
        with nc.Fori(0, GROUPS // STEP) as n:
            s = k.signals(phase, "l2f_act", "gate_ready", "sig_ready")
            with ExitStack() as own, nc.Block() as block:
                sig = tile(k, own, "l2f_sigmoid", P, 2, CH2 * GT)
                us, gts = ([kept_group(a, n * STEP + g) for g in range(STEP)] for a in (up, gate))

                @block.vector
                def _(vec):
                    step = Steps(vec, s["vector_step"])

                    def finish(g):
                        vec.wait_ge(s["sig_ready"], g + 1)
                        sg = sig[:, g % 2, :]
                        step(nc.vector.tensor_scalar(sg, sg, SIG_STEPS, ROUND, MUL, ADD))
                        step(nc.vector.tensor_scalar(sg, sg, ROUND, SIG_STEPS - 1.0, SUB, MIN))
                        step(nc.vector.scalar_tensor_tensor(gts[g], sg, 1.0 / SIG_STEPS, gts[g], MUL, MUL))
                        step(nc.vector.reduce_max(new[:, 0:1], gts[g], X, apply_absolute_value=True))
                        step(nc.vector.tensor_tensor(big[:, 0:1], big[:, 0:1], new[:, 0:1], MAX))

                    for g in range(STEP):
                        quantise(k, step, gts[g], gts[g], scale(1, 1, 1), scale(1, 0, 1), s["gate_ready"])
                        if g > 0:
                            finish(g - 1)
                        quantise(k, step, us[g], us[g], scale(1, 1, 0), scale(1, 0, 0))
                    finish(STEP - 1)

                @block.scalar
                def _(act):
                    for g in range(STEP):
                        act.wait_ge(s["gate_ready"], g + 1)
                        nc.scalar.activation(sig[:, g % 2, :], gts[g], ACT.Sigmoid).then_inc(s["sig_ready"], 1)
            k.clear_signals()
        scale_of_largest(k, phase, "l2f_act_scale", (big[:, 0:1],), scales[:, 2, :, :])

        clear_largest("l2f_clear_o")
        k.clear_signals()
        with nc.Fori(0, GROUPS // STEP) as n:
            s = k.signals(phase, "l2f_mul")
            with nc.Block() as block:
                @block.vector
                def _(vec):
                    step = Steps(vec, s["vector_step"])
                    for g in range(STEP):
                        u, gt = kept_group(up, n * STEP + g), kept_group(gate, n * STEP + g)
                        quantise(k, step, gt, gt, scale(2, 1, 0), scale(2, 0, 0))
                        step(nc.vector.tensor_tensor(gt, gt, u, MUL))
                        step(nc.vector.reduce_max(new[:, 0:1], gt, X, apply_absolute_value=True))
                        step(nc.vector.tensor_tensor(big[:, 0:1], big[:, 0:1], new[:, 0:1], MAX))
            k.clear_signals()
        scale_of_largest(k, phase, "l2f_o_scale", (big[:, 0:1],), scales[:, 3, :, :])

        k.clear_signals()
        with nc.Fori(0, GROUPS // STEP) as n:
            s = k.signals(phase, "l2f_down", "oq_ready", "psum")
            with ExitStack() as own, nc.Block() as block:
                oq = tile(k, own, "l2f_oq", P, 2, CH2, GT)

                @block.vector
                def _(vec):
                    step = Steps(vec, s["vector_step"])

                    def add(g):
                        vec.wait_ge(s["psum"], g + 1)
                        x = kept_group(k.x_all, n * STEP + g)
                        step(nc.vector.tensor_tensor(x, x, ps[:, g, :], ADD))

                    for g in range(STEP):
                        quantise(k, step, oq[:, g % 2, :, :].rearrange("p c n -> p (c n)"), kept_group(gate, n * STEP + g), scale(3, 1, 0), scale(3, 0, 0), s["oq_ready"])
                        if g > 0:
                            add(g - 1)
                    add(STEP - 1)

                @block.tensor
                def _(pe):
                    for g in range(STEP):
                        pe.wait_ge(s["oq_ready"], g + 1)
                        for t in range(T):
                            for c in range(CH2):
                                last = nc.tensor.matmul(ps[:, g, t * D:(t + 1) * D], oq[:, g % 2, c, t * P:(t + 1) * P], wdown[:, c, :], start=c == 0, stop=c == CH2 - 1)
                        last.then_inc(s["psum"], 1)
            k.clear_signals()


CHUNKS = GB * S2
Q = 4


def l3_xattn(k, phase, w, rowv, colv, x_kept, next_ctxt, next_mask):
    nc, ps = k.nc, k.ps
    s = k.signals(phase, "l3x", *NORM, "q_psum", "qx_ready", "kt_psum", "kt_ready", "v_psum", "v_ready", "last_psum", "last_ready", "masks_ready",
                  "scores", "top_ready", "exps", "p_ready", "last_turned", "turned", "ptl_ready", "pt_ready", "o_psum", "om_ready", "o_ready", "z_psum", "residual")
    scale = DH ** -0.5
    with ExitStack() as own, nc.Block() as block:
        k.qx = tile(k, own, "l3x_q_by_head", P, GB, 4, L)
        kt = tile(k, own, "l3x_kt", P, GB, S2)
        v = tile(k, own, "l3x_v", P, GB, 2, D)
        vl = tile(k, own, "l3x_v_last", Q, GB, D)
        sc = tile(k, own, "l3x_scores", P, 2, Q, S2)
        st = tile(k, own, "l3x_stats", P, 2, 3, Q)
        pt = tile(k, own, "l3x_pt", P, 2, 2, Q, P)
        ptl = tile(k, own, "l3x_pt_last", Q, 2, P)
        om = tile(k, own, "l3x_om", P, 4, L)
        k.ot = tile(k, own, "l3x_ot", P, GT)
        ktf = kt[:].rearrange("p b s -> p (b s)")
        ctf = k.ctxt[:].rearrange("p b s -> p (b s)")
        strips = [(i, min(512, CHUNKS - i)) for i in range(0, CHUNKS, 512)]

        @block.sync
        def _(sp):
            sp.wait_ge(s["masks_ready"], 1)
            for h in range(4):
                sp.dma_start(k.maski[L * h:L * h + L, :, :], next_mask).then_inc(k.next_loaded, 16)
            sp.wait_ge(s["kt_psum"], len(strips))
            sp.dma_start(k.ctxt[:], next_ctxt).then_inc(k.next_loaded, 16)

        @block.gpsimd
        def _(pool):
            nc.gpsimd.tensor_scalar(k.maskf[:], k.maski[:], 0.0, -1e9 / scale, EQ, MUL).then_inc(s["masks_ready"], 1)

        @block.vector
        def _(vec):
            step = Steps(vec, s["vector_step"])
            step(nc.vector.tensor_copy(k.xg[:].rearrange("p t d -> p (t d)"), x_kept))
            norm_vector(k, vec, step, s)
            q_by_head(k, vec, step, s, bias=colv["l3x_bq"])
            for i in range(4):
                vec.wait_ge(s["v_psum"], 2 * i + 2)
                step(nc.vector.tensor_copy(v[:, 4 * i:4 * i + 4, :, :].rearrange("p b c d -> p (b c d)"), ps[:, 4 + 2 * (i % 2):6 + 2 * (i % 2), :].rearrange("p a n -> p (a n)")), s["v_ready"])
            vec.wait_ge(s["last_psum"], 1)
            step(nc.vector.tensor_tensor(vl[:], ps[0:Q, 0:4, :].rearrange("p a (b d) -> p (a b) d", d=D), over(k.quad_cols[0:Q, :].unsqueeze(1), (Q, GB, D)), MUL), s["last_ready"])
            vec.wait_ge(s["masks_ready"], 1)
            for i in range(GB + 2):
                if 1 <= i <= GB:
                    h = (i - 1) % 2
                    vec.wait_ge(s["exps"], Q * i)
                    step(nc.vector.reciprocal(st[:, h, 2, :], st[:, h, 1, :]))
                    step(nc.vector.tensor_tensor(sc[:, h, :, :], sc[:, h, :, :], over(st[:, h, 2, :].unsqueeze(2), (P, Q, S2)), MUL), s["p_ready"])
                if i < GB:
                    vec.wait_ge(s["scores"], i + 1)
                    for c in range(Q):
                        step.free(nc.vector.tensor_tensor_reduce(out=sc[:, i % 2, c, :], in0=ps[:, c, 0:S2], in1=k.maskf[:, i, :], scale=scale, scalar=LOWEST,
                                                                 op0=ADD, op1=MAX, accum_out=st[:, i % 2, 0, c:c + 1]))
                    step.settled()
                    step(nc.vector.tensor_scalar(st[:, i % 2, 0, :], st[:, i % 2, 0, :], -1.0, None, MUL), s["top_ready"])
                if i >= 2:
                    vec.wait_ge(s["o_psum"], i - 1)
                    step(nc.vector.tensor_tensor(om[:], ps[:, 6, 0:D].rearrange("p (h n) -> p h n", n=L), over(k.quad_head.unsqueeze(2), (P, 4, L)), MUL), s["om_ready"])
                    step(nc.vector.reduce_sum(k.ot[:, (i - 2) * L:(i - 1) * L], om[:].rearrange("p h n -> p n h"), X), s["o_ready"])
            add_projection(k, vec, step, s, CORE_BANKS, rowv["l3x_bo"])

        @block.scalar
        def _(act):
            step = Steps(act, s["scalar_step"])
            for n, (at, width) in enumerate(strips):
                act.wait_ge(s["kt_psum"], n + 1)
                step(nc.scalar.activation(ktf[:, at:at + width], ps[:, 2 + n % 2, 0:width], ACT.Identity, bias=colv["l3x_bq"]), s["kt_ready"])
            norm_scalar(k, act, step, s)
            for i in range(GB + 1):
                if i > 0:
                    h = (i - 1) % 2
                    act.wait_ge(s["last_turned"], i)
                    step(nc.scalar.activation(ptl[:, h, :], ps[0:Q, 6, P:2 * P], ACT.Copy), s["ptl_ready"])
                    act.wait_ge(s["turned"], i)
                    step(nc.scalar.activation(pt[:, h, :, :, :].rearrange("p i c n -> p (i c n)"), ps[:, 4:6, :].rearrange("p i n -> p (i n)"), ACT.Copy), s["pt_ready"])
                if i < GB:
                    act.wait_ge(s["top_ready"], i + 1)
                    for c in range(Q):
                        step.free(nc.scalar.activation(sc[:, i % 2, c, :], sc[:, i % 2, c, :], ACT.Exp, bias=st[:, i % 2, 0, c:c + 1],
                                                       accum_out=st[:, i % 2, 1, c:c + 1]), s["exps"])
                    step.settled(s["exps"])

        @block.tensor
        def _(pe):
            for n, (at, width) in enumerate(strips):
                if n >= 2:
                    pe.wait_ge(s["kt_ready"], n - 1)
                nc.tensor.matmul(ps[:, 2 + n % 2, 0:width], w["l3x_q"], ctf[:, at:at + width], start=True, stop=True).then_inc(s["kt_psum"], 1)
            norm_tensor(k, pe, s)
            pe.wait_ge(s["xt_ready"], 1)
            nc.tensor.matmul(ps[:, 1, :], w["l3x_q"], k.xt[:], start=True, stop=True).then_inc(s["q_psum"], 1)
            pe.wait_ge(s["kt_ready"], len(strips))
            for n in range(GB // 2):
                if n >= 4 and n % 2 == 0:
                    pe.wait_ge(s["v_ready"], n // 2 - 1)
                for j in range(2):
                    for i in range(2):
                        last = nc.tensor.transpose(ps[:, 4 + n % 4, (2 * j + i) * P:(2 * j + i + 1) * P], kt[:, 2 * n + j, i * P:(i + 1) * P], k.ident)
                last.then_inc(s["v_psum"], 1)
            pe.wait_ge(s["qx_ready"], 4)
            for b in range(GB):
                last = nc.tensor.matmul(ps[0:Q, b // 4, (b % 4) * D:(b % 4 + 1) * D], over(kt[:, b, S2 - 1:S2], (P, Q)), k.ident, start=True, stop=True)
            last.then_inc(s["last_psum"], 1)
            pe.wait_ge(s["last_ready"], 1)
            pe.wait_ge(s["v_ready"], 4)

            def scores(b):
                if b > 0:
                    pe.wait_ge(s["top_ready"], b)
                for c in range(Q):
                    r = slice(L * c, L * c + L)
                    last = nc.tensor.matmul(ps[:, c, 0:S2], k.qx[r, b, :, :].rearrange("p h n -> p (h n)"), kt[r, b, :], start=True, stop=True)
                last.then_inc(s["scores"], 1)

            def turn(b):
                pe.wait_ge(s["p_ready"], b + 1)
                if b > 1:
                    pe.wait_ge(s["om_ready"], b - 1)
                nc.tensor.transpose(ps[0:Q, 6, P:2 * P], sc[:, b % 2, :, 2 * P], k.ident).then_inc(s["last_turned"], 1)
                if b > 0:
                    pe.wait_ge(s["pt_ready"], b)
                for c in range(Q):
                    for i in range(2):
                        last = nc.tensor.transpose(ps[:, 4 + i, c * P:(c + 1) * P], sc[:, b % 2, c, i * P:(i + 1) * P], k.ident)
                last.then_inc(s["turned"], 1)

            def outputs(b):
                pe.wait_ge(s["pt_ready"], b + 1)
                if b > 0:
                    pe.wait_ge(s["om_ready"], b)
                pe.wait_ge(s["ptl_ready"], min(b + 2, GB))
                nc.tensor.matmul(ps[:, 6, 0:D], vl[:, b, :], ptl[:, b % 2, :], start=True, stop=False)
                for i in range(2):
                    for c in range(Q):
                        r = slice(L * c, L * c + L)
                        last = nc.tensor.matmul(ps[r, 6, 0:D], v[:, b, i, r], pt[:, b % 2, i, c, :], start=False, stop=i == 1)
                last.then_inc(s["o_psum"], 1)

            scores(0)
            for b in range(GB):
                if b + 1 < GB:
                    scores(b + 1)
                turn(b)
                if b > 0:
                    outputs(b - 1)
            outputs(GB - 1)
            pe.wait_ge(s["o_ready"], GB)
            project(k, pe, s, w["l3x_o"], CORE_BANKS)


def l3_ffn(k, phase, up_w, up_b, down_w, rowv, store):
    nc, ps = k.nc, k.ps
    s = k.signals(phase, "l3f", *NORM, "hidden_psum", "hidden_ready", "z_psum", "residual", "stored")
    with ExitStack() as own, nc.Block() as block:
        hid = tile(k, own, "l3f_hidden", P, 4, GT)

        @block.vector
        def _(vec):
            step = Steps(vec, s["vector_step"])
            norm_vector(k, vec, step, s)
            step(nc.vector.tensor_tensor(k.xg[:], k.xg[:], over(rowv["l3f_bd"].unsqueeze(1), (P, T, D)), ADD))
            add_projection(k, vec, step, s, (5, 6, 7, 0), rowv["l3f_bc"], parts=False)

        @block.scalar
        def _(act):
            step = Steps(act, s["scalar_step"])
            norm_scalar(k, act, step, s)
            for c in range(4):
                act.wait_ge(s["hidden_psum"], c + 1)
                step(nc.scalar.activation(hid[:, c, :], ps[:, 1 + c, :], ACT.Gelu, bias=up_b[:, c:c + 1]), s["hidden_ready"])

        @block.tensor
        def _(pe):
            norm_tensor(k, pe, s)
            pe.wait_ge(s["xt_ready"], 1)
            for c in range(4):
                nc.tensor.matmul(ps[:, 1 + c, :], up_w[:, c * P:(c + 1) * P], k.xt[:], start=True, stop=True).then_inc(s["hidden_psum"], 1)
            pe.wait_ge(s["hidden_ready"], 4)
            for t in range(T):
                for c in range(4):
                    last = nc.tensor.matmul(ps[:, (5, 6, 7, 0)[t], 0:D], hid[:, c, t * P:(t + 1) * P], down_w[:, c, :], start=c == 0, stop=c == 3)
                last.then_inc(s["z_psum"], 1)

        @block.sync
        def _(sp):
            sp.wait_ge(s["residual"], T)
            sp.dma_start(store, k.xg[:]).then_inc(s["stored"], 16)
            sp.wait_ge(s["stored"], 16)
            sp.wait_ge(k.next_loaded, 16 * 5)


def phase_e(k, dram):
    nc = k.nc
    with ExitStack() as phase:
        wp = tile(k, phase, "e_weights", P, len(E_MATS), D)
        rp = tile(k, phase, "e_rows", P, len(E_ROWS), D)
        cp = tile(k, phase, "e_cols", P, len(E_COLS))
        w = {n: wp[:, i, :] for i, n in enumerate(E_MATS)}
        rowv = {n: rp[:, i, :] for i, n in enumerate(E_ROWS)}
        colv = {n: cp[:, i:i + 1] for i, n in enumerate(E_COLS)}
        k.ctxt = tile(k, phase, "e_ctx_t", P, GB, S2)
        k.maski = tile(k, phase, "e_mask", P, GB, S2, dtype=I32)
        mask_group = lambda g: dram["mask_i32"].rearrange("q (g b s) -> g q b s", g=GROUPS, b=GB)[g]
        loaded = k.flag(phase, "e_weights_loaded")
        k.first_loaded = k.flag(phase, "e_first_loaded")
        with nc.Block() as block:
            @block.sync
            def _(sp):
                for dst, name in ((wp, "e_mats"), (cp, "e_cols")):
                    sp.dma_start(dst[:], dram[name]).then_inc(loaded, 16)
                sp.dma_start(rp[:], dram["e_rows"].partition_broadcast(P)).then_inc(loaded, 16)
                sp.dma_start(k.ctxt[:], context_group(dram, 0)[0]).then_inc(k.first_loaded, 16)
                for h in range(4):
                    sp.dma_start(k.maski[L * h:L * h + L, :, :], mask_group(0)).then_inc(k.first_loaded, 16)
                sp.wait_ge(loaded, 48)
                sp.wait_ge(k.first_loaded, 80)
        k.maskf = tile(k, phase, "e_mask_added", P, GB, S2)
        k.clear_signals()
        with nc.Fori(0, GROUPS) as g:
            k.next_loaded = k.flag(phase, "e_next_loaded")
            after = (g + 1) % GROUPS
            l3_xattn(k, phase, w, rowv, colv, kept_group(k.x_all, g), context_group(dram, after)[0], mask_group(after))
            self_attn(k, phase, "l3a", w["l3a_q"], w["l3a_k"], w["l3a_v"], w["l3a_p"], DH ** -0.5)
            l3_ffn(k, phase, k.up_w, k.up_b, k.down_w, rowv, token_group(dram["out"], g))
            k.clear_signals()
A_MATS = ["l0x_q", "l0x_k", "l0x_v", "l0x_c", "l0a_q", "l0a_k", "l0a_v", "l0a_o", "l1x_q", "l1x_k", "l1x_v", "l1x_o",
          "l1a_q", "l1a_k", "l1a_v", "l1a_p"]
A_ROWS = ["l0a_bv", "l0a_bo", "l1x_bk", "l1x_bv", "l1x_bo", "l1x_g", "l1x_b", "l1a_bp"]
A_COLS = ["l0a_bq", "l0a_bk", "l1x_bq", "l1x_bk", "l1a_w0", "l1a_w1", "l1a_w2", "l1a_bc"]
C_MATS = ["l2a_q", "l2a_k", "l2a_v", "l2a_u"]
C_ROWS = ["l2x_bl", "l2a_bu"]
C_COLS = ["l2x_wcq", "l2x_wq", "l2x_wc"]
E_MATS = ["l3x_q", "l3x_o", "l3a_q", "l3a_k", "l3a_v", "l3a_p"]
E_ROWS = ["l3x_bo", "l3f_bc", "l3f_bd"]
E_COLS = ["l3x_bq"]
CONSTS = {"ident": P, "same_head": P, "v_heads": P, "earlier": P, "causal": L, "quad_head": 4, "tile_batch": 4, "countdown": E0,
          "count4": CAP0, "row_base": T, "fold": L, "quad_cols": P, "ones": P, "same_batch": P}


def constants():
    p = np.arange(P)[:, None]
    c = np.arange(P)[None, :]
    made = {
        "ident": p == c,
        "same_head": p // DH == c // DH,
        "v_heads": p // L == (c // DH) % 4,
        "earlier": (p // L == c // L) & (p < c),
        "causal": np.where(p % L > np.arange(L)[None, :], NEG, 0.0),
        "quad_head": (p // DH) % 4 == np.arange(4)[None, :],
        "tile_batch": p // L == np.arange(4)[None, :],
        "countdown": np.broadcast_to(E0 - np.arange(E0)[None, :], (P, E0)),
        "count4": np.broadcast_to(np.arange(CAP0)[None, :], (P, CAP0)),
        "row_base": (np.arange(T)[None, :] * BPT + p // L) * S2,
        "quad_cols": p == c // L,
        "ones": np.ones((P, P)),
        "same_batch": p // L == c // L,
        "fold": p % L == np.arange(L)[None, :],
    }
    return np.concatenate([made[n].astype(np.float32) for n in CONSTS], axis=1)


def layout(i):
    st = lambda a: np.ascontiguousarray(a)
    ctx = i["ctx_1024"].reshape(NB * S2, D)
    with_one = np.concatenate([i["ctx_1024"], np.ones((NB, S2, 1), np.float32)], axis=2)
    wkv = i["L0_xattn_Wkv"]
    w5 = i["L1_attn_w_qkv"]
    def by_head(a):
        out = np.zeros((H, DH, H, DH), np.float32)
        for h in range(H):
            out[h, :, h, :] = a.T
        return out.reshape(D, D)

    def by_place(a):
        return a.reshape(-1, 4, 4, DH).transpose(0, 2, 1, 3).reshape(-1, D)

    wa = i["L3_attn_w_attn"]
    mats = {"l3x_q": i["L3_xattn_Wq"].T, "l3x_o": i["L3_xattn_Wo"].T, "l3a_q": wa[:D].T, "l3a_k": wa[D:2 * D].T, "l3a_v": by_place(wa[2 * D:].T),
            "l3a_p": by_place(i["L3_attn_w_proj"]).T,
            "l2a_q": by_head(i["L2_attn_Wq"]), "l2a_k": by_head(i["L2_attn_Wk"]), "l2a_v": by_place(by_head(i["L2_attn_Wv"])), "l2a_u": by_place(i["L2_attn_Wu"]).T,
            "l0x_q": i["L0_xattn_Wq"].T, "l0x_k": np.tile(wkv[:DH].T, (1, H)), "l0x_v": by_place(np.tile(wkv[DH:].T, (1, H))), "l0x_c": by_place(i["L0_xattn_Wc"]).T,
            "l0a_q": i["L0_attn_Wq"], "l0a_k": i["L0_attn_Wk"], "l0a_v": i["L0_attn_Wv"], "l0a_o": i["L0_attn_Wo"],
            "l1x_q": i["L1_xattn_wq_w"].T, "l1x_k": i["L1_xattn_wk_w"].T, "l1x_v": i["L1_xattn_wv_w"].T, "l1x_o": i["L1_xattn_wo_w"].T,
            "l1a_q": w5[:D].T, "l1a_k": w5[D:2 * D].T, "l1a_v": w5[2 * D:].T, "l1a_p": i["L1_attn_w_proj"].T}
    rows = {"l3x_bo": i["L3_xattn_bo"], "l3f_bc": i["L3_ffn_b_con"], "l3f_bd": i["L3_ffn_down_bias"],
            "l2x_bl": i["L2_xattn_b_l"], "l2a_bu": i["L2_attn_bu"],
            "l0a_bv": i["L0_attn_bv"], "l0a_bo": i["L0_attn_bo"], "l1x_bk": i["L1_xattn_wk_b"], "l1x_bv": i["L1_xattn_wv_b"],
            "l1x_bo": i["L1_xattn_wo_b"], "l1x_g": i["L1_xattn_ln_g"], "l1x_b": i["L1_xattn_ln_b"], "l1a_bp": i["L1_attn_b_proj"]}
    cols = {"l3x_bq": i["L3_xattn_bq"],
            "l2x_wcq": i["L2_xattn_w_cq"], "l2x_wq": i["L2_xattn_w_q"], "l2x_wc": i["L2_xattn_w_c"],
            "l0a_bq": i["L0_attn_bq"], "l0a_bk": i["L0_attn_bk"], "l1x_bq": i["L1_xattn_wq_b"], "l1x_bk": i["L1_xattn_wk_b"],
            "l1a_w0": i["L1_attn_w_dwc"][:, 0], "l1a_w1": i["L1_attn_w_dwc"][:, 1], "l1a_w2": i["L1_attn_w_dwc"][:, 2], "l1a_bc": i["L1_attn_b_dwc"]}
    return {
        "x": st(i["x"].reshape(TOKENS, D)), "ctx": st(ctx), "ctx_t": st(ctx.T),
        "mask_bool": st(i["mask_Bx1xSxS2_bf0"].reshape(TOKENS, S2)),
        "ctx_rows": st(with_one[:, :2 * P].reshape(NB, 2, P, D + 1).transpose(2, 0, 1, 3)), "ctx_last": st(with_one[None, :, 2 * P]),
        "consts": constants(),
        "a_mats": st(np.stack([mats[n] for n in A_MATS], axis=1)),
        "a_rows": st(np.stack([rows[n] for n in A_ROWS])),
        "a_cols": st(np.stack([cols[n] for n in A_COLS], axis=1)),
        "c_mats": st(np.stack([mats[n] for n in C_MATS], axis=1)),
        "c_rows": st(np.stack([rows[n] for n in C_ROWS])),
        "c_cols": st(np.stack([cols[n] for n in C_COLS], axis=1)),
        "l2x_l": st(i["L2_xattn_W_l"].reshape(D, 4, D).transpose(2, 1, 0).reshape(D, 4 * D)),
        "l2x_biases": st(np.stack([i["L2_xattn_b_c"], i["L2_xattn_b_q"], i["L2_xattn_b_cq"]])),
        "l1f_w1": st(i["L1_ffn_W1"].transpose(2, 0, 1, 3)), "l1f_w2": st(i["L1_ffn_W2"].transpose(2, 0, 1, 3)),
        "l1f_b1": st(i["L1_ffn_b1"].reshape(E1 * S1, P).T), "l1f_b2": st(i["L1_ffn_b2"].reshape(E1, D)),
        "e_mats": st(np.stack([mats[n] for n in E_MATS], axis=1)),
        "e_rows": st(np.stack([rows[n] for n in E_ROWS])),
        "e_cols": st(np.stack([cols[n] for n in E_COLS], axis=1)),
        "mask_i32": st(i["mask_Bx1xSxS2_if1"].reshape(NB, L, S2).transpose(1, 0, 2).reshape(L, NB * S2)),
        "l3f_up": st(i["L3_ffn_up_weights"].reshape(STAGES, 2 * HID3)), "l3f_down": st(i["L3_ffn_down_weights"].reshape(STAGES, 2 * HID3)),
        "l3f_exp": st(i["L3_ffn_W_exp"]), "l3f_b_exp": st(i["L3_ffn_b_exp"]), "l3f_up_bias": st(i["L3_ffn_up_bias"].reshape(1, HID3)),
        "l3f_con": st(i["L3_ffn_W_con"].T),
        "l2f_up": st(i["L2_ffn_w_up"].reshape(CH2, P, D).transpose(1, 0, 2).reshape(P, I2)),
        "l2f_gate": st(i["L2_ffn_w_gate"].reshape(CH2, P, D).transpose(1, 0, 2).reshape(P, I2)), "l2f_down": st(i["L2_ffn_w_down"]),
        "l0f_g": st(i["L0_ffn_Wg"]), "l1f_r": st(i["L1_ffn_Wr"].T),
        "l0f_w1": st(i["L0_ffn_W1"].transpose(1, 0, 2)),
        "l0f_w2": st(i["L0_ffn_W2"].reshape(E0, 4, P, D).transpose(2, 0, 1, 3)),
    }


SCRATCH = {"xn_a": (TOKENS, D), "logits": (E1, TOKENS), **{f"sums_{j}": (TOKENS, D) for j in range(PER)}}


def build(nc, dram):
    k = Kit(nc)
    with ExitStack() as whole:
        consts = tile(k, whole, "const_tiles", P, sum(CONSTS.values()))
        ends = np.cumsum(list(CONSTS.values())).tolist()
        (k.ident, k.same_head, k.v_heads, k.earlier, k.causal, k.quad_head, k.tile_batch, k.countdown,
         k.count4, k.row_base, k.fold, k.quad_cols, k.ones, k.same_batch) = (consts[:, end - n:end] for end, n in zip(ends, CONSTS.values()))
        k.xg = tile(k, whole, "x_group", P, T, D)
        k.x_all = tile(k, whole, "x_all", P, GROUPS, T * D)
        k.x_next = tile(k, whole, "x_group_next", P, T, D)
        k.x_in = k.xg
        k.xn = tile(k, whole, "xn_group", P, T, D)
        k.xt = tile(k, whole, "xn_group_t", P, GT)
        k.stat = tile(k, whole, "stat", P, 2, T)
        k.parts = tile(k, whole, "stat_parts", P, T, 6)
        k.mv = tile(k, whole, "mean_variance", P, T, 2)
        k.parts_known = False
        k.up_w, k.up_b, k.down_w = tile(k, whole, "l3f_up_w", P, HID3), tile(k, whole, "l3f_up_b", P, 4), tile(k, whole, "l3f_down_w", P, 4, D)
        k.ps = whole.enter_context(nc.psum_tensor("ps", [P, 8, 512], F32))
        got = k.flag(whole, "consts_loaded")
        with nc.Block() as block:
            @block.sync
            def _(sp):
                sp.dma_start(consts[:], dram["consts"]).then_inc(got, 16)
                sp.wait_ge(got, 16)
        largest = tile(k, whole, "largest", P, 1)
        phase_a(k, dram)
        phase_b(k, dram)
        k.xt_all = tile(k, whole, "xn_all_t", P, GROUPS, GT)
        phase_c(k, dram, largest[:])
        phase_d(k, dram, largest[:])
        phase_e(k, dram)


def kernel(**inputs):
    import numpy as np
    import concourse.bacc as bacc
    from concourse.bass_utils import run_bass_kernel_spmd

    nc = bacc.Bacc("TRN2", target_bir_lowering=False, num_devices=1)
    arrays = layout({n: np.asarray(a) for n, a in inputs.items()})
    dram = {n: nc.dram_tensor("in_" + n, a.shape, mybir.dt.from_np(a.dtype), kind="ExternalInput").ap() for n, a in arrays.items()}
    dram.update({n: nc.dram_tensor("scratch_" + n, shape, F32, kind="Internal").ap() for n, shape in SCRATCH.items()})
    dram["out"] = nc.dram_tensor("out_x", (TOKENS, D), F32, kind="ExternalOutput").ap()
    build(nc, dram)
    r = run_bass_kernel_spmd(nc, [{"in_" + n: a for n, a in arrays.items()}], core_ids=[0])
    return r.results[0]["out_x"].reshape(NB, L, D)
```
